# Optimizing a Trainium2 kernel written in Bass

```python
import numpy as np
import jax
import jax.numpy as jnp

def _softmax(x, axis=-1):
    return jax.nn.softmax(x, axis=axis)

def _gelu(x):
    return jax.nn.gelu(x, approximate=True)

def _silu(x):
    return jax.nn.silu(x)

def _sigmoid(x):
    return jax.nn.sigmoid(x)

def _layernorm(x, axis=-1, eps=1e-05):
    m = jnp.mean(x, axis=axis, keepdims=True)
    v = jnp.var(x, axis=axis, keepdims=True)
    return (x - m) / jnp.sqrt(v + eps)

def _scatter_add(tgt, idx, src, axis=0):
    return tgt.at[idx].add(src)

def _segment_sum(src, seg, n):
    return jax.ops.segment_sum(src, seg, n)
kernel_name = 'mk_flamingo_gated_d4_seqx_r4_e79939'

def setup_inputs(seed: int=0):
    np.random.seed(seed)
    _w = jnp.asarray

    def _rec_inputs():
        import jax
        import jax.numpy as jnp
        _rk = jax.random.key(seed)
        x = -0.0003929 + 0.9999 * jax.random.normal(jax.random.fold_in(_rk, 1), (8, 256, 256), jnp.float32)
        _lenS = 256 - jax.random.randint(jax.random.fold_in(_rk, 7), (8,), 0, max(1, 256 // 4) + 1, jnp.int32)
        _lenS2 = 77 - jax.random.randint(jax.random.fold_in(_rk, 8), (8,), 0, max(1, 77 // 4) + 1, jnp.int32)
        _ctx_1024P = jax.random.normal(jax.random.fold_in(_rk, 11), (8, 16, 256), jnp.float32)
        _ctx_1024c = jax.random.dirichlet(jax.random.fold_in(_rk, 511), 0.3 * jnp.ones((16,), jnp.float32), (8, 77))
        _ctx_1024t = jnp.einsum('bsk,bkd->bsd', _ctx_1024c, _ctx_1024P)
        _ctx_1024t = _ctx_1024t * jax.lax.rsqrt(jnp.mean(jnp.square(_ctx_1024t)) + 1e-12) * 0.953939
        ctx_1024 = 2.81802e-05 + 1.00001 * (_ctx_1024t + 0.3 * jax.random.normal(jax.random.fold_in(_rk, 611), (8, 77, 256), jnp.float32))
        fside_BxS2_0 = -0.00600047 + 0.990131 * jax.random.normal(jax.random.fold_in(_rk, 12), (8, 77), jnp.float32)
        _validS = jnp.arange(256)[None, :] < _lenS[:, None]
        _validS2 = jnp.arange(77)[None, :] < _lenS2[:, None]
        _causal = jnp.tril(jnp.ones((256, 256), dtype=bool))
        mask_BxS2_bk0 = jnp.logical_not(jnp.broadcast_to(_validS2[:, :], (8, 77)))
        _g = jax.random.normal(jax.random.fold_in(_rk, 9001), (2, 4), jnp.float32)
        _g = jnp.sign(_g) * jnp.maximum(jnp.abs(_g), 1.0) + (_g == 0) * 1.0
        g_xattn = _g[0]
        g_ffn = _g[1]
        return (x, ctx_1024, fside_BxS2_0, mask_BxS2_bk0, g_xattn, g_ffn)
    x, ctx_1024, fside_BxS2_0, mask_BxS2_bk0, g_xattn, g_ffn = _rec_inputs()

    def _L0_xattn_setup():
        import jax, jax.numpy as jnp
        import numpy as np
        D = 256
        key = jax.random.key(seed)
        ks = jax.random.split(key, 9)
        B, Nq, Nk = (8, 512, 512)
        s = 1.0 / np.sqrt(D)
        return {'query': jax.random.normal(ks[0], (B, Nq, D), jnp.float32), 'key': jax.random.normal(ks[1], (B, Nk, D), jnp.float32), 'value': jax.random.normal(ks[2], (B, Nk, D), jnp.float32), 'Wq': jax.random.uniform(ks[3], (D, D), jnp.float32, -s, s), 'bq': jax.random.uniform(ks[4], (D,), jnp.float32, -s, s), 'Wk': jax.random.uniform(ks[5], (D, D), jnp.float32, -s, s), 'bk': jax.random.uniform(ks[6], (D,), jnp.float32, -s, s), 'Wv': jax.random.uniform(ks[7], (D, D), jnp.float32, -s, s), 'bv': jax.random.uniform(ks[8], (D,), jnp.float32, -s, s)}
    _L0_xattn_all = _L0_xattn_setup()
    _L0_xattn_in = {k: v for k, v in _L0_xattn_all.items() if k in ('Wq', 'bq', 'Wk', 'bk', 'Wv', 'bv')}
    del _L0_xattn_all

    def _L0_ffn_setup():
        import jax, jax.numpy as jnp
        import numpy as np
        DIM = 256
        INTER = 256
        N_EXPERTS = 8
        TOPK = 2
        N_SHARED = 2
        key = jax.random.key(seed)
        ks = jax.random.split(key, 10)
        s = 0.02
        return {'x': jax.random.normal(ks[0], (4, 512, DIM), dtype=jnp.float32), 'gate_w': jax.random.normal(ks[1], (N_EXPERTS, DIM), dtype=jnp.float32) * s, 'gate_bias': jax.random.normal(ks[2], (N_EXPERTS,), dtype=jnp.float32) * s, 'w1': jax.random.normal(ks[3], (N_EXPERTS, INTER, DIM), dtype=jnp.float32) * s, 'w3': jax.random.normal(ks[4], (N_EXPERTS, INTER, DIM), dtype=jnp.float32) * s, 'w2': jax.random.normal(ks[5], (N_EXPERTS, DIM, INTER), dtype=jnp.float32) * s, 'sw1': jax.random.normal(ks[6], (N_SHARED * INTER, DIM), dtype=jnp.float32) * s, 'sw3': jax.random.normal(ks[7], (N_SHARED * INTER, DIM), dtype=jnp.float32) * s, 'sw2': jax.random.normal(ks[8], (DIM, N_SHARED * INTER), dtype=jnp.float32) * s}
    _L0_ffn_all = _L0_ffn_setup()
    _L0_ffn_in = {k: v for k, v in _L0_ffn_all.items() if k in ('gate_w', 'gate_bias', 'w1', 'w3', 'w2', 'sw1', 'sw3', 'sw2')}
    del _L0_ffn_all

    def _L1_xattn_setup():
        import jax, jax.numpy as jnp
        import numpy as np
        EMBED = 256
        NHEAD = 16
        HEAD_DIM = EMBED // NHEAD
        key = jax.random.key(seed)
        ks = jax.random.split(key, 8)
        B, SQ, SKV = (2, 512, 512)
        scale = 1.0 / np.sqrt(EMBED)
        return {'query': jax.random.normal(ks[0], (B, SQ, EMBED), dtype=jnp.float32), 'key': jax.random.normal(ks[1], (B, SKV, EMBED), dtype=jnp.float32), 'value': jax.random.normal(ks[2], (B, SKV, EMBED), dtype=jnp.float32), 'attention_bias': jax.random.normal(ks[3], (B, SKV), dtype=jnp.float32), 'Wq': jax.random.normal(ks[4], (EMBED, EMBED), dtype=jnp.float32) * scale, 'Wk': jax.random.normal(ks[5], (EMBED, EMBED), dtype=jnp.float32) * scale, 'Wv': jax.random.normal(ks[6], (EMBED, EMBED), dtype=jnp.float32) * scale, 'Wo': jax.random.normal(ks[7], (EMBED, EMBED), dtype=jnp.float32) * scale}
    _L1_xattn_all = _L1_xattn_setup()
    _L1_xattn_in = {k: v for k, v in _L1_xattn_all.items() if k in ('Wq', 'Wk', 'Wv', 'Wo')}
    del _L1_xattn_all

    def _L1_ffn_setup():
        import jax, jax.numpy as jnp
        import numpy as np
        B, S, D, F, E = (8, 256, 256, 1024, 8)
        EPS = 1e-05
        key = jax.random.key(seed)
        ks = jax.random.split(key, 4)
        s = 0.02
        return {'input_features': jax.random.normal(ks[0], (B, S, D), jnp.float32), 'centroids': jax.random.normal(ks[1], (E, D), jnp.float32) * 0.1, 'ln_g': jnp.ones((E, D), jnp.float32), 'ln_b': jnp.zeros((E, D), jnp.float32), 'w1': jax.random.normal(ks[2], (E, D, F), jnp.float32) * s, 'b1': jnp.zeros((E, F), jnp.float32), 'w2': jax.random.normal(ks[3], (E, F, D), jnp.float32) * s, 'b2': jnp.zeros((E, D), jnp.float32)}
    _L1_ffn_all = _L1_ffn_setup()
    _L1_ffn_in = {k: v for k, v in _L1_ffn_all.items() if k in ('centroids', 'ln_g', 'ln_b', 'w1', 'b1', 'w2', 'b2')}
    del _L1_ffn_all

    def _L2_xattn_setup():
        import jax, jax.numpy as jnp
        import numpy as np
        DIM = 256
        DIM_LATENT = 256
        DIM_HEAD = 64
        INNER = max(DIM, DIM_LATENT)
        HEADS = INNER // DIM_HEAD
        SCALE = DIM_HEAD ** (-0.5)
        LN_EPS = 1e-05
        RMS_EPS = 1e-08

        def layernorm(x, g, b):
            mu = jnp.mean(x, axis=-1, keepdims=True)
            var = jnp.mean(jnp.square(x - mu), axis=-1, keepdims=True)
            return (x - mu) * jax.lax.rsqrt(var + LN_EPS) * g + b

        def rmsnorm(x, gamma):
            n = jnp.linalg.norm(x, axis=-1, keepdims=True) * x.shape[-1] ** (-0.5)
            return x / jnp.maximum(n, RMS_EPS) * gamma
        key = jax.random.key(seed)
        ks = jax.random.split(key, 8)
        b, n, nl = (8, 512, 128)
        x = jax.random.normal(ks[0], (b, n, DIM), dtype=jnp.float32)
        latents = jax.random.normal(ks[1], (b, nl, DIM_LATENT), dtype=jnp.float32)
        mask = jax.random.randint(ks[2], (b, n), 0, 2).astype(bool)
        init = lambda k, shape, fan_in: jax.random.normal(k, shape, jnp.float32) * fan_in ** (-0.5)
        return {'x': x, 'latents': latents, 'mask': mask, 'ln_x_g': jnp.ones((DIM,), jnp.float32), 'ln_x_b': jnp.zeros((DIM,), jnp.float32), 'ln_l_g': jnp.ones((DIM_LATENT,), jnp.float32), 'ln_l_b': jnp.zeros((DIM_LATENT,), jnp.float32), 'q_gamma': jnp.ones((DIM_HEAD,), jnp.float32), 'k_gamma': jnp.ones((DIM_HEAD,), jnp.float32), 'W_q': init(ks[3], (DIM_LATENT, INNER), DIM_LATENT), 'W_kv': init(ks[4], (DIM, 2 * INNER), DIM), 'W_out': init(ks[5], (INNER, DIM_LATENT), INNER), 'b_out': jnp.zeros((DIM_LATENT,), jnp.float32)}
    _L2_xattn_all = _L2_xattn_setup()
    _L2_xattn_in = {k: v for k, v in _L2_xattn_all.items() if k in ('ln_x_g', 'ln_x_b', 'ln_l_g', 'ln_l_b', 'q_gamma', 'k_gamma', 'W_q', 'W_kv', 'W_out', 'b_out')}
    del _L2_xattn_all

    def _L2_ffn_setup():
        import jax, jax.numpy as jnp
        import numpy as np
        D_MODEL = 256
        EXPERT_DIM = 128
        N_EXPERTS = 8
        TOP_K = 2

        def _sq_relu(h):
            return jnp.square(jax.nn.relu(h))
        key = jax.random.key(seed)
        ks = jax.random.split(key, 6)
        s = 0.02
        x = jax.random.normal(ks[0], (2, 512, D_MODEL), dtype=jnp.float32)
        Ws1 = jax.random.normal(ks[1], (D_MODEL, EXPERT_DIM), dtype=jnp.float32) * s
        Ws2 = jax.random.normal(ks[2], (EXPERT_DIM, D_MODEL), dtype=jnp.float32) * s
        W1 = jax.random.normal(ks[3], (N_EXPERTS, D_MODEL, EXPERT_DIM), dtype=jnp.float32) * s
        W2 = jax.random.normal(ks[4], (N_EXPERTS, EXPERT_DIM, D_MODEL), dtype=jnp.float32) * s
        Wr = jax.random.normal(ks[5], (D_MODEL, N_EXPERTS), dtype=jnp.float32) * s
        return {'x': x, 'Ws1': Ws1, 'Ws2': Ws2, 'W1': W1, 'W2': W2, 'Wr': Wr}
    _L2_ffn_all = _L2_ffn_setup()
    _L2_ffn_in = {k: v for k, v in _L2_ffn_all.items() if k in ('Ws1', 'Ws2', 'W1', 'W2', 'Wr')}
    del _L2_ffn_all

    def _L3_xattn_setup():
        import jax, jax.numpy as jnp
        import numpy as np
        WIDTH = 256
        DATA_WIDTH = 256
        HEADS = 16
        INIT_SCALE = 0.02
        key = jax.random.key(seed)
        ks = jax.random.split(key, 8)
        x = jax.random.normal(ks[0], (2, 256, WIDTH), dtype=jnp.float32)
        data = jax.random.normal(ks[1], (2, 1024, DATA_WIDTH), dtype=jnp.float32)
        Wq = jax.random.normal(ks[2], (WIDTH, WIDTH), dtype=jnp.float32) * INIT_SCALE
        bq = jnp.zeros((WIDTH,), dtype=jnp.float32)
        Wkv = jax.random.normal(ks[3], (DATA_WIDTH, 2 * WIDTH), dtype=jnp.float32) * INIT_SCALE
        bkv = jnp.zeros((2 * WIDTH,), dtype=jnp.float32)
        Wp = jax.random.normal(ks[4], (WIDTH, WIDTH), dtype=jnp.float32) * INIT_SCALE
        bp = jnp.zeros((WIDTH,), dtype=jnp.float32)
        return {'x': x, 'data': data, 'Wq': Wq, 'bq': bq, 'Wkv': Wkv, 'bkv': bkv, 'Wp': Wp, 'bp': bp}
    _L3_xattn_all = _L3_xattn_setup()
    _L3_xattn_in = {k: v for k, v in _L3_xattn_all.items() if k in ('Wq', 'bq', 'Wkv', 'bkv', 'Wp', 'bp')}
    del _L3_xattn_all

    def _L3_ffn_setup():
        import jax, jax.numpy as jnp
        import numpy as np
        IN_DIM = 256
        OUT_DIM = 256
        NUM_EXPERTS = 8
        TOP_K = 2
        key = jax.random.key(seed)
        ks = jax.random.split(key, 5)
        s = 1.0 / np.sqrt(IN_DIM)
        x = jax.random.normal(ks[0], (4, 512, IN_DIM), dtype=jnp.float32)
        Wg = jax.random.uniform(ks[1], (IN_DIM, NUM_EXPERTS), jnp.float32, -s, s)
        bg = jnp.zeros((NUM_EXPERTS,), jnp.float32)
        We = jax.random.uniform(ks[2], (NUM_EXPERTS, OUT_DIM, IN_DIM), jnp.float32, -s, s)
        be = jax.random.uniform(ks[3], (NUM_EXPERTS, OUT_DIM), jnp.float32, -s, s)
        return {'x': x, 'Wg': Wg, 'bg': bg, 'We': We, 'be': be}
    _L3_ffn_all = _L3_ffn_setup()
    _L3_ffn_in = {k: v for k, v in _L3_ffn_all.items() if k in ('Wg', 'bg', 'We', 'be')}
    del _L3_ffn_all
    return {'x': x, 'ctx_1024': ctx_1024, 'fside_BxS2_0': fside_BxS2_0, 'mask_BxS2_bk0': mask_BxS2_bk0, 'g_xattn': g_xattn, 'g_ffn': g_ffn, 'L0_xattn_Wq': _L0_xattn_in['Wq'], 'L0_xattn_bq': _L0_xattn_in['bq'], 'L0_xattn_Wk': _L0_xattn_in['Wk'], 'L0_xattn_bk': _L0_xattn_in['bk'], 'L0_xattn_Wv': _L0_xattn_in['Wv'], 'L0_xattn_bv': _L0_xattn_in['bv'], 'L0_ffn_gate_w': _L0_ffn_in['gate_w'], 'L0_ffn_gate_bias': _L0_ffn_in['gate_bias'], 'L0_ffn_w1': _L0_ffn_in['w1'], 'L0_ffn_w3': _L0_ffn_in['w3'], 'L0_ffn_w2': _L0_ffn_in['w2'], 'L0_ffn_sw1': _L0_ffn_in['sw1'], 'L0_ffn_sw3': _L0_ffn_in['sw3'], 'L0_ffn_sw2': _L0_ffn_in['sw2'], 'L1_xattn_Wq': _L1_xattn_in['Wq'], 'L1_xattn_Wk': _L1_xattn_in['Wk'], 'L1_xattn_Wv': _L1_xattn_in['Wv'], 'L1_xattn_Wo': _L1_xattn_in['Wo'], 'L1_ffn_centroids': _L1_ffn_in['centroids'], 'L1_ffn_ln_g': _L1_ffn_in['ln_g'], 'L1_ffn_ln_b': _L1_ffn_in['ln_b'], 'L1_ffn_w1': _L1_ffn_in['w1'], 'L1_ffn_b1': _L1_ffn_in['b1'], 'L1_ffn_w2': _L1_ffn_in['w2'], 'L1_ffn_b2': _L1_ffn_in['b2'], 'L2_xattn_ln_x_g': _L2_xattn_in['ln_x_g'], 'L2_xattn_ln_x_b': _L2_xattn_in['ln_x_b'], 'L2_xattn_ln_l_g': _L2_xattn_in['ln_l_g'], 'L2_xattn_ln_l_b': _L2_xattn_in['ln_l_b'], 'L2_xattn_q_gamma': _L2_xattn_in['q_gamma'], 'L2_xattn_k_gamma': _L2_xattn_in['k_gamma'], 'L2_xattn_W_q': _L2_xattn_in['W_q'], 'L2_xattn_W_kv': _L2_xattn_in['W_kv'], 'L2_xattn_W_out': _L2_xattn_in['W_out'], 'L2_xattn_b_out': _L2_xattn_in['b_out'], 'L2_ffn_Ws1': _L2_ffn_in['Ws1'], 'L2_ffn_Ws2': _L2_ffn_in['Ws2'], 'L2_ffn_W1': _L2_ffn_in['W1'], 'L2_ffn_W2': _L2_ffn_in['W2'], 'L2_ffn_Wr': _L2_ffn_in['Wr'], 'L3_xattn_Wq': _L3_xattn_in['Wq'], 'L3_xattn_bq': _L3_xattn_in['bq'], 'L3_xattn_Wkv': _L3_xattn_in['Wkv'], 'L3_xattn_bkv': _L3_xattn_in['bkv'], 'L3_xattn_Wp': _L3_xattn_in['Wp'], 'L3_xattn_bp': _L3_xattn_in['bp'], 'L3_ffn_Wg': _L3_ffn_in['Wg'], 'L3_ffn_bg': _L3_ffn_in['bg'], 'L3_ffn_We': _L3_ffn_in['We'], 'L3_ffn_be': _L3_ffn_in['be']}

def reference(x, ctx_1024, fside_BxS2_0, mask_BxS2_bk0, g_xattn, g_ffn, L0_xattn_Wq, L0_xattn_bq, L0_xattn_Wk, L0_xattn_bk, L0_xattn_Wv, L0_xattn_bv, L0_ffn_gate_w, L0_ffn_gate_bias, L0_ffn_w1, L0_ffn_w3, L0_ffn_w2, L0_ffn_sw1, L0_ffn_sw3, L0_ffn_sw2, L1_xattn_Wq, L1_xattn_Wk, L1_xattn_Wv, L1_xattn_Wo, L1_ffn_centroids, L1_ffn_ln_g, L1_ffn_ln_b, L1_ffn_w1, L1_ffn_b1, L1_ffn_w2, L1_ffn_b2, L2_xattn_ln_x_g, L2_xattn_ln_x_b, L2_xattn_ln_l_g, L2_xattn_ln_l_b, L2_xattn_q_gamma, L2_xattn_k_gamma, L2_xattn_W_q, L2_xattn_W_kv, L2_xattn_W_out, L2_xattn_b_out, L2_ffn_Ws1, L2_ffn_Ws2, L2_ffn_W1, L2_ffn_W2, L2_ffn_Wr, L3_xattn_Wq, L3_xattn_bq, L3_xattn_Wkv, L3_xattn_bkv, L3_xattn_Wp, L3_xattn_bp, L3_ffn_Wg, L3_ffn_bg, L3_ffn_We, L3_ffn_be):
    import jax
    import jax.numpy as jnp

    def _L0_xattn_ref(query, key, value, Wq, bq, Wk, bk, Wv, bv):
        import jax, jax.numpy as jnp
        import numpy as np
        D = 256
        q = jnp.einsum('bnd,ed->bne', query, Wq) + bq
        k = jnp.einsum('bnd,ed->bne', key, Wk) + bk
        v = jnp.einsum('bnd,ed->bne', value, Wv) + bv
        scores = jnp.einsum('bqd,bkd->bqk', q, k)
        attn = jax.nn.softmax(scores, axis=-1)
        return jnp.einsum('bqk,bkd->bqd', attn, v)

    def _L0_ffn_ref(x, gate_w, gate_bias, w1, w3, w2, sw1, sw3, sw2):
        import jax, jax.numpy as jnp
        import numpy as np
        DIM = 256
        INTER = 256
        N_EXPERTS = 8
        TOPK = 2
        N_SHARED = 2
        shape = x.shape
        xt = x.reshape(-1, shape[-1])
        scores = jax.nn.softmax((xt @ gate_w.T).astype(jnp.float32), axis=-1)
        _, idx = jax.lax.top_k(scores + gate_bias, TOPK)
        weights = jnp.take_along_axis(scores, idx, axis=1).astype(x.dtype)
        y = jnp.zeros_like(xt)
        for e in range(N_EXPERTS):
            gate_e = jnp.sum(jnp.where(idx == e, weights, 0.0), axis=1)
            h = jax.nn.silu(xt @ w1[e].T) * (xt @ w3[e].T)
            y = y + gate_e[:, None] * (h @ w2[e].T)
        z = jax.nn.silu(xt @ sw1.T) * (xt @ sw3.T) @ sw2.T
        return (y + z).reshape(shape)

    def _L1_xattn_ref(query, key, value, attention_bias, Wq, Wk, Wv, Wo):
        import jax, jax.numpy as jnp
        import numpy as np
        EMBED = 256
        NHEAD = 16
        HEAD_DIM = EMBED // NHEAD
        B, SQ, _ = query.shape
        SKV = key.shape[1]

        def proj(x, W, S):
            return (x @ W.T).reshape(B, S, NHEAD, HEAD_DIM).transpose(0, 2, 1, 3)
        q = proj(query, Wq, SQ)
        k = proj(key, Wk, SKV)
        v = proj(value, Wv, SKV)
        scores = jnp.einsum('bhqd,bhkd->bhqk', q, k) / np.sqrt(HEAD_DIM)
        scores = scores + attention_bias[:, None, None, :]
        probs = jax.nn.softmax(scores, axis=-1)
        out = jnp.einsum('bhqk,bhkd->bhqd', probs, v)
        out = out.transpose(0, 2, 1, 3).reshape(B, SQ, EMBED)
        return out @ Wo.T

    def _L1_ffn_ref(input_features, centroids, ln_g, ln_b, w1, b1, w2, b2):
        import jax, jax.numpy as jnp
        import numpy as np
        B, S, D, F, E = (8, 256, 256, 1024, 8)
        EPS = 1e-05
        x = input_features.reshape(-1, D)
        aff = jax.lax.stop_gradient(x @ centroids.T)
        eid = jnp.argmax(aff, axis=-1)
        alpha = jax.nn.sigmoid(jnp.sum(x * centroids[eid], axis=-1, keepdims=True))
        mu = jnp.mean(x, axis=-1, keepdims=True)
        var = jnp.mean((x - mu) ** 2, axis=-1, keepdims=True)
        xn = (x - mu) * jax.lax.rsqrt(var + EPS)
        xln = xn * ln_g[eid] + ln_b[eid]
        onehot = jax.nn.one_hot(eid, E, dtype=x.dtype)
        ffn = jnp.zeros_like(x)
        for e in range(E):
            h = jax.nn.relu(xln @ w1[e] + b1[e])
            ffn = ffn + onehot[:, e:e + 1] * (h @ w2[e] + b2[e])
        out = x + alpha * ffn
        return out.reshape(input_features.shape)

    def _L2_xattn_ref(x, latents, mask, ln_x_g, ln_x_b, ln_l_g, ln_l_b, q_gamma, k_gamma, W_q, W_kv, W_out, b_out):
        import jax, jax.numpy as jnp
        import numpy as np
        DIM = 256
        DIM_LATENT = 256
        DIM_HEAD = 64
        INNER = max(DIM, DIM_LATENT)
        HEADS = INNER // DIM_HEAD
        SCALE = DIM_HEAD ** (-0.5)
        LN_EPS = 1e-05
        RMS_EPS = 1e-08

        def layernorm(x, g, b):
            mu = jnp.mean(x, axis=-1, keepdims=True)
            var = jnp.mean(jnp.square(x - mu), axis=-1, keepdims=True)
            return (x - mu) * jax.lax.rsqrt(var + LN_EPS) * g + b

        def rmsnorm(x, gamma):
            n = jnp.linalg.norm(x, axis=-1, keepdims=True) * x.shape[-1] ** (-0.5)
            return x / jnp.maximum(n, RMS_EPS) * gamma
        b, n, _ = x.shape
        nl = latents.shape[1]
        xn = layernorm(x, ln_x_g, ln_x_b)
        ln = layernorm(latents, ln_l_g, ln_l_b)
        q = ln @ W_q
        kv = jnp.concatenate([xn @ W_kv, ln @ W_kv], axis=1)
        k, v = (kv[..., :INNER], kv[..., INNER:])
        to_heads = lambda t: t.reshape(t.shape[0], t.shape[1], HEADS, DIM_HEAD).transpose(0, 2, 1, 3)
        q, k, v = (to_heads(q), to_heads(k), to_heads(v))
        qn = rmsnorm(q, q_gamma) * SCALE
        kn = rmsnorm(k, k_gamma)
        sim = jnp.einsum('bhid,bhjd->bhij', qn, kn)
        full_mask = jnp.pad(mask, ((0, 0), (0, nl)), constant_values=True)
        neg = -jnp.finfo(sim.dtype).max
        sim = jnp.where(full_mask[:, None, None, :], sim, neg)
        attn = jax.nn.softmax(sim.astype(jnp.float32), axis=-1).astype(sim.dtype)
        out = jnp.einsum('bhij,bhjd->bhid', attn, v)
        out = out.transpose(0, 2, 1, 3).reshape(b, nl, INNER)
        return out @ W_out + b_out

    def _L2_ffn_ref(x, Ws1, Ws2, W1, W2, Wr):
        import jax, jax.numpy as jnp
        import numpy as np
        D_MODEL = 256
        EXPERT_DIM = 128
        N_EXPERTS = 8
        TOP_K = 2

        def _sq_relu(h):
            return jnp.square(jax.nn.relu(h))
        shape = x.shape
        xf = x.reshape(-1, D_MODEL)
        out_shared = _sq_relu(xf @ Ws1) @ Ws2
        logits = xf @ Wr
        top_vals, top_idx = jax.lax.top_k(logits, TOP_K)
        rw = jax.nn.softmax(top_vals.astype(jnp.float32), axis=-1).astype(x.dtype)
        onehot = jax.nn.one_hot(top_idx, N_EXPERTS, dtype=x.dtype)
        prob = jnp.einsum('tk,tke->te', rw, onehot)
        prob = jnp.trunc(prob)
        h = _sq_relu(jnp.einsum('td,edf->tef', xf, W1))
        y = jnp.einsum('tef,efd->ted', h, W2)
        out_routed = jnp.einsum('ted,te->td', y, prob)
        return (out_shared + out_routed).reshape(shape)

    def _L3_xattn_ref(x, data, Wq, bq, Wkv, bkv, Wp, bp):
        import jax, jax.numpy as jnp
        import numpy as np
        WIDTH = 256
        DATA_WIDTH = 256
        HEADS = 16
        INIT_SCALE = 0.02
        bs, n_ctx, _ = x.shape
        _, n_data, _ = data.shape
        d = WIDTH // HEADS
        q = (x @ Wq + bq).reshape(bs, n_ctx, HEADS, d)
        kv = (data @ Wkv + bkv).reshape(bs, n_data, HEADS, 2 * d)
        k, v = (kv[..., :d], kv[..., d:])
        scale = 1.0 / np.sqrt(d).astype(np.float32)
        scores = jnp.einsum('bqhd,bkhd->bhqk', q, k) * scale
        attn = jax.nn.softmax(scores, axis=-1)
        out = jnp.einsum('bhqk,bkhd->bqhd', attn, v).reshape(bs, n_ctx, WIDTH)
        return out @ Wp + bp

    def _L3_ffn_ref(x, Wg, bg, We, be):
        import jax, jax.numpy as jnp
        import numpy as np
        IN_DIM = 256
        OUT_DIM = 256
        NUM_EXPERTS = 8
        TOP_K = 2
        gate = jax.nn.softmax(x @ Wg + bg, axis=-1)
        topk_vals, topk_idx = jax.lax.top_k(gate, TOP_K)
        onehot = jax.nn.one_hot(topk_idx, NUM_EXPERTS, dtype=gate.dtype)
        gate_sparse = jnp.einsum('bsk,bske->bse', topk_vals, onehot)
        gate_sparse = gate_sparse / jnp.sum(gate_sparse, axis=-1, keepdims=True)
        y = jnp.einsum('bsi,eoi->bseo', x, We) + be[None, None, :, :].transpose(0, 1, 2, 3)
        out = jnp.einsum('bseo,bse->bso', y, gate_sparse)
        return out
    x = x + jnp.tanh(g_xattn[0]) * _L0_xattn_ref(_layernorm(x, axis=-1), ctx_1024, ctx_1024, L0_xattn_Wq, L0_xattn_bq, L0_xattn_Wk, L0_xattn_bk, L0_xattn_Wv, L0_xattn_bv)
    x = x + jnp.tanh(g_ffn[0]) * _L0_ffn_ref(_layernorm(x, axis=-1), L0_ffn_gate_w, L0_ffn_gate_bias, L0_ffn_w1, L0_ffn_w3, L0_ffn_w2, L0_ffn_sw1, L0_ffn_sw3, L0_ffn_sw2)
    x = x + jnp.tanh(g_xattn[1]) * _L1_xattn_ref(_layernorm(x, axis=-1), ctx_1024, ctx_1024, fside_BxS2_0, L1_xattn_Wq, L1_xattn_Wk, L1_xattn_Wv, L1_xattn_Wo)
    x = x + jnp.tanh(g_ffn[1]) * _L1_ffn_ref(_layernorm(x, axis=-1), L1_ffn_centroids, L1_ffn_ln_g, L1_ffn_ln_b, L1_ffn_w1, L1_ffn_b1, L1_ffn_w2, L1_ffn_b2)
    x = x + jnp.tanh(g_xattn[2]) * _L2_xattn_ref(ctx_1024, _layernorm(x, axis=-1), mask_BxS2_bk0, L2_xattn_ln_x_g, L2_xattn_ln_x_b, L2_xattn_ln_l_g, L2_xattn_ln_l_b, L2_xattn_q_gamma, L2_xattn_k_gamma, L2_xattn_W_q, L2_xattn_W_kv, L2_xattn_W_out, L2_xattn_b_out)
    x = x + jnp.tanh(g_ffn[2]) * _L2_ffn_ref(_layernorm(x, axis=-1), L2_ffn_Ws1, L2_ffn_Ws2, L2_ffn_W1, L2_ffn_W2, L2_ffn_Wr)
    x = x + jnp.tanh(g_xattn[3]) * _L3_xattn_ref(_layernorm(x, axis=-1), ctx_1024, L3_xattn_Wq, L3_xattn_bq, L3_xattn_Wkv, L3_xattn_bkv, L3_xattn_Wp, L3_xattn_bp)
    x = x + jnp.tanh(g_ffn[3]) * _L3_ffn_ref(_layernorm(x, axis=-1), L3_ffn_Wg, L3_ffn_bg, L3_ffn_We, L3_ffn_be)
    return x

_drawn_inputs = setup_inputs


def setup_inputs(seed=0):
    import zlib

    import numpy as np

    out = dict(_drawn_inputs(seed))
    spreads = {'L1_ffn_ln_g': (1.0, 0.6),
     'L1_ffn_ln_b': (0.0, 2.0),
     'L1_ffn_b1': (0.0, 1.729),
     'L1_ffn_b2': (0.0, 0.718),
     'L2_xattn_ln_x_g': (1.0, 0.6),
     'L2_xattn_ln_x_b': (0.0, 2.0),
     'L2_xattn_ln_l_g': (1.0, 0.6),
     'L2_xattn_ln_l_b': (0.0, 0.68),
     'L2_xattn_q_gamma': (1.0, 0.6),
     'L2_xattn_k_gamma': (1.0, 0.6),
     'L2_xattn_b_out': (0.0, 0.724),
     'L3_xattn_bq': (0.0, 2.0),
     'L3_xattn_bkv': (0.0, 2.0),
     'L3_xattn_bp': (0.0, 0.8),
     'L3_ffn_bg': (0.0, 1.126)}
    factors = {'g_ffn': 23.832,
     'L0_xattn_bk': 200.0,
     'L0_ffn_gate_w': 8.0,
     'L0_ffn_gate_bias': 8.0,
     'L0_ffn_w1': 7.877,
     'L0_ffn_w3': 8.0,
     'L0_ffn_w2': 8.0,
     'L2_ffn_Ws1': 3.688,
     'L2_ffn_Ws2': 3.865,
     'L3_xattn_Wq': 64.0,
     'L3_ffn_be': 20.167,
     'fside_BxS2_0': 2.745,
     'L0_ffn_sw1': 8.0,
     'L0_ffn_sw3': 8.0,
     'L0_ffn_sw2': 8.0,
     'L3_xattn_Wkv': 8.0,
     'L3_xattn_Wp': 4.758,
     'L1_xattn_Wq': 2.76,
     'L1_xattn_Wk': 2.713,
     'L1_ffn_w1': 2.701}
    for name, (base, spread) in spreads.items():
        noise = np.random.default_rng([zlib.crc32(name.encode()), seed]).standard_normal(out[name].shape)
        drawn = base * np.exp(spread * noise) if base else spread * noise
        out[name] = jnp.asarray(drawn.astype(out[name].dtype))
    for name, factor in factors.items():
        out[name] = (out[name] * factor).astype(out[name].dtype)
    return out
```

```python
from contextlib import ExitStack

import concourse.bass as bass
from concourse import mybir

F32 = mybir.dt.float32
BF16 = mybir.dt.bfloat16
I32 = mybir.dt.int32
U8 = mybir.dt.uint8
ALU = mybir.AluOpType
ACT = mybir.ActivationFunctionType
AX_X = mybir.AxisListType.X

P = 128
BATCH, SEQ, DIM = 8, 256, 256
TOKENS = BATCH * SEQ
TILES = TOKENS // P
TPB = SEQ // P
KD = DIM // P
KEYS = 77
CTX = BATCH * KEYS
EXPERTS = 8
LN_EPS = 1e-5


def wait(eng, sem, value):
    if isinstance(value, int) and value <= 0:
        return
    eng.wait_ge(sem, value)


def wait_apart(eng, sem, value, passed):
    wait(eng, sem, value)
    eng.sem_inc(passed, 1)


def steps(eng, n, body):
    body(0)
    with eng.Fori(1, n - 1) as i:
        body(i)
    body(n - 1)


def is_step(i, n):
    return isinstance(i, int) and i == n


def batches(eng, body):
    body(0, 3)
    body(1, 3)
    with eng.Fori(2, BATCH - 3) as b:
        body(b, 3)
    for left in (2, 1, 0):
        body(BATCH - 1 - left, left)


def nth(ap, i):
    if isinstance(i, int):
        return ap[:, i, :]
    return ap[:, bass.ds(i, 1), :].rearrange("p a d -> p (a d)")


def span(i, width):
    return slice(i * width, (i + 1) * width) if isinstance(i, int) else bass.ds(i * width, width)


class Chip:

    def __init__(self, nc, ctx):
        self.nc, self.ctx = nc, ctx
        sb = self.sb
        self.x = sb("x_res", [P, TILES, DIM], F32)
        self.xnT = sb("xnT", [P, KD, TOKENS], F32)
        self.ident = sb("ident", [P, P], F32)
        self.gate = sb("gate", [P, 8], F32)
        self.powers = sb("powers", [P, 4], F32)
        self.keep = sb("keep", [P, TILES, DIM], F32)
        self.bank = ctx.enter_context(nc.psum_tensor("bank", [P, 8, 512], F32))

        self.finished = []

    def release(self):
        self.nc.all_engine_barrier()
        self.nc.clear_and_free_semaphores(self.finished)
        self.nc.all_engine_barrier()
        self.finished = []

    def sb(self, name, shape, dt):
        return self.ctx.enter_context(self.nc.sbuf_tensor(name, shape, dt))


class Stage:

    def __init__(self, chip, name, ctx):
        self.chip, self.nc, self.name, self.ctx = chip, chip.nc, name, ctx

    def sb(self, name, shape, dt=F32):
        return self.ctx.enter_context(self.nc.sbuf_tensor(f"{self.name}_{name}", shape, dt))

    def sem(self, name):
        semaphore = self.nc.alloc_semaphore(name=f"{self.name}_{name}")
        self.chip.finished.append(semaphore)
        return semaphore


class Moments:

    def __init__(self, st, name, depth):
        self.depth = depth
        self.stats = st.sb(f"{name}_stats", [P, depth, 6])
        self.mv = st.sb(f"{name}_mv", [P, depth, 2])
        self.stats_done = st.sem(f"{name}_stats_done")
        self.ready = st.sem(f"{name}_moments_ready")
        self.passed = st.sem(f"{name}_passed")

    def statistics(self, dve, t, u, rows):
        dve.bn_stats(self.stats[:, u, :], rows).then_inc(self.stats_done, 1)
        wait_apart(dve, self.stats_done, t + 1, self.passed)
        dve.bn_aggr(self.mv[:, u, :], self.stats[:, u, :]).then_inc(self.ready, 1)


class Normed:

    def __init__(self, st, name, moments, again=False):
        self.constants, self.moments, self.again = st.chip.powers, moments, again
        self.shifted = st.sb(f"{name}_shifted", [P, moments.depth])
        self.rstd = st.sb(f"{name}_rstd", [P, moments.depth])
        self.widened = st.sem(f"{name}_widened")
        self.shifted_done = st.sem(f"{name}_shifted_done")
        self.rstd_ready = st.sem(f"{name}_rstd_ready")
        self.normed = st.sem(f"{name}_normed")

    def power(self, pool, t, u):
        variance, shifted = self.moments.mv[:, u, 1:2], self.shifted[:, u:u + 1]
        pool.wait_ge(self.moments.ready, t + 1)
        if self.again:
            pool.tensor_tensor(shifted, variance, self.constants[:, 2:3], ALU.mult).then_inc(self.widened, 1)
            pool.wait_ge(self.widened, t + 1)
            pool.tensor_tensor(shifted, shifted, self.constants[:, 3:4], ALU.add).then_inc(self.shifted_done, 1)
        else:
            pool.tensor_tensor(shifted, variance, self.constants[:, 1:2], ALU.add).then_inc(self.shifted_done, 1)
        wait(pool, self.normed, t - self.moments.depth + 1)
        pool.wait_ge(self.shifted_done, t + 1)
        pool.tensor_tensor(self.rstd[:, u:u + 1], shifted, self.constants[:, 0:1], ALU.pow).then_inc(self.rstd_ready, 1)

    def apply(self, dve, t, u, rows, out):
        dve.wait_ge(self.rstd_ready, t + 1)
        dve.tensor_scalar(out, rows, self.moments.mv[:, u, 0:1], self.rstd[:, u:u + 1], ALU.subtract,
                          ALU.mult).then_inc(self.normed, 1)


class NextNorm:

    def __init__(self, st, bank, keep=None, keep_again=None, affine=None, share=None, depth=2):
        self.chip, self.bank, self.depth = st.chip, bank, depth
        self.keep, self.keep_again, self.affine, self.share = keep, keep_again, affine, share
        self.xn = st.sb("xn", [P, depth, DIM])
        self.x_updated = st.sem("x_updated")
        self.transposed = st.sem("xn_transposed")
        self.copied = st.sem("xnT_copied")
        self.kept = st.sem("xn_kept")
        self.shared = st.sem("xn_shared")
        self.moments = Moments(st, "ln", depth)
        self.main = Normed(st, "ln", self.moments, again=affine is not None)
        self.twice = Normed(st, "ln2", self.moments, again=True) if keep_again is not None else None

    def vector_stats(self, dve, t, u):
        wait_apart(dve, self.x_updated, t + 1, self.moments.passed)
        self.moments.statistics(dve, t, u, nth(self.chip.x, t))

    def vector_apply(self, dve, t, u):
        before = t - self.depth + 1
        wait(dve, self.transposed, before)
        if self.keep is not None:
            wait(dve, self.kept, before)
        if self.share is not None:
            wait(dve, self.shared, before)
        self.main.apply(dve, t, u, nth(self.chip.x, t), self.xn[:, u, :])

    def vector_apply_again(self, dve, t, u):
        if self.keep_again is not None:
            self.twice.apply(dve, t, u, nth(self.chip.x, t), nth(self.keep_again, t))
        if self.share is not None:
            dve.wait_ge(self.main.normed, t + 1)
            dve.wait_ge(self.twice.normed, t + 1)
            dve.scalar_tensor_tensor(out=nth(self.chip.x, t), in0=self.xn[:, u, :], scalar=self.share,
                                     in1=nth(self.chip.x, t), op0=ALU.mult, op1=ALU.add).then_inc(self.shared, 1)

    def gpsimd(self, pool, t, u):
        self.main.power(pool, t, u)
        if self.twice is not None:
            self.twice.power(pool, t, u)

    def tensor(self, pe, t, u):
        pe.wait_ge(self.main.normed, t + 1)
        wait(pe, self.copied, t)
        for k in range(KD):
            last = pe.transpose(self.bank[:, k * P:(k + 1) * P], self.xn[:, u, k * P:(k + 1) * P],
                                self.chip.ident[:, :])
        last.then_inc(self.transposed, 1)

    def scalar(self, act, t, u):
        if self.keep is not None:
            act.wait_ge(self.main.normed, t + 1)
            act.activation(nth(self.keep, t), self.xn[:, u, :], ACT.Copy).then_inc(self.kept, 1)
        act.wait_ge(self.transposed, t + 1)
        if self.affine is None:
            act.activation(self.chip.xnT[:, :, span(t, P)],
                           self.bank[:, 0:DIM].rearrange("p (k n) -> p k n", k=KD),
                           ACT.Copy).then_inc(self.copied, 1)
        else:
            for k in range(KD):
                last = act.activation(self.chip.xnT[:, k, span(t, P)], self.bank[:, k * P:(k + 1) * P], ACT.Identity,
                                      scale=self.affine[0][:, k:k + 1], bias=self.affine[1][:, k:k + 1])
            last.then_inc(self.copied, 1)


def load_rows(w):
    return w.rearrange("(k p) n -> p k n", p=P)


def begin(chip, a):
    nc = chip.nc
    with ExitStack() as ctx:
        st = Stage(chip, "begin", ctx)
        norm = NextNorm(st, chip.bank[:, 0, :], depth=4)
        per = 4
        raw_gate = st.sb("raw_gate", [P, 8])
        x_loaded = [st.sem(f"x_loaded{u}") for u in range(TILES // per)]
        small_loaded = st.sem("small_loaded")
        gate_ready = st.sem("gate_ready")
        powers_ready = st.sem("powers_ready")
        zeros = st.sb("zeros", [P, 2048])
        zeros_ready, cleared = st.sem("zeros_ready"), st.sem("cleared")
        block = ctx.enter_context(nc.Block())
        x_rows = a["x"].rearrange("(t p) d -> p t d", p=P)

        @block.sync
        def _(sp):
            for u in range(TILES // per):
                sp.dma_start(chip.x[:, u * per:(u + 1) * per, :],
                             x_rows[:, u * per:(u + 1) * per, :]).then_inc(x_loaded[u], 16)
            sp.dma_start(chip.ident[:, :], a["ident"]).then_inc(small_loaded, 16)
            for n, g in enumerate((a["g_xattn"], a["g_ffn"])):
                sp.dma_start(raw_gate[:, 4 * n:4 * n + 4], g.partition_broadcast(P)).then_inc(small_loaded, 16)
            sp.wait_ge(zeros_ready, 1)
            strips = 0
            for scratch in chip.scratch:
                slots = scratch.rows.rearrange("(p r) d -> p (r d)", p=P)
                for at in range(0, slots.shape[1], 2048):
                    sp.dma_start(slots[:, at:at + 2048], zeros[:, :]).then_inc(cleared, 16)
                    strips += 1
            sp.wait_ge(cleared, 16 * strips)

        @block.vector
        def _(dve):
            dve.memset(zeros[:, :], 0.0).then_inc(zeros_ready, 1)
            for n, value in enumerate((-0.5, LN_EPS, 1 + LN_EPS, LN_EPS ** 2)):
                dve.memset(chip.powers[:, n:n + 1], value).then_inc(powers_ready, 1)

            for q in range(TILES // per):
                dve.wait_ge(x_loaded[q], 16)
                dve.sem_inc(norm.x_updated, per)
                for u in range(per):
                    norm.vector_stats(dve, per * q + u, u)
                for u in range(per):
                    norm.vector_apply(dve, per * q + u, u)

        @block.gpsimd
        def _(pool):
            pool.wait_ge(powers_ready, 4)
            pool.wait_ge(small_loaded, 48)

            for t in range(TILES):
                norm.gpsimd(pool, t, t % per)

        @block.tensor
        def _(pe):
            pe.wait_ge(small_loaded, 48)

            for t in range(TILES):
                norm.tensor(pe, t, t % per)

        @block.scalar
        def _(act):
            act.wait_ge(small_loaded, 48)
            act.activation(chip.gate[:, :], raw_gate[:, :], ACT.Tanh).then_inc(gate_ready, 1)
            for t in range(TILES):
                norm.scalar(act, t, t % per)


def single_head_attention(chip, a, feed):
    nc = chip.nc
    with ExitStack() as ctx:
        st = Stage(chip, "l0x", ctx)
        bank = chip.bank
        s_bank = [bank[:, 0, :], bank[:, 1, :]]
        p_bank = [bank[:, 2, :], bank[:, 3, :]]
        o_bank = [bank[:, 4, :], bank[:, 5, :]]
        q_bank = bank[:, 6, :]
        norm = NextNorm(st, bank[:, 7, :], keep=chip.keep)
        w = {n: st.sb(n, [P, KD, DIM]) for n in ("Wq", "Wk", "Wv")}
        bias = {n: st.sb(n, [P, KD]) for n in ("bq", "bk")}
        bv = st.sb("bv", [KEYS, DIM])
        ctxT = st.sb("ctxT", [P, KD, CTX])
        kT = st.sb("kT", [P, KD, CTX])
        v = st.sb("v", [KEYS, BATCH, DIM])
        qT = st.sb("qT", [P, KD, SEQ])
        probs = st.sb("probs", [P, TPB, KEYS])
        probsT = st.sb("probsT", [KEYS, TPB, P])
        neg_max = st.sb("neg_max", [P, TPB])
        total = st.sb("total", [P, TPB])
        scale = st.sb("scale", [P, TPB])
        loaded = st.sem("loaded")
        kT_projected = st.sem("kT_projected")
        kT_ready = st.sem("kT_ready")
        v_projected = st.sem("v_projected")
        v_ready = st.sem("v_ready")
        q_projected = st.sem("q_projected")
        q_ready = st.sem("q_ready")
        scores_ready = st.sem("scores_ready")
        max_ready = st.sem("max_ready")
        probs_ready = st.sem("probs_ready")
        probs_transposed = st.sem("probs_transposed")
        probsT_ready = st.sem("probsT_ready")
        attended = st.sem("attended")
        inverse_done = st.sem("inverse_done")
        scale_ready = st.sem("scale_ready")
        loads = 7
        halves = CTX // 2
        block = ctx.enter_context(nc.Block())

        @block.sync
        def _(sp):
            sp.dma_start(ctxT[:, :, :], load_rows(a["ctxT"])).then_inc(loaded, 16)
            for n in ("Wk", "Wv", "Wq"):
                sp.dma_start(w[n][:, :, :], load_rows(a[f"L0_xattn_{n}"])).then_inc(loaded, 16)
            for n in ("bq", "bk"):
                sp.dma_start(bias[n][:, :], a[f"L0_xattn_{n}"]).then_inc(loaded, 16)
            sp.dma_start(bv[:, :], a["L0_xattn_bv"].partition_broadcast(KEYS)).then_inc(loaded, 16)
            feed.sync_all(sp)

        @block.tensor
        def _(pe):
            pe.wait_ge(loaded, 16 * loads)
            for m in range(KD):
                for h in range(2):
                    for k in range(KD):
                        last = pe.matmul(bank[:, 2 * m + h, 0:halves], w["Wk"][:, k, m * P:(m + 1) * P],
                                         ctxT[:, k, h * halves:(h + 1) * halves], start=(k == 0), stop=(k == KD - 1))
                    last.then_inc(kT_projected, 1)
            for b in range(BATCH):
                wait(pe, v_ready, b - 1)
                for k in range(KD):
                    last = pe.matmul(o_bank[b % 2][0:KEYS, 0:DIM], ctxT[:, k, b * KEYS:(b + 1) * KEYS],
                                     w["Wv"][:, k, :], start=(k == 0), stop=(k == KD - 1))
                last.then_inc(v_projected, 1)

            def project_q(b):
                for m in range(KD):
                    for k in range(KD):
                        last = pe.matmul(q_bank[:, m * SEQ:(m + 1) * SEQ], w["Wq"][:, k, m * P:(m + 1) * P],
                                         chip.xnT[:, k, span(b, SEQ)], start=(k == 0), stop=(k == KD - 1))
                last.then_inc(q_projected, 1)

            def scores(b):
                pe.wait_ge(q_ready, KD * b + KD)
                for u in range(TPB):
                    wait(pe, probs_ready, TPB * b + u - 1)
                    for m in range(KD):
                        last = pe.matmul(s_bank[u][:, 0:KEYS], qT[:, m, u * P:(u + 1) * P],
                                         kT[:, m, span(b, KEYS)], start=(m == 0), stop=(m == KD - 1))
                    last.then_inc(scores_ready, 1)

            project_q(0)
            pe.wait_ge(kT_ready, 2 * KD)
            pe.wait_ge(v_ready, BATCH)
            scores(0)
            project_q(1)

            def batch(b, ahead):
                for u in range(TPB):
                    pe.wait_ge(probs_ready, TPB * b + u + 1)
                    wait(pe, probsT_ready, TPB * b + u - 1)
                    pe.transpose(p_bank[u][0:KEYS, 0:P], probs[:, u, :],
                                 chip.ident[:, :]).then_inc(probs_transposed, 1)
                if ahead >= 1:
                    scores(b + 1)
                for u in range(TPB):
                    pe.wait_ge(probsT_ready, TPB * b + u + 1)
                    wait(pe, norm.x_updated, TPB * b + u - 1)
                    pe.matmul(o_bank[u][:, 0:DIM], probsT[:, u, :],
                              v[:, span(b, 1), :].rearrange("p a d -> p (a d)"),
                              start=True, stop=True).then_inc(attended, 1)
                if ahead >= 2:
                    project_q(b + 2)
                if not is_step(b, 0):
                    for u in range(TPB):
                        norm.tensor(pe, TPB * b + u - TPB, u)

            batches(pe, batch)
            for u in range(TPB):
                norm.tensor(pe, TILES - TPB + u, u)

        @block.scalar
        def _(act):
            act.wait_ge(loaded, 16 * loads)
            for m in range(KD):
                for h in range(2):
                    act.wait_ge(kT_projected, 2 * m + h + 1)
                    act.activation(kT[:, m, h * halves:(h + 1) * halves], bank[:, 2 * m + h, 0:halves],
                                   ACT.Identity, bias=bias["bk"][:, m:m + 1]).then_inc(kT_ready, 1)

            def copy_q(b):
                act.wait_ge(q_projected, b + 1)
                wait(act, scores_ready, TPB * b)
                for m in range(KD):
                    act.activation(qT[:, m, :], q_bank[:, m * SEQ:(m + 1) * SEQ], ACT.Identity,
                                   bias=bias["bq"][:, m:m + 1]).then_inc(q_ready, 1)

            def exponents(b):
                for u in range(TPB):
                    act.wait_ge(max_ready, TPB * b + u + 1)
                    wait(act, probs_transposed, TPB * b + u - 1)
                    wait(act, scale_ready, TPB * b + u - 1)
                    act.activation(probs[:, u, :], s_bank[u][:, 0:KEYS], ACT.Exp, bias=neg_max[:, u:u + 1],
                                   accum_out=total[:, u:u + 1]).then_inc(probs_ready, 1)

            copy_q(0)
            exponents(0)
            copy_q(1)

            def batch(b, ahead):
                if ahead >= 1:
                    exponents(b + 1)
                if ahead >= 2:
                    copy_q(b + 2)
                if not is_step(b, 0):
                    for u in range(TPB):
                        norm.scalar(act, TPB * b + u - TPB, u)
                for u in range(2):
                    feed.high(act, b, u)

            batches(act, batch)
            for u in range(TPB):
                norm.scalar(act, TILES - TPB + u, u)

        @block.vector
        def _(dve):
            dve.wait_ge(loaded, 16 * loads)
            for b in range(BATCH):
                dve.wait_ge(v_projected, b + 1)
                dve.tensor_tensor(v[:, b, :], o_bank[b % 2][0:KEYS, 0:DIM], bv[:, :],
                                  ALU.add).then_inc(v_ready, 1)

            def maxima(b):
                for u in range(TPB):
                    dve.wait_ge(scores_ready, TPB * b + u + 1)
                    dve.tensor_reduce(neg_max[:, u:u + 1], s_bank[u][:, 0:KEYS], AX_X, ALU.max,
                                      negate=True).then_inc(max_ready, 1)

            maxima(0)

            def batch(b, ahead):
                for u in range(TPB):
                    dve.wait_ge(probs_transposed, TPB * b + u + 1)
                    wait(dve, attended, TPB * b + u - 1)
                    dve.tensor_copy(probsT[:, u, :], p_bank[u][0:KEYS, 0:P]).then_inc(probsT_ready, 1)
                for u in range(TPB):
                    t = TPB * b + u
                    dve.wait_ge(probs_ready, t + 1)
                    dve.reciprocal(scale[:, u:u + 1], total[:, u:u + 1]).then_inc(inverse_done, 1)
                    dve.wait_ge(inverse_done, t + 1)
                    dve.tensor_scalar(scale[:, u:u + 1], scale[:, u:u + 1], chip.gate[:, 0:1], None,
                                      ALU.mult).then_inc(scale_ready, 1)
                if ahead >= 1:
                    maxima(b + 1)
                for u in range(TPB):
                    t = TPB * b + u
                    dve.wait_ge(attended, t + 1)
                    dve.wait_ge(scale_ready, t + 1)
                    dve.scalar_tensor_tensor(out=nth(chip.x, t), in0=o_bank[u][:, 0:DIM], scalar=scale[:, u:u + 1],
                                             in1=nth(chip.x, t), op0=ALU.mult, op1=ALU.add).then_inc(norm.x_updated, 1)
                for u in range(TPB):
                    norm.vector_stats(dve, TPB * b + u, u)
                for u in range(TPB):
                    norm.vector_apply(dve, TPB * b + u, u)

            batches(dve, batch)

        @block.gpsimd
        def _(pool):
            def batch(b, ahead):
                for u in range(TPB):
                    norm.gpsimd(pool, TPB * b + u, u)
                for u in range(2):
                    feed.low(pool, b, u)
            batches(pool, batch)


HEADS, HEAD = 16, 16
CHUNK_HEADS = P // HEAD
GROUP = 4
GROUPS = HEADS // GROUP


def multi_head_attention(chip, a, layer, gate, key_bias, norm_args, feed=None):
    nc = chip.nc
    pre = f"L{layer}_xattn_"
    with ExitStack() as ctx:
        st = Stage(chip, f"l{layer}x", ctx)
        bank = chip.bank
        s_bank = [bank[:, 0, :], bank[:, 1, :]]
        p_bank = [bank[:, 2, :], bank[:, 3, :]]
        o_bank, q_bank, y_bank, n_bank = (bank[:, n, :] for n in (4, 5, 6, 7))
        norm = NextNorm(st, n_bank, **norm_args(st))
        w = {n: st.sb(n, [P, KD, DIM]) for n in ("Wq", "Wk", "Wv", "Wo")}
        ctxT = st.sb("ctxT", [P, KD, CTX])
        kT = st.sb("kT", [P, KD, CTX])
        k_diag = st.sb("k_diag", [P, 2, KD * CHUNK_HEADS * KEYS])
        v1 = st.sb("v1", [KEYS, BATCH, HEADS, HEAD + 1])
        qT = st.sb("qT", [P, KD, SEQ])
        probs = st.sb("probs", [P, TPB, HEADS * KEYS])
        probsT = st.sb("probsT", [KEYS, HEADS * P])
        row_max = st.sb("row_max", [P, TPB, HEADS])
        inverse = st.sb("inverse", [P, HEADS])
        mixed = st.sb("mixed", [P, DIM])
        mixedT = st.sb("mixedT", [P, KD, P])
        head_of = st.sb("head_of", [P, CHUNK_HEADS])
        if key_bias:
            bias4 = st.sb("bias4", [P, BATCH, KEYS])
        else:
            bq, bk = st.sb("bq", [P, KD]), st.sb("bk", [P, KD])
            bv, bo = st.sb("bv", [KEYS, DIM]), st.sb("bo", [P, DIM])
        loaded = st.sem("loaded")
        kT_projected = st.sem("kT_projected")
        kT_ready = st.sem("kT_ready")
        v_projected = st.sem("v_projected")
        v_ready = st.sem("v_ready")
        ones_ready = st.sem("ones_ready")
        bias_ready = st.sem("bias_ready")
        k_diag_ready = st.sem("k_diag_ready")
        q_projected = st.sem("q_projected")
        q_ready = st.sem("q_ready")
        scores_ready = st.sem("scores_ready")
        scores_copied = st.sem("scores_copied")
        max_ready = st.sem("max_ready")
        shifted = st.sem("shifted")
        probs_ready = st.sem("probs_ready")
        probs_transposed = st.sem("probs_transposed")
        even_copied = st.sem("even_probsT_copied")
        odd_copied = st.sem("odd_probsT_copied")
        attended = st.sem("attended")
        inverse_done = st.sem("inverse_done")
        mixed_ready = st.sem("mixed_ready")
        mixed_transposed = st.sem("mixed_transposed")
        mixedT_ready = st.sem("mixedT_ready")
        out_ready = st.sem("out_ready")
        x_biased = st.sem("x_biased")
        halves = CTX // 2
        width = GROUP * KEYS
        loads = 7 if key_bias else 10
        block = ctx.enter_context(nc.Block())

        @block.sync
        def _(sp):
            sp.dma_start(ctxT[:, :, :], load_rows(a["ctxT"])).then_inc(loaded, 16)
            for n in ("Wk", "Wv", "Wq", "Wo"):
                sp.dma_start(w[n][:, :, :], load_rows(a[pre + n])).then_inc(loaded, 16)
            sp.dma_start(head_of[:, :], a["head_of"]).then_inc(loaded, 16)
            if key_bias:
                sp.dma_start(bias4[:, :, :].rearrange("p b k -> p (b k)"),
                             a["key_bias"].partition_broadcast(P)).then_inc(loaded, 16)
            else:
                sp.dma_start(bq[:, :], a[pre + "bq"]).then_inc(loaded, 16)
                sp.dma_start(bk[:, :], a[pre + "bk"]).then_inc(loaded, 16)
                sp.dma_start(bv[:, :], a[pre + "bv"].partition_broadcast(KEYS)).then_inc(loaded, 16)
                sp.dma_start(bo[:, :], a[pre + "bp"].partition_broadcast(P)).then_inc(loaded, 16)
            if feed is not None:
                feed.sync_all(sp)

        @block.tensor
        def _(pe):
            pe.wait_ge(loaded, 16 * loads)
            for m in range(KD):
                for h in range(2):
                    for k in range(KD):
                        last = pe.matmul(bank[:, 2 * m + h, 0:halves], w["Wk"][:, k, m * P:(m + 1) * P],
                                         ctxT[:, k, h * halves:(h + 1) * halves], start=(k == 0), stop=(k == KD - 1))
                    last.then_inc(kT_projected, 1)

            def project_q(b):
                for m in range(KD):
                    for k in range(KD):
                        last = pe.matmul(q_bank[:, m * SEQ:(m + 1) * SEQ], w["Wq"][:, k, m * P:(m + 1) * P],
                                         chip.xnT[:, k, span(b, SEQ)], start=(k == 0), stop=(k == KD - 1))
                last.then_inc(q_projected, 1)

            project_q(0)
            v_bank = [o_bank, y_bank]
            for b in range(BATCH):
                wait(pe, v_ready, b - 1)
                for k in range(KD):
                    last = pe.matmul(v_bank[b % 2][0:KEYS, 0:DIM], ctxT[:, k, b * KEYS:(b + 1) * KEYS],
                                     w["Wv"][:, k, :], start=(k == 0), stop=(k == KD - 1))
                last.then_inc(v_projected, 1)

            def scores(b, u, slot):
                t = TPB * b + u
                pe.wait_ge(q_ready, KD * b + KD)
                pe.wait_ge(k_diag_ready, KD * b + KD)
                for g in range(GROUPS):
                    wait(pe, scores_copied, GROUPS * t + g - 1)
                    c = g // 2
                    at = (c * CHUNK_HEADS + (g % 2) * GROUP) * KEYS
                    keys = (k_diag[:, slot, at:at + width] if isinstance(slot, int) else
                            k_diag[:, bass.ds(slot, 1), at:at + width].rearrange("p a n -> p (a n)"))
                    pe.matmul(s_bank[g % 2][:, 0:width], qT[:, c, u * P:(u + 1) * P], keys,
                              start=True, stop=True).then_inc(scores_ready, 1)

            def transpose_probs(t, u, g):
                copied = even_copied if g % 2 == 0 else odd_copied
                wait(pe, copied, 2 * t + g // 2)
                for h in range(GROUP):
                    at = (g * GROUP + h) * KEYS
                    last = pe.transpose(p_bank[g % 2][0:KEYS, h * P:(h + 1) * P],
                                        probs[:, u, at:at + KEYS], chip.ident[:, :])
                last.then_inc(probs_transposed, 1)

            def attend(b, t):
                wait(pe, mixed_ready, t)
                for g in range(GROUPS):
                    pe.wait_ge(even_copied if g % 2 == 0 else odd_copied, 2 * t + g // 2 + 1)
                    for h in range(g * GROUP, (g + 1) * GROUP):
                        last = pe.matmul(o_bank[:, h * (HEAD + 1):(h + 1) * (HEAD + 1)],
                                         probsT[:, h * P:(h + 1) * P],
                                         v1[:, span(b, 1), h, :].rearrange("p a d -> p (a d)"),
                                         start=True, stop=True)
                last.then_inc(attended, 1)

            def transpose_mixed(t):
                pe.wait_ge(mixed_ready, t + 1)
                wait(pe, norm.copied, t - 1)
                for k in range(KD):
                    last = pe.transpose(n_bank[:, k * P:(k + 1) * P], mixed[:, k * P:(k + 1) * P],
                                        chip.ident[:, :])
                last.then_inc(mixed_transposed, 1)

            def project_out(t):
                pe.wait_ge(mixedT_ready, t + 1)
                wait(pe, norm.x_updated, t)
                for k in range(KD):
                    last = pe.matmul(y_bank[:, 0:DIM], mixedT[:, k, :], w["Wo"][:, k, :],
                                     start=(k == 0), stop=(k == KD - 1))
                last.then_inc(out_ready, 1)

            pe.wait_ge(v_ready, BATCH)
            scores(0, 0, 0)

            def batch(b):
                for u in range(TPB):
                    t = TPB * b + u
                    first = is_step(t, 0)
                    if u == 0:
                        scores(b, 1, b % 2)
                    elif not is_step(b, BATCH - 1):
                        scores(b + 1, 0, (b + 1) % 2)
                    pe.wait_ge(probs_ready, t + 1)
                    if not first:
                        transpose_mixed(t - 1)
                    transpose_probs(t, u, 0)
                    transpose_probs(t, u, 1)
                    if not first:
                        project_out(t - 1)
                    transpose_probs(t, u, 2)
                    transpose_probs(t, u, 3)
                    if u == 0 and not is_step(b, BATCH - 1):
                        project_q(b + 1)
                    attend(b, t)
                    if not is_step(b, 0):
                        norm.tensor(pe, t - 2, u)

            steps(pe, BATCH, batch)
            transpose_mixed(TILES - 1)
            project_out(TILES - 1)
            for u in range(TPB):
                norm.tensor(pe, TILES - TPB + u, u)

        @block.scalar
        def _(act):
            act.wait_ge(loaded, 16 * loads)
            for m in range(KD):
                for h in range(2):
                    act.wait_ge(kT_projected, 2 * m + h + 1)
                    act.activation(kT[:, m, h * halves:(h + 1) * halves], bank[:, 2 * m + h, 0:halves],
                                   ACT.Identity, bias=0.0 if key_bias else bk[:, m:m + 1]).then_inc(kT_ready, 1)

            def copy_q(b):
                act.wait_ge(q_projected, b + 1)
                for m in range(KD):
                    act.activation(qT[:, m, :], q_bank[:, m * SEQ:(m + 1) * SEQ], ACT.Identity,
                                   bias=0.0 if key_bias else bq[:, m:m + 1]).then_inc(q_ready, 1)

            def copy_scores(t, u):
                wait(act, probs_transposed, GROUPS * (t - 1))
                for g in range(GROUPS):
                    act.wait_ge(scores_ready, GROUPS * t + g + 1)
                    act.activation(probs[:, u, g * width:(g + 1) * width], s_bank[g % 2][:, 0:width],
                                   ACT.Copy).then_inc(scores_copied, 1)

            def exponents(t, u):
                act.wait_ge(shifted, t + 1)
                act.activation(probs[:, u, :], probs[:, u, :], ACT.Exp,
                               scale=HEAD ** -0.5).then_inc(probs_ready, 1)

            def copy_probsT(t, g):
                act.wait_ge(probs_transposed, GROUPS * t + g + 1)
                wait(act, attended, t)
                act.activation(probsT[:, g * GROUP * P:(g + 1) * GROUP * P], p_bank[0][0:KEYS, 0:GROUP * P],
                               ACT.Copy).then_inc(even_copied, 1)

            def copy_mixedT(t):
                act.wait_ge(mixed_transposed, t + 1)
                wait(act, out_ready, t)
                act.activation(mixedT[:, :, :], n_bank[:, 0:DIM].rearrange("p (k n) -> p k n", k=KD),
                               ACT.Copy).then_inc(mixedT_ready, 1)

            copy_q(0)
            if not key_bias:
                copy_scores(0, 0)
            exponents(0, 0)

            def batch(b):
                for u in range(TPB):
                    t = TPB * b + u
                    more = not (u == 1 and is_step(b, BATCH - 1))
                    if more and not key_bias:
                        copy_scores(t + 1, 1 - u)
                    if not is_step(t, 0):
                        copy_mixedT(t - 1)
                    copy_probsT(t, 0)
                    copy_probsT(t, 2)
                    if u == 0 and not is_step(b, BATCH - 1):
                        copy_q(b + 1)
                    if more:
                        exponents(t + 1, 1 - u)
                    if feed is not None:
                        feed.high(act, b, u)
                    if not is_step(b, 0):
                        norm.scalar(act, t - 2, u)

            steps(act, BATCH, batch)
            copy_mixedT(TILES - 1)
            for u in range(TPB):
                norm.scalar(act, TILES - TPB + u, u)

        @block.vector
        def _(dve):
            dve.memset(v1[:, :, :, HEAD:HEAD + 1].rearrange("p b h d -> p (b h) d"), 1.0).then_inc(ones_ready, 1)
            dve.wait_ge(loaded, 16 * loads)
            dve.wait_ge(ones_ready, 1)
            if key_bias:
                dve.tensor_scalar(bias4[:, :, :], bias4[:, :, :], HEAD ** 0.5, None,
                                  ALU.mult).then_inc(bias_ready, 1)
                dve.wait_ge(bias_ready, 1)
            else:
                dve.tensor_scalar(bo[:, :], bo[:, :], chip.gate[:, gate:gate + 1], None,
                                  ALU.mult).then_inc(bias_ready, 1)
            for b in range(BATCH):
                dve.wait_ge(v_projected, b + 1)
                source = (o_bank if b % 2 == 0 else y_bank)[0:KEYS, 0:DIM].rearrange("p (h d) -> p h d", h=HEADS)
                if key_bias:
                    dve.tensor_copy(v1[:, b, :, 0:HEAD], source).then_inc(v_ready, 1)
                else:
                    dve.tensor_tensor(v1[:, b, :, 0:HEAD], source, bv[:, :].rearrange("p (h d) -> p h d", h=HEADS),
                                      ALU.add).then_inc(v_ready, 1)

            def maxima(b, u):
                t = TPB * b + u
                if key_bias:
                    wait(dve, probs_transposed, GROUPS * (t - 1))
                    for g in range(GROUPS):
                        dve.wait_ge(scores_ready, GROUPS * t + g + 1)
                        dve.tensor_tensor(
                            probs[:, u, g * width:(g + 1) * width].rearrange("p (h k) -> p h k", h=GROUP),
                            s_bank[g % 2][:, 0:width].rearrange("p (h k) -> p h k", h=GROUP),
                            bias4[:, span(b, 1), :].to_broadcast([P, GROUP, KEYS]),
                            ALU.add).then_inc(scores_copied, 1)
                wait(dve, shifted, t - 1)
                dve.wait_ge(scores_copied, GROUPS * t + GROUPS)
                dve.tensor_reduce(row_max[:, u, :], probs[:, u, :].rearrange("p (h k) -> p h k", h=HEADS),
                                  AX_X, ALU.max).then_inc(max_ready, 1)

            def copy_probsT(t, g):
                dve.wait_ge(probs_transposed, GROUPS * t + g + 1)
                wait(dve, attended, t)
                dve.tensor_copy(probsT[:, g * GROUP * P:(g + 1) * GROUP * P],
                                p_bank[1][0:KEYS, 0:GROUP * P]).then_inc(odd_copied, 1)

            def update_x(t, u):
                dve.wait_ge(out_ready, t + 1)
                if not key_bias:
                    dve.wait_ge(x_biased, t + 1)
                dve.scalar_tensor_tensor(out=nth(chip.x, t), in0=y_bank[:, 0:DIM], scalar=chip.gate[:, gate:gate + 1],
                                         in1=nth(chip.x, t), op0=ALU.mult, op1=ALU.add).then_inc(norm.x_updated, 1)
                norm.vector_stats(dve, t, u)

            def normalise(t):
                attended_of = o_bank[:, 0:HEADS * (HEAD + 1)].rearrange("p (h d) -> p h d", h=HEADS)
                dve.wait_ge(attended, t + 1)
                dve.reciprocal(inverse[:, :], attended_of[:, :, HEAD:HEAD + 1].rearrange("p h d -> p (h d)")
                               ).then_inc(inverse_done, 1)
                dve.wait_ge(inverse_done, t + 1)
                wait(dve, mixed_transposed, t)
                dve.tensor_tensor(mixed[:, :].rearrange("p (h d) -> p h d", h=HEADS), attended_of[:, :, 0:HEAD],
                                  inverse[:, :].unsqueeze(2).to_broadcast([P, HEADS, HEAD]),
                                  ALU.mult).then_inc(mixed_ready, 1)

            maxima(0, 0)

            def batch(b):
                for u in range(TPB):
                    t = TPB * b + u
                    if u == 0:
                        maxima(b, 1)
                    elif not is_step(b, BATCH - 1):
                        maxima(b + 1, 0)
                    copy_probsT(t, 1)
                    if not is_step(t, 0):
                        update_x(t - 1, 1 - u)
                    copy_probsT(t, 3)
                    if not is_step(t, 0):
                        norm.vector_apply(dve, t - 1, 1 - u)
                    normalise(t)
                    if not is_step(t, 0):
                        norm.vector_apply_again(dve, t - 1, 1 - u)

            steps(dve, BATCH, batch)
            update_x(TILES - 1, 1)
            norm.vector_apply(dve, TILES - 1, 1)
            norm.vector_apply_again(dve, TILES - 1, 1)

        @block.gpsimd
        def _(pool):
            pool.wait_ge(loaded, 16 * loads)
            if not key_bias:
                pool.wait_ge(bias_ready, 1)

            def spread_keys(b, slot):
                wait(pool, scores_ready, GROUPS * TPB * (b - 1))
                for c in range(KD):
                    at = c * CHUNK_HEADS * KEYS
                    out = (k_diag[:, slot, at:at + CHUNK_HEADS * KEYS] if isinstance(slot, int) else
                           k_diag[:, bass.ds(slot, 1), at:at + CHUNK_HEADS * KEYS].rearrange("p a n -> p (a n)"))
                    pool.tensor_tensor(out.rearrange("p (h k) -> p h k", h=CHUNK_HEADS),
                                       kT[:, c, span(b, KEYS)].unsqueeze(1).to_broadcast([P, CHUNK_HEADS, KEYS]),
                                       head_of[:, :].unsqueeze(2).to_broadcast([P, CHUNK_HEADS, KEYS]),
                                       ALU.mult).then_inc(k_diag_ready, 1)

            def shift(t, u):
                pool.wait_ge(max_ready, t + 1)
                rows = probs[:, u, :].rearrange("p (h k) -> p h k", h=HEADS)
                pool.tensor_tensor(rows, rows, row_max[:, u, :].unsqueeze(2).to_broadcast([P, HEADS, KEYS]),
                                   ALU.subtract).then_inc(shifted, 1)

            pool.wait_ge(kT_ready, 2 * KD)
            spread_keys(0, 0)
            shift(0, 0)

            def batch(b):
                for u in range(TPB):
                    t = TPB * b + u
                    if not (u == 1 and is_step(b, BATCH - 1)):
                        shift(t + 1, 1 - u)
                    if u == 0 and not is_step(b, BATCH - 1):
                        spread_keys(b + 1, (b + 1) % 2)
                    if not key_bias:
                        pool.tensor_tensor(nth(chip.x, t), nth(chip.x, t), bo[:, :], ALU.add).then_inc(x_biased, 1)
                    if feed is not None:
                        feed.low(pool, b, u)
                    if not is_step(t, 0):
                        norm.gpsimd(pool, t - 1, 1 - u)

            steps(pool, BATCH, batch)
            norm.gpsimd(pool, TILES - 1, 1)


L2_HEADS, L2_HEAD = 4, 64
L2_KEYS = KEYS + SEQ
MASKED = -1e30
RMS_EPS = 1e-8
V_SLOTS = 4


def latent_attention(chip, a):
    nc = chip.nc
    gate, both = 2, 2 * DIM
    with ExitStack() as ctx:
        st = Stage(chip, "l2x", ctx)
        bank = chip.bank
        s_bank = [bank[:, 0, :], bank[:, 1, :]]
        p_bank = [bank[:, 2, :], bank[:, 3, :]]
        o_bank, q_bank, y_bank, n_bank = (bank[:, n, :] for n in (4, 5, 6, 7))
        norm = NextNorm(st, n_bank)
        w_q, w_out = st.sb("W_q", [P, KD, DIM]), st.sb("W_out", [P, KD, DIM])
        w_kv = st.sb("W_kv", [P, KD, both])
        b_out = st.sb("b_out", [P, DIM])
        context_g, context_b = st.sb("ln_x_g", [P, KD]), st.sb("ln_x_b", [P, KD])
        gammas = st.sb("gammas", [P, 2, L2_HEAD])
        gamma = st.sb("gamma", [P, L2_HEAD])
        half = st.sb("half", [P, 1])
        mask = st.sb("mask", [P, CTX], U8)
        mask_row = st.sb("mask_row", [P, CTX])
        mask_now = st.sb("mask_now", [P, KEYS])
        mask_one = st.sb("mask_one", [P, P])
        context = st.sb("context", [KEYS, BATCH, DIM])
        c_stats = st.sb("c_stats", [KEYS, BATCH, 6])
        c_mv = st.sb("c_mv", [KEYS, BATCH, 2])
        c_rstd = st.sb("c_rstd", [KEYS, BATCH])
        c_norm = st.sb("c_norm", [KEYS, BATCH, DIM])
        c_normT = st.sb("c_normT", [P, 2, KD, KEYS])
        c_k = st.sb("c_k", [KEYS, BATCH, DIM])
        c_square = st.sb("c_square", [KEYS, 2, DIM])
        c_rms = st.sb("c_rms", [KEYS, 3, BATCH * L2_HEADS])
        c_kT = st.sb("c_kT", [P, KD, CTX])
        c_v = st.sb("c_v", [KEYS, BATCH, DIM])
        latT = st.sb("latT", [P, KD, SEQ])
        qk = st.sb("qk", [P, TPB, both])
        square = st.sb("square", [P, both])
        rms = st.sb("rms", [P, 3, 2 * L2_HEADS])
        qT = st.sb("qT", [P, KD, SEQ])
        kT = st.sb("kT", [P, KD, L2_KEYS])
        v = st.sb("v", [P, V_SLOTS, TPB * DIM])
        probs = st.sb("probs", [P, TPB * L2_HEADS, L2_KEYS])
        probsT = st.sb("probsT", [P, TPB * L2_HEADS, 3 * P])
        neg_max = st.sb("neg_max", [P, TPB * L2_HEADS])
        total = st.sb("total", [P, TPB * L2_HEADS])
        inverse = st.sb("inverse", [P, TPB * L2_HEADS])
        mixed = st.sb("mixed", [P, TPB, DIM])
        mixedT = st.sb("mixedT", [P, TPB, KD, P])
        sem = st.sem
        loaded, consts_ready = sem("loaded"), sem("consts_ready")
        c_stats_done, c_moments_ready, c_var_eps_done = sem("c_stats_done"), sem("c_moments_ready"), sem("c_var_eps_done")
        c_rstd_ready, c_normed = sem("c_rstd_ready"), sem("c_normed")
        c_norm_transposed, c_normT_ready = sem("c_norm_transposed"), sem("c_normT_ready")
        c_kv_projected, c_k_copied, c_v_copied = sem("c_kv_projected"), sem("c_k_copied"), sem("c_v_copied")
        c_squared, c_summed, c_rooted = sem("c_squared"), sem("c_summed"), sem("c_rooted")
        c_clamped, c_inverted, c_k_normed = sem("c_clamped"), sem("c_inverted"), sem("c_k_normed")
        c_k_transposed, c_kT_ready = sem("c_k_transposed"), sem("c_kT_ready")
        latT_ready, projected, qk_copied, v_copied = sem("latT_ready"), sem("projected"), sem("qk_copied"), sem("v_copied")
        squared, summed, rooted = sem("squared"), sem("summed"), sem("rooted")
        clamped, inverted, qk_normed, q_scaled = sem("clamped"), sem("inverted"), sem("qk_normed"), sem("q_scaled")
        qk_transposed, qkT_ready, c_kT_placed = sem("qk_transposed"), sem("qkT_ready"), sem("c_kT_placed")
        scores_ready, max_ready, probs_ready = sem("scores_ready"), sem("max_ready"), sem("probs_ready")
        probs_transposed = sem("probs_transposed")
        even_copied, odd_copied = sem("even_probsT_copied"), sem("odd_probsT_copied")
        attended, sums_inverted, mixed_ready = sem("attended"), sem("sums_inverted"), sem("mixed_ready")
        mixed_transposed, mixedT_ready = sem("mixed_transposed"), sem("mixedT_ready")
        out_ready, x_biased = sem("out_ready"), sem("x_biased")
        SH = TPB * L2_HEADS
        loads = 10
        consts = 5
        block = ctx.enter_context(nc.Block())

        @block.sync
        def _(sp):
            pre = "L2_xattn_"
            sp.dma_start(context[:, :, :], a["context"].rearrange("(b k) d -> k b d", b=BATCH)).then_inc(loaded, 16)
            sp.dma_start(context_g[:, :], a[pre + "ln_x_g"]).then_inc(loaded, 16)
            sp.dma_start(context_b[:, :], a[pre + "ln_x_b"]).then_inc(loaded, 16)
            sp.dma_start(b_out[:, :], a[pre + "b_out"].partition_broadcast(P)).then_inc(loaded, 16)
            sp.dma_start(w_kv[:, :, :], load_rows(a[pre + "W_kv"])).then_inc(loaded, 16)
            sp.dma_start(w_q[:, :, :], load_rows(a[pre + "W_q"])).then_inc(loaded, 16)
            sp.dma_start(w_out[:, :, :], load_rows(a[pre + "W_out"])).then_inc(loaded, 16)
            for n, g in enumerate(("q_gamma", "k_gamma")):
                sp.dma_start(gammas[:, n, :], a[pre + g].partition_broadcast(P)).then_inc(loaded, 16)
            sp.dma_start(mask[:, :], a["mask"].partition_broadcast(P)).then_inc(loaded, 16)

        @block.tensor
        def _(pe):
            pe.wait_ge(loaded, 16 * loads)

            turn_bank, kv_bank = [n_bank, o_bank], [y_bank, q_bank]

            def transpose_context(b):
                pe.wait_ge(c_normed, b + 1)
                wait(pe, c_normT_ready, b - 1)
                for k in range(KD):
                    last = pe.transpose(turn_bank[b % 2][:, k * KEYS:(k + 1) * KEYS], c_norm[:, b, k * P:(k + 1) * P],
                                        chip.ident[0:KEYS, 0:KEYS])
                last.then_inc(c_norm_transposed, 1)

            def project_context():
                transpose_context(0)
                for b in range(BATCH):
                    if b + 1 < BATCH:
                        transpose_context(b + 1)
                    pe.wait_ge(c_normT_ready, b + 1)
                    wait(pe, c_v_copied, b - 1)
                    for k in range(KD):
                        last = pe.matmul(kv_bank[b % 2][0:KEYS, :], c_normT[:, b % 2, k, :], w_kv[:, k, :],
                                         start=(k == 0), stop=(k == KD - 1))
                    last.then_inc(c_kv_projected, 1)
                pe.wait_ge(c_k_normed, 1)
                for b in range(BATCH):
                    wait(pe, c_kT_ready, b - 1)
                    for k in range(KD):
                        last = pe.transpose(turn_bank[b % 2][:, k * KEYS:(k + 1) * KEYS], c_k[:, b, k * P:(k + 1) * P],
                                            chip.ident[0:KEYS, 0:KEYS])
                    last.then_inc(c_k_transposed, 1)

            def project(b, u):
                t = TPB * b + u
                if u == 0:
                    pe.wait_ge(latT_ready, b + 1)
                wait(pe, v_copied, t)
                wait(pe, norm.x_updated, TPB * (b - 3 + u))
                for k in range(KD):
                    pe.matmul(q_bank[:, 0:DIM], latT[:, k, u * P:(u + 1) * P], w_q[:, k, :],
                              start=(k == 0), stop=(k == KD - 1))
                for k in range(KD):
                    last = pe.matmul(y_bank[:, :], latT[:, k, u * P:(u + 1) * P], w_kv[:, k, :],
                                     start=(k == 0), stop=(k == KD - 1))
                last.then_inc(projected, 1)

            def transpose_qk(b, u):
                t = TPB * b + u
                pe.wait_ge(q_scaled, t + 1)
                wait(pe, qkT_ready, 2 * t)
                wait(pe, norm.copied, TPB * b - 2 * TPB)
                for k in range(2 * KD):
                    last = pe.transpose(n_bank[:, k * P:(k + 1) * P], qk[:, u, k * P:(k + 1) * P],
                                        chip.ident[:, :])
                last.then_inc(qk_transposed, 1)

            def scores(b, s):
                u, h = s // L2_HEADS, s % L2_HEADS
                if s == 0:
                    pe.wait_ge(qkT_ready, 2 * TPB * b + 2 * TPB)
                    pe.wait_ge(c_kT_placed, (KD + 1) * b + KD + 1)
                wait(pe, probs_ready, SH * b + s - 1)
                at = slice(L2_HEAD * (h % 2), L2_HEAD * (h % 2) + L2_HEAD)
                pe.matmul(s_bank[h % 2][:, 0:L2_KEYS], qT[at, h // 2, u * P:(u + 1) * P], kT[at, h // 2, :],
                          start=True, stop=False)
                pe.matmul(s_bank[h % 2][:, 0:KEYS], mask_one[at, :], mask_now[at, :],
                          start=False, stop=True).then_inc(scores_ready, 1)

            def transpose_probs(b, s):
                h = s % L2_HEADS
                copied = even_copied if h % 2 == 0 else odd_copied
                n = SH // 2 * b + s // 2
                pe.wait_ge(probs_ready, SH * b + s + 1)
                wait(pe, copied, n)
                pe.transpose(p_bank[h % 2][0:KEYS, 0:P], probs[:, s, 0:KEYS], chip.ident[:, :])
                for k in range(TPB):
                    last = pe.transpose(p_bank[h % 2][:, (k + 1) * P:(k + 2) * P],
                                        probs[:, s, KEYS + k * P:KEYS + (k + 1) * P], chip.ident[:, :])
                last.then_inc(probs_transposed, 1)

            def attend(b, s):
                u, h, slot = s // L2_HEADS, s % L2_HEADS, b % V_SLOTS
                if h == 0:
                    wait(pe, mixed_ready, TPB * b + u)
                pe.wait_ge(even_copied if h % 2 == 0 else odd_copied, SH // 2 * b + s // 2 + 1)
                out = o_bank[:, h * L2_HEAD:(h + 1) * L2_HEAD]
                pe.matmul(out, probsT[0:KEYS, s, 0:P],
                          c_v[:, span(b, 1), h * L2_HEAD:(h + 1) * L2_HEAD].rearrange("p a d -> p (a d)"),
                          start=True, stop=False)
                for k in range(TPB):
                    at = k * DIM + h * L2_HEAD
                    last = pe.matmul(out, probsT[:, s, (k + 1) * P:(k + 2) * P],
                                     v[:, slot, at:at + L2_HEAD] if isinstance(slot, int) else
                                     v[:, bass.ds(slot, 1), at:at + L2_HEAD].rearrange("p a d -> p (a d)"),
                                     start=False, stop=(k == TPB - 1))
                if h == L2_HEADS - 1:
                    last.then_inc(attended, 1)

            def transpose_mixed(b):
                pe.wait_ge(mixed_ready, TPB * b + TPB)
                for u in range(TPB):
                    for k in range(KD):
                        last = pe.transpose(n_bank[:, (KD * u + k) * P:(KD * u + k + 1) * P],
                                            mixed[:, u, k * P:(k + 1) * P], chip.ident[:, :])
                last.then_inc(mixed_transposed, 1)

            def project_out(b, u):
                t = TPB * b + u
                pe.wait_ge(mixedT_ready, b + 1)
                wait(pe, norm.x_updated, t)
                for k in range(KD):
                    last = pe.matmul(y_bank[:, 0:DIM], mixedT[:, u, k, :], w_out[:, k, :],
                                     start=(k == 0), stop=(k == KD - 1))
                last.then_inc(out_ready, 1)

            project_context()
            pe.wait_ge(c_kT_ready, BATCH)
            pe.wait_ge(c_v_copied, BATCH)
            pe.wait_ge(consts_ready, consts)
            for b in range(2):
                for u in range(TPB):
                    project(b, u)
                for u in range(TPB):
                    if b == 0:
                        transpose_qk(0, u)
            for s in range(SH):
                scores(0, s)
            for u in range(TPB):
                transpose_qk(1, u)

            def batch(b, ahead):
                behind = not is_step(b, 0)
                for s in range(SH):
                    u = s // L2_HEADS
                    if ahead >= 1:
                        scores(b + 1, s)
                    transpose_probs(b, s)
                    if ahead >= 2 and s == SH - 1:
                        transpose_qk(b + 2, 0)
                    if s > 0:
                        attend(b, s - 1)
                    if ahead >= 2 and s % L2_HEADS == 0:
                        project(b + 2, u)
                    if behind and s == 1:
                        transpose_mixed(b - 1)
                    if behind and s in (2, 3):
                        pe.wait_ge(v_copied, TPB * b + 2 * TPB + 1 if ahead >= 2 else TILES)
                        project_out(b - 1, s - 2)
                    if behind and s in (5, 6):
                        norm.tensor(pe, TPB * b - TPB + s - 5, s - 5)
                if ahead >= 2:
                    transpose_qk(b + 2, 1)
                attend(b, SH - 1)

            batches(pe, batch)
            wait(pe, norm.copied, TILES - TPB)
            transpose_mixed(BATCH - 1)
            for u in range(TPB):
                project_out(BATCH - 1, u)
            for u in range(TPB):
                norm.tensor(pe, TILES - TPB + u, u)

        @block.scalar
        def _(act):
            act.wait_ge(loaded, 16 * loads)
            turn_bank, kv_bank = [n_bank, o_bank], [y_bank, q_bank]

            def copy_context_turned(b):
                act.wait_ge(c_norm_transposed, b + 1)
                wait(act, c_kv_projected, b - 1)
                for k in range(KD):
                    last = act.activation(c_normT[:, b % 2, k, :], turn_bank[b % 2][:, k * KEYS:(k + 1) * KEYS],
                                          ACT.Identity, scale=context_g[:, k:k + 1], bias=context_b[:, k:k + 1])
                last.then_inc(c_normT_ready, 1)

            def copy_context():
                copy_context_turned(0)
                for b in range(BATCH):
                    if b + 1 < BATCH:
                        copy_context_turned(b + 1)
                    act.wait_ge(c_kv_projected, b + 1)
                    act.activation(c_k[:, b, :], kv_bank[b % 2][0:KEYS, 0:DIM], ACT.Copy).then_inc(c_k_copied, 1)
                    act.activation(c_v[:, b, :], kv_bank[b % 2][0:KEYS, DIM:both], ACT.Copy).then_inc(c_v_copied, 1)
                    act.wait_ge(c_k_copied, b + 1)
                    wait(act, c_summed, b - 1)
                    act.activation(c_square[:, b % 2, :], c_k[:, b, :], ACT.Square).then_inc(c_squared, 1)
                for b in range(BATCH):
                    act.wait_ge(c_k_transposed, b + 1)
                    act.activation(c_kT[:, :, b * KEYS:(b + 1) * KEYS], turn_bank[b % 2][:, 0:KD * KEYS].rearrange(
                        "p (k n) -> p k n", k=KD), ACT.Copy).then_inc(c_kT_ready, 1)

            def latents(b):
                wait(act, projected, TPB * b)
                act.activation(latT[:, :, :], chip.xnT[:, :, span(b, SEQ)], ACT.Copy).then_inc(latT_ready, 1)

            def copy_projections(b, u):
                t, slot = TPB * b + u, b % V_SLOTS
                act.wait_ge(projected, t + 1)
                wait(act, qk_transposed, t - 1)
                wait(act, attended, TPB * (b - V_SLOTS + 1))
                act.activation(qk[:, u, 0:DIM], q_bank[:, 0:DIM], ACT.Copy).then_inc(qk_copied, 1)
                act.activation(qk[:, u, DIM:both], y_bank[:, 0:DIM], ACT.Copy).then_inc(qk_copied, 1)
                out = (v[:, slot, u * DIM:(u + 1) * DIM] if isinstance(slot, int) else
                       v[:, bass.ds(slot, 1), u * DIM:(u + 1) * DIM].rearrange("p a d -> p (a d)"))
                act.activation(out, y_bank[:, DIM:both], ACT.Copy).then_inc(v_copied, 1)
                act.wait_ge(qk_copied, 2 * t + 2)
                wait(act, summed, t)
                act.activation(square[:, :], qk[:, u, :], ACT.Square).then_inc(squared, 1)

            def place_qkT(b):
                for u in range(TPB):
                    wait(act, scores_ready, SH * b)
                    act.wait_ge(qk_transposed, TPB * b + u + 1)
                    act.activation(qT[:, :, u * P:(u + 1) * P], n_bank[:, 0:KD * P].rearrange("p (k n) -> p k n", k=KD),
                                   ACT.Copy).then_inc(qkT_ready, 1)
                    act.activation(kT[:, :, KEYS + u * P:KEYS + (u + 1) * P],
                                   n_bank[:, KD * P:2 * KD * P].rearrange("p (k n) -> p k n", k=KD),
                                   ACT.Copy).then_inc(qkT_ready, 1)

            def exponents(b, s):
                u = s // L2_HEADS
                act.wait_ge(max_ready, SH * b + s + 1)
                wait(act, probs_transposed, SH * b - SH + s + 1)
                wait(act, sums_inverted, TPB * b - TPB + u + 1)
                act.activation(probs[:, s, :], s_bank[s % 2][:, 0:L2_KEYS], ACT.Exp, bias=neg_max[:, s:s + 1],
                               accum_out=total[:, s:s + 1]).then_inc(probs_ready, 1)

            def copy_probsT(b, s):
                act.wait_ge(probs_transposed, SH * b + s + 1)
                wait(act, attended, TPB * b - TPB + s // L2_HEADS + 1)
                act.activation(probsT[0:KEYS, s, 0:P], p_bank[0][0:KEYS, 0:P], ACT.Copy)
                act.activation(probsT[:, s, P:3 * P], p_bank[0][:, P:3 * P], ACT.Copy).then_inc(even_copied, 1)

            def copy_mixedT(b):
                act.wait_ge(mixed_transposed, b + 1)
                wait(act, out_ready, TPB * b)
                act.activation(mixedT[:, :, :, :].rearrange("p u k n -> p (u k n)"), n_bank[:, 0:TPB * DIM],
                               ACT.Copy).then_inc(mixedT_ready, 1)

            copy_context()
            for b in range(2):
                if b == 0:
                    latents(0)
                for u in range(TPB):
                    copy_projections(b, u)
                latents(b + 1)
                if b == 0:
                    place_qkT(0)
            for s in range(SH):
                exponents(0, s)
            place_qkT(1)

            def batch(b, ahead):
                for s in range(SH):
                    if s % 2 == 0:
                        copy_probsT(b, s)
                    if ahead >= 1:
                        exponents(b + 1, s)
                    if ahead >= 2 and s % L2_HEADS == 0:
                        copy_projections(b + 2, s // L2_HEADS)
                    if not is_step(b, 0):
                        if s == 1:
                            copy_mixedT(b - 1)
                        if s in (6, 7):
                            norm.scalar(act, TPB * b - TPB + s - 6, s - 6)
                    if ahead >= 3 and s == SH - 2:
                        latents(b + 3)
                if ahead >= 2:
                    place_qkT(b + 2)

            batches(act, batch)
            copy_mixedT(BATCH - 1)
            for u in range(TPB):
                norm.scalar(act, TILES - TPB + u, u)

        @block.vector
        def _(dve):
            dve.memset(half[:, :], 0.5).then_inc(consts_ready, 1)
            dve.memset(mask_one[:, :], 0.0).then_inc(consts_ready, 1)
            dve.memset(mask_row[:, :], 0.0).then_inc(consts_ready, 1)
            dve.wait_ge(consts_ready, 3)
            dve.wait_ge(loaded, 16 * loads)
            for r in range(0, P, L2_HEAD):
                dve.memset(mask_one[r:r + 1, :], 1.0)
                last = dve.tensor_scalar(mask_row[r:r + 1, :], mask[r:r + 1, :], 1.0, -MASKED,
                                         ALU.subtract, ALU.mult)
            last.then_inc(consts_ready, 1)
            dve.tensor_scalar(b_out[:, :], b_out[:, :], chip.gate[:, gate:gate + 1], None, ALU.mult)
            dve.scalar_tensor_tensor(out=gamma[:, :], in0=gammas[:, 0, :], scalar=L2_HEAD ** -0.5, in1=gammas[:, 1, :],
                                     op0=ALU.mult, op1=ALU.mult).then_inc(consts_ready, 1)

            def norm_context():
                for b in range(BATCH):
                    dve.bn_stats(c_stats[:, b, :], context[:, b, :]).then_inc(c_stats_done, 1)
                dve.wait_ge(c_stats_done, BATCH)
                for b in range(BATCH):
                    dve.bn_aggr(c_mv[:, b, :], c_stats[:, b, :]).then_inc(c_moments_ready, 1)
                dve.wait_ge(c_rstd_ready, 1)
                for b in range(BATCH):
                    dve.tensor_scalar(c_norm[:, b, :], context[:, b, :], c_mv[:, b, 0:1], c_rstd[:, b:b + 1],
                                      ALU.subtract, ALU.mult).then_inc(c_normed, 1)
                for b in range(BATCH):
                    dve.wait_ge(c_squared, b + 1)
                    dve.tensor_reduce(c_rms[:, 0, b * L2_HEADS:(b + 1) * L2_HEADS],
                                      c_square[:, b % 2, :].rearrange("p (h d) -> p h d", h=L2_HEADS),
                                      AX_X, ALU.add).then_inc(c_summed, 1)
                dve.wait_ge(c_rooted, 1)
                dve.tensor_scalar(c_rms[:, 2, :], c_rms[:, 1, :], L2_HEAD ** -0.5, RMS_EPS, ALU.mult,
                                  ALU.max).then_inc(c_clamped, 1)
                dve.wait_ge(c_clamped, 1)
                dve.reciprocal(c_rms[:, 2, :], c_rms[:, 2, :]).then_inc(c_inverted, 1)
                dve.wait_ge(c_inverted, 1)
                heads = c_k[:, :, :].rearrange("p b (h d) -> p (b h) d", d=L2_HEAD)
                dve.tensor_tensor(heads, heads, c_rms[:, 2, :].unsqueeze(2).to_broadcast([KEYS, BATCH * L2_HEADS, L2_HEAD]),
                                  ALU.mult).then_inc(c_k_normed, 1)

            def rms_norm(b, u):
                t = TPB * b + u
                heads = qk[:, u, :].rearrange("p (h d) -> p h d", h=2 * L2_HEADS)
                dve.wait_ge(squared, t + 1)
                dve.tensor_reduce(rms[:, 0, :], square[:, :].rearrange("p (h d) -> p h d", h=2 * L2_HEADS),
                                  AX_X, ALU.add).then_inc(summed, 1)
                dve.wait_ge(rooted, t + 1)
                dve.tensor_scalar(rms[:, 2, :], rms[:, 1, :], L2_HEAD ** -0.5, RMS_EPS, ALU.mult,
                                  ALU.max).then_inc(clamped, 1)
                dve.wait_ge(clamped, t + 1)
                dve.reciprocal(rms[:, 2, :], rms[:, 2, :]).then_inc(inverted, 1)
                dve.wait_ge(inverted, t + 1)
                dve.tensor_tensor(heads, heads,
                                  rms[:, 2, :].unsqueeze(2).to_broadcast([P, 2 * L2_HEADS, L2_HEAD]),
                                  ALU.mult).then_inc(qk_normed, 1)

            def maximum(b, s):
                dve.wait_ge(scores_ready, SH * b + s + 1)
                wait(dve, probs_ready, SH * b + s + 1 - SH)
                dve.tensor_reduce(neg_max[:, s:s + 1], s_bank[s % 2][:, 0:L2_KEYS], AX_X, ALU.max,
                                  negate=True).then_inc(max_ready, 1)

            def copy_probsT(b, s):
                dve.wait_ge(probs_transposed, SH * b + s + 1)
                wait(dve, attended, TPB * b - TPB + s // L2_HEADS + 1)
                dve.tensor_copy(probsT[0:KEYS, s, 0:P], p_bank[1][0:KEYS, 0:P])
                dve.tensor_copy(probsT[:, s, P:3 * P], p_bank[1][:, P:3 * P]).then_inc(odd_copied, 1)

            def invert_sums(b):
                wait(dve, mixed_ready, TPB * b)
                for u in range(TPB):
                    at = slice(u * L2_HEADS, (u + 1) * L2_HEADS)
                    dve.wait_ge(probs_ready, SH * b + (u + 1) * L2_HEADS)
                    dve.reciprocal(inverse[:, at], total[:, at]).then_inc(sums_inverted, 1)

            def normalise(b, u):
                t = TPB * b + u
                at = slice(u * L2_HEADS, (u + 1) * L2_HEADS)
                dve.wait_ge(sums_inverted, t + 1)
                dve.wait_ge(attended, t + 1)
                wait(dve, mixed_transposed, b)
                dve.tensor_tensor(mixed[:, u, :].rearrange("p (h d) -> p h d", h=L2_HEADS),
                                  o_bank[:, 0:DIM].rearrange("p (h d) -> p h d", h=L2_HEADS),
                                  inverse[:, at].unsqueeze(2).to_broadcast([P, L2_HEADS, L2_HEAD]),
                                  ALU.mult).then_inc(mixed_ready, 1)

            def update_x(t, u):
                dve.wait_ge(out_ready, t + 1)
                dve.wait_ge(x_biased, t + 1)
                dve.scalar_tensor_tensor(out=nth(chip.x, t), in0=y_bank[:, 0:DIM], scalar=chip.gate[:, gate:gate + 1],
                                         in1=nth(chip.x, t), op0=ALU.mult, op1=ALU.add).then_inc(norm.x_updated, 1)
                norm.vector_stats(dve, t, u)

            norm_context()
            for t in range(2 * TPB):
                rms_norm(t // TPB, t % TPB)
            for s in range(SH):
                maximum(0, s)

            def batch(b, ahead):
                invert_sums(b)
                for s in range(SH):
                    if ahead >= 1:
                        maximum(b + 1, s)
                    if s % 2 == 1:
                        copy_probsT(b, s)
                    if ahead >= 2 and s % L2_HEADS == 2:
                        rms_norm(b + 2, s // L2_HEADS)
                    if s == L2_HEADS:
                        normalise(b, 0)
                    if not is_step(b, 0):
                        if s in (2, 3):
                            update_x(TPB * b - TPB + s - 2, s - 2)
                        if s in (4, 5):
                            norm.vector_apply(dve, TPB * b - TPB + s - 4, s - 4)
                normalise(b, 1)

            batches(dve, batch)
            for u in range(TPB):
                update_x(TILES - TPB + u, u)
            for u in range(TPB):
                norm.vector_apply(dve, TILES - TPB + u, u)

        @block.gpsimd
        def _(pool):
            pool.wait_ge(loaded, 16 * loads)
            pool.wait_ge(consts_ready, consts)

            def root(sums, n, ready, count, done):
                pool.wait_ge(ready, count)
                pool.tensor_tensor(sums[:, 1, :], sums[:, 0, :], half[0:sums.shape[0], :].to_broadcast([sums.shape[0], n]),
                                   ALU.pow).then_inc(done, 1)

            def scale_context():
                pool.wait_ge(c_moments_ready, BATCH)
                pool.tensor_tensor(c_rstd[:, :], c_mv[:, :, 1:2].rearrange("p b n -> p (b n)"),
                                   chip.powers[0:KEYS, 1:2].to_broadcast([KEYS, BATCH]), ALU.add).then_inc(c_var_eps_done, 1)
                pool.wait_ge(c_var_eps_done, 1)
                pool.tensor_tensor(c_rstd[:, :], c_rstd[:, :], chip.powers[0:KEYS, 0:1].to_broadcast([KEYS, BATCH]),
                                   ALU.pow).then_inc(c_rstd_ready, 1)
                root(c_rms, BATCH * L2_HEADS, c_summed, BATCH, c_rooted)

            def queries(b, u):
                t = TPB * b + u
                root(rms, 2 * L2_HEADS, summed, t + 1, rooted)
                pool.wait_ge(qk_normed, t + 1)
                heads = qk[:, u, 0:DIM].rearrange("p (h d) -> p h d", h=L2_HEADS)
                pool.tensor_tensor(heads, heads, gamma[:, :].unsqueeze(1).to_broadcast([P, L2_HEADS, L2_HEAD]),
                                   ALU.mult).then_inc(q_scaled, 1)

            def place_context(b):
                wait(pool, scores_ready, SH * b)
                for k in range(KD):
                    pool.tensor_copy(kT[:, k, 0:KEYS], c_kT[:, k, span(b, KEYS)]).then_inc(c_kT_placed, 1)
                pool.tensor_copy(mask_now[:, :], mask_row[:, span(b, KEYS)]).then_inc(c_kT_placed, 1)

            scale_context()
            pool.wait_ge(c_kT_ready, BATCH)
            for b in range(2):
                for u in range(TPB):
                    queries(b, u)
                place_context(b)

            def batch(b, ahead):
                for u in range(TPB):
                    t = TPB * b + u
                    pool.tensor_tensor(nth(chip.x, t), nth(chip.x, t), b_out[:, :],
                                       ALU.add).then_inc(x_biased, 1)
                if ahead >= 2:
                    queries(b + 2, 0)
                if not is_step(b, 0):
                    for u in range(TPB):
                        norm.gpsimd(pool, TPB * b - TPB + u, u)
                if ahead >= 2:
                    queries(b + 2, 1)
                    place_context(b + 2)

            batches(pool, batch)
            for u in range(TPB):
                norm.gpsimd(pool, TILES - TPB + u, u)


class Chain:

    def __init__(self, eng, sem):
        self.eng, self.sem, self.count = eng, sem, 0

    def __call__(self, instruction):
        self.count += 1
        instruction.then_inc(self.sem, 1)
        self.eng.wait_ge(self.sem, self.count)


class Feed:

    def __init__(self, st, dram, high, low, chunk, name=""):
        self.dram, self.high_part, self.low_part, self.chunk = dram, high, low, chunk
        self.chunks = dram.shape[1] // chunk
        self.staging = st.sb(f"{name}staging", [P, 2, chunk])
        self.loaded = [st.sem(f"{name}weights_loaded{u}") for u in range(2)]
        self.high_ready = st.sem(f"{name}high_ready")
        self.low_ready = st.sem(f"{name}low_ready")

    def sync(self, sp, i, u):
        c = 2 * i + u
        wait(sp, self.low_ready, c - 1)
        sp.dma_start(self.staging[:, u, :], self.dram[:, span(c, self.chunk)]).then_inc(self.loaded[u], 16)

    def sync_all(self, sp):
        pairs(sp, self.chunks, lambda i, u: self.sync(sp, i, u))

    def high(self, act, i, u):
        c = 2 * i + u
        act.wait_ge(self.loaded[u], 16 * i + 16)
        act.activation(self.high_part[:, span(c, self.chunk)], self.staging[:, u, :],
                       ACT.Copy).then_inc(self.high_ready, 1)

    def low(self, eng, i, u):
        c = 2 * i + u
        eng.wait_ge(self.high_ready, c + 1)
        eng.tensor_tensor(self.low_part[:, span(c, self.chunk)], self.staging[:, u, :],
                          self.high_part[:, span(c, self.chunk)], ALU.subtract).then_inc(self.low_ready, 1)


def pairs(eng, n, body):
    def pair(i):
        for u in range(2):
            body(i, u)
    steps(eng, n // 2, pair)


def feed_alone(chip, dram, high, low, chunk, name):
    with ExitStack() as ctx:
        st = Stage(chip, name, ctx)
        feed = Feed(st, dram, high, low, chunk)
        block = ctx.enter_context(chip.nc.Block())

        @block.sync
        def _(sp):
            pairs(sp, feed.chunks, lambda i, u: feed.sync(sp, i, u))

        @block.scalar
        def _(act):
            pairs(act, feed.chunks, lambda i, u: feed.high(act, i, u))

        @block.vector
        def _(dve):
            pairs(dve, feed.chunks, lambda i, u: feed.low(dve, i, u))


def gate_logits(pe, chip, weights, out, ready):
    for t in range(TILES):
        for k in range(KD):
            last = pe.matmul(out[:, t * EXPERTS:(t + 1) * EXPERTS], chip.xnT[:, k, t * P:(t + 1) * P],
                             weights[:, k, :], start=(k == 0), stop=(k == KD - 1))
    last.then_inc(ready, 1)


def wide(column):
    return column[:, :].unsqueeze(2).to_broadcast([P, TILES, EXPERTS])


def tall(row):
    return row[:, :].unsqueeze(1).to_broadcast([P, TILES, EXPERTS])


def pick_largest(dve, chain, values, order, picked, work, column):
    chain(dve.tensor_reduce(column[:, :], values[:, :, :], AX_X, ALU.max))
    chain(dve.tensor_tensor(work[:, :, :], values[:, :, :], wide(column), ALU.is_equal))
    chain(dve.tensor_tensor(work[:, :, :], work[:, :, :], tall(order), ALU.mult))
    chain(dve.tensor_reduce(column[:, :], work[:, :, :], AX_X, ALU.min))
    chain(dve.tensor_tensor(picked[:, :, :], tall(order), wide(column), ALU.is_equal))


HIDE = 1e30


def relu_square_experts(chip, a):
    nc = chip.nc
    gate = 4 + 2
    with ExitStack() as ctx:
        st = Stage(chip, "l2f", ctx)
        bank = chip.bank
        norm = NextNorm(st, bank[:, 7, :], depth=4)
        sb, sem = st.sb, st.sem
        ws1, ws2, wr = sb("Ws1", [P, KD, P]), sb("Ws2", [P, DIM]), sb("Wr", [P, KD, EXPERTS])
        order, ones = sb("order", [P, EXPERTS]), sb("ones", [P, P])
        logits, rest, work = (sb(n, [P, TILES, EXPERTS]) for n in ("logits", "rest", "work"))
        first, prob = sb("first", [P, TILES, EXPERTS]), sb("prob", [P, TILES, EXPERTS])
        top, second, column = (sb(n, [P, TILES]) for n in ("top", "second", "column"))
        used, count = sb("used", [P, 1]), sb("count", [1, 1], I32)
        r, h = sb("r", [P, 512]), sb("h", [P, 512])
        w1, w2 = sb("W1", [P, KD, P]), sb("W2", [P, DIM])
        loaded, logits_ready, routed, chained = sem("loaded"), sem("logits_ready"), sem("routed"), sem("chained")
        exp_ready, exp_wanted, counted, count_ready = sem("exp_ready"), sem("exp_wanted"), sem("counted"), sem("count_ready")
        blocks, width = 4, 512
        per = width // P

        with nc.Block() as block:
            @block.sync
            def _(sp):
                sp.dma_start(wr[:, :, :], load_rows(a["L2_ffn_Wr"])).then_inc(loaded, 16)
                sp.dma_start(order[:, :], a["order"].partition_broadcast(P)).then_inc(loaded, 16)
                sp.dma_start(ws1[:, :, :], load_rows(a["L2_ffn_Ws1"])).then_inc(loaded, 16)
                sp.dma_start(ws2[:, :], a["L2_ffn_Ws2"]).then_inc(loaded, 16)

            @block.tensor
            def _(pe):
                pe.wait_ge(loaded, 64)
                gate_logits(pe, chip, wr, bank[:, 0, :], logits_ready)
                pe.wait_ge(routed, 1)
                pe.matmul(bank[:, 1, 0:1], ones[:, :], used[:, :], start=True, stop=True).then_inc(counted, 1)

            @block.scalar
            def _(act):
                act.wait_ge(exp_wanted, 1)
                act.activation(second[:, :], second[:, :], ACT.Exp).then_inc(exp_ready, 1)

            @block.vector
            def _(dve):
                chain = Chain(dve, chained)
                chain(dve.memset(ones[:, :], 1.0))
                dve.wait_ge(loaded, 64)
                dve.wait_ge(logits_ready, 1)
                chain(dve.tensor_copy(logits[:, :, :], bank[:, 0, 0:TILES * EXPERTS].rearrange(
                    "p (t e) -> p t e", t=TILES)))
                pick_largest(dve, chain, logits, order, first, work, column)
                chain(dve.tensor_reduce(top[:, :], logits[:, :, :], AX_X, ALU.max))
                chain(dve.scalar_tensor_tensor(out=rest[:, :, :], in0=first[:, :, :], scalar=-HIDE, in1=logits[:, :, :],
                                               op0=ALU.mult, op1=ALU.add))
                chain(dve.tensor_reduce(second[:, :], rest[:, :, :], AX_X, ALU.max))
                chain(dve.tensor_tensor(second[:, :], second[:, :], top[:, :], ALU.subtract))
                dve.sem_inc(exp_wanted, 1)
                dve.wait_ge(exp_ready, 1)
                chain(dve.tensor_scalar(second[:, :], second[:, :], 1.0, None, ALU.add))
                chain(dve.reciprocal(second[:, :], second[:, :]))
                chain(dve.tensor_scalar(second[:, :], second[:, :], 1.0, None, ALU.is_ge))
                chain(dve.tensor_tensor(prob[:, :, :], first[:, :, :], wide(second), ALU.mult))
                dve.tensor_reduce(used[:, :], second[:, :], AX_X, ALU.add).then_inc(routed, 1)
                chain(dve.tensor_scalar(prob[:, :, :], prob[:, :, :], chip.gate[:, gate:gate + 1], None, ALU.mult))
                dve.wait_ge(counted, 1)
                dve.tensor_copy(count[:, :], bank[0:1, 1, 0:1]).then_inc(count_ready, 1)

        w_loaded, w_used, h_ready, r_ready, h2_ready = (sem(n) for n in (
            "w_loaded", "w_used", "h_ready", "r_ready", "h2_ready"))
        y_ready, added = sem("y_ready"), sem("added")

        def if_routed(eng, body):
            n = eng.value_load(count[0:1, 0:1])
            with eng.If(n != 0):
                body()

        with nc.Block() as block:
            @block.sync
            def _(sp):
                def body():
                    def expert(e):
                        wait(sp, added, TILES * e)
                        sp.dma_start(w1[:, :, :].rearrange("p k n -> p (k n)"),
                                     nth_row(a["L2_ffn_W1"], e)).then_inc(w_loaded, 16)
                        sp.dma_start(w2[:, :], nth_row(a["L2_ffn_W2"], e)).then_inc(w_loaded, 16)
                    steps(sp, EXPERTS, expert)
                if_routed(sp, body)

            @block.tensor
            def _(pe):
                def body():
                    def expert(e):
                        pe.wait_ge(w_loaded, 32 * e + 32)
                        for n in range(blocks):
                            wait(pe, h2_ready, blocks * e + n)
                            for k in range(KD):
                                last = pe.matmul(bank[:, 0, :], w1[:, k, :], chip.xnT[:, k, n * width:(n + 1) * width],
                                                 start=(k == 0), stop=(k == KD - 1))
                            last.then_inc(h_ready, 1)
                            pe.wait_ge(h2_ready, blocks * e + n + 1)
                            for j in range(per):
                                wait(pe, added, TILES * e + n * per + j)
                                pe.matmul(bank[:, 1, 0:DIM], h[:, j * P:(j + 1) * P], w2[:, :], start=True,
                                          stop=True).then_inc(y_ready, 1)
                    steps(pe, EXPERTS, expert)
                if_routed(pe, body)

            @block.scalar
            def _(act):
                def body():
                    def expert(e):
                        for n in range(blocks):
                            act.wait_ge(h_ready, blocks * e + n + 1)
                            wait(act, h2_ready, blocks * e + n)
                            act.activation(r[:, :], bank[:, 0, :], ACT.Relu).then_inc(r_ready, 1)
                    steps(act, EXPERTS, expert)
                if_routed(act, body)

            @block.vector
            def _(dve):
                def body():
                    def expert(e):
                        for n in range(blocks):
                            dve.wait_ge(r_ready, blocks * e + n + 1)
                            wait(dve, y_ready, TILES * e + n * per)
                            dve.tensor_tensor(h[:, :], r[:, :], r[:, :], ALU.mult).then_inc(h2_ready, 1)
                            for j in range(per):
                                t = n * per + j
                                dve.wait_ge(y_ready, TILES * e + t + 1)
                                share = prob[:, t, e:e + 1] if isinstance(e, int) else prob[:, t, bass.ds(e, 1)]
                                dve.scalar_tensor_tensor(out=chip.x[:, t, :], in0=bank[:, 1, 0:DIM], scalar=share,
                                                         in1=chip.x[:, t, :], op0=ALU.mult,
                                                         op1=ALU.add).then_inc(added, 1)
                    steps(dve, EXPERTS, expert)
                if_routed(dve, body)

        hidden_ready, relu_ready, squared, out_ready = (sem(n) for n in (
            "hidden_ready", "relu_ready", "squared", "out_ready"))
        with nc.Block() as block:
            @block.tensor
            def _(pe):
                def hidden(n):
                    for k in range(KD):
                        last = pe.matmul(bank[:, 0, :], ws1[:, k, :], chip.xnT[:, k, span(n, width)],
                                         start=(k == 0), stop=(k == KD - 1))
                    last.then_inc(hidden_ready, 1)

                hidden(0)

                def step(n):
                    pe.wait_ge(squared, n + 1)
                    for j in range(per):
                        wait(pe, norm.x_updated, per * n + j - 1)
                        pe.matmul(bank[:, 2 + j % 2, 0:DIM], h[:, j * P:(j + 1) * P], ws2[:, :], start=True,
                                  stop=True).then_inc(out_ready, 1)
                    if not is_step(n, blocks - 1):
                        hidden(n + 1)
                    for j in range(per):
                        norm.tensor(pe, per * n + j, j)
                steps(pe, blocks, step)

            @block.scalar
            def _(act):
                def step(n):
                    act.wait_ge(hidden_ready, n + 1)
                    wait(act, squared, n)
                    act.activation(r[:, :], bank[:, 0, :], ACT.Relu).then_inc(relu_ready, 1)
                    for j in range(per):
                        norm.scalar(act, per * n + j, j)
                steps(act, blocks, step)

            @block.vector
            def _(dve):
                def step(n):
                    dve.wait_ge(relu_ready, n + 1)
                    wait(dve, out_ready, per * n)
                    dve.tensor_tensor(h[:, :], r[:, :], r[:, :], ALU.mult).then_inc(squared, 1)
                    for j in range(per):
                        t = per * n + j
                        dve.wait_ge(out_ready, t + 1)
                        dve.scalar_tensor_tensor(out=nth(chip.x, t), in0=bank[:, 2 + j % 2, 0:DIM],
                                                 scalar=chip.gate[:, gate:gate + 1], in1=nth(chip.x, t),
                                                 op0=ALU.mult, op1=ALU.add).then_inc(norm.x_updated, 1)
                        norm.vector_stats(dve, t, j)
                    for j in range(per):
                        norm.vector_apply(dve, per * n + j, j)
                steps(dve, blocks, step)

            @block.gpsimd
            def _(pool):
                def step(n):
                    for j in range(per):
                        norm.gpsimd(pool, per * n + j, j)
                steps(pool, blocks, step)


def nth_row(dram, i):
    if isinstance(i, int):
        return dram[i]
    return dram[bass.ds(i, 1), :, :].rearrange("a p m -> p (a m)")


def linear_experts(chip, a, high, low):
    nc = chip.nc
    gate = 4 + 3
    with ExitStack() as ctx:
        st = Stage(chip, "l3f", ctx)
        bank = chip.bank
        sb, sem = st.sb, st.sem
        x_high, x_low = (sb(n, [P, KD, TOKENS], BF16) for n in ("x_high", "x_low"))
        wg, bg, be = sb("Wg", [P, KD, EXPERTS]), sb("bg", [P, EXPERTS]), sb("be", [EXPERTS, DIM])
        order = sb("order", [P, EXPERTS])
        gates, rest, work = (sb(n, [P, TILES, EXPERTS]) for n in ("gates", "rest", "work"))
        first, second = (sb(n, [P, TILES, EXPERTS]) for n in ("first", "second"))
        column = sb("column", [P, TILES])
        share = sb("share", [P, 2, EXPERTS])
        shareT = sb("shareT", [EXPERTS, P])
        total = sb("total", [P, 2, DIM])
        loaded, logits_ready, chained = sem("loaded"), sem("logits_ready"), sem("chained")
        exp_wanted, exp_ready, gates_ready = sem("exp_wanted"), sem("exp_ready"), sem("gates_ready")
        x_high_ready, x_split = sem("x_high_ready"), sem("x_split")
        share_ready, share_transposed, shareT_ready = sem("share_ready"), sem("share_transposed"), sem("shareT_ready")
        bias_ready, experts_ready, added, x_done = sem("bias_ready"), sem("experts_ready"), sem("added"), sem("x_done")
        passed = sem("passed")
        halves = EXPERTS // 2
        block = ctx.enter_context(nc.Block())

        @block.sync
        def _(sp):
            sp.dma_start(wg[:, :, :], load_rows(a["L3_ffn_Wg"])).then_inc(loaded, 16)
            sp.dma_start(bg[:, :], a["L3_ffn_bg"].partition_broadcast(P)).then_inc(loaded, 16)
            sp.dma_start(be[:, :], a["L3_ffn_be"]).then_inc(loaded, 16)
            sp.dma_start(order[:, :], a["order"].partition_broadcast(P)).then_inc(loaded, 16)

        @block.tensor
        def _(pe):
            pe.wait_ge(loaded, 64)
            gate_logits(pe, chip, wg, bank[:, 0, :], logits_ready)
            pe.wait_ge(x_split, KD)
            pe.wait_ge(gates_ready, 1)

            def step(i):
                for u in range(2):
                    t = 2 * i + u
                    pe.wait_ge(share_ready, t + 1)
                    wait(pe, shareT_ready, t)
                    pe.transpose(bank[0:EXPERTS, 4, 0:P], share[:, u, :], chip.ident[:, :]).then_inc(share_transposed, 1)
                    for j in range(halves):
                        wait(pe, added, EXPERTS * t - EXPERTS + 2 * j + 2)
                        n = 0
                        for left, right in ((x_high, high), (x_low, high), (x_high, low)):
                            for k in range(KD):
                                n += 1
                                at = k * EXPERTS * DIM + 2 * j * DIM
                                last = pe.matmul(bank[:, j, :], left[:, k, span(t, P)], right[:, at:at + 2 * DIM],
                                                 start=(n == 1), stop=(n == 3 * KD))
                        last.then_inc(experts_ready, 1)
                    pe.wait_ge(shareT_ready, t + 1)
                    wait(pe, x_done, t)
                    pe.matmul(bank[:, 5, 0:DIM], shareT[:, :], be[:, :], start=True, stop=True).then_inc(bias_ready, 1)

            steps(pe, TILES // 2, step)

        @block.scalar
        def _(act):
            for k in range(KD):
                act.activation(x_high[:, k, :], chip.xnT[:, k, :], ACT.Copy).then_inc(x_high_ready, 1)
            act.wait_ge(exp_wanted, 1)
            act.activation(gates[:, :, :], gates[:, :, :], ACT.Exp).then_inc(exp_ready, 1)

            def step(i):
                for u in range(2):
                    t = 2 * i + u
                    act.wait_ge(share_transposed, t + 1)
                    wait(act, bias_ready, t)
                    act.activation(shareT[:, :], bank[0:EXPERTS, 4, 0:P], ACT.Copy).then_inc(shareT_ready, 1)
            steps(act, TILES // 2, step)

        @block.vector
        def _(dve):
            chain = Chain(dve, chained)
            dve.wait_ge(loaded, 64)
            dve.wait_ge(logits_ready, 1)
            chain(dve.tensor_tensor(gates[:, :, :], bank[:, 0, 0:TILES * EXPERTS].rearrange(
                "p (t e) -> p t e", t=TILES), tall(bg), ALU.add))
            chain(dve.tensor_reduce(column[:, :], gates[:, :, :], AX_X, ALU.max))
            chain(dve.tensor_tensor(gates[:, :, :], gates[:, :, :], wide(column), ALU.subtract))
            dve.sem_inc(exp_wanted, 1)
            for k in range(KD):
                dve.wait_ge(x_high_ready, k + 1)
                dve.tensor_tensor(x_low[:, k, :], chip.xnT[:, k, :], x_high[:, k, :], ALU.subtract).then_inc(x_split, 1)
            dve.wait_ge(exp_ready, 1)
            chain(dve.tensor_reduce(column[:, :], gates[:, :, :], AX_X, ALU.add))
            chain(dve.reciprocal(column[:, :], column[:, :]))
            chain(dve.tensor_tensor(gates[:, :, :], gates[:, :, :], wide(column), ALU.mult))
            pick_largest(dve, chain, gates, order, first, work, column)
            chain(dve.scalar_tensor_tensor(out=rest[:, :, :], in0=first[:, :, :], scalar=-HIDE, in1=gates[:, :, :],
                                           op0=ALU.mult, op1=ALU.add))
            pick_largest(dve, chain, rest, order, second, work, column)
            chain(dve.tensor_tensor(first[:, :, :], first[:, :, :], second[:, :, :], ALU.add))
            chain(dve.tensor_tensor(gates[:, :, :], gates[:, :, :], first[:, :, :], ALU.mult))
            chain(dve.tensor_reduce(column[:, :], gates[:, :, :], AX_X, ALU.add))
            chain(dve.reciprocal(column[:, :], column[:, :]))
            chain(dve.tensor_scalar(column[:, :], column[:, :], chip.gate[:, gate:gate + 1], None, ALU.mult))
            chain(dve.tensor_tensor(gates[:, :, :], gates[:, :, :], wide(column), ALU.mult))
            dve.sem_inc(gates_ready, 1)

            def step(i):
                for u in range(2):
                    t = 2 * i + u
                    wait(dve, share_transposed, t - 1)
                    dve.tensor_copy(share[:, u, :], nth(gates, t)).then_inc(share_ready, 1)
                    dve.wait_ge(share_ready, t + 1)
                    for e in range(EXPERTS):
                        j = e // 2
                        if e % 2 == 0:
                            dve.wait_ge(experts_ready, halves * t + j + 1)
                        source = bank[:, j, (e % 2) * DIM:(e % 2 + 1) * DIM]
                        if e == 0:
                            wait(dve, x_done, t - 1)
                            dve.tensor_scalar(total[:, u, :], source, share[:, u, 0:1], None,
                                              ALU.mult).then_inc(added, 1)
                        else:
                            dve.wait_ge(added, EXPERTS * t + e)
                            dve.scalar_tensor_tensor(out=total[:, u, :], in0=source, scalar=share[:, u, e:e + 1],
                                                     in1=total[:, u, :], op0=ALU.mult, op1=ALU.add).then_inc(added, 1)
                    dve.wait_ge(added, EXPERTS * t + EXPERTS)
                    dve.tensor_tensor(nth(chip.x, t), nth(chip.x, t), total[:, u, :], ALU.add).then_inc(passed, 1)
                    dve.wait_ge(passed, t + 1)
                    dve.wait_ge(bias_ready, t + 1)
                    dve.tensor_tensor(nth(chip.x, t), bank[:, 5, 0:DIM], nth(chip.x, t), ALU.add).then_inc(x_done, 1)
            steps(dve, TILES // 2, step)


class Scratch:

    def __init__(self, nc, name, slots):
        self.tiles = slots // P
        self.rows = nc.dram_tensor(f"{name}_rows", [slots, DIM], F32, kind="Internal").ap()
        self.results = nc.dram_tensor(f"{name}_results", [slots, DIM], F32, kind="Internal").ap()


def slot_tiles(picks):
    return picks * TILES + EXPERTS


class Sorting:

    def __init__(self, st, picks):
        self.picks, self.tiles = picks, slot_tiles(picks)
        sb, sem = st.sb, st.sem
        self.chosen = sb("chosen", [P, TILES, EXPERTS])
        self.chosen_sum = sb("chosen_sum", [P, EXPERTS])
        self.tri, self.ones = sb("tri", [P, P]), sb("ones", [P, P])
        self.starts = sb("starts", [P, TILES])
        self.before = sb("before", [P, EXPERTS, EXPERTS])
        self.numbers = sb("numbers", [P, self.tiles])
        self.counts = sb("counts", [P, EXPERTS])
        self.more = sb("more", [P, EXPERTS, TILES])
        self.tiles_of = sb("tiles_of", [P, EXPERTS])
        self.begin = sb("begin", [P, EXPERTS])
        self.place = sb("place", [P, TILES, EXPERTS])
        self.own = sb("own", [P, TILES, EXPERTS]) if picks > 1 else self.place
        self.position = sb("position", [P, TILES])
        self.slot = [sb(f"slot{k}", [P, TILES], I32) for k in range(picks)]
        self.ended = sb("ended", [P, self.tiles, EXPERTS])
        self.expert = sb("expert", [P, self.tiles])
        self.expert_of = sb("expert_of", [P, self.tiles], I32)
        self.loaded, self.chosen_ready, self.ranked = sem("sort_loaded"), sem("chosen_ready"), sem("ranked")
        self.slots_ready = sem("slots_ready")
        self.loads = 4

    def sync(self, sp, a):
        sp.dma_start(self.tri[:, :], a["tri"]).then_inc(self.loaded, 16)
        sp.dma_start(self.starts[:, :], a["starts"].partition_broadcast(P)).then_inc(self.loaded, 16)
        sp.dma_start(self.before[:, :, :].rearrange("p a b -> p (a b)"),
                     a["before"].partition_broadcast(P)).then_inc(self.loaded, 16)
        sp.dma_start(self.numbers[:, :], a["numbers"][0:self.tiles].partition_broadcast(P)).then_inc(self.loaded, 16)

    def tensor(self, pe, rank_bank, count_bank):
        pe.wait_ge(self.loaded, 16 * self.loads)
        pe.wait_ge(self.chosen_ready, 1)
        every = self.chosen[:, :, :].rearrange("p t e -> p (t e)")
        width = TILES * EXPERTS
        pe.matmul(rank_bank[:, 0:width], self.tri[:, :], every, start=True, stop=False)
        for s in range(1, TILES):
            pe.matmul(rank_bank[:, s * EXPERTS:width], self.ones[:, :], every[:, 0:width - s * EXPERTS],
                      start=False, stop=(s == TILES - 1))
        pe.matmul(count_bank[:, 0:EXPERTS], self.ones[:, :], self.chosen_sum[:, :], start=True,
                  stop=True).then_inc(self.ranked, 1)

    def vector(self, dve, chain, masks, rank_bank, count_bank):
        chain(dve.memset(self.ones[:, :], 1.0))
        if self.picks == 1:
            chain(dve.tensor_copy(self.chosen[:, :, :], masks[0][:, :, :]))
        else:
            chain(dve.tensor_tensor(self.chosen[:, :, :], masks[0][:, :, :], masks[1][:, :, :], ALU.add))
        chain(dve.tensor_reduce(self.chosen_sum[:, :], self.chosen[:, :, :].rearrange("p t e -> p e t"),
                                AX_X, ALU.add))
        dve.sem_inc(self.chosen_ready, 1)
        dve.wait_ge(self.loaded, 16 * self.loads)
        dve.wait_ge(self.ranked, 1)
        chain(dve.tensor_copy(self.counts[:, :], count_bank[:, 0:EXPERTS]))
        shape = [P, EXPERTS, TILES]
        chain(dve.tensor_tensor(self.more[:, :, :], self.counts[:, :].unsqueeze(2).to_broadcast(shape),
                                self.starts[:, :].unsqueeze(1).to_broadcast(shape), ALU.is_gt))
        chain(dve.tensor_reduce(self.tiles_of[:, :], self.more[:, :, :], AX_X, ALU.add))
        chain(dve.tensor_tensor(self.before[:, :, :], self.before[:, :, :],
                                self.tiles_of[:, :].unsqueeze(1).to_broadcast([P, EXPERTS, EXPERTS]), ALU.mult))
        chain(dve.tensor_reduce(self.begin[:, :], self.before[:, :, :], AX_X, ALU.add))
        chain(dve.tensor_scalar(self.counts[:, :], self.begin[:, :], float(P), None, ALU.mult))
        chain(dve.tensor_tensor(self.place[:, :, :], rank_bank[:, 0:TILES * EXPERTS].rearrange(
            "p (t e) -> p t e", t=TILES), tall(self.counts), ALU.add))
        for k in range(self.picks):
            chain(dve.tensor_tensor(self.own[:, :, :], self.place[:, :, :], masks[k][:, :, :], ALU.mult))
            chain(dve.tensor_reduce(self.position[:, :], self.own[:, :, :], AX_X, ALU.add))
            chain(dve.tensor_copy(self.slot[k][:, :], self.position[:, :]))
        dve.sem_inc(self.slots_ready, 1)
        chain(dve.tensor_tensor(self.begin[:, :], self.begin[:, :], self.tiles_of[:, :], ALU.add))
        shape = [P, self.tiles, EXPERTS]
        chain(dve.tensor_tensor(self.ended[:, :, :], self.begin[:, :].unsqueeze(1).to_broadcast(shape),
                                self.numbers[:, :].unsqueeze(2).to_broadcast(shape), ALU.is_le))
        chain(dve.tensor_reduce(self.expert[:, :], self.ended[:, :, :], AX_X, ALU.add))
        chain(dve.tensor_scalar(self.expert[:, :], self.expert[:, :], float(EXPERTS - 1), None, ALU.min))
        chain(dve.tensor_copy(self.expert_of[:, :], self.expert[:, :]))


def scatter_rows(pool, slot, t, source, scratch, scattered):
    pool.indirect_dma_start(out=scratch.rows, out_offset=bass.IndirectOffsetOnAxis(ap=slot[:, t:t + 1], axis=0),
                            in_=source[:, t, :], in_offset=None).then_inc(scattered, 16)


def gather_rows(pool, slot, t, target, scratch, gathered):
    pool.indirect_dma_start(out=target[:, t, :], out_offset=None, in_=scratch.results,
                            in_offset=bass.IndirectOffsetOnAxis(ap=slot[:, t:t + 1], axis=0)).then_inc(gathered, 16)


def expert_part(weights, e, at, width):
    return weights[:, bass.ds(e, 1), :].rearrange("p a n -> p (a n)")[:, at:at + width]


PARTS = 3


class SharedExperts:

    WIDTH, CHUNKS = 2 * P, 4
    TILES_EACH = WIDTH // P

    def __init__(self, st, weights, half_gate):
        self.chip, self.weights, self.half_gate = st.chip, weights, half_gate
        self.bank = st.chip.bank
        width, chunks = self.WIDTH, self.CHUNKS
        self.x_high, self.x_low = (st.sb(n, [P, 2, KD, width], BF16) for n in ("x_high", "x_low"))
        self.hidden_high, self.hidden_low = (st.sb(n, [P, 2, chunks, width], BF16) for n in ("s_high", "s_low"))
        self.squash, self.hidden = (st.sb(n, [P, 2, width]) for n in ("s_squash", "s_hidden"))
        self.x_high_ready, self.x_low_ready, self.h_ready, self.squashed = (st.sem(n) for n in (
            "x_high_ready", "x_low_ready", "s_h_ready", "s_squashed"))
        self.gated, self.hidden_ready, self.high_ready, self.low_ready = (st.sem(n) for n in (
            "s_gated", "s_hidden_ready", "s_high_ready", "s_low_ready"))
        self.out_ready, self.x_added = st.sem("s_out_ready"), st.sem("s_x_added")

    def up(self, pe, n):
        width = self.WIDTH
        pe.wait_ge(self.x_low_ready, n + 1)
        for c in range(self.CHUNKS):
            wait(pe, self.hidden_ready, self.CHUNKS * (n - 1) + c + 1)
            for branch in range(2):
                i = 0
                for x, w in ((self.x_high, 0), (self.x_low, 0), (self.x_high, 1)):
                    for k in range(KD):
                        i += 1
                        at = k * 4 * DIM + branch * 2 * DIM + c * P
                        last = pe.matmul(self.bank[:, c, branch * width:(branch + 1) * width],
                                         self.weights[w][:, at:at + P], x[:, n % 2, k, :],
                                         start=(i == 1), stop=(i == PARTS * KD))
            last.then_inc(self.h_ready, 1)

    def down(self, pe, n):
        pe.wait_ge(self.low_ready, self.CHUNKS * n + self.CHUNKS)
        for j in range(self.TILES_EACH):
            wait(pe, self.x_added, self.TILES_EACH * n + j - 1)
            i = 0
            for h, w in ((self.hidden_high, 0), (self.hidden_low, 0), (self.hidden_high, 1)):
                for c in range(self.CHUNKS):
                    i += 1
                    at = 8 * DIM + c * DIM
                    last = pe.matmul(self.bank[:, 4 + j, 0:DIM], h[:, n % 2, c, j * P:(j + 1) * P],
                                     self.weights[w][:, at:at + DIM], start=(i == 1), stop=(i == PARTS * self.CHUNKS))
            last.then_inc(self.out_ready, 1)

    def high_x(self, act, n):
        wait(act, self.h_ready, self.CHUNKS * (n - 1))
        act.activation(self.x_high[:, n % 2, :, :], self.chip.xnT[:, :, span(n, self.WIDTH)],
                       ACT.Copy).then_inc(self.x_high_ready, 1)

    def low_x(self, dve, n):
        dve.wait_ge(self.x_high_ready, n + 1)
        dve.tensor_tensor(self.x_low[:, n % 2, :, :], self.chip.xnT[:, :, span(n, self.WIDTH)],
                          self.x_high[:, n % 2, :, :], ALU.subtract).then_inc(self.x_low_ready, 1)

    def scalar(self, act, n):
        for c in range(self.CHUNKS):
            m = self.CHUNKS * n + c
            act.wait_ge(self.h_ready, m + 1)
            wait(act, self.gated, m - 1)
            act.activation(self.squash[:, c % 2, :], self.bank[:, c, 0:self.WIDTH], ACT.Tanh,
                           scale=0.5).then_inc(self.squashed, 1)
            act.wait_ge(self.hidden_ready, m + 1)
            if c == 0:
                wait(act, self.out_ready, self.TILES_EACH * (n - 1))
            act.activation(self.hidden_high[:, n % 2, c, :], self.hidden[:, c % 2, :], ACT.Copy).then_inc(self.high_ready, 1)

    def vector(self, dve, n):
        def low(c):
            dve.wait_ge(self.high_ready, self.CHUNKS * n + c + 1)
            dve.tensor_tensor(self.hidden_low[:, n % 2, c, :], self.hidden[:, c % 2, :], self.hidden_high[:, n % 2, c, :],
                              ALU.subtract).then_inc(self.low_ready, 1)

        for c in range(self.CHUNKS):
            m = self.CHUNKS * n + c
            dve.wait_ge(self.squashed, m + 1)
            wait(dve, self.low_ready, m - 1)
            dve.scalar_tensor_tensor(out=self.squash[:, c % 2, :], in0=self.squash[:, c % 2, :], scalar=1.0,
                                     in1=self.bank[:, c, 0:self.WIDTH], op0=ALU.add, op1=ALU.mult).then_inc(self.gated, 1)
            dve.wait_ge(self.gated, m + 1)
            dve.tensor_tensor(self.hidden[:, c % 2, :], self.squash[:, c % 2, :],
                              self.bank[:, c, self.WIDTH:2 * self.WIDTH], ALU.mult).then_inc(self.hidden_ready, 1)
            if c > 0:
                low(c - 1)
        low(self.CHUNKS - 1)

    def add(self, dve, n):
        for j in range(self.TILES_EACH):
            t = self.TILES_EACH * n + j
            dve.wait_ge(self.out_ready, t + 1)
            dve.scalar_tensor_tensor(out=nth(self.chip.x, t), in0=self.bank[:, 4 + j, 0:DIM], scalar=self.half_gate[:, 0:1],
                                     in1=nth(self.chip.x, t), op0=ALU.mult, op1=ALU.add).then_inc(self.x_added, 1)

    def tensor_part(self, pe, part, between=lambda n: None):
        self.up(pe, part[0])
        for n in part:
            if n + 1 in part:
                self.up(pe, n + 1)
            self.down(pe, n)
            between(n)

    def scalar_part(self, act, part, between=lambda n: None):
        self.high_x(act, part[0])
        for n in part:
            if n + 1 in part:
                self.high_x(act, n + 1)
            self.scalar(act, n)
            between(n)

    def vector_part(self, dve, part, between=lambda n: None):
        self.low_x(dve, part[0])
        for n in part:
            if n + 1 in part:
                self.low_x(dve, n + 1)
            self.vector(dve, n)
            if n > part[0]:
                self.add(dve, n - 1)
            between(n)
        self.add(dve, part[-1])


def silu_experts(chip, a, high, low):
    nc = chip.nc
    gate = 4 + 0
    with ExitStack() as ctx:
        st = Stage(chip, "l0f", ctx)
        bank = chip.bank
        sb, sem = st.sb, st.sem
        scratch = chip.scratch[0]
        experts_width = EXPERTS * 6 * DIM
        split = [w[:, 0:experts_width].rearrange("p (e n) -> p e n", e=EXPERTS) for w in (high, low)]
        width = split[0].shape[2]
        sort = Sorting(st, 2)
        wg, bg, order = sb("gate_w", [P, KD, EXPERTS]), sb("gate_bias", [P, EXPERTS]), sb("order", [P, EXPERTS])
        scores, biased, work = (sb(n, [P, TILES, EXPERTS]) for n in ("scores", "biased", "work"))
        masks = [sb(f"mask{k}", [P, TILES, EXPERTS]) for k in range(2)]
        weight = [sb(f"weight{k}", [P, TILES]) for k in range(2)]
        column, half_gate = sb("column", [P, TILES]), sb("half_gate", [P, 1])
        loaded, logits_ready, chained = sem("loaded"), sem("logits_ready"), sem("chained")
        shared = SharedExperts(st, [w[:, experts_width:] for w in (high, low)], half_gate)
        blocks = range(TOKENS // SharedExperts.WIDTH)
        parts = blocks[:len(blocks) // 2], blocks[len(blocks) // 2:]
        exp_wanted, exp_ready, scattered = sem("exp_wanted"), sem("exp_ready"), sem("scattered")

        with nc.Block() as block:
            @block.sync
            def _(sp):
                sp.dma_start(wg[:, :, :], load_rows(a["L0_ffn_gate_w"])).then_inc(loaded, 16)
                sp.dma_start(bg[:, :], a["L0_ffn_gate_bias"].partition_broadcast(P)).then_inc(loaded, 16)
                sp.dma_start(order[:, :], a["order"].partition_broadcast(P)).then_inc(loaded, 16)
                sort.sync(sp, a)

            @block.tensor
            def _(pe):
                pe.wait_ge(loaded, 48)
                gate_logits(pe, chip, wg, bank[:, 0, :], logits_ready)
                sort.tensor(pe, bank[:, 1, :], bank[:, 2, :])

            @block.scalar
            def _(act):
                act.wait_ge(exp_wanted, 1)
                act.activation(scores[:, :, :], scores[:, :, :], ACT.Exp).then_inc(exp_ready, 1)

            @block.vector
            def _(dve):
                chain = Chain(dve, chained)
                dve.wait_ge(loaded, 48)
                dve.wait_ge(logits_ready, 1)
                logits = bank[:, 0, 0:TILES * EXPERTS].rearrange("p (t e) -> p t e", t=TILES)
                chain(dve.tensor_reduce(column[:, :], logits, AX_X, ALU.max))
                chain(dve.tensor_tensor(scores[:, :, :], logits, wide(column), ALU.subtract))
                dve.sem_inc(exp_wanted, 1)
                dve.wait_ge(exp_ready, 1)
                chain(dve.tensor_reduce(column[:, :], scores[:, :, :], AX_X, ALU.add))
                chain(dve.reciprocal(column[:, :], column[:, :]))
                chain(dve.tensor_tensor(scores[:, :, :], scores[:, :, :], wide(column), ALU.mult))
                chain(dve.tensor_tensor(biased[:, :, :], scores[:, :, :], tall(bg), ALU.add))
                pick_largest(dve, chain, biased, order, masks[0], work, column)
                chain(dve.scalar_tensor_tensor(out=biased[:, :, :], in0=masks[0][:, :, :], scalar=-HIDE,
                                               in1=biased[:, :, :], op0=ALU.mult, op1=ALU.add))
                pick_largest(dve, chain, biased, order, masks[1], work, column)
                sort.vector(dve, chain, masks, bank[:, 1, :], bank[:, 2, :])
                chain(dve.tensor_scalar(half_gate[:, :], chip.gate[:, gate:gate + 1], 0.5, None, ALU.mult))
                for k in range(2):
                    chain(dve.tensor_tensor(work[:, :, :], scores[:, :, :], masks[k][:, :, :], ALU.mult))
                    chain(dve.tensor_reduce(weight[k][:, :], work[:, :, :], AX_X, ALU.add))
                    chain(dve.tensor_scalar(weight[k][:, :], weight[k][:, :], half_gate[:, 0:1], None, ALU.mult))

        with nc.Block() as block:
            @block.gpsimd
            def _(pool):
                for k in range(2):
                    for t in range(TILES):
                        scatter_rows(pool, sort.slot[k], t, chip.keep, scratch, scattered)
                pool.wait_ge(scattered, 16 * 2 * TILES)

            @block.tensor
            def _(pe):
                shared.tensor_part(pe, parts[0])

            @block.scalar
            def _(act):
                shared.scalar_part(act, parts[0])

            @block.vector
            def _(dve):
                shared.vector_part(dve, parts[0])

        with ExitStack() as inner:
            st3 = Stage(chip, "l0r", inner)
            n = sort.tiles
            lanes = SlotLanes(st3, scratch, bank[:, 7, :], n, sort.expert_of)
            placed = PlacedWeights(st3, split, width, lanes.AHEAD)
            hidden_high, hidden_low = (st3.sb(nm, [P, 2, DIM], BF16) for nm in ("hidden_high", "hidden_low"))
            squash, hidden = (st3.sb(nm, [P, 2, DIM]) for nm in ("squash", "hidden"))
            sem3 = st3.sem
            h_ready, squashed, gated, hidden_ready = (sem3(nm) for nm in (
                "h_ready", "squashed", "gated", "hidden_ready"))
            high_ready, low_ready = sem3("high_ready"), sem3("low_ready")
            block = inner.enter_context(nc.Block())

            @block.sync
            def _(sp):
                lanes.sync(sp, placed, lanes.y_ready)

            @block.tensor
            def _(pe):
                def up(i, q):
                    j, u = lanes.AHEAD * i + q, q % 2
                    placed.ready(pe, i, q)
                    pe.wait_ge(lanes.low_ready, j + 1)
                    wait(pe, hidden_ready, j - 1)
                    for m in range(4):
                        s = 0
                        for x, w in ((lanes.high, 0), (lanes.low, 0), (lanes.high, 1)):
                            for k in range(KD):
                                s += 1
                                at = k * 2 * DIM + m * P
                                last = pe.matmul(bank[:, u, m * P:(m + 1) * P], placed.parts[w][:, q, at:at + P],
                                                 x[:, u, k, :], start=(s == 1), stop=(s == PARTS * KD))
                    last.then_inc(h_ready, 1)

                def down(i, q):
                    j, u = lanes.AHEAD * i + q, q % 2
                    pe.wait_ge(low_ready, j + 1)
                    wait(pe, lanes.y_copied, j - 1)
                    s = 0
                    for h, w in ((hidden_high, 0), (hidden_low, 0), (hidden_high, 1)):
                        for c in range(KD):
                            s += 1
                            at = 4 * DIM + c * DIM
                            last = pe.matmul(bank[:, 2 + u, 0:DIM], h[:, u, c * P:(c + 1) * P],
                                             placed.parts[w][:, q, at:at + DIM], start=(s == 1), stop=(s == PARTS * KD))
                    last.then_inc(lanes.y_ready, 1)

                lanes.tensor_loop(pe, up, down)

            @block.scalar
            def _(act):
                def step(i, u):
                    j = 2 * i + u
                    act.wait_ge(h_ready, j + 1)
                    wait(act, gated, j - 1)
                    act.activation(squash[:, u, :], bank[:, u, 0:DIM], ACT.Tanh, scale=0.5).then_inc(squashed, 1)
                    act.wait_ge(hidden_ready, j + 1)
                    wait(act, lanes.y_ready, j - 1)
                    act.activation(hidden_high[:, u, :], hidden[:, u, :], ACT.Copy).then_inc(high_ready, 1)
                lanes.scalar_loop(act, step, bank)

            @block.vector
            def _(dve):
                def step(i, u):
                    j = 2 * i + u
                    dve.wait_ge(squashed, j + 1)
                    wait(dve, low_ready, j - 1)
                    dve.scalar_tensor_tensor(out=squash[:, u, :], in0=squash[:, u, :], scalar=1.0,
                                             in1=bank[:, u, 0:DIM], op0=ALU.add, op1=ALU.mult).then_inc(gated, 1)
                    dve.wait_ge(gated, j + 1)
                    dve.tensor_tensor(hidden[:, u, :], squash[:, u, :], bank[:, u, DIM:2 * DIM],
                                      ALU.mult).then_inc(hidden_ready, 1)
                lanes.vector_loop(dve, step)

            @block.gpsimd
            def _(pool):
                def step(i, u):
                    j = 2 * i + u
                    pool.wait_ge(high_ready, j + 1)
                    pool.tensor_tensor(hidden_low[:, u, :], hidden[:, u, :], hidden_high[:, u, :],
                                       ALU.subtract).then_inc(low_ready, 1)
                pairs(pool, n, step)

        combine(chip, "l0c", ctx, sort, scratch, weight, {}, shared, parts[1])


class PlacedWeights:

    def __init__(self, st, split, width, slots, room=None):
        self.split, self.width, self.slots = split, width, slots
        self.parts = room or [st.sb(f"placed_{n}", [P, slots, width], BF16) for n in ("high", "low")]
        self.copied = [st.sem(f"placed{q}") for q in range(slots)]

    def copy(self, sp, lanes, i, q, released):
        j, slot = lanes.AHEAD * i + q, q % self.slots
        e = lanes.expert(sp, j)
        wait(sp, released, j - self.slots + 1)
        for part, source in zip(self.parts, self.split):
            sp.dma_start(part[:, slot, :], source[:, bass.ds(e, 1), 0:self.width].rearrange("p a n -> p (a n)")).then_inc(
                self.copied[slot], 16)

    def ready(self, pe, i, q):
        rounds = SlotLanes.AHEAD // self.slots
        pe.wait_ge(self.copied[q % self.slots], 32 * (rounds * i + q // self.slots) + 32)


class SlotLanes:

    AHEAD = 4

    def __init__(self, st, scratch, turn_bank, n, expert_of, room=None):
        self.chip, self.scratch, self.turn_bank, self.n = st.chip, scratch, turn_bank, n
        self.expert_of = expert_of
        sb, sem = st.sb, st.sem
        if room is None:
            room = sb("room", [P, self.AHEAD + 2, DIM])
        self.rows, self.y = room[:, 0:self.AHEAD, :], room[:, self.AHEAD:self.AHEAD + 2, :]
        self.high, self.low = (sb(nm, [P, 2, KD, P], BF16) for nm in ("xT_high", "xT_low"))
        self.rows_loaded = [sem(f"rows_loaded{u}") for u in range(self.AHEAD)]
        self.turned, self.high_ready, self.low_ready = sem("turned"), sem("xT_high_ready"), sem("xT_low_ready")
        self.y_ready, self.y_copied = sem("y_ready"), sem("y_copied")
        self.stored = [sem(f"stored{u}") for u in range(2)]

    def rows_of(self, dram, j):
        return dram[span(j, P), :]

    def expert(self, eng, j):
        at = self.expert_of[0:1, j:j + 1] if isinstance(j, int) else self.expert_of[0:1, bass.ds(j, 1)]
        return eng.value_load(at, min_val=0, max_val=EXPERTS - 1)

    def sync(self, sp, placed, released):
        def load(i, q):
            j = self.AHEAD * i + q
            wait(sp, self.turned, j - self.AHEAD + 1)
            sp.dma_start(self.rows[:, q, :], self.rows_of(self.scratch.rows, j)).then_inc(self.rows_loaded[q], 16)

        def store(j, u):
            sp.wait_ge(self.y_copied, j + 1)
            sp.dma_start(self.rows_of(self.scratch.results, j), self.y[:, u, :]).then_inc(self.stored[u], 16)

        for q in range(self.AHEAD):
            load(0, q)
            if q < placed.slots:
                placed.copy(sp, self, 0, q, released)

        def step(i):
            for q in range(self.AHEAD):
                last = is_step(i, self.n // self.AHEAD - 1)
                if not (last and q + placed.slots >= self.AHEAD):
                    placed.copy(sp, self, i + (q + placed.slots) // self.AHEAD, (q + placed.slots) % self.AHEAD, released)
                if not last:
                    load(i + 1, q)
                store(self.AHEAD * i + q, q % 2)
        steps(sp, self.n // self.AHEAD, step)
        for u in range(2):
            sp.wait_ge(self.stored[u], 16 * (self.n // 2))

    def tensor_loop(self, pe, up, down):
        def turn(i, q):
            j = self.AHEAD * i + q
            pe.wait_ge(self.rows_loaded[q], 16 * i + 16)
            wait(pe, self.low_ready, j)
            for k in range(KD):
                last = pe.transpose(self.turn_bank[:, k * P:(k + 1) * P], self.rows[:, q, k * P:(k + 1) * P],
                                    self.chip.ident[:, :])
            last.then_inc(self.turned, 1)

        groups = self.n // self.AHEAD
        turn(0, 0)

        def step(i):
            for q in range(self.AHEAD):
                j = self.AHEAD * i + q
                if q + 1 < self.AHEAD:
                    turn(i, q + 1)
                elif not is_step(i, groups - 1):
                    turn(i + 1, 0)
                up(i, q)
                if q > 0:
                    down(i, q - 1)
                elif not is_step(i, 0):
                    down(i - 1, self.AHEAD - 1)
        steps(pe, groups, step)
        down(groups - 1, self.AHEAD - 1)

    def scalar_loop(self, act, body, bank):
        def split(j, u):
            act.wait_ge(self.turned, j + 1)
            wait(act, self.y_ready, j - 2)
            act.activation(self.high[:, u, :, :], self.turn_bank[:, 0:DIM].rearrange("p (k n) -> p k n", k=KD),
                           ACT.Copy).then_inc(self.high_ready, 1)

        def copy_y(j, u):
            act.wait_ge(self.y_ready, j + 1)
            self.wait_stored(act, j, u)
            act.activation(self.y[:, u, :], bank[:, 2 + u, 0:DIM], ACT.Copy).then_inc(self.y_copied, 1)

        self.split, self.copy_y = split, copy_y
        split(0, 0)

        def step(i, u):
            j = 2 * i + u
            if not (u == 1 and is_step(i, self.n // 2 - 1)):
                split(j + 1, 1 - u)
            body(i, u)
            if not is_step(j, 0):
                copy_y(j - 1, 1 - u)
        pairs(act, self.n, step)
        copy_y(self.n - 1, (self.n - 1) % 2)

    def wait_stored(self, act, j, u):
        if isinstance(j, int):
            wait(act, self.stored[u], 16 * (j // 2))
        else:
            act.wait_ge(self.stored[u], (j - u) * 8)

    def vector_loop(self, dve, body):
        def split(j, u):
            dve.wait_ge(self.high_ready, j + 1)
            dve.tensor_tensor(self.low[:, u, :, :], self.turn_bank[:, 0:DIM].rearrange("p (k n) -> p k n", k=KD),
                              self.high[:, u, :, :], ALU.subtract).then_inc(self.low_ready, 1)

        split(0, 0)

        def step(i, u):
            if not (u == 1 and is_step(i, self.n // 2 - 1)):
                split(2 * i + u + 1, 1 - u)
            body(i, u)
        pairs(dve, self.n, step)


def combine(chip, name, ctx, sort, scratch, weight, norm_args, shared=None, part=()):
    with ExitStack() as inner:
        st = Stage(chip, name, inner)
        groups = 4
        per = TILES // groups
        norm = NextNorm(st, chip.bank[:, 7, :], depth=per, **norm_args)
        targets = [chip.keep] + [st.sb(f"gathered{k}", [P, TILES, DIM]) for k in range(1, sort.picks)]
        gathered = [st.sem(f"gathered{g}") for g in range(groups)]
        part_added = st.sem("part_added")

        def in_turn(shared_part, eng, group, after):
            early = groups // 2 if shared_part else 0
            if shared_part:
                shared_part(eng, part, lambda n: group(n - part[after]) if n in part[after:after + early] else None)
            for g in range(early, groups):
                group(g)

        block = inner.enter_context(chip.nc.Block())

        @block.gpsimd
        def _(pool):
            for g in range(groups + 1):
                for t in range(per * g, min(per * g + per, TILES)):
                    for k in range(sort.picks):
                        gather_rows(pool, sort.slot[k], t, targets[k], scratch, gathered[g])
                for t in range(per * g - per, per * g):
                    if t >= 0:
                        norm.gpsimd(pool, t, t % per)

        @block.vector
        def _(dve):
            def group(g):
                dve.wait_ge(gathered[g], 16 * per * sort.picks)
                for k in range(sort.picks):
                    for u in range(per):
                        t = per * g + u
                        if k > 0:
                            dve.wait_ge(part_added, (sort.picks - 1) * t + k)
                        dve.scalar_tensor_tensor(out=chip.x[:, t, :], in0=targets[k][:, t, :], scalar=weight[k][:, t:t + 1],
                                                 in1=chip.x[:, t, :], op0=ALU.mult, op1=ALU.add).then_inc(
                            norm.x_updated if k == sort.picks - 1 else part_added, 1)
                for u in range(per):
                    norm.vector_stats(dve, per * g + u, u)
                for u in range(per):
                    norm.vector_apply(dve, per * g + u, u)

            in_turn(shared and shared.vector_part, dve, group, 1)

        @block.tensor
        def _(pe):
            def group(g):
                for u in range(per):
                    norm.tensor(pe, per * g + u, u)
            in_turn(shared and shared.tensor_part, pe, group, 2)

        @block.scalar
        def _(act):
            def group(g):
                for u in range(per):
                    norm.scalar(act, per * g + u, u)
            in_turn(shared and shared.scalar_part, act, group, 2)


def relu_experts(chip, a):
    nc = chip.nc
    gate = 4 + 1
    with ExitStack() as ctx:
        st = Stage(chip, "l1f", ctx)
        bank = chip.bank
        sb, sem = st.sb, st.sem
        scratch = chip.scratch[1]
        hidden_width = a["L1_ffn_b1"].shape[1] // EXPERTS * P
        chunks = hidden_width // P
        per_expert = KD * hidden_width + chunks * DIM
        high, low = (sb(n, [P, EXPERTS * per_expert], BF16) for n in ("high", "low"))
        split = [w[:, :].rearrange("p (e n) -> p e n", e=EXPERTS) for w in (high, low)]
        sort = Sorting(st, 1)
        centroids, order = sb("centroids", [P, KD, EXPERTS]), sb("order", [P, EXPERTS])
        b1, ln, b2 = sb("b1", [P, EXPERTS * chunks]), sb("ln", [EXPERTS, 2 * DIM]), sb("b2", [EXPERTS, DIM])
        latent_g, latent_b = sb("ln_l_g", [P, KD]), sb("ln_l_b", [P, KD])
        nearness, work, mask = (sb(n, [P, TILES, EXPERTS]) for n in ("nearness", "work", "mask"))
        weight, column = sb("weight", [P, TILES]), sb("column", [P, TILES])
        maskT = sb("maskT", [EXPERTS, 2, 4, P])
        loaded, logits_ready, chained = sem("loaded"), sem("logits_ready"), sem("chained")
        picked, weight_ready, scattered = sem("picked"), sem("weight_ready"), sem("scattered")
        turned, maskT_ready, affine_ready = sem("mask_turned"), sem("maskT_ready"), sem("affine_ready")
        tanh_wanted, tanh_ready = sem("tanh_wanted"), sem("tanh_ready")
        scaled, row_ready, bias_added = sem("scaled"), sem("row_ready"), sem("bias_added")
        loads = 8
        per = 4

        chunk, slots = 1024, 4
        group, by_vector = 2 * slots, (2, 5, 7)
        groups = EXPERTS * per_expert // (group * chunk)
        staging_ctx = ctx.enter_context(ExitStack())
        staging = Stage(chip, "l1w", staging_ctx).sb("staging", [P, slots, chunk])
        w_loaded, w_split = [sem(f"w_loaded{q}") for q in range(slots)], [sem(f"w_split{q}") for q in range(slots)]
        high_ready = sem("w_high_ready")

        def load_weights(sp, g):
            for n in range(group):
                c, turn = group * g + n, 2 * g + n // slots
                wait(sp, w_split[n % slots], turn)
                sp.dma_start(staging[:, n % slots, :], a["L1_ffn_weights"][:, span(c, chunk)]).then_inc(
                    w_loaded[n % slots], 16)

        def high_parts(act, g):
            for n in range(group):
                c, turn = group * g + n, 2 * g + n // slots
                act.wait_ge(w_loaded[n % slots], 16 * turn + 16)
                act.activation(high[:, span(c, chunk)], staging[:, n % slots, :], ACT.Copy).then_inc(high_ready, 1)

        def low_part(eng, g, n):
            c = group * g + n
            eng.wait_ge(high_ready, c + 1)
            eng.tensor_tensor(low[:, span(c, chunk)], staging[:, n % slots, :], high[:, span(c, chunk)],
                              ALU.subtract).then_inc(w_split[n % slots], 1)

        def low_parts(dve, g):
            for n in by_vector:
                low_part(dve, g, n)

        with nc.Block() as block:
            @block.sync
            def _(sp):
                sp.dma_start(centroids[:, :, :], load_rows(a["L1_ffn_centroids"])).then_inc(loaded, 16)
                sp.dma_start(order[:, :], a["order"].partition_broadcast(P)).then_inc(loaded, 16)
                sp.dma_start(b1[:, :], a["L1_ffn_b1"]).then_inc(loaded, 16)
                for n, w in enumerate(("ln_g", "ln_b")):
                    sp.dma_start(ln[:, n * DIM:(n + 1) * DIM], a[f"L1_ffn_{w}"]).then_inc(loaded, 16)
                sp.dma_start(b2[:, :], a["L1_ffn_b2"]).then_inc(loaded, 16)
                for rows, w in ((latent_g, "ln_l_g"), (latent_b, "ln_l_b")):
                    sp.dma_start(rows[:, :], a[f"L2_xattn_{w}"]).then_inc(loaded, 16)
                sort.sync(sp, a)
                steps(sp, groups, lambda g: load_weights(sp, g))

            @block.tensor
            def _(pe):
                pe.wait_ge(loaded, 16 * loads)
                gate_logits(pe, chip, centroids, bank[:, 0, :], logits_ready)
                pe.wait_ge(picked, 1)
                sort.tensor(pe, bank[:, 1, :], bank[:, 2, :])
                for g in range(TILES // per):
                    wait(pe, maskT_ready, g)
                    for j in range(per):
                        last = pe.transpose(bank[0:EXPERTS, 3, j * P:(j + 1) * P], mask[:, g * per + j, :],
                                            chip.ident[:, :])
                    last.then_inc(turned, 1)
                    pe.wait_ge(maskT_ready, g + 1)
                    for j in range(per):
                        t = g * per + j
                        wait(pe, row_ready, t - 1)
                        pe.matmul(bank[:, 4 + j % 2, :], maskT[:, g % 2, j, :], ln[:, :], start=True, stop=True)
                        pe.matmul(bank[:, 6 + j % 2, 0:DIM], maskT[:, g % 2, j, :], b2[:, :], start=True,
                                  stop=True).then_inc(affine_ready, 1)

            @block.scalar
            def _(act):
                high_parts(act, 0)
                act.wait_ge(tanh_wanted, 1)
                act.activation(weight[:, :], weight[:, :], ACT.Tanh, scale=0.5).then_inc(tanh_ready, 1)
                for g in range(TILES // per):
                    act.wait_ge(turned, g + 1)
                    wait(act, affine_ready, per * (g - 1))
                    act.activation(maskT[:, g % 2, :, :].rearrange("p a b -> p (a b)"), bank[0:EXPERTS, 3, :],
                                   ACT.Copy).then_inc(maskT_ready, 1)
                for g in range(1, groups):
                    high_parts(act, g)

            @block.vector
            def _(dve):
                chain = Chain(dve, chained)
                dve.wait_ge(loaded, 16 * loads)
                dve.wait_ge(logits_ready, 1)
                chain(dve.tensor_copy(nearness[:, :, :], bank[:, 0, 0:TILES * EXPERTS].rearrange(
                    "p (t e) -> p t e", t=TILES)))
                chain(dve.tensor_reduce(weight[:, :], nearness[:, :, :], AX_X, ALU.max))
                dve.sem_inc(tanh_wanted, 1)
                pick_largest(dve, chain, nearness, order, mask, work, column)
                dve.sem_inc(picked, 1)
                low_parts(dve, 0)
                dve.wait_ge(tanh_ready, 1)
                chain(dve.tensor_scalar(weight[:, :], weight[:, :], 0.5, 0.5, ALU.mult, ALU.add))
                chain(dve.tensor_scalar(weight[:, :], weight[:, :], chip.gate[:, gate:gate + 1], None, ALU.mult))
                sort.vector(dve, chain, [mask], bank[:, 1, :], bank[:, 2, :])
                for t in range(TILES):
                    dve.wait_ge(affine_ready, t + 1)
                    dve.tensor_tensor(chip.keep[:, t, :], chip.keep[:, t, :], bank[:, 4 + t % 2, 0:DIM],
                                      ALU.mult).then_inc(scaled, 1)
                    dve.scalar_tensor_tensor(out=chip.x[:, t, :], in0=bank[:, 6 + t % 2, 0:DIM],
                                             scalar=weight[:, t:t + 1], in1=chip.x[:, t, :], op0=ALU.mult,
                                             op1=ALU.add).then_inc(bias_added, 1)
                    dve.wait_ge(scaled, t + 1)
                    dve.tensor_tensor(chip.keep[:, t, :], chip.keep[:, t, :], bank[:, 4 + t % 2, DIM:2 * DIM],
                                      ALU.add).then_inc(row_ready, 1)
                for g in range(1, groups):
                    low_parts(dve, g)

            @block.gpsimd
            def _(pool):
                def rest(g):
                    for n in range(group):
                        if n not in by_vector:
                            low_part(pool, g, n)
                rest(0)
                pool.wait_ge(sort.slots_ready, 1)
                for t in range(TILES):
                    pool.wait_ge(row_ready, t + 1)
                    scatter_rows(pool, sort.slot[0], t, chip.keep, scratch, scattered)
                for g in range(1, groups):
                    rest(g)
                pool.wait_ge(scattered, 16 * TILES)

        staging_ctx.close()

        with ExitStack() as inner:
            st2 = Stage(chip, "l1r", inner)
            n = sort.tiles
            hidden_high, hidden_low = (st2.sb(nm, [P, 2, hidden_width], BF16) for nm in ("hidden_high", "hidden_low"))
            lane_tiles = hidden_width // DIM
            lanes = SlotLanes(st2, scratch, bank[:, 7, :], n, sort.expert_of, chip.keep[:, 2 * lane_tiles:, :])
            hidden = [chip.keep[:, u * lane_tiles:(u + 1) * lane_tiles, :].rearrange("p a n -> p (a n)") for u in range(2)]
            places = chip.xnT[:, :, :].rearrange("p k n -> p (k n)").bitcast(BF16).rearrange(
                "p (w s n) -> p w s n", w=2, s=2)
            placed = PlacedWeights(st2, split, KD * hidden_width, 2, [places[:, w, :, :] for w in range(2)])
            h_banks = hidden_width // 512
            h_bank = [bank[:, 4 * u:4 * u + h_banks, :].rearrange("p a n -> p (a n)") for u in range(2)]
            h_ready, biased, high_ready, low_ready = (st2.sem(nm) for nm in (
                "h_ready", "biased", "high_ready", "low_ready"))
            block = inner.enter_context(nc.Block())

            @block.sync
            def _(sp):
                lanes.sync(sp, placed, h_ready)

            @block.tensor
            def _(pe):
                def up(i, q):
                    j, u = lanes.AHEAD * i + q, q % 2
                    placed.ready(pe, i, q)
                    pe.wait_ge(lanes.low_ready, j + 1)
                    wait(pe, biased, j - 1)
                    for m in range(chunks):
                        s = 0
                        for x, w in ((lanes.high, 0), (lanes.low, 0), (lanes.high, 1)):
                            for k in range(KD):
                                s += 1
                                at = k * hidden_width + m * P
                                last = pe.matmul(h_bank[u][:, m * P:(m + 1) * P], placed.parts[w][:, u, at:at + P],
                                                 x[:, u, k, :], start=(s == 1), stop=(s == PARTS * KD))
                    last.then_inc(h_ready, 1)

                def down(i, q):
                    j, u = lanes.AHEAD * i + q, q % 2
                    e = lanes.expert(pe, j)
                    pe.wait_ge(low_ready, j + 1)
                    wait(pe, lanes.y_copied, j - 1)
                    s = 0
                    for h, w in ((hidden_high, 0), (hidden_low, 0), (hidden_high, 1)):
                        for c in range(chunks):
                            s += 1
                            last = pe.matmul(bank[:, 2 + u, 0:DIM], h[:, u, c * P:(c + 1) * P],
                                             expert_part(split[w], e, KD * hidden_width + c * DIM, DIM),
                                             start=(s == 1), stop=(s == PARTS * chunks))
                    last.then_inc(lanes.y_ready, 1)

                lanes.tensor_loop(pe, up, down)

            @block.scalar
            def _(act):
                def step(i, u):
                    j = 2 * i + u
                    act.wait_ge(biased, j + 1)
                    wait(act, lanes.y_ready, j - 1)
                    act.activation(hidden_high[:, u, :], hidden[u], ACT.Relu).then_inc(high_ready, 1)
                lanes.scalar_loop(act, step, bank)

            @block.vector
            def _(dve):
                def step(i, u):
                    j = 2 * i + u
                    e = lanes.expert(dve, j)
                    dve.wait_ge(h_ready, j + 1)
                    wait(dve, low_ready, j - 1)
                    dve.tensor_tensor(hidden[u].rearrange("p (c n) -> p c n", c=chunks),
                                      h_bank[u].rearrange("p (c n) -> p c n", c=chunks),
                                      b1[:, bass.ds(e * chunks, chunks)].unsqueeze(2).to_broadcast([P, chunks, P]),
                                      ALU.add).then_inc(biased, 1)
                    dve.wait_ge(high_ready, j + 1)
                    dve.scalar_tensor_tensor(out=hidden_low[:, u, :], in0=hidden[u], scalar=0.0, in1=hidden_high[:, u, :],
                                             op0=ALU.max, op1=ALU.subtract).then_inc(low_ready, 1)
                lanes.vector_loop(dve, step)

        combine(chip, "l1c", ctx, sort, scratch, [weight], {"affine": (latent_g, latent_b)})


def layer0(chip, a, attend=True):
    with ExitStack() as ctx:
        st = Stage(chip, "l0", ctx)
        width = a["L0_ffn_weights"].shape[1]
        high, low = (st.sb(n, [P, width], BF16) for n in ("high", "low"))
        with ExitStack() as inner:
            feed = Feed(Stage(chip, "l0w", inner), a["L0_ffn_weights"], high, low, width // TILES)
            single_head_attention(chip, a, feed)
        silu_experts(chip, a, high, low)


def layer1(chip, a):
    multi_head_attention(chip, a, 1, 1, True, lambda st: {"keep_again": chip.keep, "share": chip.gate[:, 5:6]})
    chip.release()
    relu_experts(chip, a)


def layer2(chip, a):
    latent_attention(chip, a)
    chip.release()
    relu_square_experts(chip, a)


def layer3(chip, a):
    with ExitStack() as ctx:
        st = Stage(chip, "l3", ctx)
        width = a["L3_ffn_We"].shape[1]
        high, low = (st.sb(n, [P, width], BF16) for n in ("We_high", "We_low"))
        with ExitStack() as inner:
            feed = Feed(Stage(chip, "l3w", inner), a["L3_ffn_We"], high, low, width // TILES)
            multi_head_attention(chip, a, 3, 3, False, lambda st: {}, feed)
        linear_experts(chip, a, high, low)


LAYERS = [layer0, layer1, layer2, layer3]




def finish(chip, out):
    nc = chip.nc
    with ExitStack() as ctx:
        st = Stage(chip, "finish", ctx)
        stored = st.sem("stored")
        block = ctx.enter_context(nc.Block())

        @block.sync
        def _(sp):
            sp.dma_start(out.rearrange("(t p) d -> p t d", p=P), chip.x[:, :, :]).then_inc(stored, 16)
            sp.wait_ge(stored, 16)


def program(nc, a, out):
    with ExitStack() as ctx:
        chip = Chip(nc, ctx)
        chip.scratch = [Scratch(nc, "l0", slot_tiles(2) * P), Scratch(nc, "l1", slot_tiles(1) * P)]
        begin(chip, a)
        for layer in LAYERS:
            layer(chip, a)
            chip.release()
        finish(chip, out)


def lay_out(inputs):
    import numpy as np

    a = {}
    a["x"] = inputs["x"].reshape(TOKENS, DIM)
    a["ctxT"] = inputs["ctx_1024"].reshape(CTX, DIM).T
    a["g_xattn"], a["g_ffn"] = inputs["g_xattn"], inputs["g_ffn"]
    a["ident"] = np.eye(P, dtype=np.float32)
    for n in ("Wq", "Wk", "Wv"):
        a[f"L0_xattn_{n}"] = inputs[f"L0_xattn_{n}"].T
    for n in ("bq", "bk"):
        a[f"L0_xattn_{n}"] = inputs[f"L0_xattn_{n}"].reshape(KD, P).T
    a["L0_xattn_bv"] = inputs["L0_xattn_bv"]
    for n in ("Wq", "Wk", "Wv", "Wo"):
        a[f"L1_xattn_{n}"] = inputs[f"L1_xattn_{n}"].T
    a["key_bias"] = inputs["fside_BxS2_0"].reshape(CTX)
    a["head_of"] = np.kron(np.eye(CHUNK_HEADS, dtype=np.float32), np.ones((HEAD, 1), np.float32))
    a["L3_xattn_Wq"], a["L3_xattn_Wo"] = inputs["L3_xattn_Wq"], inputs["L3_xattn_Wp"]
    kv = inputs["L3_xattn_Wkv"].reshape(DIM, HEADS, 2, HEAD)
    a["L3_xattn_Wk"], a["L3_xattn_Wv"] = (kv[:, :, n, :].reshape(DIM, DIM) for n in range(2))
    kv = inputs["L3_xattn_bkv"].reshape(HEADS, 2, HEAD)
    a["L3_xattn_bk"], a["L3_xattn_bv"] = kv[:, 0, :].reshape(KD, P).T, kv[:, 1, :].reshape(DIM)
    a["L3_xattn_bq"] = inputs["L3_xattn_bq"].reshape(KD, P).T
    a["L3_xattn_bp"] = inputs["L3_xattn_bp"]
    for n in ("W_q", "W_kv", "W_out", "b_out", "q_gamma", "k_gamma"):
        a[f"L2_xattn_{n}"] = inputs[f"L2_xattn_{n}"]
    for n in ("ln_x_g", "ln_x_b", "ln_l_g", "ln_l_b"):
        a[f"L2_xattn_{n}"] = inputs[f"L2_xattn_{n}"].reshape(KD, P).T
    a["context"] = inputs["ctx_1024"].reshape(CTX, DIM)
    a["mask"] = inputs["mask_BxS2_bk0"].reshape(CTX)
    a["order"] = np.arange(EXPERTS, dtype=np.float32) - EXPERTS
    for n in ("Ws1", "Ws2", "Wr"):
        a[f"L2_ffn_{n}"] = inputs[f"L2_ffn_{n}"]
    a["L2_ffn_W1"] = inputs["L2_ffn_W1"].reshape(EXPERTS, KD, P, P).transpose(0, 2, 1, 3).reshape(EXPERTS, P, DIM)
    a["L2_ffn_W2"] = inputs["L2_ffn_W2"]
    for n in ("Wg", "bg", "be"):
        a[f"L3_ffn_{n}"] = inputs[f"L3_ffn_{n}"]
    a["L3_ffn_We"] = inputs["L3_ffn_We"].reshape(EXPERTS, DIM, KD, P).transpose(3, 2, 0, 1).reshape(P, -1)
    a["tri"] = np.triu(np.ones((P, P), np.float32), 1)
    a["starts"] = np.arange(TILES, dtype=np.float32) * P
    a["before"] = np.tril(np.ones((EXPERTS, EXPERTS), np.float32), -1).reshape(-1)
    a["numbers"] = np.arange(slot_tiles(2), dtype=np.float32)
    a["L0_ffn_gate_w"], a["L0_ffn_gate_bias"] = inputs["L0_ffn_gate_w"].T, inputs["L0_ffn_gate_bias"]

    def by_rows(w, chunks):
        w = w.reshape(-1, w.shape[-2], chunks, P)
        return w.transpose(3, 0, 2, 1)

    up = np.concatenate([inputs["L0_ffn_w1"], inputs["L0_ffn_w3"]], axis=1)
    experts = np.concatenate([by_rows(up, KD).reshape(P, EXPERTS, -1),
                              by_rows(inputs["L0_ffn_w2"], KD).reshape(P, EXPERTS, -1)], axis=2)
    up = np.concatenate([inputs["L0_ffn_sw1"], inputs["L0_ffn_sw3"]], axis=0)
    a["L0_ffn_weights"] = np.concatenate([experts.reshape(P, -1), by_rows(up, KD).reshape(P, -1),
                                          by_rows(inputs["L0_ffn_sw2"], 4).reshape(P, -1)], axis=1)
    a["L1_ffn_centroids"] = inputs["L1_ffn_centroids"].T
    for n in ("ln_g", "ln_b", "b2"):
        a[f"L1_ffn_{n}"] = inputs[f"L1_ffn_{n}"]
    a["L1_ffn_b1"] = inputs["L1_ffn_b1"].reshape(-1, P).T
    a["L1_ffn_weights"] = np.concatenate(
        [inputs[f"L1_ffn_{n}"].reshape(EXPERTS, -1, P, inputs[f"L1_ffn_{n}"].shape[2]).transpose(2, 0, 1, 3)
         .reshape(P, EXPERTS, -1) for n in ("w1", "w2")], axis=2).reshape(P, -1)
    return {n: np.ascontiguousarray(v) for n, v in a.items()}


def kernel(**inputs):
    import numpy as np
    import concourse.bacc as bacc
    from concourse.bass_utils import run_bass_kernel_spmd

    nc = bacc.Bacc("TRN2", target_bir_lowering=False, num_devices=1)
    arrays = {f"in_{n}": v for n, v in lay_out({n: np.asarray(v) for n, v in inputs.items()}).items()}
    places = {n[len("in_"):]: nc.dram_tensor(n, v.shape, mybir.dt.from_np(v.dtype), kind="ExternalInput").ap()
              for n, v in arrays.items()}
    out = nc.dram_tensor("out_x", [TOKENS, DIM], F32, kind="ExternalOutput").ap()
    program(nc, places, out)
    result = run_bass_kernel_spmd(nc, [arrays], core_ids=[0])
    return result.results[0]["out_x"].reshape(BATCH, SEQ, DIM)
```

```python
from contextlib import ExitStack

import concourse.bass as bass
from concourse import mybir

F32 = mybir.dt.float32
BF16 = mybir.dt.bfloat16
I32 = mybir.dt.int32
U8 = mybir.dt.uint8
ALU = mybir.AluOpType
ACT = mybir.ActivationFunctionType
AX_X = mybir.AxisListType.X

P = 128
BATCH, SEQ, DIM = 8, 256, 256
TOKENS = BATCH * SEQ
TILES = TOKENS // P
TPB = SEQ // P
KD = DIM // P
KEYS = 77
CTX = BATCH * KEYS
EXPERTS = 8
LN_EPS = 1e-5


def wait(eng, sem, value):
    if isinstance(value, int) and value <= 0:
        return
    eng.wait_ge(sem, value)


def wait_apart(eng, sem, value, passed):
    wait(eng, sem, value)
    eng.sem_inc(passed, 1)


def steps(eng, n, body):
    body(0)
    with eng.Fori(1, n - 1) as i:
        body(i)
    body(n - 1)


def is_step(i, n):
    return isinstance(i, int) and i == n


def batches(eng, body):
    body(0, 3)
    body(1, 3)
    with eng.Fori(2, BATCH - 3) as b:
        body(b, 3)
    for left in (2, 1, 0):
        body(BATCH - 1 - left, left)


def nth(ap, i):
    if isinstance(i, int):
        return ap[:, i, :]
    return ap[:, bass.ds(i, 1), :].rearrange("p a d -> p (a d)")


def span(i, width):
    return slice(i * width, (i + 1) * width) if isinstance(i, int) else bass.ds(i * width, width)


class Chip:

    def __init__(self, nc, ctx):
        self.nc, self.ctx = nc, ctx
        sb = self.sb
        self.x = sb("x_res", [P, TILES, DIM], F32)
        self.xnT = sb("xnT", [P, KD, TOKENS], F32)
        self.ident = sb("ident", [P, P], F32)
        self.gate = sb("gate", [P, 8], F32)
        self.powers = sb("powers", [P, 4], F32)
        self.keep = sb("keep", [P, TILES, DIM], F32)
        self.bank = ctx.enter_context(nc.psum_tensor("bank", [P, 8, 512], F32))

        self.finished = []

    def release(self):
        self.nc.all_engine_barrier()
        self.nc.clear_and_free_semaphores(self.finished)
        self.nc.all_engine_barrier()
        self.finished = []

    def sb(self, name, shape, dt):
        return self.ctx.enter_context(self.nc.sbuf_tensor(name, shape, dt))


class Stage:

    def __init__(self, chip, name, ctx):
        self.chip, self.nc, self.name, self.ctx = chip, chip.nc, name, ctx

    def sb(self, name, shape, dt=F32):
        return self.ctx.enter_context(self.nc.sbuf_tensor(f"{self.name}_{name}", shape, dt))

    def sem(self, name):
        semaphore = self.nc.alloc_semaphore(name=f"{self.name}_{name}")
        self.chip.finished.append(semaphore)
        return semaphore


class Moments:

    def __init__(self, st, name, depth):
        self.depth = depth
        self.stats = st.sb(f"{name}_stats", [P, depth, 6])
        self.mv = st.sb(f"{name}_mv", [P, depth, 2])
        self.stats_done = st.sem(f"{name}_stats_done")
        self.ready = st.sem(f"{name}_moments_ready")
        self.passed = st.sem(f"{name}_passed")

    def statistics(self, dve, t, u, rows):
        dve.bn_stats(self.stats[:, u, :], rows).then_inc(self.stats_done, 1)
        wait_apart(dve, self.stats_done, t + 1, self.passed)
        dve.bn_aggr(self.mv[:, u, :], self.stats[:, u, :]).then_inc(self.ready, 1)


class Normed:

    def __init__(self, st, name, moments, again=False):
        self.constants, self.moments, self.again = st.chip.powers, moments, again
        self.shifted = st.sb(f"{name}_shifted", [P, moments.depth])
        self.rstd = st.sb(f"{name}_rstd", [P, moments.depth])
        self.widened = st.sem(f"{name}_widened")
        self.shifted_done = st.sem(f"{name}_shifted_done")
        self.rstd_ready = st.sem(f"{name}_rstd_ready")
        self.normed = st.sem(f"{name}_normed")

    def power(self, pool, t, u):
        variance, shifted = self.moments.mv[:, u, 1:2], self.shifted[:, u:u + 1]
        pool.wait_ge(self.moments.ready, t + 1)
        if self.again:
            pool.tensor_tensor(shifted, variance, self.constants[:, 2:3], ALU.mult).then_inc(self.widened, 1)
            pool.wait_ge(self.widened, t + 1)
            pool.tensor_tensor(shifted, shifted, self.constants[:, 3:4], ALU.add).then_inc(self.shifted_done, 1)
        else:
            pool.tensor_tensor(shifted, variance, self.constants[:, 1:2], ALU.add).then_inc(self.shifted_done, 1)
        wait(pool, self.normed, t - self.moments.depth + 1)
        pool.wait_ge(self.shifted_done, t + 1)
        pool.tensor_tensor(self.rstd[:, u:u + 1], shifted, self.constants[:, 0:1], ALU.pow).then_inc(self.rstd_ready, 1)

    def apply(self, dve, t, u, rows, out):
        dve.wait_ge(self.rstd_ready, t + 1)
        dve.tensor_scalar(out, rows, self.moments.mv[:, u, 0:1], self.rstd[:, u:u + 1], ALU.subtract,
                          ALU.mult).then_inc(self.normed, 1)


class NextNorm:

    def __init__(self, st, bank, keep=None, keep_again=None, affine=None, share=None, depth=2):
        self.chip, self.bank, self.depth = st.chip, bank, depth
        self.keep, self.keep_again, self.affine, self.share = keep, keep_again, affine, share
        self.xn = st.sb("xn", [P, depth, DIM])
        self.x_updated = st.sem("x_updated")
        self.transposed = st.sem("xn_transposed")
        self.copied = st.sem("xnT_copied")
        self.kept = st.sem("xn_kept")
        self.shared = st.sem("xn_shared")
        self.moments = Moments(st, "ln", depth)
        self.main = Normed(st, "ln", self.moments, again=affine is not None)
        self.twice = Normed(st, "ln2", self.moments, again=True) if keep_again is not None else None

    def vector_stats(self, dve, t, u):
        wait_apart(dve, self.x_updated, t + 1, self.moments.passed)
        self.moments.statistics(dve, t, u, nth(self.chip.x, t))

    def vector_apply(self, dve, t, u):
        before = t - self.depth + 1
        wait(dve, self.transposed, before)
        if self.keep is not None:
            wait(dve, self.kept, before)
        if self.share is not None:
            wait(dve, self.shared, before)
        self.main.apply(dve, t, u, nth(self.chip.x, t), self.xn[:, u, :])

    def vector_apply_again(self, dve, t, u):
        if self.keep_again is not None:
            self.twice.apply(dve, t, u, nth(self.chip.x, t), nth(self.keep_again, t))
        if self.share is not None:
            dve.wait_ge(self.main.normed, t + 1)
            dve.wait_ge(self.twice.normed, t + 1)
            dve.scalar_tensor_tensor(out=nth(self.chip.x, t), in0=self.xn[:, u, :], scalar=self.share,
                                     in1=nth(self.chip.x, t), op0=ALU.mult, op1=ALU.add).then_inc(self.shared, 1)

    def gpsimd(self, pool, t, u):
        self.main.power(pool, t, u)
        if self.twice is not None:
            self.twice.power(pool, t, u)

    def tensor(self, pe, t, u):
        pe.wait_ge(self.main.normed, t + 1)
        wait(pe, self.copied, t)
        for k in range(KD):
            last = pe.transpose(self.bank[:, k * P:(k + 1) * P], self.xn[:, u, k * P:(k + 1) * P],
                                self.chip.ident[:, :])
        last.then_inc(self.transposed, 1)

    def scalar(self, act, t, u):
        if self.keep is not None:
            act.wait_ge(self.main.normed, t + 1)
            act.activation(nth(self.keep, t), self.xn[:, u, :], ACT.Copy).then_inc(self.kept, 1)
        act.wait_ge(self.transposed, t + 1)
        if self.affine is None:
            act.activation(self.chip.xnT[:, :, span(t, P)],
                           self.bank[:, 0:DIM].rearrange("p (k n) -> p k n", k=KD),
                           ACT.Copy).then_inc(self.copied, 1)
        else:
            for k in range(KD):
                last = act.activation(self.chip.xnT[:, k, span(t, P)], self.bank[:, k * P:(k + 1) * P], ACT.Identity,
                                      scale=self.affine[0][:, k:k + 1], bias=self.affine[1][:, k:k + 1])
            last.then_inc(self.copied, 1)


def load_rows(w):
    return w.rearrange("(k p) n -> p k n", p=P)


def begin(chip, a):
    nc = chip.nc
    with ExitStack() as ctx:
        st = Stage(chip, "begin", ctx)
        norm = NextNorm(st, chip.bank[:, 0, :], depth=4)
        per = 4
        raw_gate = st.sb("raw_gate", [P, 8])
        x_loaded = [st.sem(f"x_loaded{u}") for u in range(TILES // per)]
        small_loaded = st.sem("small_loaded")
        gate_ready = st.sem("gate_ready")
        powers_ready = st.sem("powers_ready")
        zeros = st.sb("zeros", [P, 2048])
        zeros_ready, cleared = st.sem("zeros_ready"), st.sem("cleared")
        block = ctx.enter_context(nc.Block())
        x_rows = a["x"].rearrange("(t p) d -> p t d", p=P)

        @block.sync
        def _(sp):
            for u in range(TILES // per):
                sp.dma_start(chip.x[:, u * per:(u + 1) * per, :],
                             x_rows[:, u * per:(u + 1) * per, :]).then_inc(x_loaded[u], 16)
            sp.dma_start(chip.ident[:, :], a["ident"]).then_inc(small_loaded, 16)
            for n, g in enumerate((a["g_xattn"], a["g_ffn"])):
                sp.dma_start(raw_gate[:, 4 * n:4 * n + 4], g.partition_broadcast(P)).then_inc(small_loaded, 16)
            sp.wait_ge(zeros_ready, 1)
            strips = 0
            for scratch in chip.scratch:
                slots = scratch.rows.rearrange("(p r) d -> p (r d)", p=P)
                for at in range(0, slots.shape[1], 2048):
                    sp.dma_start(slots[:, at:at + 2048], zeros[:, :]).then_inc(cleared, 16)
                    strips += 1
            sp.wait_ge(cleared, 16 * strips)

        @block.vector
        def _(dve):
            dve.memset(zeros[:, :], 0.0).then_inc(zeros_ready, 1)
            for n, value in enumerate((-0.5, LN_EPS, 1 + LN_EPS, LN_EPS ** 2)):
                dve.memset(chip.powers[:, n:n + 1], value).then_inc(powers_ready, 1)

            for q in range(TILES // per):
                dve.wait_ge(x_loaded[q], 16)
                dve.sem_inc(norm.x_updated, per)
                for u in range(per):
                    norm.vector_stats(dve, per * q + u, u)
                for u in range(per):
                    norm.vector_apply(dve, per * q + u, u)

        @block.gpsimd
        def _(pool):
            pool.wait_ge(powers_ready, 4)
            pool.wait_ge(small_loaded, 48)

            for t in range(TILES):
                norm.gpsimd(pool, t, t % per)

        @block.tensor
        def _(pe):
            pe.wait_ge(small_loaded, 48)

            for t in range(TILES):
                norm.tensor(pe, t, t % per)

        @block.scalar
        def _(act):
            act.wait_ge(small_loaded, 48)
            act.activation(chip.gate[:, :], raw_gate[:, :], ACT.Tanh).then_inc(gate_ready, 1)
            for t in range(TILES):
                norm.scalar(act, t, t % per)


def single_head_attention(chip, a, feed):
    nc = chip.nc
    with ExitStack() as ctx:
        st = Stage(chip, "l0x", ctx)
        bank = chip.bank
        s_bank = [bank[:, 0, :], bank[:, 1, :]]
        p_bank = [bank[:, 2, :], bank[:, 3, :]]
        o_bank = [bank[:, 4, :], bank[:, 5, :]]
        q_bank = bank[:, 6, :]
        norm = NextNorm(st, bank[:, 7, :], keep=chip.keep)
        w = {n: st.sb(n, [P, KD, DIM]) for n in ("Wq", "Wk", "Wv")}
        bias = {n: st.sb(n, [P, KD]) for n in ("bq", "bk")}
        bv = st.sb("bv", [KEYS, DIM])
        ctxT = st.sb("ctxT", [P, KD, CTX])
        kT = st.sb("kT", [P, KD, CTX])
        v = st.sb("v", [KEYS, BATCH, DIM])
        qT = st.sb("qT", [P, KD, SEQ])
        probs = st.sb("probs", [P, TPB, KEYS])
        probsT = st.sb("probsT", [KEYS, TPB, P])
        neg_max = st.sb("neg_max", [P, TPB])
        total = st.sb("total", [P, TPB])
        scale = st.sb("scale", [P, TPB])
        loaded = st.sem("loaded")
        kT_projected = st.sem("kT_projected")
        kT_ready = st.sem("kT_ready")
        v_projected = st.sem("v_projected")
        v_ready = st.sem("v_ready")
        q_projected = st.sem("q_projected")
        q_ready = st.sem("q_ready")
        scores_ready = st.sem("scores_ready")
        max_ready = st.sem("max_ready")
        probs_ready = st.sem("probs_ready")
        probs_transposed = st.sem("probs_transposed")
        probsT_ready = st.sem("probsT_ready")
        attended = st.sem("attended")
        inverse_done = st.sem("inverse_done")
        scale_ready = st.sem("scale_ready")
        loads = 7
        halves = CTX // 2
        block = ctx.enter_context(nc.Block())

        @block.sync
        def _(sp):
            sp.dma_start(ctxT[:, :, :], load_rows(a["ctxT"])).then_inc(loaded, 16)
            for n in ("Wk", "Wv", "Wq"):
                sp.dma_start(w[n][:, :, :], load_rows(a[f"L0_xattn_{n}"])).then_inc(loaded, 16)
            for n in ("bq", "bk"):
                sp.dma_start(bias[n][:, :], a[f"L0_xattn_{n}"]).then_inc(loaded, 16)
            sp.dma_start(bv[:, :], a["L0_xattn_bv"].partition_broadcast(KEYS)).then_inc(loaded, 16)
            feed.sync_all(sp)

        @block.tensor
        def _(pe):
            pe.wait_ge(loaded, 16 * loads)
            for m in range(KD):
                for h in range(2):
                    for k in range(KD):
                        last = pe.matmul(bank[:, 2 * m + h, 0:halves], w["Wk"][:, k, m * P:(m + 1) * P],
                                         ctxT[:, k, h * halves:(h + 1) * halves], start=(k == 0), stop=(k == KD - 1))
                    last.then_inc(kT_projected, 1)
            for b in range(BATCH):
                wait(pe, v_ready, b - 1)
                for k in range(KD):
                    last = pe.matmul(o_bank[b % 2][0:KEYS, 0:DIM], ctxT[:, k, b * KEYS:(b + 1) * KEYS],
                                     w["Wv"][:, k, :], start=(k == 0), stop=(k == KD - 1))
                last.then_inc(v_projected, 1)

            def project_q(b):
                for m in range(KD):
                    for k in range(KD):
                        last = pe.matmul(q_bank[:, m * SEQ:(m + 1) * SEQ], w["Wq"][:, k, m * P:(m + 1) * P],
                                         chip.xnT[:, k, span(b, SEQ)], start=(k == 0), stop=(k == KD - 1))
                last.then_inc(q_projected, 1)

            def scores(b):
                pe.wait_ge(q_ready, KD * b + KD)
                for u in range(TPB):
                    wait(pe, probs_ready, TPB * b + u - 1)
                    for m in range(KD):
                        last = pe.matmul(s_bank[u][:, 0:KEYS], qT[:, m, u * P:(u + 1) * P],
                                         kT[:, m, span(b, KEYS)], start=(m == 0), stop=(m == KD - 1))
                    last.then_inc(scores_ready, 1)

            project_q(0)
            pe.wait_ge(kT_ready, 2 * KD)
            pe.wait_ge(v_ready, BATCH)
            scores(0)
            project_q(1)

            def batch(b, ahead):
                for u in range(TPB):
                    pe.wait_ge(probs_ready, TPB * b + u + 1)
                    wait(pe, probsT_ready, TPB * b + u - 1)
                    pe.transpose(p_bank[u][0:KEYS, 0:P], probs[:, u, :],
                                 chip.ident[:, :]).then_inc(probs_transposed, 1)
                if ahead >= 1:
                    scores(b + 1)
                for u in range(TPB):
                    pe.wait_ge(probsT_ready, TPB * b + u + 1)
                    wait(pe, norm.x_updated, TPB * b + u - 1)
                    pe.matmul(o_bank[u][:, 0:DIM], probsT[:, u, :],
                              v[:, span(b, 1), :].rearrange("p a d -> p (a d)"),
                              start=True, stop=True).then_inc(attended, 1)
                if ahead >= 2:
                    project_q(b + 2)
                if not is_step(b, 0):
                    for u in range(TPB):
                        norm.tensor(pe, TPB * b + u - TPB, u)

            batches(pe, batch)
            for u in range(TPB):
                norm.tensor(pe, TILES - TPB + u, u)

        @block.scalar
        def _(act):
            act.wait_ge(loaded, 16 * loads)
            for m in range(KD):
                for h in range(2):
                    act.wait_ge(kT_projected, 2 * m + h + 1)
                    act.activation(kT[:, m, h * halves:(h + 1) * halves], bank[:, 2 * m + h, 0:halves],
                                   ACT.Identity, bias=bias["bk"][:, m:m + 1]).then_inc(kT_ready, 1)

            def copy_q(b):
                act.wait_ge(q_projected, b + 1)
                wait(act, scores_ready, TPB * b)
                for m in range(KD):
                    act.activation(qT[:, m, :], q_bank[:, m * SEQ:(m + 1) * SEQ], ACT.Identity,
                                   bias=bias["bq"][:, m:m + 1]).then_inc(q_ready, 1)

            def exponents(b):
                for u in range(TPB):
                    act.wait_ge(max_ready, TPB * b + u + 1)
                    wait(act, probs_transposed, TPB * b + u - 1)
                    wait(act, scale_ready, TPB * b + u - 1)
                    act.activation(probs[:, u, :], s_bank[u][:, 0:KEYS], ACT.Exp, bias=neg_max[:, u:u + 1],
                                   accum_out=total[:, u:u + 1]).then_inc(probs_ready, 1)

            copy_q(0)
            exponents(0)
            copy_q(1)

            def batch(b, ahead):
                if ahead >= 1:
                    exponents(b + 1)
                if ahead >= 2:
                    copy_q(b + 2)
                if not is_step(b, 0):
                    for u in range(TPB):
                        norm.scalar(act, TPB * b + u - TPB, u)
                for u in range(2):
                    feed.high(act, b, u)

            batches(act, batch)
            for u in range(TPB):
                norm.scalar(act, TILES - TPB + u, u)

        @block.vector
        def _(dve):
            dve.wait_ge(loaded, 16 * loads)
            for b in range(BATCH):
                dve.wait_ge(v_projected, b + 1)
                dve.tensor_tensor(v[:, b, :], o_bank[b % 2][0:KEYS, 0:DIM], bv[:, :],
                                  ALU.add).then_inc(v_ready, 1)

            def maxima(b):
                for u in range(TPB):
                    dve.wait_ge(scores_ready, TPB * b + u + 1)
                    dve.tensor_reduce(neg_max[:, u:u + 1], s_bank[u][:, 0:KEYS], AX_X, ALU.max,
                                      negate=True).then_inc(max_ready, 1)

            maxima(0)

            def batch(b, ahead):
                for u in range(TPB):
                    dve.wait_ge(probs_transposed, TPB * b + u + 1)
                    wait(dve, attended, TPB * b + u - 1)
                    dve.tensor_copy(probsT[:, u, :], p_bank[u][0:KEYS, 0:P]).then_inc(probsT_ready, 1)
                for u in range(TPB):
                    t = TPB * b + u
                    dve.wait_ge(probs_ready, t + 1)
                    dve.reciprocal(scale[:, u:u + 1], total[:, u:u + 1]).then_inc(inverse_done, 1)
                    dve.wait_ge(inverse_done, t + 1)
                    dve.tensor_scalar(scale[:, u:u + 1], scale[:, u:u + 1], chip.gate[:, 0:1], None,
                                      ALU.mult).then_inc(scale_ready, 1)
                if ahead >= 1:
                    maxima(b + 1)
                for u in range(TPB):
                    t = TPB * b + u
                    dve.wait_ge(attended, t + 1)
                    dve.wait_ge(scale_ready, t + 1)
                    dve.scalar_tensor_tensor(out=nth(chip.x, t), in0=o_bank[u][:, 0:DIM], scalar=scale[:, u:u + 1],
                                             in1=nth(chip.x, t), op0=ALU.mult, op1=ALU.add).then_inc(norm.x_updated, 1)
                for u in range(TPB):
                    norm.vector_stats(dve, TPB * b + u, u)
                for u in range(TPB):
                    norm.vector_apply(dve, TPB * b + u, u)

            batches(dve, batch)

        @block.gpsimd
        def _(pool):
            def batch(b, ahead):
                for u in range(TPB):
                    norm.gpsimd(pool, TPB * b + u, u)
                for u in range(2):
                    feed.low(pool, b, u)
            batches(pool, batch)


HEADS, HEAD = 16, 16
CHUNK_HEADS = P // HEAD
GROUP = 4
GROUPS = HEADS // GROUP


def multi_head_attention(chip, a, layer, gate, key_bias, norm_args, feed=None):
    nc = chip.nc
    pre = f"L{layer}_xattn_"
    with ExitStack() as ctx:
        st = Stage(chip, f"l{layer}x", ctx)
        bank = chip.bank
        s_bank = [bank[:, 0, :], bank[:, 1, :]]
        p_bank = [bank[:, 2, :], bank[:, 3, :]]
        o_bank, q_bank, y_bank, n_bank = (bank[:, n, :] for n in (4, 5, 6, 7))
        norm = NextNorm(st, n_bank, **norm_args(st))
        w = {n: st.sb(n, [P, KD, DIM]) for n in ("Wq", "Wk", "Wv", "Wo")}
        ctxT = st.sb("ctxT", [P, KD, CTX])
        kT = st.sb("kT", [P, KD, CTX])
        k_diag = st.sb("k_diag", [P, 2, KD * CHUNK_HEADS * KEYS])
        v1 = st.sb("v1", [KEYS, BATCH, HEADS, HEAD + 1])
        v_parts = [st.sb(f"v_{n}", [KEYS, BATCH, HEADS * (HEAD + 1)], BF16) for n in ("high", "low")]
        v_now = [st.sb(f"v_{n}_now", [KEYS, HEADS * (HEAD + 1)], BF16) for n in ("high", "low")]
        v_high_ready, v_split = st.sem("v_high_ready"), st.sem("v_split")
        zeros = st.sb("zeros", [KEYS, HEADS * (HEAD + 1)], BF16)
        v_placed = st.sem("v_placed")
        qT = st.sb("qT", [P, KD, SEQ])
        raw = st.sb("scores", [P, TPB, HEADS * KEYS])
        probs = st.sb("probs", [P, TPB, HEADS * KEYS])
        probsT = [st.sb(f"probsT_{n}", [KEYS, HEADS * P], BF16) for n in ("high", "low")]
        row_max = st.sb("row_max", [P, TPB, HEADS])
        inverse = st.sb("inverse", [P, HEADS])
        mixed = st.sb("mixed", [P, DIM])
        mixedT = st.sb("mixedT", [P, KD, P])
        head_of = st.sb("head_of", [P, CHUNK_HEADS])
        if key_bias:
            bias4 = st.sb("bias4", [P, BATCH, KEYS])
        else:
            bq, bk = st.sb("bq", [P, KD]), st.sb("bk", [P, KD])
            bv, bo = st.sb("bv", [KEYS, DIM]), st.sb("bo", [P, DIM])
        loaded = st.sem("loaded")
        kT_projected = st.sem("kT_projected")
        kT_ready = st.sem("kT_ready")
        v_projected = st.sem("v_projected")
        v_ready = st.sem("v_ready")
        ones_ready = st.sem("ones_ready")
        bias_ready = st.sem("bias_ready")
        k_diag_ready = st.sem("k_diag_ready")
        q_projected = st.sem("q_projected")
        q_ready = st.sem("q_ready")
        scores_ready = st.sem("scores_ready")
        scores_copied = st.sem("scores_copied")
        max_ready = st.sem("max_ready")
        shifted = st.sem("shifted")
        probs_ready = st.sem("probs_ready")
        probs_transposed = st.sem("probs_transposed")
        high_copied = st.sem("probsT_high_copied")
        low_copied = st.sem("probsT_low_copied")
        attended = st.sem("attended")
        inverse_done = st.sem("inverse_done")
        mixed_ready = st.sem("mixed_ready")
        mixed_transposed = st.sem("mixed_transposed")
        mixedT_ready = st.sem("mixedT_ready")
        out_ready = st.sem("out_ready")
        x_biased = st.sem("x_biased")
        halves = CTX // 2
        width = GROUP * KEYS
        loads = 7 if key_bias else 10
        block = ctx.enter_context(nc.Block())

        @block.sync
        def _(sp):
            sp.dma_start(ctxT[:, :, :], load_rows(a["ctxT"])).then_inc(loaded, 16)
            for n in ("Wk", "Wv", "Wq", "Wo"):
                sp.dma_start(w[n][:, :, :], load_rows(a[pre + n])).then_inc(loaded, 16)
            sp.dma_start(head_of[:, :], a["head_of"]).then_inc(loaded, 16)
            if key_bias:
                sp.dma_start(bias4[:, :, :].rearrange("p b k -> p (b k)"),
                             a["key_bias"].partition_broadcast(P)).then_inc(loaded, 16)
            else:
                sp.dma_start(bq[:, :], a[pre + "bq"]).then_inc(loaded, 16)
                sp.dma_start(bk[:, :], a[pre + "bk"]).then_inc(loaded, 16)
                sp.dma_start(bv[:, :], a[pre + "bv"].partition_broadcast(KEYS)).then_inc(loaded, 16)
                sp.dma_start(bo[:, :], a[pre + "bp"].partition_broadcast(P)).then_inc(loaded, 16)
            if feed is not None:
                feed.sync_all(sp)

        @block.tensor
        def _(pe):
            pe.wait_ge(loaded, 16 * loads)
            for m in range(KD):
                for h in range(2):
                    for k in range(KD):
                        last = pe.matmul(bank[:, 2 * m + h, 0:halves], w["Wk"][:, k, m * P:(m + 1) * P],
                                         ctxT[:, k, h * halves:(h + 1) * halves], start=(k == 0), stop=(k == KD - 1))
                    last.then_inc(kT_projected, 1)

            def project_q(b):
                for m in range(KD):
                    for k in range(KD):
                        last = pe.matmul(q_bank[:, m * SEQ:(m + 1) * SEQ], w["Wq"][:, k, m * P:(m + 1) * P],
                                         chip.xnT[:, k, span(b, SEQ)], start=(k == 0), stop=(k == KD - 1))
                last.then_inc(q_projected, 1)

            project_q(0)
            v_bank = [o_bank, y_bank]
            for b in range(BATCH):
                wait(pe, v_ready, b - 1)
                for k in range(KD):
                    last = pe.matmul(v_bank[b % 2][0:KEYS, 0:DIM], ctxT[:, k, b * KEYS:(b + 1) * KEYS],
                                     w["Wv"][:, k, :], start=(k == 0), stop=(k == KD - 1))
                last.then_inc(v_projected, 1)

            def scores(b, u, slot, groups=range(GROUPS)):
                t = TPB * b + u
                pe.wait_ge(q_ready, KD * b + KD)
                pe.wait_ge(k_diag_ready, KD * b + KD)
                for g in groups:
                    wait(pe, scores_copied, GROUPS * t + g - 1)
                    c = g // 2
                    at = (c * CHUNK_HEADS + (g % 2) * GROUP) * KEYS
                    keys = (k_diag[:, slot, at:at + width] if isinstance(slot, int) else
                            k_diag[:, bass.ds(slot, 1), at:at + width].rearrange("p a n -> p (a n)"))
                    pe.matmul(s_bank[g % 2][:, 0:width], qT[:, c, u * P:(u + 1) * P], keys,
                              start=True, stop=True).then_inc(scores_ready, 1)

            def transpose_probs(t, u, g):
                wait(pe, low_copied, GROUPS * t + g - 1)
                for h in range(GROUP):
                    at = (g * GROUP + h) * KEYS
                    last = pe.transpose(p_bank[g % 2][0:KEYS, h * P:(h + 1) * P],
                                        probs[:, u, at:at + KEYS], chip.ident[:, :])
                last.then_inc(probs_transposed, 1)

            def attend(b, t):
                wait(pe, mixed_ready, t)
                pe.wait_ge(v_placed, 2 * b + 2)
                for g in range(GROUPS):
                    pe.wait_ge(low_copied, GROUPS * t + g + 1)
                    for h in range(g * GROUP, (g + 1) * GROUP):
                        at = slice(h * (HEAD + 1), (h + 1) * (HEAD + 1))
                        for n, (left, right) in enumerate(((0, 0), (1, 0), (0, 1))):
                            last = pe.matmul(o_bank[:, at], probsT[left][:, h * P:(h + 1) * P], v_now[right][:, at],
                                             start=(n == 0), stop=(n == 2))
                last.then_inc(attended, 1)

            def transpose_mixed(t):
                pe.wait_ge(mixed_ready, t + 1)
                wait(pe, norm.copied, t - 1)
                for k in range(KD):
                    last = pe.transpose(n_bank[:, k * P:(k + 1) * P], mixed[:, k * P:(k + 1) * P],
                                        chip.ident[:, :])
                last.then_inc(mixed_transposed, 1)

            def project_out(t):
                pe.wait_ge(mixedT_ready, t + 1)
                wait(pe, norm.x_updated, t)
                for k in range(KD):
                    last = pe.matmul(y_bank[:, 0:DIM], mixedT[:, k, :], w["Wo"][:, k, :],
                                     start=(k == 0), stop=(k == KD - 1))
                last.then_inc(out_ready, 1)

            pe.wait_ge(v_ready, BATCH)
            for u in range(TPB):
                scores(0, u, 0)
            project_q(1)

            def batch(b, ahead):
                for u in range(TPB):
                    t = TPB * b + u
                    first = is_step(t, 0)
                    pe.wait_ge(probs_ready, t + 1)
                    for half in range(2):
                        groups = (2 * half, 2 * half + 1)
                        for g in groups:
                            transpose_probs(t, u, g)
                        if half == 1 and not first:
                            project_out(t - 1)
                        if ahead >= 1:
                            scores(b + 1, u, (b + 1) % 2, groups)
                        if half == 0 and not first:
                            transpose_mixed(t - 1)
                    if u == 1 and ahead >= 2:
                        project_q(b + 2)
                    attend(b, t)
                    if not is_step(b, 0):
                        norm.tensor(pe, t - 2, u)

            batches(pe, batch)
            transpose_mixed(TILES - 1)
            project_out(TILES - 1)
            for u in range(TPB):
                norm.tensor(pe, TILES - TPB + u, u)

        @block.scalar
        def _(act):
            act.wait_ge(loaded, 16 * loads)
            for m in range(KD):
                for h in range(2):
                    act.wait_ge(kT_projected, 2 * m + h + 1)
                    act.activation(kT[:, m, h * halves:(h + 1) * halves], bank[:, 2 * m + h, 0:halves],
                                   ACT.Identity, bias=0.0 if key_bias else bk[:, m:m + 1]).then_inc(kT_ready, 1)

            def copy_q(b):
                act.wait_ge(q_projected, b + 1)
                wait(act, scores_ready, GROUPS * TPB * b)
                for m in range(KD):
                    act.activation(qT[:, m, :], q_bank[:, m * SEQ:(m + 1) * SEQ], ACT.Identity,
                                   bias=0.0 if key_bias else bq[:, m:m + 1]).then_inc(q_ready, 1)

            def copy_scores(t, u, groups=range(GROUPS)):
                wait(act, shifted, t - 1)
                for g in groups:
                    act.wait_ge(scores_ready, GROUPS * t + g + 1)
                    act.activation(raw[:, u, g * width:(g + 1) * width], s_bank[g % 2][:, 0:width],
                                   ACT.Copy).then_inc(scores_copied, 1)

            def exponents(t, u):
                act.wait_ge(shifted, t + 1)
                act.activation(probs[:, u, :], probs[:, u, :], ACT.Exp,
                               scale=HEAD ** -0.5).then_inc(probs_ready, 1)

            def high_probsT(t, g):
                act.wait_ge(probs_transposed, GROUPS * t + g + 1)
                wait(act, attended, t)
                act.activation(probsT[0][:, g * GROUP * P:(g + 1) * GROUP * P], p_bank[g % 2][0:KEYS, 0:GROUP * P],
                               ACT.Copy).then_inc(high_copied, 1)

            def copy_mixedT(t):
                act.wait_ge(mixed_transposed, t + 1)
                wait(act, out_ready, t)
                act.activation(mixedT[:, :, :], n_bank[:, 0:DIM].rearrange("p (k n) -> p k n", k=KD),
                               ACT.Copy).then_inc(mixedT_ready, 1)

            copy_q(0)
            act.wait_ge(v_ready, BATCH)
            act.wait_ge(ones_ready, 2)
            act.activation(v_parts[0][:, :, :], v1[:, :, :, :].rearrange("p b h d -> p b (h d)"),
                           ACT.Copy).then_inc(v_high_ready, 1)
            if not key_bias:
                for u in range(TPB):
                    copy_scores(u, u)
            copy_q(1)
            exponents(0, 0)

            def batch(b, ahead):
                for u in range(TPB):
                    t = TPB * b + u
                    for half in range(2):
                        groups = (2 * half, 2 * half + 1)
                        for g in groups:
                            high_probsT(t, g)
                        if ahead >= 1 and not key_bias:
                            copy_scores(t + TPB, u, groups)
                        if half == 0 and not is_step(t, 0):
                            copy_mixedT(t - 1)
                    if u == 1 and ahead >= 2:
                        copy_q(b + 2)
                    if ahead >= 1 or u == 0:
                        exponents(t + 1, 1 - u)
                    if feed is not None:
                        feed.high(act, b, u)
                    if not is_step(b, 0):
                        norm.scalar(act, t - 2, u)

            batches(act, batch)
            copy_mixedT(TILES - 1)
            for u in range(TPB):
                norm.scalar(act, TILES - TPB + u, u)

        @block.vector
        def _(dve):
            dve.memset(v1[:, :, :, HEAD:HEAD + 1].rearrange("p b h d -> p (b h) d"), 1.0).then_inc(ones_ready, 1)
            dve.wait_ge(loaded, 16 * loads)
            dve.memset(zeros[:, :], 0.0).then_inc(ones_ready, 1)
            dve.wait_ge(ones_ready, 2)
            if key_bias:
                dve.tensor_scalar(bias4[:, :, :], bias4[:, :, :], HEAD ** 0.5, None,
                                  ALU.mult).then_inc(bias_ready, 1)
                dve.wait_ge(bias_ready, 1)
            else:
                dve.tensor_scalar(bo[:, :], bo[:, :], chip.gate[:, gate:gate + 1], None,
                                  ALU.mult).then_inc(bias_ready, 1)
            for b in range(BATCH):
                dve.wait_ge(v_projected, b + 1)
                source = (o_bank if b % 2 == 0 else y_bank)[0:KEYS, 0:DIM].rearrange("p (h d) -> p h d", h=HEADS)
                if key_bias:
                    dve.tensor_copy(v1[:, b, :, 0:HEAD], source).then_inc(v_ready, 1)
                else:
                    dve.tensor_tensor(v1[:, b, :, 0:HEAD], source, bv[:, :].rearrange("p (h d) -> p h d", h=HEADS),
                                      ALU.add).then_inc(v_ready, 1)

            def biased_scores(b, u, groups):
                t = TPB * b + u
                wait(dve, shifted, t - 1)
                for g in groups:
                    dve.wait_ge(scores_ready, GROUPS * t + g + 1)
                    dve.tensor_tensor(
                        raw[:, u, g * width:(g + 1) * width].rearrange("p (h k) -> p h k", h=GROUP),
                        s_bank[g % 2][:, 0:width].rearrange("p (h k) -> p h k", h=GROUP),
                        bias4[:, span(b, 1), :].to_broadcast([P, GROUP, KEYS]),
                        ALU.add).then_inc(scores_copied, 1)

            def maxima(t, u):
                wait(dve, shifted, t - 1)
                dve.wait_ge(scores_copied, GROUPS * t + GROUPS)
                dve.tensor_reduce(row_max[:, u, :], raw[:, u, :].rearrange("p (h k) -> p h k", h=HEADS),
                                  AX_X, ALU.max).then_inc(max_ready, 1)

            def low_probsT(t, g):
                dve.wait_ge(high_copied, GROUPS * t + g + 1)
                at = slice(g * GROUP * P, (g + 1) * GROUP * P)
                dve.tensor_tensor(probsT[1][:, at], p_bank[g % 2][0:KEYS, 0:GROUP * P], probsT[0][:, at],
                                  ALU.subtract).then_inc(low_copied, 1)

            def update_x(t, u):
                dve.wait_ge(out_ready, t + 1)
                if not key_bias:
                    dve.wait_ge(x_biased, t + 1)
                dve.scalar_tensor_tensor(out=nth(chip.x, t), in0=y_bank[:, 0:DIM], scalar=chip.gate[:, gate:gate + 1],
                                         in1=nth(chip.x, t), op0=ALU.mult, op1=ALU.add).then_inc(norm.x_updated, 1)
                norm.vector_stats(dve, t, u)

            def normalise(t):
                attended_of = o_bank[:, 0:HEADS * (HEAD + 1)].rearrange("p (h d) -> p h d", h=HEADS)
                dve.wait_ge(attended, t + 1)
                dve.reciprocal(inverse[:, :], attended_of[:, :, HEAD:HEAD + 1].rearrange("p h d -> p (h d)")
                               ).then_inc(inverse_done, 1)
                dve.wait_ge(inverse_done, t + 1)
                wait(dve, mixed_transposed, t)
                dve.tensor_tensor(mixed[:, :].rearrange("p (h d) -> p h d", h=HEADS), attended_of[:, :, 0:HEAD],
                                  inverse[:, :].unsqueeze(2).to_broadcast([P, HEADS, HEAD]),
                                  ALU.mult).then_inc(mixed_ready, 1)

            dve.wait_ge(v_high_ready, 1)
            dve.wait_ge(v_ready, BATCH)
            dve.tensor_tensor(v_parts[1][:, :, :], v1[:, :, :, :].rearrange("p b h d -> p b (h d)"), v_parts[0][:, :, :],
                              ALU.subtract).then_inc(v_split, 1)
            for u in range(TPB):
                if key_bias:
                    biased_scores(0, u, range(GROUPS))
                maxima(u, u)

            def batch(b, ahead):
                for u in range(TPB):
                    t = TPB * b + u
                    for half in range(2):
                        groups = (2 * half, 2 * half + 1)
                        for g in groups:
                            low_probsT(t, g)
                        if half == 1 and not is_step(t, 0):
                            update_x(t - 1, 1 - u)
                        if ahead >= 1 and key_bias:
                            biased_scores(b + 1, u, groups)
                    normalise(t)
                    if not is_step(t, 0):
                        norm.vector_apply(dve, t - 1, 1 - u)
                    if ahead >= 1:
                        maxima(t + TPB, u)
                    if not is_step(t, 0):
                        norm.vector_apply_again(dve, t - 1, 1 - u)

            batches(dve, batch)
            update_x(TILES - 1, 1)
            norm.vector_apply(dve, TILES - 1, 1)
            norm.vector_apply_again(dve, TILES - 1, 1)

        @block.gpsimd
        def _(pool):
            pool.wait_ge(loaded, 16 * loads)
            if not key_bias:
                pool.wait_ge(bias_ready, 1)

            def spread_keys(b, slot):
                wait(pool, scores_ready, GROUPS * TPB * (b - 1))
                for c in range(KD):
                    at = c * CHUNK_HEADS * KEYS
                    out = (k_diag[:, slot, at:at + CHUNK_HEADS * KEYS] if isinstance(slot, int) else
                           k_diag[:, bass.ds(slot, 1), at:at + CHUNK_HEADS * KEYS].rearrange("p a n -> p (a n)"))
                    pool.tensor_tensor(out.rearrange("p (h k) -> p h k", h=CHUNK_HEADS),
                                       kT[:, c, span(b, KEYS)].unsqueeze(1).to_broadcast([P, CHUNK_HEADS, KEYS]),
                                       head_of[:, :].unsqueeze(2).to_broadcast([P, CHUNK_HEADS, KEYS]),
                                       ALU.mult).then_inc(k_diag_ready, 1)

            def shift(t, u):
                pool.wait_ge(max_ready, t + 1)
                wait(pool, probs_transposed, GROUPS * (t - 1))
                pool.tensor_tensor(probs[:, u, :].rearrange("p (h k) -> p h k", h=HEADS),
                                   raw[:, u, :].rearrange("p (h k) -> p h k", h=HEADS), row_max[:, u, :].unsqueeze(2).to_broadcast([P, HEADS, KEYS]),
                                   ALU.subtract).then_inc(shifted, 1)

            def place_values(b):
                wait(pool, attended, TPB * b)
                for part, now in zip(v_parts, v_now):
                    pool.tensor_tensor(now[:, :], nth(part, b), zeros[:, :], ALU.add).then_inc(v_placed, 1)

            pool.wait_ge(kT_ready, 2 * KD)
            spread_keys(0, 0)
            pool.wait_ge(v_split, 1)
            spread_keys(1, 1)
            for u in range(TPB):
                shift(u, u)

            def batch(b, ahead):
                for u in range(TPB):
                    t = TPB * b + u
                    if u == 0:
                        place_values(b)
                    if not key_bias:
                        pool.tensor_tensor(nth(chip.x, t), nth(chip.x, t), bo[:, :], ALU.add).then_inc(x_biased, 1)
                    if not is_step(t, 0):
                        norm.gpsimd(pool, t - 1, 1 - u)
                    if u == 0 and ahead >= 2:
                        spread_keys(b + 2, b % 2)
                    if feed is not None:
                        feed.low(pool, b, u)
                    if ahead >= 1:
                        shift(t + TPB, u)

            batches(pool, batch)
            norm.gpsimd(pool, TILES - 1, 1)


L2_HEADS, L2_HEAD = 4, 64
L2_KEYS = KEYS + SEQ
MASKED = -1e30
RMS_EPS = 1e-8
V_SLOTS = 4


def latent_attention(chip, a):
    nc = chip.nc
    gate, both = 2, 2 * DIM
    with ExitStack() as ctx:
        st = Stage(chip, "l2x", ctx)
        bank = chip.bank
        s_bank = [bank[:, 0, :], bank[:, 1, :]]
        p_bank = [bank[:, 2, :], bank[:, 3, :]]
        o_bank, q_bank, y_bank, n_bank = (bank[:, n, :] for n in (4, 5, 6, 7))
        norm = NextNorm(st, n_bank)
        w_q, w_out = st.sb("W_q", [P, KD, DIM]), st.sb("W_out", [P, KD, DIM])
        w_kv = st.sb("W_kv", [P, KD, both])
        b_out = st.sb("b_out", [P, DIM])
        context_g, context_b = st.sb("ln_x_g", [P, KD]), st.sb("ln_x_b", [P, KD])
        gammas = st.sb("gammas", [P, 2])
        gamma = st.sb("gamma", [P, 1])
        mask = st.sb("mask", [P, CTX], U8)
        mask_row = st.sb("mask_row", [P, CTX])
        mask_now = st.sb("mask_now", [P, KEYS])
        mask_one = st.sb("mask_one", [P, P])
        context = st.sb("context", [KEYS, BATCH, DIM])
        c_stats = st.sb("c_stats", [KEYS, BATCH, 6])
        c_mv = st.sb("c_mv", [KEYS, BATCH, 2])
        c_rstd = st.sb("c_rstd", [KEYS, BATCH])
        c_norm = st.sb("c_norm", [KEYS, BATCH, DIM])
        c_normT = st.sb("c_normT", [P, 2, KD, KEYS])
        c_k = st.sb("c_k", [KEYS, BATCH, DIM])
        c_square = st.sb("c_square", [KEYS, 2, DIM])
        c_rms = st.sb("c_rms", [KEYS, 3, BATCH * L2_HEADS])
        c_kT = st.sb("c_kT", [P, KD, CTX])
        c_v = st.sb("c_v", [KEYS, BATCH, DIM])
        latT = st.sb("latT", [P, KD, SEQ])
        qk = st.sb("qk", [P, TPB, both])
        square = st.sb("square", [P, both])
        rms = st.sb("rms", [P, 3, 2 * L2_HEADS])
        qT = st.sb("qT", [P, KD, SEQ])
        kT = st.sb("kT", [P, KD, L2_KEYS])
        v = st.sb("v", [P, V_SLOTS, TPB * DIM])
        probs = st.sb("probs", [P, TPB * L2_HEADS, L2_KEYS])
        probsT = st.sb("probsT", [P, TPB * L2_HEADS, 3 * P])
        neg_max = st.sb("neg_max", [P, TPB * L2_HEADS])
        total = st.sb("total", [P, TPB * L2_HEADS])
        inverse = st.sb("inverse", [P, TPB * L2_HEADS])
        mixed = st.sb("mixed", [P, TPB, DIM])
        mixedT = st.sb("mixedT", [P, TPB, KD, P])
        sem = st.sem
        context_loaded, loaded, consts_ready = sem("context_loaded"), sem("loaded"), sem("consts_ready")
        c_stats_done, c_moments_ready, c_var_eps_done = sem("c_stats_done"), sem("c_moments_ready"), sem("c_var_eps_done")
        c_rstd_ready, c_normed = sem("c_rstd_ready"), sem("c_normed")
        c_norm_transposed, c_normT_ready = sem("c_norm_transposed"), sem("c_normT_ready")
        c_kv_projected, c_k_copied, c_v_copied = sem("c_kv_projected"), sem("c_k_copied"), sem("c_v_copied")
        c_squared, c_summed, c_rooted = sem("c_squared"), sem("c_summed"), sem("c_rooted")
        c_clamped, c_k_normed = sem("c_clamped"), sem("c_k_normed")
        c_k_transposed, c_kT_ready = sem("c_k_transposed"), sem("c_kT_ready")
        latT_ready, projected, qk_copied, v_copied = sem("latT_ready"), sem("projected"), sem("qk_copied"), sem("v_copied")
        squared, summed, rooted = sem("squared"), sem("summed"), sem("rooted")
        clamped, qk_normed = sem("clamped"), sem("qk_normed")
        qk_transposed, qkT_ready, c_kT_placed = sem("qk_transposed"), sem("qkT_ready"), sem("c_kT_placed")
        scores_ready, max_ready, probs_ready = sem("scores_ready"), sem("max_ready"), sem("probs_ready")
        probs_transposed = sem("probs_transposed")
        even_copied, odd_copied = sem("even_probsT_copied"), sem("odd_probsT_copied")
        attended, sums_inverted, mixed_ready = sem("attended"), sem("sums_inverted"), sem("mixed_ready")
        mixed_transposed, mixedT_ready = sem("mixed_transposed"), sem("mixedT_ready")
        out_ready, x_biased = sem("out_ready"), sem("x_biased")
        SH = TPB * L2_HEADS
        loads = 11
        consts = 4
        block = ctx.enter_context(nc.Block())

        @block.sync
        def _(sp):
            pre = "L2_xattn_"
            sp.dma_start(context[:, :, :], a["context"].rearrange("(b k) d -> k b d", b=BATCH)).then_inc(context_loaded, 16)
            sp.dma_start(context_g[:, :], a[pre + "ln_x_g"]).then_inc(loaded, 16)
            sp.dma_start(context_b[:, :], a[pre + "ln_x_b"]).then_inc(loaded, 16)
            sp.dma_start(b_out[:, :], a[pre + "b_out"].partition_broadcast(P)).then_inc(loaded, 16)
            sp.dma_start(w_kv[:, :, :], load_rows(a[pre + "W_kv"])).then_inc(loaded, 16)
            sp.dma_start(w_q[:, :, :], load_rows(a[pre + "W_q"])).then_inc(loaded, 16)
            sp.dma_start(w_out[:, :, :], load_rows(a[pre + "W_out"])).then_inc(loaded, 16)
            for n, g in enumerate(("q_gamma", "k_gamma")):
                for r in range(0, P, L2_HEAD):
                    sp.dma_start(gammas[r:r + L2_HEAD, n:n + 1], a[pre + g]).then_inc(loaded, 16)
            sp.dma_start(mask[:, :], a["mask"].partition_broadcast(P)).then_inc(loaded, 16)

        @block.tensor
        def _(pe):
            pe.wait_ge(loaded, 16 * loads)

            turn_bank, kv_bank = p_bank, s_bank
            qk_bank = [q_bank, n_bank]

            def transpose_context(b):
                pe.wait_ge(c_normed, b + 1)
                wait(pe, c_normT_ready, b - 1)
                for k in range(KD):
                    last = pe.transpose(turn_bank[b % 2][:, k * KEYS:(k + 1) * KEYS], c_norm[:, b, k * P:(k + 1) * P],
                                        chip.ident[0:KEYS, 0:KEYS])
                last.then_inc(c_norm_transposed, 1)

            def project_context():
                transpose_context(0)
                for b in range(BATCH):
                    if b + 1 < BATCH:
                        transpose_context(b + 1)
                    pe.wait_ge(c_normT_ready, b + 1)
                    wait(pe, c_v_copied, b - 1)
                    for k in range(KD):
                        last = pe.matmul(kv_bank[b % 2][0:KEYS, :], c_normT[:, b % 2, k, :], w_kv[:, k, :],
                                         start=(k == 0), stop=(k == KD - 1))
                    last.then_inc(c_kv_projected, 1)

            def transpose_context_keys():
                for b in range(BATCH):
                    pe.wait_ge(c_k_normed, b + 1)
                    wait(pe, c_kT_ready, b - 1)
                    for k in range(KD):
                        last = pe.transpose(turn_bank[b % 2][:, k * KEYS:(k + 1) * KEYS], c_k[:, b, k * P:(k + 1) * P],
                                            chip.ident[0:KEYS, 0:KEYS])
                    last.then_inc(c_k_transposed, 1)

            def project(b, u):
                t = TPB * b + u
                if u == 0:
                    pe.wait_ge(latT_ready, b + 1)
                wait(pe, v_copied, t)
                wait(pe, qkT_ready, 2 * TPB * (b - 1) + 2)
                wait(pe, norm.x_updated, TPB * (b - 3))
                for k in range(KD):
                    pe.matmul(q_bank[:, 0:DIM], latT[:, k, u * P:(u + 1) * P], w_q[:, k, :],
                              start=(k == 0), stop=(k == KD - 1))
                for k in range(KD):
                    last = pe.matmul(y_bank[:, :], latT[:, k, u * P:(u + 1) * P], w_kv[:, k, :],
                                     start=(k == 0), stop=(k == KD - 1))
                last.then_inc(projected, 1)

            def transpose_qk(b, u):
                t = TPB * b + u
                pe.wait_ge(qk_normed, t + 1)
                if u == 0:
                    pe.wait_ge(v_copied, TPB * (b + 1))
                else:
                    wait(pe, norm.copied, TPB * (b - 2))
                for k in range(2 * KD):
                    last = pe.transpose(qk_bank[u][:, k * P:(k + 1) * P], qk[:, u, k * P:(k + 1) * P],
                                        chip.ident[:, :])
                last.then_inc(qk_transposed, 1)

            def scores(b, s):
                u, h = s // L2_HEADS, s % L2_HEADS
                if s == 0:
                    pe.wait_ge(qkT_ready, 2 * TPB * b + 2 * TPB)
                    pe.wait_ge(c_kT_placed, (KD + 1) * b + KD + 1)
                wait(pe, probs_ready, SH * b + s - 1)
                at = slice(L2_HEAD * (h % 2), L2_HEAD * (h % 2) + L2_HEAD)
                pe.matmul(s_bank[h % 2][:, 0:L2_KEYS], qT[at, h // 2, u * P:(u + 1) * P], kT[at, h // 2, :],
                          start=True, stop=False)
                pe.matmul(s_bank[h % 2][:, 0:KEYS], mask_one[at, :], mask_now[at, :],
                          start=False, stop=True).then_inc(scores_ready, 1)

            def transpose_probs(b, s):
                h = s % L2_HEADS
                copied = even_copied if h % 2 == 0 else odd_copied
                n = SH // 2 * b + s // 2
                pe.wait_ge(probs_ready, SH * b + s + 1)
                wait(pe, copied, n)
                pe.transpose(p_bank[h % 2][0:KEYS, 0:P], probs[:, s, 0:KEYS], chip.ident[:, :])
                for k in range(TPB):
                    last = pe.transpose(p_bank[h % 2][:, (k + 1) * P:(k + 2) * P],
                                        probs[:, s, KEYS + k * P:KEYS + (k + 1) * P], chip.ident[:, :])
                last.then_inc(probs_transposed, 1)

            def attend(b, s):
                u, h, slot = s // L2_HEADS, s % L2_HEADS, b % V_SLOTS
                if h == 0:
                    wait(pe, mixed_ready, TPB * b + u)
                pe.wait_ge(even_copied if h % 2 == 0 else odd_copied, SH // 2 * b + s // 2 + 1)
                out = o_bank[:, h * L2_HEAD:(h + 1) * L2_HEAD]
                pe.matmul(out, probsT[0:KEYS, s, 0:P],
                          c_v[:, span(b, 1), h * L2_HEAD:(h + 1) * L2_HEAD].rearrange("p a d -> p (a d)"),
                          start=True, stop=False)
                for k in range(TPB):
                    at = k * DIM + h * L2_HEAD
                    last = pe.matmul(out, probsT[:, s, (k + 1) * P:(k + 2) * P],
                                     v[:, slot, at:at + L2_HEAD] if isinstance(slot, int) else
                                     v[:, bass.ds(slot, 1), at:at + L2_HEAD].rearrange("p a d -> p (a d)"),
                                     start=False, stop=(k == TPB - 1))
                if h == L2_HEADS - 1:
                    last.then_inc(attended, 1)

            def transpose_mixed(b):
                pe.wait_ge(mixed_ready, TPB * b + TPB)
                for u in range(TPB):
                    for k in range(KD):
                        last = pe.transpose(n_bank[:, (KD * u + k) * P:(KD * u + k + 1) * P],
                                            mixed[:, u, k * P:(k + 1) * P], chip.ident[:, :])
                last.then_inc(mixed_transposed, 1)

            def project_out(b, u):
                t = TPB * b + u
                pe.wait_ge(mixedT_ready, b + 1)
                wait(pe, norm.x_updated, t)
                for k in range(KD):
                    last = pe.matmul(y_bank[:, 0:DIM], mixedT[:, u, k, :], w_out[:, k, :],
                                     start=(k == 0), stop=(k == KD - 1))
                last.then_inc(out_ready, 1)

            project_context()
            for u in range(TPB):
                project(0, u)
            transpose_context_keys()
            for u in range(TPB):
                transpose_qk(0, u)
            pe.wait_ge(c_kT_ready, BATCH)
            pe.wait_ge(c_v_copied, BATCH)
            pe.wait_ge(consts_ready, consts)
            for s in range(SH):
                scores(0, s)
                if s in (0, 2):
                    project(1, s // 2)
                if s == 5:
                    transpose_qk(1, 0)
            transpose_qk(1, 1)

            def batch(b, ahead):
                behind = not is_step(b, 0)
                for s in range(SH):
                    u = s // L2_HEADS
                    if ahead >= 1:
                        scores(b + 1, s)
                    transpose_probs(b, s)
                    if ahead >= 2 and s == 5:
                        transpose_qk(b + 2, 0)
                    if s > 0:
                        attend(b, s - 1)
                    if ahead >= 2 and s in (0, 2):
                        project(b + 2, s // 2)
                    if behind and s == 1:
                        transpose_mixed(b - 1)
                    if behind and s in (3, 4):
                        pe.wait_ge(v_copied, TPB * b + 3 * TPB if ahead >= 2 else TILES)
                        project_out(b - 1, s - 3)
                    if behind and s in (6, 7):
                        norm.tensor(pe, TPB * b - TPB + s - 6, s - 6)
                if ahead >= 2:
                    transpose_qk(b + 2, 1)
                attend(b, SH - 1)

            batches(pe, batch)
            wait(pe, norm.copied, TILES - TPB)
            transpose_mixed(BATCH - 1)
            for u in range(TPB):
                project_out(BATCH - 1, u)
            for u in range(TPB):
                norm.tensor(pe, TILES - TPB + u, u)

        @block.scalar
        def _(act):
            act.wait_ge(loaded, 16 * loads)
            turn_bank, kv_bank = p_bank, s_bank
            qk_bank = [q_bank, n_bank]

            def copy_context_turned(b):
                act.wait_ge(c_norm_transposed, b + 1)
                wait(act, c_kv_projected, b - 1)
                for k in range(KD):
                    last = act.activation(c_normT[:, b % 2, k, :], turn_bank[b % 2][:, k * KEYS:(k + 1) * KEYS],
                                          ACT.Identity, scale=context_g[:, k:k + 1], bias=context_b[:, k:k + 1])
                last.then_inc(c_normT_ready, 1)

            def copy_context():
                copy_context_turned(0)
                for b in range(BATCH):
                    if b + 1 < BATCH:
                        copy_context_turned(b + 1)
                    act.wait_ge(c_kv_projected, b + 1)
                    act.activation(c_k[:, b, :], kv_bank[b % 2][0:KEYS, 0:DIM], ACT.Copy).then_inc(c_k_copied, 1)
                    act.activation(c_v[:, b, :], kv_bank[b % 2][0:KEYS, DIM:both], ACT.Copy).then_inc(c_v_copied, 1)
                    act.wait_ge(c_k_copied, b + 1)
                    wait(act, c_summed, b - 1)
                    act.activation(c_square[:, b % 2, :], c_k[:, b, :], ACT.Square).then_inc(c_squared, 1)

            def copy_context_keys():
                for b in range(BATCH):
                    act.wait_ge(c_k_transposed, b + 1)
                    act.activation(c_kT[:, :, b * KEYS:(b + 1) * KEYS], turn_bank[b % 2][:, 0:KD * KEYS].rearrange(
                        "p (k n) -> p k n", k=KD), ACT.Copy).then_inc(c_kT_ready, 1)

            def latents(b):
                wait(act, projected, TPB * b)
                act.activation(latT[:, :, :], chip.xnT[:, :, span(b, SEQ)], ACT.Copy).then_inc(latT_ready, 1)

            def copy_projections(b, u):
                t, slot = TPB * b + u, b % V_SLOTS
                act.wait_ge(projected, t + 1)
                wait(act, qk_transposed, t - 1)
                wait(act, attended, TPB * (b - V_SLOTS + 1))
                act.activation(qk[:, u, 0:DIM], q_bank[:, 0:DIM], ACT.Copy).then_inc(qk_copied, 1)
                act.activation(qk[:, u, DIM:both], y_bank[:, 0:DIM], ACT.Copy).then_inc(qk_copied, 1)
                out = (v[:, slot, u * DIM:(u + 1) * DIM] if isinstance(slot, int) else
                       v[:, bass.ds(slot, 1), u * DIM:(u + 1) * DIM].rearrange("p a d -> p (a d)"))
                act.activation(out, y_bank[:, DIM:both], ACT.Copy).then_inc(v_copied, 1)
                act.wait_ge(qk_copied, 2 * t + 2)
                wait(act, summed, t)
                act.activation(square[:, :], qk[:, u, :], ACT.Square).then_inc(squared, 1)

            def place_qkT(b):
                for u in range(TPB):
                    wait(act, scores_ready, SH * b)
                    act.wait_ge(qk_transposed, TPB * b + u + 1)
                    act.activation(qT[:, :, u * P:(u + 1) * P], qk_bank[u][:, 0:KD * P].rearrange("p (k n) -> p k n", k=KD),
                                   ACT.Copy, scale=gamma[:, 0:1]).then_inc(qkT_ready, 1)
                    act.activation(kT[:, :, KEYS + u * P:KEYS + (u + 1) * P],
                                   qk_bank[u][:, KD * P:2 * KD * P].rearrange("p (k n) -> p k n", k=KD),
                                   ACT.Copy).then_inc(qkT_ready, 1)

            def exponents(b, s):
                u = s // L2_HEADS
                act.wait_ge(max_ready, SH * b + s + 1)
                wait(act, probs_transposed, SH * b - SH + s + 1)
                wait(act, sums_inverted, TPB * b - TPB + u + 1)
                act.activation(probs[:, s, :], s_bank[s % 2][:, 0:L2_KEYS], ACT.Exp, bias=neg_max[:, s:s + 1],
                               accum_out=total[:, s:s + 1]).then_inc(probs_ready, 1)

            def copy_probsT(b, s):
                act.wait_ge(probs_transposed, SH * b + s + 1)
                wait(act, attended, TPB * b - TPB + s // L2_HEADS + 1)
                act.activation(probsT[0:KEYS, s, 0:P], p_bank[0][0:KEYS, 0:P], ACT.Copy)
                act.activation(probsT[:, s, P:3 * P], p_bank[0][:, P:3 * P], ACT.Copy).then_inc(even_copied, 1)

            def copy_mixedT(b):
                act.wait_ge(mixed_transposed, b + 1)
                wait(act, out_ready, TPB * b)
                act.activation(mixedT[:, :, :, :].rearrange("p u k n -> p (u k n)"), n_bank[:, 0:TPB * DIM],
                               ACT.Copy).then_inc(mixedT_ready, 1)

            latents(0)
            copy_context()
            for u in range(TPB):
                copy_projections(0, u)
            latents(1)
            copy_context_keys()
            place_qkT(0)
            for s in range(SH):
                exponents(0, s)
                if s in (0, 2):
                    copy_projections(1, s // 2)
                if s == SH - 2:
                    latents(2)
            place_qkT(1)

            def batch(b, ahead):
                for s in range(SH):
                    if s % 2 == 0:
                        copy_probsT(b, s)
                    if ahead >= 1:
                        exponents(b + 1, s)
                    if ahead >= 2 and s in (0, 2):
                        copy_projections(b + 2, s // 2)
                    if not is_step(b, 0):
                        if s == 1:
                            copy_mixedT(b - 1)
                        if s in (6, 7):
                            norm.scalar(act, TPB * b - TPB + s - 6, s - 6)
                    if ahead >= 3 and s == SH - 2:
                        latents(b + 3)
                if ahead >= 2:
                    place_qkT(b + 2)

            batches(act, batch)
            copy_mixedT(BATCH - 1)
            for u in range(TPB):
                norm.scalar(act, TILES - TPB + u, u)

        @block.vector
        def _(dve):
            def constants():
                dve.memset(mask_one[:, :], 0.0).then_inc(consts_ready, 1)
                dve.memset(mask_row[:, :], 0.0).then_inc(consts_ready, 1)
                dve.wait_ge(consts_ready, 2)
                dve.wait_ge(loaded, 16 * loads)
                for r in range(0, P, L2_HEAD):
                    dve.memset(mask_one[r:r + 1, :], 1.0)
                    last = dve.tensor_scalar(mask_row[r:r + 1, :], mask[r:r + 1, :], 1.0, -MASKED,
                                             ALU.subtract, ALU.mult)
                last.then_inc(consts_ready, 1)
                dve.tensor_scalar(b_out[:, :], b_out[:, :], chip.gate[:, gate:gate + 1], None, ALU.mult)
                dve.scalar_tensor_tensor(out=gamma[:, :], in0=gammas[:, 0:1], scalar=L2_HEAD ** -0.5, in1=gammas[:, 1:2],
                                         op0=ALU.mult, op1=ALU.mult).then_inc(consts_ready, 1)

            def norm_context():
                dve.wait_ge(context_loaded, 16)
                for b in range(BATCH):
                    dve.bn_stats(c_stats[:, b, :], context[:, b, :]).then_inc(c_stats_done, 1)
                dve.wait_ge(c_stats_done, BATCH)
                for b in range(BATCH):
                    dve.bn_aggr(c_mv[:, b, :], c_stats[:, b, :]).then_inc(c_moments_ready, 1)
                dve.wait_ge(c_rstd_ready, 1)
                for b in range(BATCH):
                    dve.tensor_scalar(c_norm[:, b, :], context[:, b, :], c_mv[:, b, 0:1], c_rstd[:, b:b + 1],
                                      ALU.subtract, ALU.mult).then_inc(c_normed, 1)

            def norm_context_keys():
                for b in range(BATCH + 2):
                    if b < BATCH:
                        at = slice(b * L2_HEADS, (b + 1) * L2_HEADS)
                        dve.wait_ge(c_squared, b + 1)
                        dve.tensor_reduce(c_rms[:, 0, at], c_square[:, b % 2, :].rearrange("p (h d) -> p h d", h=L2_HEADS),
                                          AX_X, ALU.add).then_inc(c_summed, 1)
                        dve.wait_ge(c_summed, b + 1)
                        dve.tensor_scalar(c_rms[:, 1, at], c_rms[:, 0, at], 1 / L2_HEAD, RMS_EPS ** 2, ALU.mult,
                                          ALU.max).then_inc(c_clamped, 1)
                    if b >= 2:
                        dve.wait_ge(c_rooted, b - 1)
                        heads = c_k[:, b - 2, :].rearrange("p (h d) -> p h d", d=L2_HEAD)
                        roots = c_rms[:, 2, (b - 2) * L2_HEADS:(b - 1) * L2_HEADS]
                        dve.tensor_tensor(heads, heads, roots.unsqueeze(2).to_broadcast([KEYS, L2_HEADS, L2_HEAD]),
                                          ALU.mult).then_inc(c_k_normed, 1)

            def rms_sums(b, u):
                t = TPB * b + u
                dve.wait_ge(squared, t + 1)
                dve.tensor_reduce(rms[:, 0, :], square[:, :].rearrange("p (h d) -> p h d", h=2 * L2_HEADS),
                                  AX_X, ALU.add).then_inc(summed, 1)
                dve.wait_ge(summed, t + 1)
                dve.tensor_scalar(rms[:, 1, :], rms[:, 0, :], 1 / L2_HEAD, RMS_EPS ** 2, ALU.mult,
                                  ALU.max).then_inc(clamped, 1)

            def rms_norm(b, u):
                heads = qk[:, u, :].rearrange("p (h d) -> p h d", h=2 * L2_HEADS)
                dve.wait_ge(rooted, TPB * b + u + 1)
                dve.tensor_tensor(heads, heads,
                                  rms[:, 2, :].unsqueeze(2).to_broadcast([P, 2 * L2_HEADS, L2_HEAD]),
                                  ALU.mult).then_inc(qk_normed, 1)

            def maximum(b, s):
                dve.wait_ge(scores_ready, SH * b + s + 1)
                wait(dve, probs_ready, SH * b + s + 1 - SH)
                dve.tensor_reduce(neg_max[:, s:s + 1], s_bank[s % 2][:, 0:L2_KEYS], AX_X, ALU.max,
                                  negate=True).then_inc(max_ready, 1)

            def copy_probsT(b, s):
                dve.wait_ge(probs_transposed, SH * b + s + 1)
                wait(dve, attended, TPB * b - TPB + s // L2_HEADS + 1)
                dve.tensor_copy(probsT[0:KEYS, s, 0:P], p_bank[1][0:KEYS, 0:P])
                dve.tensor_copy(probsT[:, s, P:3 * P], p_bank[1][:, P:3 * P]).then_inc(odd_copied, 1)

            def invert_sums(b):
                wait(dve, mixed_ready, TPB * b)
                for u in range(TPB):
                    at = slice(u * L2_HEADS, (u + 1) * L2_HEADS)
                    dve.wait_ge(probs_ready, SH * b + (u + 1) * L2_HEADS)
                    dve.reciprocal(inverse[:, at], total[:, at]).then_inc(sums_inverted, 1)

            def normalise(b, u):
                t = TPB * b + u
                at = slice(u * L2_HEADS, (u + 1) * L2_HEADS)
                dve.wait_ge(sums_inverted, t + 1)
                dve.wait_ge(attended, t + 1)
                wait(dve, mixed_transposed, b)
                dve.tensor_tensor(mixed[:, u, :].rearrange("p (h d) -> p h d", h=L2_HEADS),
                                  o_bank[:, 0:DIM].rearrange("p (h d) -> p h d", h=L2_HEADS),
                                  inverse[:, at].unsqueeze(2).to_broadcast([P, L2_HEADS, L2_HEAD]),
                                  ALU.mult).then_inc(mixed_ready, 1)

            def update_x(t, u):
                dve.wait_ge(out_ready, t + 1)
                dve.wait_ge(x_biased, t + 1)
                dve.scalar_tensor_tensor(out=nth(chip.x, t), in0=y_bank[:, 0:DIM], scalar=chip.gate[:, gate:gate + 1],
                                         in1=nth(chip.x, t), op0=ALU.mult, op1=ALU.add).then_inc(norm.x_updated, 1)
                norm.vector_stats(dve, t, u)

            norm_context()
            constants()
            norm_context_keys()
            for u in range(TPB):
                rms_sums(0, u)
                rms_norm(0, u)
            for s in range(SH):
                maximum(0, s)
                if s in (4, 6):
                    rms_norm(1, s // 2 - 2)
                if s in (2, 4):
                    rms_sums(1, s // 2 - 1)

            def batch(b, ahead):
                invert_sums(b)
                for s in range(SH):
                    if ahead >= 1:
                        maximum(b + 1, s)
                    if s % 2 == 1:
                        copy_probsT(b, s)
                    if s == L2_HEADS:
                        normalise(b, 0)
                    if ahead >= 2 and s in (4, 6):
                        rms_norm(b + 2, s // 2 - 2)
                    if not is_step(b, 0):
                        if s in (3, 4):
                            update_x(TPB * b - TPB + s - 3, s - 3)
                        if s in (5, 6):
                            norm.vector_apply(dve, TPB * b - TPB + s - 5, s - 5)
                    if ahead >= 2 and s in (2, 4):
                        rms_sums(b + 2, s // 2 - 1)
                normalise(b, 1)

            batches(dve, batch)
            for u in range(TPB):
                update_x(TILES - TPB + u, u)
            for u in range(TPB):
                norm.vector_apply(dve, TILES - TPB + u, u)

        @block.gpsimd
        def _(pool):
            def root(sums, ready, count, done):
                pool.wait_ge(ready, count)
                pool.tensor_tensor(sums[:, 2, :], sums[:, 1, :],
                                   chip.powers[0:sums.shape[0], 0:1].to_broadcast([sums.shape[0], sums.shape[2]]),
                                   ALU.pow).then_inc(done, 1)

            def scale_context():
                pool.wait_ge(c_moments_ready, BATCH)
                pool.tensor_tensor(c_rstd[:, :], c_mv[:, :, 1:2].rearrange("p b n -> p (b n)"),
                                   chip.powers[0:KEYS, 1:2].to_broadcast([KEYS, BATCH]), ALU.add).then_inc(c_var_eps_done, 1)
                pool.wait_ge(c_var_eps_done, 1)
                pool.tensor_tensor(c_rstd[:, :], c_rstd[:, :], chip.powers[0:KEYS, 0:1].to_broadcast([KEYS, BATCH]),
                                   ALU.pow).then_inc(c_rstd_ready, 1)
                for b in range(BATCH):
                    root(c_rms[:, :, b * L2_HEADS:(b + 1) * L2_HEADS], c_clamped, b + 1, c_rooted)

            def place_context(b):
                wait(pool, scores_ready, SH * b)
                for k in range(KD):
                    pool.tensor_copy(kT[:, k, 0:KEYS], c_kT[:, k, span(b, KEYS)]).then_inc(c_kT_placed, 1)
                pool.tensor_copy(mask_now[:, :], mask_row[:, span(b, KEYS)]).then_inc(c_kT_placed, 1)

            scale_context()
            pool.wait_ge(loaded, 16 * loads)
            pool.wait_ge(consts_ready, consts)
            for b in range(2):
                for u in range(TPB):
                    root(rms, clamped, TPB * b + u + 1, rooted)
                if b == 0:
                    pool.wait_ge(c_kT_ready, BATCH)
                place_context(b)

            def batch(b, ahead):
                for u in range(TPB):
                    t = TPB * b + u
                    pool.tensor_tensor(nth(chip.x, t), nth(chip.x, t), b_out[:, :],
                                       ALU.add).then_inc(x_biased, 1)
                if ahead >= 2:
                    root(rms, clamped, TPB * b + 2 * TPB + 1, rooted)
                if not is_step(b, 0):
                    for u in range(TPB):
                        norm.gpsimd(pool, TPB * b - TPB + u, u)
                if ahead >= 2:
                    root(rms, clamped, TPB * b + 2 * TPB + 2, rooted)
                    place_context(b + 2)

            batches(pool, batch)
            for u in range(TPB):
                norm.gpsimd(pool, TILES - TPB + u, u)


class Chain:

    def __init__(self, eng, sem):
        self.eng, self.sem, self.count = eng, sem, 0

    def __call__(self, instruction):
        self.count += 1
        instruction.then_inc(self.sem, 1)
        self.eng.wait_ge(self.sem, self.count)


class Feed:

    def __init__(self, st, dram, high, low, chunk, name=""):
        self.dram, self.high_part, self.low_part, self.chunk = dram, high, low, chunk
        self.chunks = dram.shape[1] // chunk
        self.staging = st.sb(f"{name}staging", [P, 2, chunk])
        self.loaded = [st.sem(f"{name}weights_loaded{u}") for u in range(2)]
        self.high_ready = st.sem(f"{name}high_ready")
        self.low_ready = st.sem(f"{name}low_ready")

    def sync(self, sp, i, u):
        c = 2 * i + u
        wait(sp, self.low_ready, c - 1)
        sp.dma_start(self.staging[:, u, :], self.dram[:, span(c, self.chunk)]).then_inc(self.loaded[u], 16)

    def sync_all(self, sp):
        pairs(sp, self.chunks, lambda i, u: self.sync(sp, i, u))

    def high(self, act, i, u):
        c = 2 * i + u
        act.wait_ge(self.loaded[u], 16 * i + 16)
        act.activation(self.high_part[:, span(c, self.chunk)], self.staging[:, u, :],
                       ACT.Copy).then_inc(self.high_ready, 1)

    def low(self, eng, i, u):
        c = 2 * i + u
        eng.wait_ge(self.high_ready, c + 1)
        eng.tensor_tensor(self.low_part[:, span(c, self.chunk)], self.staging[:, u, :],
                          self.high_part[:, span(c, self.chunk)], ALU.subtract).then_inc(self.low_ready, 1)


def pairs(eng, n, body):
    def pair(i):
        for u in range(2):
            body(i, u)
    steps(eng, n // 2, pair)


def feed_alone(chip, dram, high, low, chunk, name):
    with ExitStack() as ctx:
        st = Stage(chip, name, ctx)
        feed = Feed(st, dram, high, low, chunk)
        block = ctx.enter_context(chip.nc.Block())

        @block.sync
        def _(sp):
            pairs(sp, feed.chunks, lambda i, u: feed.sync(sp, i, u))

        @block.scalar
        def _(act):
            pairs(act, feed.chunks, lambda i, u: feed.high(act, i, u))

        @block.vector
        def _(dve):
            pairs(dve, feed.chunks, lambda i, u: feed.low(dve, i, u))


def gate_logits(pe, chip, weights, out, ready):
    for t in range(TILES):
        for k in range(KD):
            last = pe.matmul(out[:, t * EXPERTS:(t + 1) * EXPERTS], chip.xnT[:, k, t * P:(t + 1) * P],
                             weights[:, k, :], start=(k == 0), stop=(k == KD - 1))
    last.then_inc(ready, 1)


def wide(column):
    return column[:, :].unsqueeze(2).to_broadcast([P, TILES, EXPERTS])


def tall(row):
    return row[:, :].unsqueeze(1).to_broadcast([P, TILES, EXPERTS])


def pick_largest(dve, chain, values, order, picked, work, column):
    chain(dve.tensor_reduce(column[:, :], values[:, :, :], AX_X, ALU.max))
    chain(dve.tensor_tensor(work[:, :, :], values[:, :, :], wide(column), ALU.is_equal))
    chain(dve.tensor_tensor(work[:, :, :], work[:, :, :], tall(order), ALU.mult))
    chain(dve.tensor_reduce(column[:, :], work[:, :, :], AX_X, ALU.min))
    chain(dve.tensor_tensor(picked[:, :, :], tall(order), wide(column), ALU.is_equal))


HIDE = 1e30


def relu_square_experts(chip, a):
    nc = chip.nc
    gate = 4 + 2
    with ExitStack() as ctx:
        st = Stage(chip, "l2f", ctx)
        bank = chip.bank
        norm = NextNorm(st, bank[:, 7, :], depth=4)
        sb, sem = st.sb, st.sem
        ws1, ws2, wr = sb("Ws1", [P, KD, P]), sb("Ws2", [P, DIM]), sb("Wr", [P, KD, EXPERTS])
        order, ones = sb("order", [P, EXPERTS]), sb("ones", [P, P])
        logits, rest, work = (sb(n, [P, TILES, EXPERTS]) for n in ("logits", "rest", "work"))
        first, prob = sb("first", [P, TILES, EXPERTS]), sb("prob", [P, TILES, EXPERTS])
        top, second, column = (sb(n, [P, TILES]) for n in ("top", "second", "column"))
        used, count = sb("used", [P, 1]), sb("count", [1, 1], I32)
        blocks, width = 4, 512
        per = width // P
        r, h = sb("r", [P, width]), sb("h", [P, width])
        s_r, s_h = sb("shared_r", [P, blocks, width]), sb("shared_h", [P, blocks, width])
        w1, w2 = sb("W1", [P, KD, P]), sb("W2", [P, DIM])
        loaded, logits_ready, routed, chained = sem("loaded"), sem("logits_ready"), sem("routed"), sem("chained")
        exp_ready, exp_wanted, counted, count_ready = sem("exp_ready"), sem("exp_wanted"), sem("counted"), sem("count_ready")
        hidden_ready, relu_ready, squared, out_ready = (sem(n) for n in (
            "hidden_ready", "relu_ready", "squared", "out_ready"))

        with nc.Block() as block:
            @block.sync
            def _(sp):
                sp.dma_start(wr[:, :, :], load_rows(a["L2_ffn_Wr"])).then_inc(loaded, 16)
                sp.dma_start(order[:, :], a["order"].partition_broadcast(P)).then_inc(loaded, 16)
                sp.dma_start(ws1[:, :, :], load_rows(a["L2_ffn_Ws1"])).then_inc(loaded, 16)
                sp.dma_start(ws2[:, :], a["L2_ffn_Ws2"]).then_inc(loaded, 16)

            @block.tensor
            def _(pe):
                pe.wait_ge(loaded, 64)
                gate_logits(pe, chip, wr, bank[:, 0, :], logits_ready)
                for n in range(blocks):
                    for k in range(KD):
                        last = pe.matmul(bank[:, 4 + n, :], ws1[:, k, :], chip.xnT[:, k, span(n, width)],
                                         start=(k == 0), stop=(k == KD - 1))
                    last.then_inc(hidden_ready, 1)
                pe.wait_ge(routed, 1)
                pe.matmul(bank[:, 1, 0:1], ones[:, :], used[:, :], start=True, stop=True).then_inc(counted, 1)
                pe.wait_ge(relu_ready, blocks)

                def results(n):
                    pe.wait_ge(squared, n + 1)
                    for j in range(per):
                        wait(pe, norm.x_updated, per * (n - 1) + j + 1)
                        hidden = s_h[:, n, j * P:(j + 1) * P]
                        pe.matmul(bank[:, 4 + j, 0:DIM], hidden, ws2[:, :], start=True, stop=True).then_inc(out_ready, 1)
                for n in range(blocks):
                    results(n)

            @block.scalar
            def _(act):
                act.wait_ge(exp_wanted, 1)
                act.activation(second[:, :], second[:, :], ACT.Exp).then_inc(exp_ready, 1)
                for n in range(blocks):
                    act.wait_ge(hidden_ready, n + 1)
                    act.activation(s_r[:, n, :], bank[:, 4 + n, :], ACT.Relu).then_inc(relu_ready, 1)

            @block.gpsimd
            def _(pool):
                for n in range(blocks):
                    pool.wait_ge(relu_ready, n + 1)
                    pool.tensor_tensor(s_h[:, n, :], s_r[:, n, :], s_r[:, n, :], ALU.mult).then_inc(squared, 1)

            @block.vector
            def _(dve):
                chain = Chain(dve, chained)
                chain(dve.memset(ones[:, :], 1.0))
                dve.wait_ge(loaded, 64)
                dve.wait_ge(logits_ready, 1)
                chain(dve.tensor_copy(logits[:, :, :], bank[:, 0, 0:TILES * EXPERTS].rearrange(
                    "p (t e) -> p t e", t=TILES)))
                pick_largest(dve, chain, logits, order, first, work, column)
                chain(dve.tensor_reduce(top[:, :], logits[:, :, :], AX_X, ALU.max))
                chain(dve.scalar_tensor_tensor(out=rest[:, :, :], in0=first[:, :, :], scalar=-HIDE, in1=logits[:, :, :],
                                               op0=ALU.mult, op1=ALU.add))
                chain(dve.tensor_reduce(second[:, :], rest[:, :, :], AX_X, ALU.max))
                chain(dve.tensor_tensor(second[:, :], second[:, :], top[:, :], ALU.subtract))
                dve.sem_inc(exp_wanted, 1)
                dve.wait_ge(exp_ready, 1)
                chain(dve.tensor_scalar(second[:, :], second[:, :], 1.0, None, ALU.add))
                chain(dve.reciprocal(second[:, :], second[:, :]))
                chain(dve.tensor_scalar(second[:, :], second[:, :], 1.0, None, ALU.is_ge))
                chain(dve.tensor_tensor(prob[:, :, :], first[:, :, :], wide(second), ALU.mult))
                dve.tensor_reduce(used[:, :], second[:, :], AX_X, ALU.add).then_inc(routed, 1)
                chain(dve.tensor_scalar(prob[:, :, :], prob[:, :, :], chip.gate[:, gate:gate + 1], None, ALU.mult))
                dve.wait_ge(counted, 1)
                dve.tensor_copy(count[:, :], bank[0:1, 1, 0:1]).then_inc(count_ready, 1)

                def add(n):
                    for j in range(per):
                        t = per * n + j
                        dve.wait_ge(out_ready, t + 1)
                        dve.scalar_tensor_tensor(out=nth(chip.x, t), in0=bank[:, 4 + j, 0:DIM],
                                                 scalar=chip.gate[:, gate:gate + 1], in1=nth(chip.x, t), op0=ALU.mult,
                                                 op1=ALU.add).then_inc(norm.x_updated, 1)
                steps(dve, blocks, add)

        w_loaded, w_used, h_ready, r_ready, h2_ready = (sem(n) for n in (
            "w_loaded", "w_used", "h_ready", "r_ready", "h2_ready"))
        y_ready, added = sem("y_ready"), sem("added")

        def if_routed(eng, body):
            n = eng.value_load(count[0:1, 0:1])
            with eng.If(n != 0):
                body()

        with nc.Block() as block:
            @block.sync
            def _(sp):
                def body():
                    def expert(e):
                        wait(sp, added, TILES * e)
                        sp.dma_start(w1[:, :, :].rearrange("p k n -> p (k n)"),
                                     nth_row(a["L2_ffn_W1"], e)).then_inc(w_loaded, 16)
                        sp.dma_start(w2[:, :], nth_row(a["L2_ffn_W2"], e)).then_inc(w_loaded, 16)
                    steps(sp, EXPERTS, expert)
                if_routed(sp, body)

            @block.tensor
            def _(pe):
                def body():
                    def expert(e):
                        pe.wait_ge(w_loaded, 32 * e + 32)
                        for n in range(blocks):
                            wait(pe, h2_ready, blocks * e + n)
                            for k in range(KD):
                                last = pe.matmul(bank[:, 0, :], w1[:, k, :], chip.xnT[:, k, n * width:(n + 1) * width],
                                                 start=(k == 0), stop=(k == KD - 1))
                            last.then_inc(h_ready, 1)
                            pe.wait_ge(h2_ready, blocks * e + n + 1)
                            for j in range(per):
                                wait(pe, added, TILES * e + n * per + j)
                                pe.matmul(bank[:, 1, 0:DIM], h[:, j * P:(j + 1) * P], w2[:, :], start=True,
                                          stop=True).then_inc(y_ready, 1)
                    steps(pe, EXPERTS, expert)
                if_routed(pe, body)

            @block.scalar
            def _(act):
                def body():
                    def expert(e):
                        for n in range(blocks):
                            act.wait_ge(h_ready, blocks * e + n + 1)
                            wait(act, h2_ready, blocks * e + n)
                            act.activation(r[:, :], bank[:, 0, :], ACT.Relu).then_inc(r_ready, 1)
                    steps(act, EXPERTS, expert)
                if_routed(act, body)

            @block.vector
            def _(dve):
                def body():
                    def expert(e):
                        for n in range(blocks):
                            dve.wait_ge(r_ready, blocks * e + n + 1)
                            wait(dve, y_ready, TILES * e + n * per)
                            dve.tensor_tensor(h[:, :], r[:, :], r[:, :], ALU.mult).then_inc(h2_ready, 1)
                            for j in range(per):
                                t = n * per + j
                                dve.wait_ge(y_ready, TILES * e + t + 1)
                                share = prob[:, t, e:e + 1] if isinstance(e, int) else prob[:, t, bass.ds(e, 1)]
                                dve.scalar_tensor_tensor(out=chip.x[:, t, :], in0=bank[:, 1, 0:DIM], scalar=share,
                                                         in1=chip.x[:, t, :], op0=ALU.mult,
                                                         op1=ALU.add).then_inc(added, 1)
                    steps(dve, EXPERTS, expert)
                if_routed(dve, body)

        with nc.Block() as block:
            def groups(eng, *bodies):
                def group(n):
                    for body in bodies:
                        for u in range(norm.depth):
                            body(eng, norm.depth * n + u, u)
                steps(eng, TILES // norm.depth, group)

            @block.tensor
            def _(pe):
                groups(pe, norm.tensor)

            @block.scalar
            def _(act):
                groups(act, norm.scalar)

            @block.gpsimd
            def _(pool):
                groups(pool, norm.gpsimd)

            @block.vector
            def _(dve):
                groups(dve, norm.vector_stats, norm.vector_apply)


def nth_row(dram, i):
    if isinstance(i, int):
        return dram[i]
    return dram[bass.ds(i, 1), :, :].rearrange("a p m -> p (a m)")


def linear_experts(chip, a, high, low):
    nc = chip.nc
    gate = 4 + 3
    with ExitStack() as ctx:
        st = Stage(chip, "l3f", ctx)
        bank = chip.bank
        sb, sem = st.sb, st.sem
        x_high, x_low = (sb(n, [P, KD, TOKENS], BF16) for n in ("x_high", "x_low"))
        wg, bg, be = sb("Wg", [P, KD, EXPERTS]), sb("bg", [P, EXPERTS]), sb("be", [EXPERTS, DIM])
        order = sb("order", [P, EXPERTS])
        gates, rest, work = (sb(n, [P, TILES, EXPERTS]) for n in ("gates", "rest", "work"))
        first, second = (sb(n, [P, TILES, EXPERTS]) for n in ("first", "second"))
        column = sb("column", [P, TILES])
        share = sb("share", [P, 2, EXPERTS])
        shareT = sb("shareT", [EXPERTS, P])
        total = sb("total", [P, 2, DIM])
        loaded, logits_ready, chained = sem("loaded"), sem("logits_ready"), sem("chained")
        exp_wanted, exp_ready, gates_ready = sem("exp_wanted"), sem("exp_ready"), sem("gates_ready")
        x_high_ready, x_split = sem("x_high_ready"), sem("x_split")
        share_ready, share_transposed, shareT_ready = sem("share_ready"), sem("share_transposed"), sem("shareT_ready")
        bias_ready, experts_ready, added, x_done = sem("bias_ready"), sem("experts_ready"), sem("added"), sem("x_done")
        passed = sem("passed")
        halves = EXPERTS // 2
        block = ctx.enter_context(nc.Block())

        @block.sync
        def _(sp):
            sp.dma_start(wg[:, :, :], load_rows(a["L3_ffn_Wg"])).then_inc(loaded, 16)
            sp.dma_start(bg[:, :], a["L3_ffn_bg"].partition_broadcast(P)).then_inc(loaded, 16)
            sp.dma_start(be[:, :], a["L3_ffn_be"]).then_inc(loaded, 16)
            sp.dma_start(order[:, :], a["order"].partition_broadcast(P)).then_inc(loaded, 16)

        @block.tensor
        def _(pe):
            pe.wait_ge(loaded, 64)
            gate_logits(pe, chip, wg, bank[:, 0, :], logits_ready)
            pe.wait_ge(x_split, KD)
            pe.wait_ge(gates_ready, 1)

            def step(i):
                for u in range(2):
                    t = 2 * i + u
                    pe.wait_ge(share_ready, t + 1)
                    wait(pe, shareT_ready, t)
                    pe.transpose(bank[0:EXPERTS, 4, 0:P], share[:, u, :], chip.ident[:, :]).then_inc(share_transposed, 1)
                    for j in range(halves):
                        wait(pe, added, EXPERTS * t - EXPERTS + 2 * j + 2)
                        n = 0
                        for left, right in ((x_high, high), (x_low, high), (x_high, low)):
                            for k in range(KD):
                                n += 1
                                at = k * EXPERTS * DIM + 2 * j * DIM
                                last = pe.matmul(bank[:, j, :], left[:, k, span(t, P)], right[:, at:at + 2 * DIM],
                                                 start=(n == 1), stop=(n == 3 * KD))
                        last.then_inc(experts_ready, 1)
                    pe.wait_ge(shareT_ready, t + 1)
                    wait(pe, x_done, t)
                    pe.matmul(bank[:, 5, 0:DIM], shareT[:, :], be[:, :], start=True, stop=True).then_inc(bias_ready, 1)

            steps(pe, TILES // 2, step)

        @block.scalar
        def _(act):
            for k in range(KD):
                act.activation(x_high[:, k, :], chip.xnT[:, k, :], ACT.Copy).then_inc(x_high_ready, 1)
            act.wait_ge(exp_wanted, 1)
            act.activation(gates[:, :, :], gates[:, :, :], ACT.Exp).then_inc(exp_ready, 1)

            def copy_share(t, u):
                wait(act, added, EXPERTS * (t - 1))
                wait(act, share_transposed, t - 1)
                act.activation(share[:, u, :], nth(gates, t), ACT.Copy).then_inc(share_ready, 1)

            act.wait_ge(gates_ready, 1)
            copy_share(0, 0)

            def step(i):
                for u in range(2):
                    t = 2 * i + u
                    if not (u == 1 and is_step(i, TILES // 2 - 1)):
                        copy_share(t + 1, 1 - u)
                    act.wait_ge(share_transposed, t + 1)
                    wait(act, bias_ready, t)
                    act.activation(shareT[:, :], bank[0:EXPERTS, 4, 0:P], ACT.Copy).then_inc(shareT_ready, 1)
            steps(act, TILES // 2, step)

        @block.vector
        def _(dve):
            chain = Chain(dve, chained)
            dve.wait_ge(loaded, 64)
            dve.wait_ge(logits_ready, 1)
            chain(dve.tensor_tensor(gates[:, :, :], bank[:, 0, 0:TILES * EXPERTS].rearrange(
                "p (t e) -> p t e", t=TILES), tall(bg), ALU.add))
            chain(dve.tensor_reduce(column[:, :], gates[:, :, :], AX_X, ALU.max))
            chain(dve.tensor_tensor(gates[:, :, :], gates[:, :, :], wide(column), ALU.subtract))
            dve.sem_inc(exp_wanted, 1)
            for k in range(KD):
                dve.wait_ge(x_high_ready, k + 1)
                dve.tensor_tensor(x_low[:, k, :], chip.xnT[:, k, :], x_high[:, k, :], ALU.subtract).then_inc(x_split, 1)
            dve.wait_ge(exp_ready, 1)
            chain(dve.tensor_reduce(column[:, :], gates[:, :, :], AX_X, ALU.add))
            chain(dve.reciprocal(column[:, :], column[:, :]))
            chain(dve.tensor_tensor(gates[:, :, :], gates[:, :, :], wide(column), ALU.mult))
            pick_largest(dve, chain, gates, order, first, work, column)
            chain(dve.scalar_tensor_tensor(out=rest[:, :, :], in0=first[:, :, :], scalar=-HIDE, in1=gates[:, :, :],
                                           op0=ALU.mult, op1=ALU.add))
            pick_largest(dve, chain, rest, order, second, work, column)
            chain(dve.tensor_tensor(first[:, :, :], first[:, :, :], second[:, :, :], ALU.add))
            chain(dve.tensor_tensor(gates[:, :, :], gates[:, :, :], first[:, :, :], ALU.mult))
            chain(dve.tensor_reduce(column[:, :], gates[:, :, :], AX_X, ALU.add))
            chain(dve.reciprocal(column[:, :], column[:, :]))
            chain(dve.tensor_scalar(column[:, :], column[:, :], chip.gate[:, gate:gate + 1], None, ALU.mult))
            chain(dve.tensor_tensor(gates[:, :, :], gates[:, :, :], wide(column), ALU.mult))
            dve.sem_inc(gates_ready, 1)

            def step(i):
                for u in range(2):
                    t = 2 * i + u
                    dve.wait_ge(share_ready, t + 1)
                    for e in range(EXPERTS):
                        j = e // 2
                        if e % 2 == 0:
                            dve.wait_ge(experts_ready, halves * t + j + 1)
                        source = bank[:, j, (e % 2) * DIM:(e % 2 + 1) * DIM]
                        if e == 0:
                            wait(dve, x_done, t - 1)
                            dve.tensor_scalar(total[:, u, :], source, share[:, u, 0:1], None,
                                              ALU.mult).then_inc(added, 1)
                        else:
                            dve.wait_ge(added, EXPERTS * t + e)
                            dve.scalar_tensor_tensor(out=total[:, u, :], in0=source, scalar=share[:, u, e:e + 1],
                                                     in1=total[:, u, :], op0=ALU.mult, op1=ALU.add).then_inc(added, 1)
                    dve.wait_ge(added, EXPERTS * t + EXPERTS)
                    dve.tensor_tensor(nth(chip.x, t), nth(chip.x, t), total[:, u, :], ALU.add).then_inc(passed, 1)
                    dve.wait_ge(passed, t + 1)
                    dve.wait_ge(bias_ready, t + 1)
                    dve.tensor_tensor(nth(chip.x, t), bank[:, 5, 0:DIM], nth(chip.x, t), ALU.add).then_inc(x_done, 1)
            steps(dve, TILES // 2, step)


class Scratch:

    def __init__(self, nc, name, slots):
        self.tiles = slots // P
        self.rows = nc.dram_tensor(f"{name}_rows", [slots, DIM], F32, kind="Internal").ap()
        self.results = nc.dram_tensor(f"{name}_results", [slots, DIM], F32, kind="Internal").ap()


def slot_tiles(picks):
    return picks * TILES + EXPERTS


class Sorting:

    def __init__(self, st, picks):
        self.picks, self.tiles = picks, slot_tiles(picks)
        sb, sem = st.sb, st.sem
        self.chosen = sb("chosen", [P, TILES, EXPERTS])
        self.chosen_sum = sb("chosen_sum", [P, EXPERTS])
        self.tri, self.ones = sb("tri", [P, P]), sb("ones", [P, P])
        self.starts = sb("starts", [P, TILES])
        self.before = sb("before", [P, EXPERTS, EXPERTS])
        self.numbers = sb("numbers", [P, self.tiles])
        self.counts = sb("counts", [P, EXPERTS])
        self.more = sb("more", [P, EXPERTS, TILES])
        self.tiles_of = sb("tiles_of", [P, EXPERTS])
        self.begin = sb("begin", [P, EXPERTS])
        self.place = sb("place", [P, TILES, EXPERTS])
        self.own = sb("own", [P, TILES, EXPERTS]) if picks > 1 else self.place
        self.position = sb("position", [P, TILES])
        self.slot = [sb(f"slot{k}", [P, TILES], I32) for k in range(picks)]
        self.ended = sb("ended", [P, self.tiles, EXPERTS])
        self.expert = sb("expert", [P, self.tiles])
        self.expert_of = sb("expert_of", [P, self.tiles], I32)
        self.loaded, self.chosen_ready, self.ranked = sem("sort_loaded"), sem("chosen_ready"), sem("ranked")
        self.slots_ready = sem("slots_ready")
        self.loads = 4

    def sync(self, sp, a):
        sp.dma_start(self.tri[:, :], a["tri"]).then_inc(self.loaded, 16)
        sp.dma_start(self.starts[:, :], a["starts"].partition_broadcast(P)).then_inc(self.loaded, 16)
        sp.dma_start(self.before[:, :, :].rearrange("p a b -> p (a b)"),
                     a["before"].partition_broadcast(P)).then_inc(self.loaded, 16)
        sp.dma_start(self.numbers[:, :], a["numbers"][0:self.tiles].partition_broadcast(P)).then_inc(self.loaded, 16)

    def tensor(self, pe, rank_bank, count_bank):
        pe.wait_ge(self.loaded, 16 * self.loads)
        pe.wait_ge(self.chosen_ready, 1)
        every = self.chosen[:, :, :].rearrange("p t e -> p (t e)")
        width = TILES * EXPERTS
        pe.matmul(rank_bank[:, 0:width], self.tri[:, :], every, start=True, stop=False)
        for s in range(1, TILES):
            pe.matmul(rank_bank[:, s * EXPERTS:width], self.ones[:, :], every[:, 0:width - s * EXPERTS],
                      start=False, stop=(s == TILES - 1))
        pe.matmul(count_bank[:, 0:EXPERTS], self.ones[:, :], self.chosen_sum[:, :], start=True,
                  stop=True).then_inc(self.ranked, 1)

    def vector(self, dve, chain, masks, rank_bank, count_bank):
        chain(dve.memset(self.ones[:, :], 1.0))
        if self.picks == 1:
            chain(dve.tensor_copy(self.chosen[:, :, :], masks[0][:, :, :]))
        else:
            chain(dve.tensor_tensor(self.chosen[:, :, :], masks[0][:, :, :], masks[1][:, :, :], ALU.add))
        chain(dve.tensor_reduce(self.chosen_sum[:, :], self.chosen[:, :, :].rearrange("p t e -> p e t"),
                                AX_X, ALU.add))
        dve.sem_inc(self.chosen_ready, 1)
        dve.wait_ge(self.loaded, 16 * self.loads)
        dve.wait_ge(self.ranked, 1)
        chain(dve.tensor_copy(self.counts[:, :], count_bank[:, 0:EXPERTS]))
        shape = [P, EXPERTS, TILES]
        chain(dve.tensor_tensor(self.more[:, :, :], self.counts[:, :].unsqueeze(2).to_broadcast(shape),
                                self.starts[:, :].unsqueeze(1).to_broadcast(shape), ALU.is_gt))
        chain(dve.tensor_reduce(self.tiles_of[:, :], self.more[:, :, :], AX_X, ALU.add))
        chain(dve.tensor_tensor(self.before[:, :, :], self.before[:, :, :],
                                self.tiles_of[:, :].unsqueeze(1).to_broadcast([P, EXPERTS, EXPERTS]), ALU.mult))
        chain(dve.tensor_reduce(self.begin[:, :], self.before[:, :, :], AX_X, ALU.add))
        chain(dve.tensor_scalar(self.counts[:, :], self.begin[:, :], float(P), None, ALU.mult))
        chain(dve.tensor_tensor(self.place[:, :, :], rank_bank[:, 0:TILES * EXPERTS].rearrange(
            "p (t e) -> p t e", t=TILES), tall(self.counts), ALU.add))
        for k in range(self.picks):
            chain(dve.tensor_tensor(self.own[:, :, :], self.place[:, :, :], masks[k][:, :, :], ALU.mult))
            chain(dve.tensor_reduce(self.position[:, :], self.own[:, :, :], AX_X, ALU.add))
            chain(dve.tensor_copy(self.slot[k][:, :], self.position[:, :]))
        dve.sem_inc(self.slots_ready, 1)
        chain(dve.tensor_tensor(self.begin[:, :], self.begin[:, :], self.tiles_of[:, :], ALU.add))
        shape = [P, self.tiles, EXPERTS]
        chain(dve.tensor_tensor(self.ended[:, :, :], self.begin[:, :].unsqueeze(1).to_broadcast(shape),
                                self.numbers[:, :].unsqueeze(2).to_broadcast(shape), ALU.is_le))
        chain(dve.tensor_reduce(self.expert[:, :], self.ended[:, :, :], AX_X, ALU.add))
        chain(dve.tensor_scalar(self.expert[:, :], self.expert[:, :], float(EXPERTS - 1), None, ALU.min))
        chain(dve.tensor_copy(self.expert_of[:, :], self.expert[:, :]))


def scatter_rows(pool, slot, t, source, scratch, scattered):
    pool.indirect_dma_start(out=scratch.rows, out_offset=bass.IndirectOffsetOnAxis(ap=slot[:, t:t + 1], axis=0),
                            in_=source[:, t, :], in_offset=None).then_inc(scattered, 16)


def gather_rows(pool, slot, t, target, scratch, gathered):
    pool.indirect_dma_start(out=target[:, t, :], out_offset=None, in_=scratch.results,
                            in_offset=bass.IndirectOffsetOnAxis(ap=slot[:, t:t + 1], axis=0)).then_inc(gathered, 16)


def expert_part(weights, e, at, width):
    return weights[:, bass.ds(e, 1), :].rearrange("p a n -> p (a n)")[:, at:at + width]


PARTS = 3


class SharedExperts:

    WIDTH, CHUNKS = 2 * P, 4
    TILES_EACH = WIDTH // P

    def __init__(self, st, weights, half_gate):
        self.chip, self.weights, self.half_gate = st.chip, weights, half_gate
        self.bank = st.chip.bank
        width, chunks = self.WIDTH, self.CHUNKS
        self.x_high, self.x_low = (st.sb(n, [P, 2, KD, width], BF16) for n in ("x_high", "x_low"))
        self.hidden_high, self.hidden_low = (st.sb(n, [P, 2, chunks, width], BF16) for n in ("s_high", "s_low"))
        self.squash, self.hidden = (st.sb(n, [P, 2, width]) for n in ("s_squash", "s_hidden"))
        self.x_high_ready, self.x_low_ready, self.h_ready, self.squashed = (st.sem(n) for n in (
            "x_high_ready", "x_low_ready", "s_h_ready", "s_squashed"))
        self.gated, self.hidden_ready, self.high_ready, self.low_ready = (st.sem(n) for n in (
            "s_gated", "s_hidden_ready", "s_high_ready", "s_low_ready"))
        self.out_ready, self.x_added = st.sem("s_out_ready"), st.sem("s_x_added")

    def up(self, pe, n):
        width = self.WIDTH
        pe.wait_ge(self.x_low_ready, n + 1)
        for c in range(self.CHUNKS):
            wait(pe, self.hidden_ready, self.CHUNKS * (n - 1) + c + 1)
            for branch in range(2):
                i = 0
                for x, w in ((self.x_high, 0), (self.x_low, 0), (self.x_high, 1)):
                    for k in range(KD):
                        i += 1
                        at = k * 4 * DIM + branch * 2 * DIM + c * P
                        last = pe.matmul(self.bank[:, c, branch * width:(branch + 1) * width],
                                         self.weights[w][:, at:at + P], x[:, n % 2, k, :],
                                         start=(i == 1), stop=(i == PARTS * KD))
            last.then_inc(self.h_ready, 1)

    def down(self, pe, n):
        pe.wait_ge(self.low_ready, self.CHUNKS * n + self.CHUNKS)
        for j in range(self.TILES_EACH):
            wait(pe, self.x_added, self.TILES_EACH * n + j - 1)
            i = 0
            for h, w in ((self.hidden_high, 0), (self.hidden_low, 0), (self.hidden_high, 1)):
                for c in range(self.CHUNKS):
                    i += 1
                    at = 8 * DIM + c * DIM
                    last = pe.matmul(self.bank[:, 4 + j, 0:DIM], h[:, n % 2, c, j * P:(j + 1) * P],
                                     self.weights[w][:, at:at + DIM], start=(i == 1), stop=(i == PARTS * self.CHUNKS))
            last.then_inc(self.out_ready, 1)

    def high_x(self, act, n):
        wait(act, self.h_ready, self.CHUNKS * (n - 1))
        act.activation(self.x_high[:, n % 2, :, :], self.chip.xnT[:, :, span(n, self.WIDTH)],
                       ACT.Copy).then_inc(self.x_high_ready, 1)

    def low_x(self, dve, n):
        dve.wait_ge(self.x_high_ready, n + 1)
        dve.tensor_tensor(self.x_low[:, n % 2, :, :], self.chip.xnT[:, :, span(n, self.WIDTH)],
                          self.x_high[:, n % 2, :, :], ALU.subtract).then_inc(self.x_low_ready, 1)

    def scalar(self, act, n):
        for c in range(self.CHUNKS):
            m = self.CHUNKS * n + c
            act.wait_ge(self.h_ready, m + 1)
            wait(act, self.gated, m - 1)
            act.activation(self.squash[:, c % 2, :], self.bank[:, c, 0:self.WIDTH], ACT.Tanh,
                           scale=0.5).then_inc(self.squashed, 1)
            act.wait_ge(self.hidden_ready, m + 1)
            if c == 0:
                wait(act, self.out_ready, self.TILES_EACH * (n - 1))
            act.activation(self.hidden_high[:, n % 2, c, :], self.hidden[:, c % 2, :], ACT.Copy).then_inc(self.high_ready, 1)

    def vector(self, dve, n):
        def low(c):
            dve.wait_ge(self.high_ready, self.CHUNKS * n + c + 1)
            dve.tensor_tensor(self.hidden_low[:, n % 2, c, :], self.hidden[:, c % 2, :], self.hidden_high[:, n % 2, c, :],
                              ALU.subtract).then_inc(self.low_ready, 1)

        for c in range(self.CHUNKS):
            m = self.CHUNKS * n + c
            dve.wait_ge(self.squashed, m + 1)
            wait(dve, self.low_ready, m - 1)
            dve.scalar_tensor_tensor(out=self.squash[:, c % 2, :], in0=self.squash[:, c % 2, :], scalar=1.0,
                                     in1=self.bank[:, c, 0:self.WIDTH], op0=ALU.add, op1=ALU.mult).then_inc(self.gated, 1)
            dve.wait_ge(self.gated, m + 1)
            dve.tensor_tensor(self.hidden[:, c % 2, :], self.squash[:, c % 2, :],
                              self.bank[:, c, self.WIDTH:2 * self.WIDTH], ALU.mult).then_inc(self.hidden_ready, 1)
            if c > 0:
                low(c - 1)
        low(self.CHUNKS - 1)

    def add(self, dve, n):
        for j in range(self.TILES_EACH):
            t = self.TILES_EACH * n + j
            dve.wait_ge(self.out_ready, t + 1)
            dve.scalar_tensor_tensor(out=nth(self.chip.x, t), in0=self.bank[:, 4 + j, 0:DIM], scalar=self.half_gate[:, 0:1],
                                     in1=nth(self.chip.x, t), op0=ALU.mult, op1=ALU.add).then_inc(self.x_added, 1)

    def tensor_part(self, pe, part, between=lambda n: None):
        self.up(pe, part[0])
        for n in part:
            if n + 1 in part:
                self.up(pe, n + 1)
            self.down(pe, n)
            between(n)

    def scalar_part(self, act, part, between=lambda n: None):
        self.high_x(act, part[0])
        for n in part:
            if n + 1 in part:
                self.high_x(act, n + 1)
            self.scalar(act, n)
            between(n)

    def vector_part(self, dve, part, between=lambda n: None):
        self.low_x(dve, part[0])
        for n in part:
            if n + 1 in part:
                self.low_x(dve, n + 1)
            self.vector(dve, n)
            if n > part[0]:
                self.add(dve, n - 1)
            between(n)
        self.add(dve, part[-1])


def silu_experts(chip, a, weights):
    nc = chip.nc
    gate = 4 + 0
    with ExitStack() as ctx:
        st = Stage(chip, "l0f", ctx)
        bank = chip.bank
        sb, sem = st.sb, st.sem
        scratch = chip.scratch[0]
        experts_width = EXPERTS * 6 * DIM
        split = weights[:, :, 0:experts_width].rearrange("p w (e n) -> p w e n", e=EXPERTS)
        width = split.shape[3]
        sort = Sorting(st, 2)
        wg, bg, order = sb("gate_w", [P, KD, EXPERTS]), sb("gate_bias", [P, EXPERTS]), sb("order", [P, EXPERTS])
        scores, biased, work = (sb(n, [P, TILES, EXPERTS]) for n in ("scores", "biased", "work"))
        masks = [sb(f"mask{k}", [P, TILES, EXPERTS]) for k in range(2)]
        weight = [sb(f"weight{k}", [P, TILES]) for k in range(2)]
        column, half_gate = sb("column", [P, TILES]), sb("half_gate", [P, 1])
        loaded, logits_ready, chained = sem("loaded"), sem("logits_ready"), sem("chained")
        shared = SharedExperts(st, [weights[:, n, experts_width:] for n in range(2)], half_gate)
        blocks = range(TOKENS // SharedExperts.WIDTH)
        parts = blocks[:len(blocks) // 2], blocks[len(blocks) // 2:]
        exp_wanted, exp_ready, scattered = sem("exp_wanted"), sem("exp_ready"), sem("scattered")

        with nc.Block() as block:
            @block.sync
            def _(sp):
                sp.dma_start(wg[:, :, :], load_rows(a["L0_ffn_gate_w"])).then_inc(loaded, 16)
                sp.dma_start(bg[:, :], a["L0_ffn_gate_bias"].partition_broadcast(P)).then_inc(loaded, 16)
                sp.dma_start(order[:, :], a["order"].partition_broadcast(P)).then_inc(loaded, 16)
                sort.sync(sp, a)

            @block.tensor
            def _(pe):
                pe.wait_ge(loaded, 48)
                gate_logits(pe, chip, wg, bank[:, 0, :], logits_ready)
                sort.tensor(pe, bank[:, 1, :], bank[:, 2, :])

            @block.scalar
            def _(act):
                act.wait_ge(exp_wanted, 1)
                act.activation(scores[:, :, :], scores[:, :, :], ACT.Exp).then_inc(exp_ready, 1)

            @block.vector
            def _(dve):
                chain = Chain(dve, chained)
                dve.wait_ge(loaded, 48)
                dve.wait_ge(logits_ready, 1)
                logits = bank[:, 0, 0:TILES * EXPERTS].rearrange("p (t e) -> p t e", t=TILES)
                chain(dve.tensor_reduce(column[:, :], logits, AX_X, ALU.max))
                chain(dve.tensor_tensor(scores[:, :, :], logits, wide(column), ALU.subtract))
                dve.sem_inc(exp_wanted, 1)
                dve.wait_ge(exp_ready, 1)
                chain(dve.tensor_reduce(column[:, :], scores[:, :, :], AX_X, ALU.add))
                chain(dve.reciprocal(column[:, :], column[:, :]))
                chain(dve.tensor_tensor(scores[:, :, :], scores[:, :, :], wide(column), ALU.mult))
                chain(dve.tensor_tensor(biased[:, :, :], scores[:, :, :], tall(bg), ALU.add))
                pick_largest(dve, chain, biased, order, masks[0], work, column)
                chain(dve.scalar_tensor_tensor(out=biased[:, :, :], in0=masks[0][:, :, :], scalar=-HIDE,
                                               in1=biased[:, :, :], op0=ALU.mult, op1=ALU.add))
                pick_largest(dve, chain, biased, order, masks[1], work, column)
                sort.vector(dve, chain, masks, bank[:, 1, :], bank[:, 2, :])
                chain(dve.tensor_scalar(half_gate[:, :], chip.gate[:, gate:gate + 1], 0.5, None, ALU.mult))
                for k in range(2):
                    chain(dve.tensor_tensor(work[:, :, :], scores[:, :, :], masks[k][:, :, :], ALU.mult))
                    chain(dve.tensor_reduce(weight[k][:, :], work[:, :, :], AX_X, ALU.add))
                    chain(dve.tensor_scalar(weight[k][:, :], weight[k][:, :], half_gate[:, 0:1], None, ALU.mult))

        with nc.Block() as block:
            @block.gpsimd
            def _(pool):
                for k in range(2):
                    for t in range(TILES):
                        scatter_rows(pool, sort.slot[k], t, chip.keep, scratch, scattered)
                pool.wait_ge(scattered, 16 * 2 * TILES)

            @block.tensor
            def _(pe):
                shared.tensor_part(pe, parts[0])

            @block.scalar
            def _(act):
                shared.scalar_part(act, parts[0])

            @block.vector
            def _(dve):
                shared.vector_part(dve, parts[0])

        with ExitStack() as inner:
            st3 = Stage(chip, "l0r", inner)
            n = sort.tiles
            lanes = SlotLanes(st3, scratch, bank[:, 7, :], n, sort.expert_of)
            placed = PlacedWeights(st3, split, 4 * DIM, lanes.AHEAD)
            hidden_high, hidden_low = (st3.sb(nm, [P, 2, DIM], BF16) for nm in ("hidden_high", "hidden_low"))
            squash, hidden = (st3.sb(nm, [P, 2, DIM]) for nm in ("squash", "hidden"))
            sem3 = st3.sem
            h_ready, squashed, gated, hidden_ready = (sem3(nm) for nm in (
                "h_ready", "squashed", "gated", "hidden_ready"))
            high_ready, low_ready = sem3("high_ready"), sem3("low_ready")
            block = inner.enter_context(nc.Block())

            @block.sync
            def _(sp):
                lanes.sync(sp, placed, h_ready)

            @block.tensor
            def _(pe):
                def up(i, q):
                    j, u = lanes.AHEAD * i + q, q % 2
                    placed.ready(pe, i, q)
                    pe.wait_ge(lanes.low_ready, j + 1)
                    wait(pe, hidden_ready, j - 1)
                    for m in range(4):
                        s = 0
                        for x, w in ((lanes.high, 0), (lanes.low, 0), (lanes.high, 1)):
                            for k in range(KD):
                                s += 1
                                at = k * 2 * DIM + m * P
                                last = pe.matmul(bank[:, u, m * P:(m + 1) * P], placed.parts[w][:, q, at:at + P],
                                                 x[:, u, k, :], start=(s == 1), stop=(s == PARTS * KD))
                    last.then_inc(h_ready, 1)

                def down(i, q):
                    j, u = lanes.AHEAD * i + q, q % 2
                    e = lanes.expert(pe, j)
                    pe.wait_ge(low_ready, j + 1)
                    wait(pe, lanes.y_copied, j - 1)
                    s = 0
                    for h, w in ((hidden_high, 0), (hidden_low, 0), (hidden_high, 1)):
                        for c in range(KD):
                            s += 1
                            last = pe.matmul(bank[:, 2 + u, 0:DIM], h[:, u, c * P:(c + 1) * P],
                                             expert_part(split[:, w, :, :], e, 4 * DIM + c * DIM, DIM), start=(s == 1), stop=(s == PARTS * KD))
                    last.then_inc(lanes.y_ready, 1)

                lanes.tensor_loop(pe, up, down)

            @block.scalar
            def _(act):
                def step(i, q):
                    j, u = lanes.AHEAD * i + q, q % 2
                    act.wait_ge(h_ready, j + 1)
                    wait(act, gated, j - 1)
                    act.activation(squash[:, u, :], bank[:, u, 0:DIM], ACT.Tanh, scale=0.5).then_inc(squashed, 1)
                    act.wait_ge(hidden_ready, j + 1)
                    wait(act, lanes.y_ready, j - 1)
                    act.activation(hidden_high[:, u, :], hidden[:, u, :], ACT.Copy).then_inc(high_ready, 1)
                lanes.scalar_loop(act, step, bank)

            @block.vector
            def _(dve):
                def step(i, q):
                    j, u = lanes.AHEAD * i + q, q % 2
                    dve.wait_ge(squashed, j + 1)
                    wait(dve, low_ready, j - 1)
                    dve.scalar_tensor_tensor(out=squash[:, u, :], in0=squash[:, u, :], scalar=1.0,
                                             in1=bank[:, u, 0:DIM], op0=ALU.add, op1=ALU.mult).then_inc(gated, 1)
                    dve.wait_ge(gated, j + 1)
                    dve.tensor_tensor(hidden[:, u, :], squash[:, u, :], bank[:, u, DIM:2 * DIM],
                                      ALU.mult).then_inc(hidden_ready, 1)
                lanes.vector_loop(dve, step, bank)

            @block.gpsimd
            def _(pool):
                def step(i, q):
                    j, u = lanes.AHEAD * i + q, q % 2
                    pool.wait_ge(high_ready, j + 1)
                    pool.tensor_tensor(hidden_low[:, u, :], hidden[:, u, :], hidden_high[:, u, :],
                                       ALU.subtract).then_inc(low_ready, 1)
                lanes.gpsimd_loop(pool, step)

        combine(chip, "l0c", ctx, sort, scratch, weight, {}, shared, parts[1])


class PlacedWeights:

    def __init__(self, st, split, width, slots, room=None):
        self.split, self.width, self.slots = split, width, slots
        self.room = room or st.sb("placed", [P, slots, 2, width], BF16)
        self.parts = [self.room[:, :, n, :] for n in range(2)]
        self.copied = [st.sem(f"placed{q}") for q in range(slots)]

    def copy(self, sp, lanes, i, q, e, released):
        slot = q % self.slots
        wait(sp, released, lanes.AHEAD * i + q - self.slots + 1)
        sp.dma_start(self.room[:, slot, :, :],
                     self.split[:, :, bass.ds(e, 1), 0:self.width].rearrange("p w a n -> p w (a n)")).then_inc(
            self.copied[slot], 16)

    def ready(self, pe, i, q):
        rounds = SlotLanes.AHEAD // self.slots
        pe.wait_ge(self.copied[q % self.slots], 16 * (rounds * i + q // self.slots) + 16)


class TileConstants:

    def __init__(self, st, columns, rows):
        self.columns, self.rows = columns, rows
        self.columns_now = st.sb("columns_now", [P, SlotLanes.AHEAD, columns.shape[2]])
        self.row_now = st.sb("row_now", [P, SlotLanes.AHEAD, DIM])
        self.loaded = [st.sem(f"constants_loaded{q}") for q in range(SlotLanes.AHEAD)]

    def load(self, sp, lanes, i, q, e):
        wait(sp, lanes.y_copied, lanes.AHEAD * i + q - lanes.AHEAD + 1)
        sp.dma_start(self.columns_now[:, q, :], self.columns[:, bass.ds(e, 1), :].rearrange("p a n -> p (a n)")).then_inc(
            self.loaded[q], 16)
        sp.dma_start(self.row_now[:, q, :],
                     self.rows[bass.ds(e, 1), :].rearrange("a n -> (a n)").partition_broadcast(P)).then_inc(
            self.loaded[q], 16)

    def ready(self, eng, i, q):
        eng.wait_ge(self.loaded[q], 32 * i + 32)


class SlotLanes:

    AHEAD = 4

    def __init__(self, st, scratch, turn_bank, n, expert_of, room=None, constants=None):
        self.chip, self.scratch, self.turn_bank, self.n = st.chip, scratch, turn_bank, n
        self.expert_of, self.constants = expert_of, constants
        sb, sem = st.sb, st.sem
        if room is None:
            room = sb("room", [P, self.AHEAD + 2, DIM])
        self.rows, self.y = room[:, 0:self.AHEAD, :], room[:, self.AHEAD:self.AHEAD + 2, :]
        self.high, self.low = (sb(nm, [P, 2, KD, P], BF16) for nm in ("xT_high", "xT_low"))
        self.rows_loaded = [sem(f"rows_loaded{u}") for u in range(self.AHEAD)]
        self.turned, self.high_ready, self.low_ready = sem("turned"), sem("xT_high_ready"), sem("xT_low_ready")
        if constants is not None:
            self.scaled = sb("xT_scaled", [P, 2, KD, P])
            self.scaled_ready = sem("xT_scaled_ready")
        self.y_ready, self.y_copied = sem("y_ready"), sem("y_copied")
        self.stored = [sem(f"stored{u}") for u in range(2)]

    def rows_of(self, dram, j):
        return dram[span(j, P), :]

    def expert(self, eng, j):
        at = self.expert_of[0:1, j:j + 1] if isinstance(j, int) else self.expert_of[0:1, bass.ds(j, 1)]
        return eng.value_load(at, min_val=0, max_val=EXPERTS - 1)

    def sync(self, sp, placed, released):
        def load(i, q):
            j = self.AHEAD * i + q
            wait(sp, self.turned, j - self.AHEAD + 1)
            sp.dma_start(self.rows[:, q, :], self.rows_of(self.scratch.rows, j)).then_inc(self.rows_loaded[q], 16)

        def bring(i, q):
            e = self.expert(sp, self.AHEAD * i + q)
            if self.constants is not None:
                self.constants.load(sp, self, i, q, e)
            placed.copy(sp, self, i, q, e, released)

        for q in range(self.AHEAD):
            load(0, q)
            if q < placed.slots:
                bring(0, q)

        def step(i):
            for q in range(self.AHEAD):
                last = is_step(i, self.n // self.AHEAD - 1)
                if not last:
                    load(i + 1, q)
                if not (last and q + placed.slots >= self.AHEAD):
                    bring(i + (q + placed.slots) // self.AHEAD, (q + placed.slots) % self.AHEAD)
        steps(sp, self.n // self.AHEAD, step)

    def gpsimd_loop(self, pool, body):
        def store(i, q):
            j = self.AHEAD * i + q
            pool.wait_ge(self.y_copied, j + 1)
            pool.dma_start(self.rows_of(self.scratch.results, j), self.y[:, q % 2, :]).then_inc(self.stored[q % 2], 16)

        self.quads(pool, lambda i, q: None, body, store)
        for u in range(2):
            pool.wait_ge(self.stored[u], 16 * (self.n // 2))

    def tensor_loop(self, pe, up, down):
        def turn(i, q):
            j = self.AHEAD * i + q
            pe.wait_ge(self.rows_loaded[q], 16 * i + 16)
            wait(pe, self.scaled_ready if self.constants else self.low_ready, j)
            for k in range(KD):
                last = pe.transpose(self.turn_bank[:, k * P:(k + 1) * P], self.rows[:, q, k * P:(k + 1) * P],
                                    self.chip.ident[:, :])
            last.then_inc(self.turned, 1)

        groups = self.n // self.AHEAD
        turn(0, 0)

        def step(i):
            for q in range(self.AHEAD):
                j = self.AHEAD * i + q
                if q + 1 < self.AHEAD:
                    turn(i, q + 1)
                elif not is_step(i, groups - 1):
                    turn(i + 1, 0)
                up(i, q)
                if q > 0:
                    down(i, q - 1)
                elif not is_step(i, 0):
                    down(i - 1, self.AHEAD - 1)
        steps(pe, groups, step)
        down(groups - 1, self.AHEAD - 1)

    def y_stored(self, eng, i, q):
        wait(eng, self.stored[q % 2], 16 * (self.AHEAD // 2 * i + q // 2))

    def quads(self, eng, split, body, finish):
        groups = self.n // self.AHEAD
        split(0, 0)

        def step(i):
            for q in range(self.AHEAD):
                if q + 1 < self.AHEAD:
                    split(i, q + 1)
                elif not is_step(i, groups - 1):
                    split(i + 1, 0)
                body(i, q)
                if q > 0:
                    finish(i, q - 1)
                elif not is_step(i, 0):
                    finish(i - 1, self.AHEAD - 1)
        steps(eng, groups, step)
        finish(groups - 1, self.AHEAD - 1)

    def turned_rows(self):
        return self.turn_bank[:, 0:DIM].rearrange("p (k n) -> p k n", k=KD)

    def scalar_loop(self, act, body, bank):
        def split(i, q):
            j, u = self.AHEAD * i + q, q % 2
            act.wait_ge(self.turned, j + 1)
            rows = self.turned_rows()
            if self.constants is not None:
                self.constants.ready(act, i, q)
                wait(act, self.low_ready, j - 1)
                columns = self.constants.columns_now
                for k in range(KD):
                    last = act.activation(self.scaled[:, u, k, :], self.turn_bank[:, k * P:(k + 1) * P], ACT.Identity,
                                          scale=columns[:, q, k:k + 1], bias=columns[:, q, KD + k:KD + k + 1])
                last.then_inc(self.scaled_ready, 1)
                act.wait_ge(self.scaled_ready, j + 1)
                rows = self.scaled[:, u, :, :]
            wait(act, self.y_ready, j - 2)
            act.activation(self.high[:, u, :, :], rows, ACT.Copy).then_inc(self.high_ready, 1)

        def copy_y(i, q):
            if self.constants is None:
                act.wait_ge(self.y_ready, self.AHEAD * i + q + 1)
                self.y_stored(act, i, q)
                act.activation(self.y[:, q % 2, :], bank[:, 2 + q % 2, 0:DIM], ACT.Copy).then_inc(self.y_copied, 1)

        self.quads(act, split, body, copy_y)

    def vector_loop(self, dve, body, bank):
        def split(i, q):
            dve.wait_ge(self.high_ready, self.AHEAD * i + q + 1)
            rows = self.turned_rows() if self.constants is None else self.scaled[:, q % 2, :, :]
            dve.tensor_tensor(self.low[:, q % 2, :, :], rows, self.high[:, q % 2, :, :],
                              ALU.subtract).then_inc(self.low_ready, 1)

        def add_bias(i, q):
            if self.constants is not None:
                dve.wait_ge(self.y_ready, self.AHEAD * i + q + 1)
                self.y_stored(dve, i, q)
                dve.tensor_tensor(self.y[:, q % 2, :], bank[:, 2 + q % 2, 0:DIM], self.constants.row_now[:, q, :],
                                  ALU.add).then_inc(self.y_copied, 1)

        self.quads(dve, split, body, add_bias)


def combine(chip, name, ctx, sort, scratch, weight, norm_args, shared=None, part=()):
    with ExitStack() as inner:
        st = Stage(chip, name, inner)
        groups = 4
        per = TILES // groups
        norm = NextNorm(st, chip.bank[:, 7, :], depth=per, **norm_args)
        targets = [chip.keep] + [st.sb(f"gathered{k}", [P, TILES, DIM]) for k in range(1, sort.picks)]
        gathered = [st.sem(f"gathered{g}") for g in range(groups)]
        part_added = st.sem("part_added")

        def in_turn(shared_part, eng, group, after):
            early = groups // 2 if shared_part else 0
            if shared_part:
                shared_part(eng, part, lambda n: group(n - part[after]) if n in part[after:after + early] else None)
            for g in range(early, groups):
                group(g)

        block = inner.enter_context(chip.nc.Block())

        @block.gpsimd
        def _(pool):
            for g in range(groups + 1):
                for t in range(per * g, min(per * g + per, TILES)):
                    for k in range(sort.picks):
                        gather_rows(pool, sort.slot[k], t, targets[k], scratch, gathered[g])
                for t in range(per * g - per, per * g):
                    if t >= 0:
                        norm.gpsimd(pool, t, t % per)

        @block.vector
        def _(dve):
            def group(g):
                dve.wait_ge(gathered[g], 16 * per * sort.picks)
                for k in range(sort.picks):
                    for u in range(per):
                        t = per * g + u
                        if k > 0:
                            dve.wait_ge(part_added, (sort.picks - 1) * t + k)
                        dve.scalar_tensor_tensor(out=chip.x[:, t, :], in0=targets[k][:, t, :], scalar=weight[k][:, t:t + 1],
                                                 in1=chip.x[:, t, :], op0=ALU.mult, op1=ALU.add).then_inc(
                            norm.x_updated if k == sort.picks - 1 else part_added, 1)
                for u in range(per):
                    norm.vector_stats(dve, per * g + u, u)
                for u in range(per):
                    norm.vector_apply(dve, per * g + u, u)

            in_turn(shared and shared.vector_part, dve, group, 1)

        @block.tensor
        def _(pe):
            def group(g):
                for u in range(per):
                    norm.tensor(pe, per * g + u, u)
            in_turn(shared and shared.tensor_part, pe, group, 2)

        @block.scalar
        def _(act):
            def group(g):
                for u in range(per):
                    norm.scalar(act, per * g + u, u)
            in_turn(shared and shared.scalar_part, act, group, 2)


def relu_experts(chip, a):
    nc = chip.nc
    gate = 4 + 1
    with ExitStack() as ctx:
        st = Stage(chip, "l1f", ctx)
        bank = chip.bank
        sb, sem = st.sb, st.sem
        scratch = chip.scratch[1]
        hidden_width = (a["L1_ffn_columns"].shape[2] - 2 * KD) * P
        chunks = hidden_width // P
        per_expert = KD * hidden_width + chunks * DIM
        weights = sb("weights", [P, 2, EXPERTS * per_expert], BF16)
        high, low = (weights[:, n, :] for n in range(2))
        split = weights[:, :, :].rearrange("p w (e n) -> p w e n", e=EXPERTS)
        sort = Sorting(st, 1)
        centroids, order = sb("centroids", [P, KD, EXPERTS]), sb("order", [P, EXPERTS])
        columns = sb("columns", [P, EXPERTS, 2 * KD + chunks])
        latent_g, latent_b = sb("ln_l_g", [P, KD]), sb("ln_l_b", [P, KD])
        nearness, work, mask = (sb(n, [P, TILES, EXPERTS]) for n in ("nearness", "work", "mask"))
        weight, column = sb("weight", [P, TILES]), sb("column", [P, TILES])
        loaded, logits_ready, chained = sem("loaded"), sem("logits_ready"), sem("chained")
        scattered = sem("scattered")
        tanh_wanted, tanh_ready = sem("tanh_wanted"), sem("tanh_ready")
        loads = 5

        chunk, slots = 1024, 4
        group = 2 * slots
        groups = EXPERTS * per_expert // (group * chunk)
        by_gpsimd = groups // 2
        staging_ctx = ctx.enter_context(ExitStack())
        staging = Stage(chip, "l1w", staging_ctx).sb("staging", [P, slots, chunk])
        w_loaded, w_split = [sem(f"w_loaded{q}") for q in range(slots)], [sem(f"w_split{q}") for q in range(slots)]
        high_ready = sem("w_high_ready")

        def load_weights(sp, g):
            for n in range(group):
                c, turn = group * g + n, 2 * g + n // slots
                wait(sp, w_split[n % slots], turn)
                sp.dma_start(staging[:, n % slots, :], a["L1_ffn_weights"][:, span(c, chunk)]).then_inc(
                    w_loaded[n % slots], 16)

        def high_parts(act, g):
            for n in range(group):
                c, turn = group * g + n, 2 * g + n // slots
                act.wait_ge(w_loaded[n % slots], 16 * turn + 16)
                act.activation(high[:, span(c, chunk)], staging[:, n % slots, :], ACT.Copy).then_inc(high_ready, 1)

        def low_parts(eng, g):
            for n in range(group):
                c = group * g + n
                eng.wait_ge(high_ready, c + 1)
                eng.tensor_tensor(low[:, span(c, chunk)], staging[:, n % slots, :], high[:, span(c, chunk)],
                                  ALU.subtract).then_inc(w_split[n % slots], 1)

        with nc.Block() as block:
            @block.sync
            def _(sp):
                sp.dma_start(centroids[:, :, :], load_rows(a["L1_ffn_centroids"])).then_inc(loaded, 16)
                sp.dma_start(order[:, :], a["order"].partition_broadcast(P)).then_inc(loaded, 16)
                sp.dma_start(columns[:, :, :], a["L1_ffn_columns"]).then_inc(loaded, 16)
                for rows, w in ((latent_g, "ln_l_g"), (latent_b, "ln_l_b")):
                    sp.dma_start(rows[:, :], a[f"L2_xattn_{w}"]).then_inc(loaded, 16)
                sort.sync(sp, a)
                steps(sp, groups, lambda g: load_weights(sp, g))

            @block.tensor
            def _(pe):
                pe.wait_ge(loaded, 16 * loads)
                gate_logits(pe, chip, centroids, bank[:, 0, :], logits_ready)
                sort.tensor(pe, bank[:, 1, :], bank[:, 2, :])

            @block.scalar
            def _(act):
                high_parts(act, 0)
                act.wait_ge(tanh_wanted, 1)
                act.activation(weight[:, :], weight[:, :], ACT.Tanh, scale=0.5).then_inc(tanh_ready, 1)
                for g in range(1, groups):
                    high_parts(act, g)

            @block.vector
            def _(dve):
                chain = Chain(dve, chained)
                dve.wait_ge(loaded, 16 * loads)
                dve.wait_ge(logits_ready, 1)
                chain(dve.tensor_copy(nearness[:, :, :], bank[:, 0, 0:TILES * EXPERTS].rearrange(
                    "p (t e) -> p t e", t=TILES)))
                chain(dve.tensor_reduce(weight[:, :], nearness[:, :, :], AX_X, ALU.max))
                dve.sem_inc(tanh_wanted, 1)
                pick_largest(dve, chain, nearness, order, mask, work, column)
                dve.wait_ge(tanh_ready, 1)
                chain(dve.tensor_scalar(weight[:, :], weight[:, :], 0.5, 0.5, ALU.mult, ALU.add))
                chain(dve.tensor_scalar(weight[:, :], weight[:, :], chip.gate[:, gate:gate + 1], None, ALU.mult))
                sort.vector(dve, chain, [mask], bank[:, 1, :], bank[:, 2, :])
                for g in range(by_gpsimd, groups):
                    low_parts(dve, g)

            @block.gpsimd
            def _(pool):
                for g in range(by_gpsimd):
                    low_parts(pool, g)
                pool.wait_ge(sort.slots_ready, 1)
                for t in range(TILES):
                    scatter_rows(pool, sort.slot[0], t, chip.keep, scratch, scattered)
                pool.wait_ge(scattered, 16 * TILES)

        staging_ctx.close()

        with ExitStack() as inner:
            st2 = Stage(chip, "l1r", inner)
            n = sort.tiles
            hidden_high, hidden_low = (st2.sb(nm, [P, 2, hidden_width], BF16) for nm in ("hidden_high", "hidden_low"))
            lane_tiles = hidden_width // DIM
            lanes = SlotLanes(st2, scratch, bank[:, 7, :], n, sort.expert_of, chip.keep[:, 2 * lane_tiles:, :],
                              TileConstants(st2, columns, a["L1_ffn_b2"]))
            hidden = [chip.keep[:, u * lane_tiles:(u + 1) * lane_tiles, :].rearrange("p a n -> p (a n)") for u in range(2)]
            places = chip.xnT[:, :, :].rearrange("p k n -> p (k n)").bitcast(BF16).rearrange(
                "p (s w n) -> p s w n", w=2, s=2)
            placed = PlacedWeights(st2, split, KD * hidden_width, 2, places)
            h_banks = hidden_width // 512
            h_bank = [bank[:, 4 * u:4 * u + h_banks, :].rearrange("p a n -> p (a n)") for u in range(2)]
            h_ready, biased, high_ready, low_ready = (st2.sem(nm) for nm in (
                "h_ready", "biased", "high_ready", "low_ready"))
            block = inner.enter_context(nc.Block())

            @block.sync
            def _(sp):
                lanes.sync(sp, placed, h_ready)

            @block.gpsimd
            def _(pool):
                lanes.gpsimd_loop(pool, lambda i, q: None)

            @block.tensor
            def _(pe):
                def up(i, q):
                    j, u = lanes.AHEAD * i + q, q % 2
                    placed.ready(pe, i, q)
                    pe.wait_ge(lanes.low_ready, j + 1)
                    wait(pe, biased, j - 1)
                    for m in range(chunks):
                        s = 0
                        for x, w in ((lanes.high, 0), (lanes.low, 0), (lanes.high, 1)):
                            for k in range(KD):
                                s += 1
                                at = k * hidden_width + m * P
                                last = pe.matmul(h_bank[u][:, m * P:(m + 1) * P], placed.parts[w][:, u, at:at + P],
                                                 x[:, u, k, :], start=(s == 1), stop=(s == PARTS * KD))
                    last.then_inc(h_ready, 1)

                def down(i, q):
                    j, u = lanes.AHEAD * i + q, q % 2
                    e = lanes.expert(pe, j)
                    pe.wait_ge(low_ready, j + 1)
                    wait(pe, lanes.y_copied, j - 1)
                    s = 0
                    for h, w in ((hidden_high, 0), (hidden_low, 0), (hidden_high, 1)):
                        for c in range(chunks):
                            s += 1
                            last = pe.matmul(bank[:, 2 + u, 0:DIM], h[:, u, c * P:(c + 1) * P],
                                             expert_part(split[:, w, :, :], e, KD * hidden_width + c * DIM, DIM),
                                             start=(s == 1), stop=(s == PARTS * chunks))
                    last.then_inc(lanes.y_ready, 1)

                lanes.tensor_loop(pe, up, down)

            @block.scalar
            def _(act):
                def step(i, q):
                    j, u = lanes.AHEAD * i + q, q % 2
                    act.wait_ge(biased, j + 1)
                    wait(act, lanes.y_ready, j - 1)
                    act.activation(hidden_high[:, u, :], hidden[u], ACT.Relu).then_inc(high_ready, 1)
                lanes.scalar_loop(act, step, bank)

            @block.vector
            def _(dve):
                def step(i, q):
                    j, u = lanes.AHEAD * i + q, q % 2
                    lanes.constants.ready(dve, i, q)
                    dve.wait_ge(h_ready, j + 1)
                    wait(dve, low_ready, j - 1)
                    dve.tensor_tensor(hidden[u].rearrange("p (c n) -> p c n", c=chunks),
                                      h_bank[u].rearrange("p (c n) -> p c n", c=chunks),
                                      lanes.constants.columns_now[:, q, 2 * KD:].unsqueeze(2).to_broadcast([P, chunks, P]),
                                      ALU.add).then_inc(biased, 1)
                    dve.wait_ge(high_ready, j + 1)
                    dve.scalar_tensor_tensor(out=hidden_low[:, u, :], in0=hidden[u], scalar=0.0, in1=hidden_high[:, u, :],
                                             op0=ALU.max, op1=ALU.subtract).then_inc(low_ready, 1)
                lanes.vector_loop(dve, step, bank)

        combine(chip, "l1c", ctx, sort, scratch, [weight], {"affine": (latent_g, latent_b)})


def layer0(chip, a, attend=True):
    with ExitStack() as ctx:
        st = Stage(chip, "l0", ctx)
        width = a["L0_ffn_weights"].shape[1]
        weights = st.sb("weights", [P, 2, width], BF16)
        with ExitStack() as inner:
            feed = Feed(Stage(chip, "l0w", inner), a["L0_ffn_weights"], weights[:, 0, :], weights[:, 1, :],
                        width // TILES)
            single_head_attention(chip, a, feed)
        silu_experts(chip, a, weights)


def layer1(chip, a):
    multi_head_attention(chip, a, 1, 1, True, lambda st: {"keep_again": chip.keep, "share": chip.gate[:, 5:6]})
    chip.release()
    relu_experts(chip, a)


def layer2(chip, a):
    latent_attention(chip, a)
    chip.release()
    relu_square_experts(chip, a)


def layer3(chip, a):
    with ExitStack() as ctx:
        st = Stage(chip, "l3", ctx)
        width = a["L3_ffn_We"].shape[1]
        high, low = (st.sb(n, [P, width], BF16) for n in ("We_high", "We_low"))
        with ExitStack() as inner:
            feed = Feed(Stage(chip, "l3w", inner), a["L3_ffn_We"], high, low, width // TILES)
            multi_head_attention(chip, a, 3, 3, False, lambda st: {}, feed)
        linear_experts(chip, a, high, low)


LAYERS = [layer0, layer1, layer2, layer3]




def finish(chip, out):
    nc = chip.nc
    with ExitStack() as ctx:
        st = Stage(chip, "finish", ctx)
        stored = st.sem("stored")
        block = ctx.enter_context(nc.Block())

        @block.sync
        def _(sp):
            sp.dma_start(out.rearrange("(t p) d -> p t d", p=P), chip.x[:, :, :]).then_inc(stored, 16)
            sp.wait_ge(stored, 16)


def program(nc, a, out):
    with ExitStack() as ctx:
        chip = Chip(nc, ctx)
        chip.scratch = [Scratch(nc, "l0", slot_tiles(2) * P), Scratch(nc, "l1", slot_tiles(1) * P)]
        begin(chip, a)
        for layer in LAYERS:
            layer(chip, a)
            chip.release()
        finish(chip, out)


def lay_out(inputs):
    import numpy as np

    a = {}
    a["x"] = inputs["x"].reshape(TOKENS, DIM)
    a["ctxT"] = inputs["ctx_1024"].reshape(CTX, DIM).T
    a["g_xattn"], a["g_ffn"] = inputs["g_xattn"], inputs["g_ffn"]
    a["ident"] = np.eye(P, dtype=np.float32)
    for n in ("Wq", "Wk", "Wv"):
        a[f"L0_xattn_{n}"] = inputs[f"L0_xattn_{n}"].T
    for n in ("bq", "bk"):
        a[f"L0_xattn_{n}"] = inputs[f"L0_xattn_{n}"].reshape(KD, P).T
    a["L0_xattn_bv"] = inputs["L0_xattn_bv"]
    for n in ("Wq", "Wk", "Wv", "Wo"):
        a[f"L1_xattn_{n}"] = inputs[f"L1_xattn_{n}"].T
    a["key_bias"] = inputs["fside_BxS2_0"].reshape(CTX)
    a["head_of"] = np.kron(np.eye(CHUNK_HEADS, dtype=np.float32), np.ones((HEAD, 1), np.float32))
    a["L3_xattn_Wq"], a["L3_xattn_Wo"] = inputs["L3_xattn_Wq"], inputs["L3_xattn_Wp"]
    kv = inputs["L3_xattn_Wkv"].reshape(DIM, HEADS, 2, HEAD)
    a["L3_xattn_Wk"], a["L3_xattn_Wv"] = (kv[:, :, n, :].reshape(DIM, DIM) for n in range(2))
    kv = inputs["L3_xattn_bkv"].reshape(HEADS, 2, HEAD)
    a["L3_xattn_bk"], a["L3_xattn_bv"] = kv[:, 0, :].reshape(KD, P).T, kv[:, 1, :].reshape(DIM)
    a["L3_xattn_bq"] = inputs["L3_xattn_bq"].reshape(KD, P).T
    a["L3_xattn_bp"] = inputs["L3_xattn_bp"]
    for n in ("W_q", "W_kv", "W_out", "b_out", "q_gamma", "k_gamma"):
        a[f"L2_xattn_{n}"] = inputs[f"L2_xattn_{n}"]
    for n in ("ln_x_g", "ln_x_b", "ln_l_g", "ln_l_b"):
        a[f"L2_xattn_{n}"] = inputs[f"L2_xattn_{n}"].reshape(KD, P).T
    a["context"] = inputs["ctx_1024"].reshape(CTX, DIM)
    a["mask"] = inputs["mask_BxS2_bk0"].reshape(CTX)
    a["order"] = np.arange(EXPERTS, dtype=np.float32) - EXPERTS
    for n in ("Ws1", "Ws2", "Wr"):
        a[f"L2_ffn_{n}"] = inputs[f"L2_ffn_{n}"]
    a["L2_ffn_W1"] = inputs["L2_ffn_W1"].reshape(EXPERTS, KD, P, P).transpose(0, 2, 1, 3).reshape(EXPERTS, P, DIM)
    a["L2_ffn_W2"] = inputs["L2_ffn_W2"]
    for n in ("Wg", "bg", "be"):
        a[f"L3_ffn_{n}"] = inputs[f"L3_ffn_{n}"]
    a["L3_ffn_We"] = inputs["L3_ffn_We"].reshape(EXPERTS, DIM, KD, P).transpose(3, 2, 0, 1).reshape(P, -1)
    a["tri"] = np.triu(np.ones((P, P), np.float32), 1)
    a["starts"] = np.arange(TILES, dtype=np.float32) * P
    a["before"] = np.tril(np.ones((EXPERTS, EXPERTS), np.float32), -1).reshape(-1)
    a["numbers"] = np.arange(slot_tiles(2), dtype=np.float32)
    a["L0_ffn_gate_w"], a["L0_ffn_gate_bias"] = inputs["L0_ffn_gate_w"].T, inputs["L0_ffn_gate_bias"]

    def by_rows(w, chunks):
        w = w.reshape(-1, w.shape[-2], chunks, P)
        return w.transpose(3, 0, 2, 1)

    up = np.concatenate([inputs["L0_ffn_w1"], inputs["L0_ffn_w3"]], axis=1)
    experts = np.concatenate([by_rows(up, KD).reshape(P, EXPERTS, -1),
                              by_rows(inputs["L0_ffn_w2"], KD).reshape(P, EXPERTS, -1)], axis=2)
    up = np.concatenate([inputs["L0_ffn_sw1"], inputs["L0_ffn_sw3"]], axis=0)
    a["L0_ffn_weights"] = np.concatenate([experts.reshape(P, -1), by_rows(up, KD).reshape(P, -1),
                                          by_rows(inputs["L0_ffn_sw2"], 4).reshape(P, -1)], axis=1)
    a["L1_ffn_centroids"] = inputs["L1_ffn_centroids"].T
    a["L1_ffn_b2"] = inputs["L1_ffn_b2"]
    a["L1_ffn_columns"] = np.concatenate([inputs[f"L1_ffn_{n}"].reshape(EXPERTS, -1, P) for n in ("ln_g", "ln_b", "b1")],
                                         axis=1).transpose(2, 0, 1)
    a["L1_ffn_weights"] = np.concatenate(
        [inputs[f"L1_ffn_{n}"].reshape(EXPERTS, -1, P, inputs[f"L1_ffn_{n}"].shape[2]).transpose(2, 0, 1, 3)
         .reshape(P, EXPERTS, -1) for n in ("w1", "w2")], axis=2).reshape(P, -1)
    return {n: np.ascontiguousarray(v) for n, v in a.items()}


def kernel(**inputs):
    import numpy as np
    import concourse.bacc as bacc
    from concourse.bass_utils import run_bass_kernel_spmd

    nc = bacc.Bacc("TRN2", target_bir_lowering=False, num_devices=1)
    arrays = {f"in_{n}": v for n, v in lay_out({n: np.asarray(v) for n, v in inputs.items()}).items()}
    places = {n[len("in_"):]: nc.dram_tensor(n, v.shape, mybir.dt.from_np(v.dtype), kind="ExternalInput").ap()
              for n, v in arrays.items()}
    out = nc.dram_tensor("out_x", [TOKENS, DIM], F32, kind="ExternalOutput").ap()
    program(nc, places, out)
    result = run_bass_kernel_spmd(nc, [arrays], core_ids=[0])
    return result.results[0]["out_x"].reshape(BATCH, SEQ, DIM)
```

```python
from contextlib import ExitStack

import concourse.bass as bass
import numpy as np
from concourse import mybir

F32 = mybir.dt.float32
BF16 = mybir.dt.bfloat16
I32 = mybir.dt.int32
U8 = mybir.dt.uint8
ALU = mybir.AluOpType
ACT = mybir.ActivationFunctionType
AX_X = mybir.AxisListType.X

P = 128
BATCH, SEQ, DIM = 8, 256, 256
TOKENS = BATCH * SEQ
TILES = TOKENS // P
TPB = SEQ // P
KD = DIM // P
KEYS = 77
CTX = BATCH * KEYS
EXPERTS = 8
LN_EPS = 1e-5
ROOM = 4608


def wait(eng, sem, value):
    if isinstance(value, int) and value <= 0:
        return
    eng.wait_ge(sem, value)


def wait_apart(eng, sem, value, passed):
    wait(eng, sem, value)
    eng.sem_inc(passed, 1)


def steps(eng, n, body):
    body(0)
    with eng.Fori(1, n - 1) as i:
        body(i)
    body(n - 1)


def is_step(i, n):
    return isinstance(i, int) and i == n


def batches(eng, body):
    body(0, 3)
    body(1, 3)
    with eng.Fori(2, BATCH - 3) as b:
        body(b, 3)
    for left in (2, 1, 0):
        body(BATCH - 1 - left, left)


def nth(ap, i):
    if isinstance(i, int):
        return ap[:, i, :]
    return ap[:, bass.ds(i, 1), :].rearrange("p a d -> p (a d)")


def span(i, width):
    return slice(i * width, (i + 1) * width) if isinstance(i, int) else bass.ds(i * width, width)


class Chip:

    def __init__(self, nc, ctx):
        self.nc, self.ctx = nc, ctx
        sb = self.sb
        self.x = sb("x_res", [P, TILES, DIM], F32)
        self.xnT = sb("xnT", [P, KD, TOKENS], F32)
        self.ident = sb("ident", [P, P], F32)
        self.gate = sb("gate", [P, 8], F32)
        self.powers = sb("powers", [P, 4], F32)
        self.keep = sb("keep", [P, TILES, DIM], F32)
        self.bank = ctx.enter_context(nc.psum_tensor("bank", [P, 8, 512], F32))

        self.ctxT = sb("ctxT", [P, KD, CTX], F32)
        self.room = sb("room", [P, ROOM], F32)
        self.mask = sb("mask", [P, CTX], U8)
        self.logits = Logits(self)
        self.finished = []

    def release(self):
        self.nc.all_engine_barrier()
        self.nc.clear_and_free_semaphores(self.finished)
        self.nc.all_engine_barrier()
        self.finished = []

    def sb(self, name, shape, dt):
        return self.ctx.enter_context(self.nc.sbuf_tensor(name, shape, dt))


class Logits:

    def __init__(self, chip):
        self.chip, self.taken = chip, 0
        self.weights = chip.sb("gate_weights", [P, KD, EXPERTS], F32)
        self.out = chip.bank[:, 0, 0:TILES * EXPERTS]

    def tile(self, pe):
        t, self.taken = self.taken, self.taken + 1
        for k in range(KD):
            last = pe.matmul(self.out[:, t * EXPERTS:(t + 1) * EXPERTS], self.chip.xnT[:, k, t * P:(t + 1) * P],
                             self.weights[:, k, :], start=(k == 0), stop=(k == KD - 1))
        return last

    def some(self, pe, n, norm):
        for _ in range(n):
            pe.wait_ge(norm.copied, self.taken + 1)
            self.tile(pe)

    def rest(self, pe, ready):
        while self.taken < TILES:
            last = self.tile(pe)
        last.then_inc(ready, 1)
        self.taken = 0


class Stage:

    def __init__(self, chip, name, ctx):
        self.chip, self.nc, self.name, self.ctx = chip, chip.nc, name, ctx

    def sb(self, name, shape, dt=F32):
        return self.ctx.enter_context(self.nc.sbuf_tensor(f"{self.name}_{name}", shape, dt))

    def sem(self, name):
        semaphore = self.nc.alloc_semaphore(name=f"{self.name}_{name}")
        self.chip.finished.append(semaphore)
        return semaphore


class LentStage(Stage):

    def __init__(self, chip, name, ctx, areas):
        super().__init__(chip, name, ctx)
        self.areas, self.used = areas, [0] * len(areas)

    def sb(self, name, shape, dt=F32):
        words = int(np.prod(shape[1:])) // (2 if dt == BF16 else 1)
        for n, area in enumerate(self.areas):
            at = self.used[n]
            if at + words <= area.shape[1]:
                self.used[n] += words
                room = area[0:shape[0], at:at + words]
                if dt != F32:
                    room = room.bitcast(dt)
                axes = ["a", "b", "c"][:len(shape) - 1]
                return room.rearrange(f"p ({' '.join(axes)}) -> p {' '.join(axes)}", **dict(zip(axes, shape[1:])))
        return super().sb(name, shape, dt)


class Moments:

    def __init__(self, st, name, depth):
        self.depth = depth
        self.stats = st.sb(f"{name}_stats", [P, depth, 6])
        self.mv = st.sb(f"{name}_mv", [P, depth, 2])
        self.stats_done = st.sem(f"{name}_stats_done")
        self.ready = st.sem(f"{name}_moments_ready")
        self.passed = st.sem(f"{name}_passed")

    def statistics(self, dve, tiles, x):
        for t, u in tiles:
            dve.bn_stats(self.stats[:, u, :], nth(x, t)).then_inc(self.stats_done, 1)
        wait_apart(dve, self.stats_done, tiles[-1][0] + 1, self.passed)
        for t, u in tiles:
            dve.bn_aggr(self.mv[:, u, :], self.stats[:, u, :]).then_inc(self.ready, 1)


class Normed:

    def __init__(self, st, name, moments, again=False):
        self.constants, self.moments, self.again = st.chip.powers, moments, again
        self.shifted = st.sb(f"{name}_shifted", [P, moments.depth])
        self.rstd = st.sb(f"{name}_rstd", [P, moments.depth])
        self.widened = st.sem(f"{name}_widened")
        self.shifted_done = st.sem(f"{name}_shifted_done")
        self.rstd_ready = st.sem(f"{name}_rstd_ready")
        self.normed = st.sem(f"{name}_normed")

    def power(self, pool, t, u, n=1):
        at = slice(u, u + n)
        variance, shifted = self.moments.mv[:, at, 1:2].rearrange("p n a -> p (n a)"), self.shifted[:, at]
        eps_scale, eps, minus_half = (self.constants[:, c:c + 1].to_broadcast([P, n]) for c in (2, 3 if self.again else 1, 0))
        pool.wait_ge(self.moments.ready, t + n)
        if self.again:
            pool.tensor_tensor(shifted, variance, eps_scale, ALU.mult).then_inc(self.widened, n)
            pool.wait_ge(self.widened, t + n)
            variance = shifted
        pool.tensor_tensor(shifted, variance, eps, ALU.add).then_inc(self.shifted_done, n)
        wait(pool, self.normed, t + n - self.moments.depth)
        pool.wait_ge(self.shifted_done, t + n)
        pool.tensor_tensor(self.rstd[:, at], shifted, minus_half, ALU.pow).then_inc(self.rstd_ready, n)

    def apply(self, dve, t, u, rows, out):
        dve.wait_ge(self.rstd_ready, t + 1)
        dve.tensor_scalar(out, rows, self.moments.mv[:, u, 0:1], self.rstd[:, u:u + 1], ALU.subtract,
                          ALU.mult).then_inc(self.normed, 1)


class NextNorm:

    def __init__(self, st, banks, keep=None, keep_again=None, affine=None, share=None, depth=2):
        self.chip, self.banks, self.depth = st.chip, banks, depth
        self.keep, self.keep_again, self.affine, self.share = keep, keep_again, affine, share
        self.xn = st.sb("xn", [P, depth, DIM])
        self.x_updated = st.sem("x_updated")
        self.transposed = st.sem("xn_transposed")
        self.copied = st.sem("xnT_copied")
        self.kept = st.sem("xn_kept")
        self.shared = st.sem("xn_shared")
        self.moments = Moments(st, "ln", depth)
        self.main = Normed(st, "ln", self.moments, again=affine is not None)
        self.twice = Normed(st, "ln2", self.moments, again=True) if keep_again is not None else None

    def vector_stats(self, dve, *tiles):
        wait_apart(dve, self.x_updated, tiles[-1][0] + 1, self.moments.passed)
        self.moments.statistics(dve, tiles, self.chip.x)

    def vector_apply(self, dve, t, u):
        before = t - self.depth + 1
        wait(dve, self.transposed, before)
        if self.keep is not None:
            wait(dve, self.kept, before)
        if self.share is not None:
            wait(dve, self.shared, before)
        self.main.apply(dve, t, u, nth(self.chip.x, t), self.xn[:, u, :])

    def vector_apply_again(self, dve, t, u):
        if self.keep_again is not None:
            self.twice.apply(dve, t, u, nth(self.chip.x, t), nth(self.keep_again, t))
        if self.share is not None:
            dve.wait_ge(self.main.normed, t + 1)
            dve.wait_ge(self.twice.normed, t + 1)
            dve.scalar_tensor_tensor(out=nth(self.chip.x, t), in0=self.xn[:, u, :], scalar=self.share,
                                     in1=nth(self.chip.x, t), op0=ALU.mult, op1=ALU.add).then_inc(self.shared, 1)

    def gpsimd(self, pool, t, u, n=1):
        self.main.power(pool, t, u, n)
        if self.twice is not None:
            self.twice.power(pool, t, u, n)

    def tensor(self, pe, t, u):
        pe.wait_ge(self.main.normed, t + 1)
        wait(pe, self.copied, t - len(self.banks) + 1)
        for k in range(KD):
            last = pe.transpose(self.banks[u % len(self.banks)][:, k * P:(k + 1) * P], self.xn[:, u, k * P:(k + 1) * P],
                                self.chip.ident[:, :])
        last.then_inc(self.transposed, 1)

    def scalar(self, act, t, u):
        if self.keep is not None:
            act.wait_ge(self.main.normed, t + 1)
            act.activation(nth(self.keep, t), self.xn[:, u, :], ACT.Copy).then_inc(self.kept, 1)
        act.wait_ge(self.transposed, t + 1)
        bank = self.banks[u % len(self.banks)]
        if self.affine is None:
            act.activation(self.chip.xnT[:, :, span(t, P)],
                           bank[:, 0:DIM].rearrange("p (k n) -> p k n", k=KD),
                           ACT.Copy).then_inc(self.copied, 1)
        else:
            for k in range(KD):
                last = act.activation(self.chip.xnT[:, k, span(t, P)], bank[:, k * P:(k + 1) * P], ACT.Identity,
                                      scale=self.affine[0][:, k:k + 1], bias=self.affine[1][:, k:k + 1])
            last.then_inc(self.copied, 1)


class AllTiles:

    def __init__(self, norm):
        self.norm, self.per = norm, norm.depth // 2
        self.groups = TILES // self.per

    def group(self, g):
        return [(t, t % self.norm.depth) for t in range(self.per * g, self.per * g + self.per)]

    def vector(self, dve, before=lambda g: None):
        for g in range(self.groups + 1):
            if g < self.groups:
                before(g)
                self.norm.vector_stats(dve, *self.group(g))
            if g > 0:
                for t, u in self.group(g - 1):
                    self.norm.vector_apply(dve, t, u)

    def gpsimd(self, pool):
        for g in range(self.groups):
            self.norm.gpsimd(pool, *self.group(g)[0], self.per)

    def tensor(self, pe, tiles=range(TILES)):
        for t in tiles:
            self.norm.tensor(pe, t, t % self.norm.depth)

    def scalar(self, act, tiles=range(TILES)):
        for t in tiles:
            self.norm.scalar(act, t, t % self.norm.depth)


class Loads:

    def __init__(self, chip, name):
        self.chip, self.at, self.copies = chip, 0, []
        self.loaded = chip.nc.alloc_semaphore(name=f"{name}_loaded")

    def place(self, dram, *shape, parts=P):
        n = int(np.prod(shape))
        room = self.chip.room[0:parts, self.at:self.at + n]
        self.at += n
        assert self.at <= ROOM
        if len(shape) == 2:
            room = room.rearrange("p (k n) -> p k n", k=shape[0])
        if dram is not None:
            self.copy(room, dram)
        return room

    def copy(self, room, dram):
        self.copies.append((room, dram))

    def weights(self, dram):
        return self.place(load_rows(dram), KD, dram.shape[1])

    def sync(self, sp):
        for room, dram in self.copies:
            sp.dma_start(room, dram).then_inc(self.loaded, 16)

    def tensor_keys(self, pe):
        pass

    def tensor_values(self, pe):
        pass

    def scalar_keys(self, act):
        pass

    def vector_values(self, dve):
        pass

    def start(self):
        self.chip.finished.append(self.loaded)
        return len(self.copies)


class Clearing:

    def __init__(self, st, scratch, strips, part=0, parts=1):
        slots = scratch.rows.rearrange("(p r) d -> p (r d)", p=P)
        size = slots.shape[1] // parts
        self.slots = slots[:, part * size:(part + 1) * size]
        self.strips, self.width = strips, size // strips
        self.zeros = st.sb("empty_rows", [P, self.width])
        self.zeros_ready, self.cleared = st.sem("zeros_ready"), st.sem("cleared")

    def vector(self, dve):
        dve.memset(self.zeros[:, :], 0.0).then_inc(self.zeros_ready, 1)

    def sync(self, sp, n):
        sp.wait_ge(self.zeros_ready, 1)
        sp.dma_start(self.slots[:, span(n, self.width)], self.zeros[:, :]).then_inc(self.cleared, 16)

    def finish(self, sp):
        sp.wait_ge(self.cleared, 16 * self.strips)


def load_rows(w):
    return w.rearrange("(k p) n -> p k n", p=P)


def begin(chip, a, ahead):
    nc = chip.nc
    with ExitStack() as ctx:
        st = Stage(chip, "begin", ctx)
        norm = NextNorm(st, [chip.bank[:, n, :] for n in (6, 7)], depth=8)
        tiles = AllTiles(norm)
        per = tiles.per
        halves = range(TILES // 2), range(TILES // 2, TILES)
        raw_gate = st.sb("raw_gate", [P, 8])
        x_loaded = [st.sem(f"x_loaded{u}") for u in range(TILES // per)]
        small_loaded = st.sem("small_loaded")
        context_loaded = st.sem("context_loaded")
        gate_ready = st.sem("gate_ready")
        powers_ready = st.sem("powers_ready")
        block = ctx.enter_context(nc.Block())
        x_rows = a["x"].rearrange("(t p) d -> p t d", p=P)

        @block.sync
        def _(sp):
            for u in range(TILES // per):
                sp.dma_start(chip.x[:, u * per:(u + 1) * per, :],
                             x_rows[:, u * per:(u + 1) * per, :]).then_inc(x_loaded[u], 16)
            sp.dma_start(chip.ident[:, :], a["ident"]).then_inc(small_loaded, 16)
            for n, g in enumerate((a["g_xattn"], a["g_ffn"])):
                sp.dma_start(raw_gate[:, 4 * n:4 * n + 4], g.partition_broadcast(P)).then_inc(small_loaded, 16)
            sp.dma_start(chip.ctxT[:, :, :], load_rows(a["ctxT"])).then_inc(context_loaded, 16)
            ahead.sync(sp)

        @block.vector
        def _(dve):
            for n, value in enumerate((-0.5, LN_EPS, 1 + LN_EPS, LN_EPS ** 2)):
                dve.memset(chip.powers[:, n:n + 1], value).then_inc(powers_ready, 1)

            def arrived(g):
                dve.wait_ge(x_loaded[g], 16)
                dve.sem_inc(norm.x_updated, per)
            tiles.vector(dve, arrived)
            ahead.vector_values(dve)

        @block.gpsimd
        def _(pool):
            pool.wait_ge(powers_ready, 4)
            pool.wait_ge(small_loaded, 48)

            tiles.gpsimd(pool)

        @block.tensor
        def _(pe):
            pe.wait_ge(small_loaded, 48)
            tiles.tensor(pe, halves[0])
            pe.wait_ge(context_loaded, 16)
            ahead.tensor_keys(pe)
            tiles.tensor(pe, halves[1])
            ahead.tensor_values(pe)

        @block.scalar
        def _(act):
            act.wait_ge(small_loaded, 48)
            act.activation(chip.gate[:, :], raw_gate[:, :], ACT.Tanh).then_inc(gate_ready, 1)
            tiles.scalar(act, halves[0])
            ahead.scalar_keys(act)
            tiles.scalar(act, halves[1])


class ContextOfOneHead(Loads):

    HALF = CTX // 2

    def __init__(self, chip, a, ctx):
        super().__init__(chip, "l0x")
        pre = "L0_xattn_"
        self.w = {n: self.weights(a[pre + n]) for n in ("Wk", "Wv", "Wq")}
        self.bias = {n: self.place(a[pre + n], KD) for n in ("bq", "bk")}
        self.bv = self.place(a[pre + "bv"].partition_broadcast(KEYS), DIM, parts=KEYS)
        self.copy(chip.logits.weights[:, :, :], load_rows(a["L0_ffn_gate_w"]))
        st = Stage(chip, "l0kv", ctx)
        self.kT, self.v = st.sb("kT", [P, KD, CTX]), st.sb("v", [KEYS, BATCH, DIM])
        self.kT_projected, self.kT_ready = st.sem("kT_projected"), st.sem("kT_ready")
        self.v_projected, self.v_ready = st.sem("v_projected"), st.sem("v_ready")
        self.groups = [(m, h) for m in range(KD) for h in range(2)]
        self.k_bank, self.v_bank = [chip.bank[:, n, :] for n in range(4)], [chip.bank[:, n, :] for n in (4, 5)]

    def ready(self, eng):
        eng.wait_ge(self.loaded, 16 * len(self.copies))

    def tensor_keys(self, pe):
        self.ready(pe)
        for m, h in self.groups:
            for k in range(KD):
                last = pe.matmul(self.k_bank[2 * m + h][:, 0:self.HALF], self.w["Wk"][:, k, m * P:(m + 1) * P],
                                 self.chip.ctxT[:, k, h * self.HALF:(h + 1) * self.HALF], start=(k == 0), stop=(k == KD - 1))
            last.then_inc(self.kT_projected, 1)

    def tensor_values(self, pe):
        for b in range(BATCH):
            wait(pe, self.v_ready, b - 1)
            for k in range(KD):
                last = pe.matmul(self.v_bank[b % 2][0:KEYS, 0:DIM], self.chip.ctxT[:, k, b * KEYS:(b + 1) * KEYS],
                                 self.w["Wv"][:, k, :], start=(k == 0), stop=(k == KD - 1))
            last.then_inc(self.v_projected, 1)

    def scalar_keys(self, act):
        self.ready(act)
        for m, h in self.groups:
            act.wait_ge(self.kT_projected, 2 * m + h + 1)
            act.activation(self.kT[:, m, h * self.HALF:(h + 1) * self.HALF], self.k_bank[2 * m + h][:, 0:self.HALF],
                           ACT.Identity, bias=self.bias["bk"][:, m:m + 1]).then_inc(self.kT_ready, 1)

    def vector_values(self, dve):
        self.ready(dve)
        for b in range(BATCH):
            dve.wait_ge(self.v_projected, b + 1)
            dve.tensor_tensor(self.v[:, b, :], self.v_bank[b % 2][0:KEYS, 0:DIM], self.bv[:, :],
                              ALU.add).then_inc(self.v_ready, 1)


def single_head_attention(chip, given, feed):
    nc = chip.nc
    with ExitStack() as ctx:
        st = Stage(chip, "l0x", ctx)
        bank = chip.bank
        s_bank = [bank[:, 0, :], bank[:, 1, :]]
        p_bank = [bank[:, 2, :], bank[:, 3, :]]
        o_bank = [bank[:, 4, :], bank[:, 5, :]]
        q_bank = bank[:, 6, :]
        norm = NextNorm(st, [bank[:, 7, :]], keep=chip.keep)
        clearing = Clearing(st, chip.scratch[0], feed.chunks, 0, 2)
        w, bias, kT, v = given.w, given.bias, given.kT, given.v
        qT = st.sb("qT", [P, KD, SEQ])
        probs = st.sb("probs", [P, TPB, KEYS])
        probsT = st.sb("probsT", [KEYS, TPB, P])
        neg_max = st.sb("neg_max", [P, TPB])
        total = st.sb("total", [P, TPB])
        scale = st.sb("scale", [P, TPB])
        loaded, loads = given.loaded, given.start()
        q_projected = st.sem("q_projected")
        q_ready = st.sem("q_ready")
        scores_ready = st.sem("scores_ready")
        max_ready = st.sem("max_ready")
        probs_ready = st.sem("probs_ready")
        probs_transposed = st.sem("probs_transposed")
        probsT_ready = st.sem("probsT_ready")
        attended = st.sem("attended")
        inverse_done = st.sem("inverse_done")
        scale_ready = st.sem("scale_ready")
        block = ctx.enter_context(nc.Block())

        @block.sync
        def _(sp):
            def chunk(i, u):
                feed.sync(sp, i, u)
                clearing.sync(sp, 2 * i + u)
            pairs(sp, feed.chunks, chunk)
            clearing.finish(sp)

        @block.tensor
        def _(pe):
            pe.wait_ge(loaded, 16 * loads)
            def project_q(b):
                for m in range(KD):
                    for k in range(KD):
                        last = pe.matmul(q_bank[:, m * SEQ:(m + 1) * SEQ], w["Wq"][:, k, m * P:(m + 1) * P],
                                         chip.xnT[:, k, span(b, SEQ)], start=(k == 0), stop=(k == KD - 1))
                last.then_inc(q_projected, 1)

            def scores(b):
                pe.wait_ge(q_ready, KD * b + KD)
                for u in range(TPB):
                    wait(pe, probs_ready, TPB * b + u - 1)
                    for m in range(KD):
                        last = pe.matmul(s_bank[u][:, 0:KEYS], qT[:, m, u * P:(u + 1) * P],
                                         kT[:, m, span(b, KEYS)], start=(m == 0), stop=(m == KD - 1))
                    last.then_inc(scores_ready, 1)

            project_q(0)
            pe.wait_ge(given.kT_ready, 2 * KD)
            pe.wait_ge(given.v_ready, BATCH)
            scores(0)
            project_q(1)

            def batch(b, ahead):
                for u in range(TPB):
                    pe.wait_ge(probs_ready, TPB * b + u + 1)
                    wait(pe, probsT_ready, TPB * b + u - 1)
                    pe.transpose(p_bank[u][0:KEYS, 0:P], probs[:, u, :],
                                 chip.ident[:, :]).then_inc(probs_transposed, 1)
                if ahead >= 1:
                    scores(b + 1)
                else:
                    chip.logits.some(pe, 4, norm)
                for u in range(TPB):
                    pe.wait_ge(probsT_ready, TPB * b + u + 1)
                    wait(pe, norm.x_updated, TPB * b + u - 1)
                    pe.matmul(o_bank[u][:, 0:DIM], probsT[:, u, :],
                              v[:, span(b, 1), :].rearrange("p a d -> p (a d)"),
                              start=True, stop=True).then_inc(attended, 1)
                if not is_step(b, 0):
                    for u in range(TPB):
                        norm.tensor(pe, TPB * b + u - TPB, u)
                if ahead >= 2:
                    project_q(b + 2)

            batches(pe, batch)
            for u in range(TPB):
                chip.logits.some(pe, 4, norm)
                norm.tensor(pe, TILES - TPB + u, u)

        @block.scalar
        def _(act):
            act.wait_ge(loaded, 16 * loads)
            def copy_q(b):
                act.wait_ge(q_projected, b + 1)
                wait(act, scores_ready, TPB * b)
                for m in range(KD):
                    act.activation(qT[:, m, :], q_bank[:, m * SEQ:(m + 1) * SEQ], ACT.Identity,
                                   bias=bias["bq"][:, m:m + 1]).then_inc(q_ready, 1)

            def exponents(b):
                for u in range(TPB):
                    act.wait_ge(max_ready, TPB * b + u + 1)
                    wait(act, probs_transposed, TPB * b + u - 1)
                    wait(act, scale_ready, TPB * b + u - 1)
                    act.activation(probs[:, u, :], s_bank[u][:, 0:KEYS], ACT.Exp, bias=neg_max[:, u:u + 1],
                                   accum_out=total[:, u:u + 1]).then_inc(probs_ready, 1)

            copy_q(0)
            exponents(0)
            copy_q(1)

            def batch(b, ahead):
                if ahead >= 1:
                    exponents(b + 1)
                if not is_step(b, 0):
                    for u in range(TPB):
                        norm.scalar(act, TPB * b + u - TPB, u)
                for u in range(2):
                    feed.high(act, b, u)
                if ahead >= 2:
                    copy_q(b + 2)

            batches(act, batch)
            for u in range(TPB):
                norm.scalar(act, TILES - TPB + u, u)

        @block.vector
        def _(dve):
            clearing.vector(dve)
            dve.wait_ge(loaded, 16 * loads)
            def maxima(b):
                for u in range(TPB):
                    dve.wait_ge(scores_ready, TPB * b + u + 1)
                    dve.tensor_reduce(neg_max[:, u:u + 1], s_bank[u][:, 0:KEYS], AX_X, ALU.max,
                                      negate=True).then_inc(max_ready, 1)

            maxima(0)

            def batch(b, ahead):
                for u in range(TPB):
                    dve.wait_ge(probs_transposed, TPB * b + u + 1)
                    wait(dve, attended, TPB * b + u - 1)
                    dve.tensor_copy(probsT[:, u, :], p_bank[u][0:KEYS, 0:P]).then_inc(probsT_ready, 1)
                for u in range(TPB):
                    t = TPB * b + u
                    dve.wait_ge(probs_ready, t + 1)
                    dve.reciprocal(scale[:, u:u + 1], total[:, u:u + 1]).then_inc(inverse_done, 1)
                    dve.wait_ge(inverse_done, t + 1)
                    dve.tensor_scalar(scale[:, u:u + 1], scale[:, u:u + 1], chip.gate[:, 0:1], None,
                                      ALU.mult).then_inc(scale_ready, 1)
                if ahead >= 1:
                    maxima(b + 1)
                for u in range(TPB):
                    t = TPB * b + u
                    dve.wait_ge(attended, t + 1)
                    dve.wait_ge(scale_ready, t + 1)
                    dve.scalar_tensor_tensor(out=nth(chip.x, t), in0=o_bank[u][:, 0:DIM], scalar=scale[:, u:u + 1],
                                             in1=nth(chip.x, t), op0=ALU.mult, op1=ALU.add).then_inc(norm.x_updated, 1)
                norm.vector_stats(dve, *((TPB * b + u, u) for u in range(TPB)))
                for u in range(TPB):
                    norm.vector_apply(dve, TPB * b + u, u)

            batches(dve, batch)

        @block.gpsimd
        def _(pool):
            def batch(b, ahead):
                for u in range(TPB):
                    norm.gpsimd(pool, TPB * b + u, u)
                for u in range(2):
                    feed.low(pool, b, u)
            batches(pool, batch)


HEADS, HEAD = 16, 16
CHUNK_HEADS = P // HEAD
GROUP = 4
GROUPS = HEADS // GROUP
BIAS_STEPS = 9


def multi_head_loads(chip, a, layer):
    loads = Loads(chip, f"l{layer}x")
    pre = f"L{layer}_xattn_"
    loads.key_bias = layer == 1
    loads.w = {n: loads.weights(a[pre + n]) for n in ("Wk", "Wv", "Wq", "Wo")}
    loads.head_of = loads.place(a["head_of"], CHUNK_HEADS)
    if loads.key_bias:
        loads.bias = loads.place(a["key_bias"].partition_broadcast(P), CTX)
    else:
        loads.bq, loads.bk = loads.place(a[pre + "bq"], KD), loads.place(a[pre + "bk"], KD)
        loads.bv = loads.place(a[pre + "bv"].partition_broadcast(KEYS), DIM, parts=KEYS)
        loads.bo = loads.place(a[pre + "bp"].partition_broadcast(P), DIM)
    loads.copy(chip.logits.weights[:, :, :], load_rows(a["L1_ffn_centroids" if layer == 1 else "L3_ffn_Wg"]))
    return loads


def multi_head_attention(chip, given, layer, gate, norm_args, feed, clear=None, areas=()):
    nc = chip.nc
    key_bias = given.key_bias
    with ExitStack() as ctx:
        st = LentStage(chip, f"l{layer}x", ctx, areas)
        bank = chip.bank
        s_bank = [bank[:, 0, :], bank[:, 1, :]]
        p_bank = [bank[:, 2, :], bank[:, 3, :]]
        o_bank, q_bank, y_bank, n_bank = (bank[:, n, :] for n in (4, 5, 6, 7))
        norm = NextNorm(st, [n_bank], **norm_args(st))
        clearing = Clearing(st, clear, 16) if clear is not None else None
        w, head_of, ctxT = given.w, given.head_of, chip.ctxT
        kT = st.sb("kT", [P, KD, CTX])
        k_diag = st.sb("k_diag", [P, 2, KD * CHUNK_HEADS * KEYS])
        v1 = st.sb("v1", [KEYS, BATCH, HEADS, HEAD + 1])
        v_parts = [st.sb(f"v_{n}", [KEYS, BATCH, HEADS * (HEAD + 1)], BF16) for n in ("high", "low")]
        v_now = [st.sb(f"v_{n}_now", [KEYS, HEADS * (HEAD + 1)], BF16) for n in ("high", "low")]
        v_high_ready, v_split = st.sem("v_high_ready"), st.sem("v_split")
        zeros = st.sb("zeros", [KEYS, HEADS * (HEAD + 1)], BF16)
        v_placed = st.sem("v_placed")
        qT = st.sb("qT", [P, KD, SEQ])
        raw = st.sb("scores", [P, TPB, HEADS * KEYS])
        probs = st.sb("probs", [P, TPB, HEADS * KEYS])
        probsT = [st.sb(f"probsT_{n}", [KEYS, HEADS * P], BF16) for n in ("high", "low")]
        row_max = st.sb("row_max", [P, TPB, HEADS])
        inverse = st.sb("inverse", [P, HEADS])
        mixed = st.sb("mixed", [P, DIM])
        mixedT = st.sb("mixedT", [P, KD, P])
        if key_bias:
            bias = given.bias
            bias_parts = [st.sb(f"bias_{n}", [P, CTX], BF16) for n in ("high", "mid")]
            bias_rows = st.sb("bias_rows", [P, CTX], BF16)
            ones = st.sb("ones", [P, P], BF16)
        else:
            bq, bk, bv, bo = given.bq, given.bk, given.bv, given.bo
        loaded, loads = given.loaded, given.start()
        kT_projected = st.sem("kT_projected")
        kT_ready = st.sem("kT_ready")
        v_projected = st.sem("v_projected")
        v_ready = st.sem("v_ready")
        ones_ready = st.sem("ones_ready")
        bias_ready = st.sem("bias_ready")
        k_diag_ready = st.sem("k_diag_ready")
        q_projected = st.sem("q_projected")
        q_ready = st.sem("q_ready")
        scores_ready = st.sem("scores_ready")
        scores_copied = st.sem("scores_copied")
        max_ready = st.sem("max_ready")
        shifted = st.sem("shifted")
        probs_ready = st.sem("probs_ready")
        probs_transposed = st.sem("probs_transposed")
        high_copied = st.sem("probsT_high_copied")
        low_copied = st.sem("probsT_low_copied")
        attended = st.sem("attended")
        inverse_done = st.sem("inverse_done")
        mixed_ready = st.sem("mixed_ready")
        mixed_transposed = st.sem("mixed_transposed")
        mixedT_ready = st.sem("mixedT_ready")
        out_ready = st.sem("out_ready")
        x_biased = st.sem("x_biased")
        halves = CTX // 2
        width = GROUP * KEYS
        block = ctx.enter_context(nc.Block())

        @block.sync
        def _(sp):
            if clearing is not None:
                for n in range(clearing.strips):
                    clearing.sync(sp, n)
            feed.sync_all(sp)
            if clearing is not None:
                clearing.finish(sp)

        @block.tensor
        def _(pe):
            pe.wait_ge(loaded, 16 * loads)
            for m in range(KD):
                for h in range(2):
                    for k in range(KD):
                        last = pe.matmul(bank[:, 2 * m + h, 0:halves], w["Wk"][:, k, m * P:(m + 1) * P],
                                         ctxT[:, k, h * halves:(h + 1) * halves], start=(k == 0), stop=(k == KD - 1))
                    last.then_inc(kT_projected, 1)

            def project_q(b):
                for m in range(KD):
                    for k in range(KD):
                        last = pe.matmul(q_bank[:, m * SEQ:(m + 1) * SEQ], w["Wq"][:, k, m * P:(m + 1) * P],
                                         chip.xnT[:, k, span(b, SEQ)], start=(k == 0), stop=(k == KD - 1))
                last.then_inc(q_projected, 1)

            project_q(0)
            v_bank = [o_bank, y_bank]

            def project_v(batches_of):
                for b in batches_of:
                    wait(pe, v_ready, b - 1)
                    for k in range(KD):
                        last = pe.matmul(v_bank[b % 2][0:KEYS, 0:DIM], ctxT[:, k, b * KEYS:(b + 1) * KEYS],
                                         w["Wv"][:, k, :], start=(k == 0), stop=(k == KD - 1))
                    last.then_inc(v_projected, 1)

            project_v(range(BATCH // 2))

            def scores(b, u, slot, groups=range(GROUPS)):
                t = TPB * b + u
                pe.wait_ge(q_ready, KD * b + KD)
                pe.wait_ge(k_diag_ready, KD * b + KD)
                for g in groups:
                    wait(pe, scores_copied, GROUPS * t + g - 1)
                    c = g // 2
                    at = (c * CHUNK_HEADS + (g % 2) * GROUP) * KEYS
                    keys = (k_diag[:, slot, at:at + width] if isinstance(slot, int) else
                            k_diag[:, bass.ds(slot, 1), at:at + width].rearrange("p a n -> p (a n)"))
                    last = pe.matmul(s_bank[g % 2][:, 0:width], qT[:, c, u * P:(u + 1) * P], keys,
                                     start=True, stop=not key_bias)
                    if key_bias:
                        last = pe.matmul(s_bank[g % 2][:, 0:width], ones[:, :],
                                         bias_rows[:, span(b, KEYS)].unsqueeze(1).to_broadcast([P, GROUP, KEYS]),
                                         start=False, stop=True)
                    last.then_inc(scores_ready, 1)

            def transpose_probs(t, u, g):
                wait(pe, low_copied, GROUPS * t + g - 1)
                for h in range(GROUP):
                    at = (g * GROUP + h) * KEYS
                    last = pe.transpose(p_bank[g % 2][0:KEYS, h * P:(h + 1) * P],
                                        probs[:, u, at:at + KEYS], chip.ident[:, :])
                last.then_inc(probs_transposed, 1)

            def attend(b, t):
                wait(pe, mixed_ready, t)
                pe.wait_ge(v_placed, 2 * b + 2)
                for g in range(GROUPS):
                    pe.wait_ge(low_copied, GROUPS * t + g + 1)
                    for h in range(g * GROUP, (g + 1) * GROUP):
                        at = slice(h * (HEAD + 1), (h + 1) * (HEAD + 1))
                        for n, (left, right) in enumerate(((0, 0), (1, 0), (0, 1))):
                            last = pe.matmul(o_bank[:, at], probsT[left][:, h * P:(h + 1) * P], v_now[right][:, at],
                                             start=(n == 0), stop=(n == 2))
                last.then_inc(attended, 1)

            def transpose_mixed(t):
                pe.wait_ge(mixed_ready, t + 1)
                wait(pe, norm.copied, t - 1)
                for k in range(KD):
                    last = pe.transpose(n_bank[:, k * P:(k + 1) * P], mixed[:, k * P:(k + 1) * P],
                                        chip.ident[:, :])
                last.then_inc(mixed_transposed, 1)

            def project_out(t):
                pe.wait_ge(mixedT_ready, t + 1)
                wait(pe, norm.x_updated, t)
                for k in range(KD):
                    last = pe.matmul(y_bank[:, 0:DIM], mixedT[:, k, :], w["Wo"][:, k, :],
                                     start=(k == 0), stop=(k == KD - 1))
                last.then_inc(out_ready, 1)

            if key_bias:
                pe.wait_ge(bias_ready, BIAS_STEPS)
            for u in range(TPB):
                scores(0, u, 0)
            pe.wait_ge(q_ready, KD)
            project_q(1)
            project_v(range(BATCH // 2, BATCH))
            pe.wait_ge(v_ready, BATCH)

            def batch(b, ahead):
                for u in range(TPB):
                    t = TPB * b + u
                    first = is_step(t, 0)
                    pe.wait_ge(probs_ready, t + 1)
                    for half in range(2):
                        groups = (2 * half, 2 * half + 1)
                        for g in groups:
                            transpose_probs(t, u, g)
                        if half == 1 and not first:
                            project_out(t - 1)
                        if ahead >= 1:
                            scores(b + 1, u, (b + 1) % 2, groups)
                        else:
                            pe.wait_ge(scores_copied, GROUPS * TILES)
                            chip.logits.some(pe, 2, norm)
                        if half == 0 and not first:
                            transpose_mixed(t - 1)
                    if u == 1 and ahead >= 2:
                        project_q(b + 2)
                    attend(b, t)
                    if not is_step(b, 0):
                        norm.tensor(pe, t - 2, u)

            batches(pe, batch)
            chip.logits.some(pe, 1, norm)
            transpose_mixed(TILES - 1)
            chip.logits.some(pe, 1, norm)
            project_out(TILES - 1)
            norm.tensor(pe, TILES - 2, 0)
            chip.logits.some(pe, 4, norm)
            norm.tensor(pe, TILES - 1, 1)

        @block.scalar
        def _(act):
            act.wait_ge(loaded, 16 * loads)
            for m in range(KD):
                for h in range(2):
                    act.wait_ge(kT_projected, 2 * m + h + 1)
                    act.activation(kT[:, m, h * halves:(h + 1) * halves], bank[:, 2 * m + h, 0:halves],
                                   ACT.Identity, bias=0.0 if key_bias else bk[:, m:m + 1]).then_inc(kT_ready, 1)

            def copy_q(b):
                act.wait_ge(q_projected, b + 1)
                wait(act, scores_ready, GROUPS * TPB * b)
                for m in range(KD):
                    act.activation(qT[:, m, :], q_bank[:, m * SEQ:(m + 1) * SEQ], ACT.Identity,
                                   bias=0.0 if key_bias else bq[:, m:m + 1]).then_inc(q_ready, 1)

            def copy_scores(t, u, groups=range(GROUPS)):
                wait(act, shifted, t - 1)
                for g in groups:
                    act.wait_ge(scores_ready, GROUPS * t + g + 1)
                    act.activation(raw[:, u, g * width:(g + 1) * width], s_bank[g % 2][:, 0:width],
                                   ACT.Copy).then_inc(scores_copied, 1)

            def exponents(t, u):
                act.wait_ge(shifted, t + 1)
                act.activation(probs[:, u, :], probs[:, u, :], ACT.Exp,
                               scale=HEAD ** -0.5).then_inc(probs_ready, 1)

            def high_probsT(t, g):
                act.wait_ge(probs_transposed, GROUPS * t + g + 1)
                wait(act, attended, t)
                act.activation(probsT[0][:, g * GROUP * P:(g + 1) * GROUP * P], p_bank[g % 2][0:KEYS, 0:GROUP * P],
                               ACT.Copy).then_inc(high_copied, 1)

            def copy_mixedT(t):
                act.wait_ge(mixed_transposed, t + 1)
                wait(act, out_ready, t)
                act.activation(mixedT[:, :, :], n_bank[:, 0:DIM].rearrange("p (k n) -> p k n", k=KD),
                               ACT.Copy).then_inc(mixedT_ready, 1)

            copy_q(0)
            for u in range(TPB):
                copy_scores(u, u)
            copy_q(1)
            exponents(0, 0)
            act.wait_ge(v_ready, BATCH)
            act.wait_ge(ones_ready, 2)
            act.activation(v_parts[0][:, :, :], v1[:, :, :, :].rearrange("p b h d -> p b (h d)"),
                           ACT.Copy).then_inc(v_high_ready, 1)

            def batch(b, ahead):
                for u in range(TPB):
                    t = TPB * b + u
                    for half in range(2):
                        groups = (2 * half, 2 * half + 1)
                        for g in groups:
                            high_probsT(t, g)
                        if ahead >= 1:
                            copy_scores(t + TPB, u, groups)
                        if half == 0 and not is_step(t, 0):
                            copy_mixedT(t - 1)
                    if ahead >= 1 or u == 0:
                        exponents(t + 1, 1 - u)
                    if u == 1 and ahead >= 2:
                        copy_q(b + 2)
                    feed.high(act, b, u)
                    if not is_step(b, 0):
                        norm.scalar(act, t - 2, u)

            batches(act, batch)
            copy_mixedT(TILES - 1)
            for u in range(TPB):
                norm.scalar(act, TILES - TPB + u, u)

        @block.vector
        def _(dve):
            if clearing is not None:
                clearing.vector(dve)
            dve.memset(v1[:, :, :, HEAD:HEAD + 1].rearrange("p b h d -> p (b h) d"), 1.0).then_inc(ones_ready, 1)
            dve.wait_ge(loaded, 16 * loads)
            dve.memset(zeros[:, :], 0.0).then_inc(ones_ready, 1)
            dve.wait_ge(ones_ready, 2)
            if key_bias:
                high, mid = bias_parts
                chain = Chain(dve, bias_ready)
                chain(dve.memset(ones[:, :], 1.0))
                chain(dve.memset(bias_rows[:, :], 0.0))
                chain(dve.tensor_scalar(bias, bias, HEAD ** 0.5, None, ALU.mult))
                chain(dve.tensor_copy(high[:, :], bias))
                chain(dve.tensor_copy(bias_rows[0:1, :], high[0:1, :]))
                chain(dve.tensor_tensor(bias, bias, high[:, :], ALU.subtract))
                chain(dve.tensor_copy(mid[:, :], bias))
                chain(dve.tensor_copy(bias_rows[32:33, :], mid[32:33, :]))
                chain(dve.tensor_tensor(bias_rows[64:65, :], bias[64:65, :], mid[64:65, :], ALU.subtract))
            else:
                dve.tensor_scalar(bo[:, :], bo[:, :], chip.gate[:, gate:gate + 1], None,
                                  ALU.mult).then_inc(bias_ready, 1)
            def copy_v(batches_of):
                for b in batches_of:
                    dve.wait_ge(v_projected, b + 1)
                    source = (o_bank if b % 2 == 0 else y_bank)[0:KEYS, 0:DIM].rearrange("p (h d) -> p h d", h=HEADS)
                    if key_bias:
                        dve.tensor_copy(v1[:, b, :, 0:HEAD], source).then_inc(v_ready, 1)
                    else:
                        dve.tensor_tensor(v1[:, b, :, 0:HEAD], source, bv[:, :].rearrange("p (h d) -> p h d", h=HEADS),
                                          ALU.add).then_inc(v_ready, 1)

            def maxima(t, u):
                wait(dve, shifted, t - 1)
                dve.wait_ge(scores_copied, GROUPS * t + GROUPS)
                dve.tensor_reduce(row_max[:, u, :], raw[:, u, :].rearrange("p (h k) -> p h k", h=HEADS),
                                  AX_X, ALU.max).then_inc(max_ready, 1)

            def low_probsT(t, g):
                dve.wait_ge(high_copied, GROUPS * t + g + 1)
                at = slice(g * GROUP * P, (g + 1) * GROUP * P)
                dve.tensor_tensor(probsT[1][:, at], p_bank[g % 2][0:KEYS, 0:GROUP * P], probsT[0][:, at],
                                  ALU.subtract).then_inc(low_copied, 1)

            def update_x(t, u):
                dve.wait_ge(out_ready, t + 1)
                if not key_bias:
                    dve.wait_ge(x_biased, t + 1)
                dve.scalar_tensor_tensor(out=nth(chip.x, t), in0=y_bank[:, 0:DIM], scalar=chip.gate[:, gate:gate + 1],
                                         in1=nth(chip.x, t), op0=ALU.mult, op1=ALU.add).then_inc(norm.x_updated, 1)
                norm.vector_stats(dve, (t, u))

            def normalise(t):
                attended_of = o_bank[:, 0:HEADS * (HEAD + 1)].rearrange("p (h d) -> p h d", h=HEADS)
                dve.wait_ge(attended, t + 1)
                dve.reciprocal(inverse[:, :], attended_of[:, :, HEAD:HEAD + 1].rearrange("p h d -> p (h d)")
                               ).then_inc(inverse_done, 1)
                dve.wait_ge(inverse_done, t + 1)
                wait(dve, mixed_transposed, t)
                dve.tensor_tensor(mixed[:, :].rearrange("p (h d) -> p h d", h=HEADS), attended_of[:, :, 0:HEAD],
                                  inverse[:, :].unsqueeze(2).to_broadcast([P, HEADS, HEAD]),
                                  ALU.mult).then_inc(mixed_ready, 1)

            copy_v(range(BATCH // 2))
            for u in range(TPB):
                maxima(u, u)
            copy_v(range(BATCH // 2, BATCH))
            dve.wait_ge(v_high_ready, 1)
            dve.wait_ge(v_ready, BATCH)
            dve.tensor_tensor(v_parts[1][:, :, :], v1[:, :, :, :].rearrange("p b h d -> p b (h d)"), v_parts[0][:, :, :],
                              ALU.subtract).then_inc(v_split, 1)

            def batch(b, ahead):
                for u in range(TPB):
                    t = TPB * b + u
                    for half in range(2):
                        groups = (2 * half, 2 * half + 1)
                        for g in groups:
                            low_probsT(t, g)
                        if half == 0 and not is_step(t, 0) and (ahead >= 1 or u == 0):
                            maxima(t + 1, 1 - u)
                        if half == 1 and not is_step(t, 0):
                            update_x(t - 1, 1 - u)
                    normalise(t)
                    if not is_step(t, 0):
                        norm.vector_apply(dve, t - 1, 1 - u)
                    if not is_step(t, 0):
                        norm.vector_apply_again(dve, t - 1, 1 - u)

            batches(dve, batch)
            update_x(TILES - 1, 1)
            norm.vector_apply(dve, TILES - 1, 1)
            norm.vector_apply_again(dve, TILES - 1, 1)

        @block.gpsimd
        def _(pool):
            pool.wait_ge(loaded, 16 * loads)
            if not key_bias:
                pool.wait_ge(bias_ready, 1)

            def spread_keys(b, slot):
                wait(pool, scores_ready, GROUPS * TPB * (b - 1))
                for c in range(KD):
                    at = c * CHUNK_HEADS * KEYS
                    out = (k_diag[:, slot, at:at + CHUNK_HEADS * KEYS] if isinstance(slot, int) else
                           k_diag[:, bass.ds(slot, 1), at:at + CHUNK_HEADS * KEYS].rearrange("p a n -> p (a n)"))
                    pool.tensor_tensor(out.rearrange("p (h k) -> p h k", h=CHUNK_HEADS),
                                       kT[:, c, span(b, KEYS)].unsqueeze(1).to_broadcast([P, CHUNK_HEADS, KEYS]),
                                       head_of[:, :].unsqueeze(2).to_broadcast([P, CHUNK_HEADS, KEYS]),
                                       ALU.mult).then_inc(k_diag_ready, 1)

            def shift(t, u):
                pool.wait_ge(max_ready, t + 1)
                wait(pool, probs_transposed, GROUPS * (t - 1))
                pool.tensor_tensor(probs[:, u, :].rearrange("p (h k) -> p h k", h=HEADS),
                                   raw[:, u, :].rearrange("p (h k) -> p h k", h=HEADS), row_max[:, u, :].unsqueeze(2).to_broadcast([P, HEADS, KEYS]),
                                   ALU.subtract).then_inc(shifted, 1)

            def place_values(b):
                wait(pool, attended, TPB * b)
                for part, now in zip(v_parts, v_now):
                    pool.tensor_tensor(now[:, :], nth(part, b), zeros[:, :], ALU.add).then_inc(v_placed, 1)

            pool.wait_ge(kT_ready, 2 * KD)
            spread_keys(0, 0)
            for u in range(TPB):
                shift(u, u)
            spread_keys(1, 1)
            pool.wait_ge(v_split, 1)

            def batch(b, ahead):
                for u in range(TPB):
                    t = TPB * b + u
                    if u == 0:
                        place_values(b)
                    if not key_bias:
                        pool.tensor_tensor(nth(chip.x, t), nth(chip.x, t), bo[:, :], ALU.add).then_inc(x_biased, 1)
                    if not is_step(t, 0) and (ahead >= 1 or u == 0):
                        shift(t + 1, 1 - u)
                    if not is_step(t, 0):
                        norm.gpsimd(pool, t - 1, 1 - u)
                    if u == 0 and ahead >= 2:
                        spread_keys(b + 2, b % 2)
                    feed.low(pool, b, u)

            batches(pool, batch)
            norm.gpsimd(pool, TILES - 1, 1)


L2_HEADS, L2_HEAD = 4, 64
L2_KEYS = KEYS + SEQ
MASKED = -1e30
RMS_EPS = 1e-8
V_SLOTS = 4


def latent_loads(chip, a):
    loads = Loads(chip, "l2x")
    pre = "L2_xattn_"
    loads.context = loads.place(a["context"].rearrange("(b k) d -> k b d", b=BATCH), BATCH, DIM, parts=KEYS)
    loads.context_g, loads.context_b = loads.place(a[pre + "ln_x_g"], KD), loads.place(a[pre + "ln_x_b"], KD)
    loads.b_out = loads.place(a[pre + "b_out"].partition_broadcast(P), DIM)
    loads.w_kv, loads.w_q, loads.w_out = (loads.weights(a[pre + n]) for n in ("W_kv", "W_q", "W_out"))
    loads.gammas = loads.place(None, 2)
    for n, g in enumerate(("q_gamma", "k_gamma")):
        for r in range(0, P, L2_HEAD):
            loads.copy(loads.gammas[r:r + L2_HEAD, n:n + 1], a[pre + g])
    loads.copy(chip.mask[:, :], a["mask"].partition_broadcast(P))
    loads.copy(chip.logits.weights[:, :, :], load_rows(a["L2_ffn_Wr"]))
    return loads


def latent_attention(chip, given):
    nc = chip.nc
    gate, both = 2, 2 * DIM
    with ExitStack() as ctx:
        st = Stage(chip, "l2x", ctx)
        bank = chip.bank
        s_bank = [bank[:, 0, :], bank[:, 1, :]]
        p_bank = [bank[:, 2, :], bank[:, 3, :]]
        o_bank, q_bank, y_bank, n_bank = (bank[:, n, :] for n in (4, 5, 6, 7))
        norm = NextNorm(st, [n_bank])
        w_q, w_out, w_kv, b_out = given.w_q, given.w_out, given.w_kv, given.b_out
        context_g, context_b, gammas, mask = given.context_g, given.context_b, given.gammas, chip.mask
        context = given.context
        gamma = st.sb("gamma", [P, 1])
        mask_row = st.sb("mask_row", [P, CTX], BF16)
        mask_now = st.sb("mask_now", [P, KEYS], BF16)
        mask_one = st.sb("mask_one", [P, P], BF16)
        c_stats = st.sb("c_stats", [KEYS, BATCH, 6])
        c_mv = st.sb("c_mv", [KEYS, BATCH, 2])
        c_rstd = st.sb("c_rstd", [KEYS, BATCH])
        c_norm = st.sb("c_norm", [KEYS, BATCH, DIM])
        c_normT = st.sb("c_normT", [P, 2, KD, KEYS])
        c_k = st.sb("c_k", [KEYS, BATCH, DIM])
        c_square = st.sb("c_square", [KEYS, 2, DIM])
        c_rms = st.sb("c_rms", [KEYS, 3, BATCH * L2_HEADS])
        c_kT = st.sb("c_kT", [P, KD, CTX])
        c_v = st.sb("c_v", [KEYS, BATCH, DIM])
        latT = st.sb("latT", [P, KD, SEQ])
        qk = st.sb("qk", [P, TPB, both])
        square = st.sb("square", [P, both])
        rms = st.sb("rms", [P, 3, 2 * L2_HEADS])
        qT = st.sb("qT", [P, KD, SEQ])
        kT = st.sb("kT", [P, KD, L2_KEYS])
        v = st.sb("v", [P, V_SLOTS, TPB * DIM])
        probs = st.sb("probs", [P, TPB * L2_HEADS, L2_KEYS])
        probsT = st.sb("probsT", [P, TPB * L2_HEADS, 3 * P])
        neg_max = st.sb("neg_max", [P, TPB * L2_HEADS])
        total = st.sb("total", [P, TPB * L2_HEADS])
        inverse = st.sb("inverse", [P, TPB * L2_HEADS])
        mixed = st.sb("mixed", [P, TPB, DIM])
        mixedT = st.sb("mixedT", [P, TPB, KD, P])
        sem = st.sem
        loaded, loads, consts_ready = given.loaded, given.start(), sem("consts_ready")
        c_stats_done, c_moments_ready, c_var_eps_done = sem("c_stats_done"), sem("c_moments_ready"), sem("c_var_eps_done")
        c_rstd_ready, c_normed = sem("c_rstd_ready"), sem("c_normed")
        c_norm_transposed, c_normT_ready = sem("c_norm_transposed"), sem("c_normT_ready")
        c_kv_projected, c_k_copied, c_v_copied = sem("c_kv_projected"), sem("c_k_copied"), sem("c_v_copied")
        c_squared, c_summed, c_rooted = sem("c_squared"), sem("c_summed"), sem("c_rooted")
        c_clamped, c_k_normed = sem("c_clamped"), sem("c_k_normed")
        c_k_transposed, c_kT_ready = sem("c_k_transposed"), sem("c_kT_ready")
        latT_ready, projected, qk_copied, v_copied = sem("latT_ready"), sem("projected"), sem("qk_copied"), sem("v_copied")
        squared, summed, rooted = sem("squared"), sem("summed"), sem("rooted")
        clamped, qk_normed = sem("clamped"), sem("qk_normed")
        qk_transposed, qkT_ready, c_kT_placed = sem("qk_transposed"), sem("qkT_ready"), sem("c_kT_placed")
        scores_ready, max_ready, probs_ready = sem("scores_ready"), sem("max_ready"), sem("probs_ready")
        probs_transposed = sem("probs_transposed")
        even_copied, odd_copied = sem("even_probsT_copied"), sem("odd_probsT_copied")
        attended, sums_inverted, mixed_ready = sem("attended"), sem("sums_inverted"), sem("mixed_ready")
        mixed_transposed, mixedT_ready = sem("mixed_transposed"), sem("mixedT_ready")
        out_ready, x_biased = sem("out_ready"), sem("x_biased")
        SH = TPB * L2_HEADS
        consts = 4
        block = ctx.enter_context(nc.Block())

        @block.tensor
        def _(pe):
            pe.wait_ge(loaded, 16 * loads)

            turn_bank, kv_bank = p_bank, s_bank
            qk_bank = [q_bank, n_bank]

            def transpose_context(b):
                pe.wait_ge(c_normed, b + 1)
                wait(pe, c_normT_ready, b - 1)
                for k in range(KD):
                    last = pe.transpose(turn_bank[b % 2][:, k * KEYS:(k + 1) * KEYS], c_norm[:, b, k * P:(k + 1) * P],
                                        chip.ident[0:KEYS, 0:KEYS])
                last.then_inc(c_norm_transposed, 1)

            def project_context():
                transpose_context(0)
                for b in range(BATCH):
                    if b + 1 < BATCH:
                        transpose_context(b + 1)
                    pe.wait_ge(c_normT_ready, b + 1)
                    wait(pe, c_v_copied, b - 1)
                    for k in range(KD):
                        last = pe.matmul(kv_bank[b % 2][0:KEYS, :], c_normT[:, b % 2, k, :], w_kv[:, k, :],
                                         start=(k == 0), stop=(k == KD - 1))
                    last.then_inc(c_kv_projected, 1)

            def transpose_context_keys():
                for b in range(BATCH):
                    pe.wait_ge(c_k_normed, b + 1)
                    wait(pe, c_kT_ready, b - 1)
                    for k in range(KD):
                        last = pe.transpose(turn_bank[b % 2][:, k * KEYS:(k + 1) * KEYS], c_k[:, b, k * P:(k + 1) * P],
                                            chip.ident[0:KEYS, 0:KEYS])
                    last.then_inc(c_k_transposed, 1)

            def project(b, u):
                t = TPB * b + u
                if u == 0:
                    pe.wait_ge(latT_ready, b + 1)
                wait(pe, v_copied, t)
                wait(pe, qkT_ready, 2 * TPB * (b - 1) + 2)
                wait(pe, norm.x_updated, TPB * (b - 3))
                for k in range(KD):
                    pe.matmul(q_bank[:, 0:DIM], latT[:, k, u * P:(u + 1) * P], w_q[:, k, :],
                              start=(k == 0), stop=(k == KD - 1))
                for k in range(KD):
                    last = pe.matmul(y_bank[:, :], latT[:, k, u * P:(u + 1) * P], w_kv[:, k, :],
                                     start=(k == 0), stop=(k == KD - 1))
                last.then_inc(projected, 1)

            def transpose_qk(b, u):
                t = TPB * b + u
                pe.wait_ge(qk_normed, t + 1)
                if u == 0:
                    pe.wait_ge(v_copied, TPB * (b + 1))
                else:
                    wait(pe, norm.copied, TPB * (b - 2))
                for k in range(2 * KD):
                    last = pe.transpose(qk_bank[u][:, k * P:(k + 1) * P], qk[:, u, k * P:(k + 1) * P],
                                        chip.ident[:, :])
                last.then_inc(qk_transposed, 1)

            def scores(b, s):
                u, h = s // L2_HEADS, s % L2_HEADS
                if s == 0:
                    pe.wait_ge(qkT_ready, 2 * TPB * b + 2 * TPB)
                    pe.wait_ge(c_kT_placed, (KD + 1) * b + KD + 1)
                wait(pe, probs_ready, SH * b + s - 1)
                at = slice(L2_HEAD * (h % 2), L2_HEAD * (h % 2) + L2_HEAD)
                pe.matmul(s_bank[h % 2][:, 0:L2_KEYS], qT[at, h // 2, u * P:(u + 1) * P], kT[at, h // 2, :],
                          start=True, stop=False)
                pe.matmul(s_bank[h % 2][:, 0:KEYS], mask_one[at, :], mask_now[at, :],
                          start=False, stop=True).then_inc(scores_ready, 1)

            def transpose_probs(b, s):
                h = s % L2_HEADS
                copied = even_copied if h % 2 == 0 else odd_copied
                n = SH // 2 * b + s // 2
                pe.wait_ge(probs_ready, SH * b + s + 1)
                wait(pe, copied, n)
                pe.transpose(p_bank[h % 2][0:KEYS, 0:P], probs[:, s, 0:KEYS], chip.ident[:, :])
                for k in range(TPB):
                    last = pe.transpose(p_bank[h % 2][:, (k + 1) * P:(k + 2) * P],
                                        probs[:, s, KEYS + k * P:KEYS + (k + 1) * P], chip.ident[:, :])
                last.then_inc(probs_transposed, 1)

            def attend(b, s):
                u, h, slot = s // L2_HEADS, s % L2_HEADS, b % V_SLOTS
                if h == 0:
                    wait(pe, mixed_ready, TPB * b + u)
                pe.wait_ge(even_copied if h % 2 == 0 else odd_copied, SH // 2 * b + s // 2 + 1)
                out = o_bank[:, h * L2_HEAD:(h + 1) * L2_HEAD]
                pe.matmul(out, probsT[0:KEYS, s, 0:P],
                          c_v[:, span(b, 1), h * L2_HEAD:(h + 1) * L2_HEAD].rearrange("p a d -> p (a d)"),
                          start=True, stop=False)
                for k in range(TPB):
                    at = k * DIM + h * L2_HEAD
                    last = pe.matmul(out, probsT[:, s, (k + 1) * P:(k + 2) * P],
                                     v[:, slot, at:at + L2_HEAD] if isinstance(slot, int) else
                                     v[:, bass.ds(slot, 1), at:at + L2_HEAD].rearrange("p a d -> p (a d)"),
                                     start=False, stop=(k == TPB - 1))
                if h == L2_HEADS - 1:
                    last.then_inc(attended, 1)

            def transpose_mixed(b):
                pe.wait_ge(mixed_ready, TPB * b + TPB)
                for u in range(TPB):
                    for k in range(KD):
                        last = pe.transpose(n_bank[:, (KD * u + k) * P:(KD * u + k + 1) * P],
                                            mixed[:, u, k * P:(k + 1) * P], chip.ident[:, :])
                last.then_inc(mixed_transposed, 1)

            def project_out(b, u):
                t = TPB * b + u
                pe.wait_ge(mixedT_ready, b + 1)
                wait(pe, norm.x_updated, t)
                for k in range(KD):
                    last = pe.matmul(y_bank[:, 0:DIM], mixedT[:, u, k, :], w_out[:, k, :],
                                     start=(k == 0), stop=(k == KD - 1))
                last.then_inc(out_ready, 1)

            project_context()
            for u in range(TPB):
                project(0, u)
            transpose_context_keys()
            for u in range(TPB):
                transpose_qk(0, u)
            pe.wait_ge(c_kT_ready, BATCH)
            pe.wait_ge(c_v_copied, BATCH)
            pe.wait_ge(consts_ready, consts)
            for s in range(SH):
                scores(0, s)
                if s in (0, 2):
                    project(1, s // 2)
                if s == 5:
                    transpose_qk(1, 0)
            transpose_qk(1, 1)

            def batch(b, ahead):
                behind = not is_step(b, 0)
                for s in range(SH):
                    u = s // L2_HEADS
                    if ahead >= 1:
                        scores(b + 1, s)
                    else:
                        pe.wait_ge(probs_ready, SH * BATCH)
                        chip.logits.some(pe, 1, norm)
                    transpose_probs(b, s)
                    if ahead >= 2 and s == 5:
                        transpose_qk(b + 2, 0)
                    if s > 0:
                        attend(b, s - 1)
                    if ahead >= 2 and s in (0, 2):
                        project(b + 2, s // 2)
                    if behind and s == 1:
                        transpose_mixed(b - 1)
                    if behind and s in (3, 4):
                        pe.wait_ge(v_copied, TPB * b + 3 * TPB if ahead >= 2 else TILES)
                        project_out(b - 1, s - 3)
                    if behind and s in (6, 7):
                        norm.tensor(pe, TPB * b - TPB + s - 6, s - 6)
                if ahead >= 2:
                    transpose_qk(b + 2, 1)
                attend(b, SH - 1)

            batches(pe, batch)
            wait(pe, norm.copied, TILES - TPB)
            chip.logits.some(pe, 1, norm)
            transpose_mixed(BATCH - 1)
            chip.logits.some(pe, 1, norm)
            for u in range(TPB):
                project_out(BATCH - 1, u)
            chip.logits.some(pe, 3, norm)
            for u in range(TPB):
                norm.tensor(pe, TILES - TPB + u, u)

        @block.scalar
        def _(act):
            act.wait_ge(loaded, 16 * loads)
            turn_bank, kv_bank = p_bank, s_bank
            qk_bank = [q_bank, n_bank]

            def copy_context_turned(b):
                act.wait_ge(c_norm_transposed, b + 1)
                wait(act, c_kv_projected, b - 1)
                for k in range(KD):
                    last = act.activation(c_normT[:, b % 2, k, :], turn_bank[b % 2][:, k * KEYS:(k + 1) * KEYS],
                                          ACT.Identity, scale=context_g[:, k:k + 1], bias=context_b[:, k:k + 1])
                last.then_inc(c_normT_ready, 1)

            def copy_context():
                copy_context_turned(0)
                for b in range(BATCH):
                    if b + 1 < BATCH:
                        copy_context_turned(b + 1)
                    act.wait_ge(c_kv_projected, b + 1)
                    act.activation(c_k[:, b, :], kv_bank[b % 2][0:KEYS, 0:DIM], ACT.Copy).then_inc(c_k_copied, 1)
                    act.activation(c_v[:, b, :], kv_bank[b % 2][0:KEYS, DIM:both], ACT.Copy).then_inc(c_v_copied, 1)
                    act.wait_ge(c_k_copied, b + 1)
                    wait(act, c_summed, b - 1)
                    act.activation(c_square[:, b % 2, :], c_k[:, b, :], ACT.Square).then_inc(c_squared, 1)

            def copy_context_keys():
                for b in range(BATCH):
                    act.wait_ge(c_k_transposed, b + 1)
                    act.activation(c_kT[:, :, b * KEYS:(b + 1) * KEYS], turn_bank[b % 2][:, 0:KD * KEYS].rearrange(
                        "p (k n) -> p k n", k=KD), ACT.Copy).then_inc(c_kT_ready, 1)

            def latents(b):
                wait(act, projected, TPB * b)
                act.activation(latT[:, :, :], chip.xnT[:, :, span(b, SEQ)], ACT.Copy).then_inc(latT_ready, 1)

            def copy_projections(b, u):
                t, slot = TPB * b + u, b % V_SLOTS
                act.wait_ge(projected, t + 1)
                wait(act, qk_transposed, t - 1)
                wait(act, attended, TPB * (b - V_SLOTS + 1))
                act.activation(qk[:, u, 0:DIM], q_bank[:, 0:DIM], ACT.Copy).then_inc(qk_copied, 1)
                act.activation(qk[:, u, DIM:both], y_bank[:, 0:DIM], ACT.Copy).then_inc(qk_copied, 1)
                out = (v[:, slot, u * DIM:(u + 1) * DIM] if isinstance(slot, int) else
                       v[:, bass.ds(slot, 1), u * DIM:(u + 1) * DIM].rearrange("p a d -> p (a d)"))
                act.activation(out, y_bank[:, DIM:both], ACT.Copy).then_inc(v_copied, 1)
                act.wait_ge(qk_copied, 2 * t + 2)
                wait(act, summed, t)
                act.activation(square[:, :], qk[:, u, :], ACT.Square).then_inc(squared, 1)

            def place_qkT(b):
                for u in range(TPB):
                    wait(act, scores_ready, SH * b)
                    act.wait_ge(qk_transposed, TPB * b + u + 1)
                    act.activation(qT[:, :, u * P:(u + 1) * P], qk_bank[u][:, 0:KD * P].rearrange("p (k n) -> p k n", k=KD),
                                   ACT.Copy, scale=gamma[:, 0:1]).then_inc(qkT_ready, 1)
                    act.activation(kT[:, :, KEYS + u * P:KEYS + (u + 1) * P],
                                   qk_bank[u][:, KD * P:2 * KD * P].rearrange("p (k n) -> p k n", k=KD),
                                   ACT.Copy).then_inc(qkT_ready, 1)

            def exponents(b, s):
                u = s // L2_HEADS
                act.wait_ge(max_ready, SH * b + s + 1)
                wait(act, probs_transposed, SH * b - SH + s + 1)
                wait(act, sums_inverted, TPB * b - TPB + u + 1)
                act.activation(probs[:, s, :], s_bank[s % 2][:, 0:L2_KEYS], ACT.Exp, bias=neg_max[:, s:s + 1],
                               accum_out=total[:, s:s + 1]).then_inc(probs_ready, 1)

            def copy_probsT(b, s):
                act.wait_ge(probs_transposed, SH * b + s + 1)
                wait(act, attended, TPB * b - TPB + s // L2_HEADS + 1)
                act.activation(probsT[0:KEYS, s, 0:P], p_bank[0][0:KEYS, 0:P], ACT.Copy)
                act.activation(probsT[:, s, P:3 * P], p_bank[0][:, P:3 * P], ACT.Copy).then_inc(even_copied, 1)

            def copy_mixedT(b):
                act.wait_ge(mixed_transposed, b + 1)
                wait(act, out_ready, TPB * b)
                act.activation(mixedT[:, :, :, :].rearrange("p u k n -> p (u k n)"), n_bank[:, 0:TPB * DIM],
                               ACT.Copy).then_inc(mixedT_ready, 1)

            latents(0)
            copy_context()
            for u in range(TPB):
                copy_projections(0, u)
            latents(1)
            copy_context_keys()
            place_qkT(0)
            for s in range(SH):
                exponents(0, s)
                if s in (0, 2):
                    copy_projections(1, s // 2)
                if s == SH - 2:
                    latents(2)
            place_qkT(1)

            def batch(b, ahead):
                for s in range(SH):
                    if s % 2 == 0:
                        copy_probsT(b, s)
                    if ahead >= 1:
                        exponents(b + 1, s)
                    if ahead >= 2 and s in (0, 2):
                        copy_projections(b + 2, s // 2)
                    if not is_step(b, 0):
                        if s == 1:
                            copy_mixedT(b - 1)
                        if s in (6, 7):
                            norm.scalar(act, TPB * b - TPB + s - 6, s - 6)
                    if ahead >= 3 and s == SH - 2:
                        latents(b + 3)
                if ahead >= 2:
                    place_qkT(b + 2)

            batches(act, batch)
            copy_mixedT(BATCH - 1)
            for u in range(TPB):
                norm.scalar(act, TILES - TPB + u, u)

        @block.vector
        def _(dve):
            def constants():
                dve.memset(mask_one[:, :], 0.0).then_inc(consts_ready, 1)
                dve.memset(mask_row[:, :], 0.0).then_inc(consts_ready, 1)
                dve.wait_ge(consts_ready, 2)
                dve.wait_ge(loaded, 16 * loads)
                for r in range(0, P, L2_HEAD):
                    dve.memset(mask_one[r:r + 1, :], 1.0)
                    last = dve.tensor_scalar(mask_row[r:r + 1, :], mask[r:r + 1, :], 1.0, -MASKED,
                                             ALU.subtract, ALU.mult)
                last.then_inc(consts_ready, 1)
                dve.tensor_scalar(b_out[:, :], b_out[:, :], chip.gate[:, gate:gate + 1], None, ALU.mult)
                dve.scalar_tensor_tensor(out=gamma[:, :], in0=gammas[:, 0:1], scalar=L2_HEAD ** -0.5, in1=gammas[:, 1:2],
                                         op0=ALU.mult, op1=ALU.mult).then_inc(consts_ready, 1)

            def norm_context():
                dve.wait_ge(loaded, 16 * loads)
                for b in range(BATCH):
                    dve.bn_stats(c_stats[:, b, :], context[:, b, :]).then_inc(c_stats_done, 1)
                dve.wait_ge(c_stats_done, BATCH)
                for b in range(BATCH):
                    dve.bn_aggr(c_mv[:, b, :], c_stats[:, b, :]).then_inc(c_moments_ready, 1)
                dve.wait_ge(c_rstd_ready, 1)
                for b in range(BATCH):
                    dve.tensor_scalar(c_norm[:, b, :], context[:, b, :], c_mv[:, b, 0:1], c_rstd[:, b:b + 1],
                                      ALU.subtract, ALU.mult).then_inc(c_normed, 1)

            def norm_context_keys():
                for b in range(BATCH + 2):
                    if b < BATCH:
                        at = slice(b * L2_HEADS, (b + 1) * L2_HEADS)
                        dve.wait_ge(c_squared, b + 1)
                        dve.tensor_reduce(c_rms[:, 0, at], c_square[:, b % 2, :].rearrange("p (h d) -> p h d", h=L2_HEADS),
                                          AX_X, ALU.add).then_inc(c_summed, 1)
                        dve.wait_ge(c_summed, b + 1)
                        dve.tensor_scalar(c_rms[:, 1, at], c_rms[:, 0, at], 1 / L2_HEAD, RMS_EPS ** 2, ALU.mult,
                                          ALU.max).then_inc(c_clamped, 1)
                    if b >= 2:
                        dve.wait_ge(c_rooted, b - 1)
                        heads = c_k[:, b - 2, :].rearrange("p (h d) -> p h d", d=L2_HEAD)
                        roots = c_rms[:, 2, (b - 2) * L2_HEADS:(b - 1) * L2_HEADS]
                        dve.tensor_tensor(heads, heads, roots.unsqueeze(2).to_broadcast([KEYS, L2_HEADS, L2_HEAD]),
                                          ALU.mult).then_inc(c_k_normed, 1)

            def rms_sums(b, u):
                t = TPB * b + u
                dve.wait_ge(squared, t + 1)
                dve.tensor_reduce(rms[:, 0, :], square[:, :].rearrange("p (h d) -> p h d", h=2 * L2_HEADS),
                                  AX_X, ALU.add).then_inc(summed, 1)
                dve.wait_ge(summed, t + 1)
                dve.tensor_scalar(rms[:, 1, :], rms[:, 0, :], 1 / L2_HEAD, RMS_EPS ** 2, ALU.mult,
                                  ALU.max).then_inc(clamped, 1)

            def rms_norm(b, u):
                heads = qk[:, u, :].rearrange("p (h d) -> p h d", h=2 * L2_HEADS)
                dve.wait_ge(rooted, TPB * b + u + 1)
                dve.tensor_tensor(heads, heads,
                                  rms[:, 2, :].unsqueeze(2).to_broadcast([P, 2 * L2_HEADS, L2_HEAD]),
                                  ALU.mult).then_inc(qk_normed, 1)

            def maximum(b, s):
                dve.wait_ge(scores_ready, SH * b + s + 1)
                wait(dve, probs_ready, SH * b + s + 1 - SH)
                dve.tensor_reduce(neg_max[:, s:s + 1], s_bank[s % 2][:, 0:L2_KEYS], AX_X, ALU.max,
                                  negate=True).then_inc(max_ready, 1)

            def copy_probsT(b, s):
                dve.wait_ge(probs_transposed, SH * b + s + 1)
                wait(dve, attended, TPB * b - TPB + s // L2_HEADS + 1)
                dve.tensor_copy(probsT[0:KEYS, s, 0:P], p_bank[1][0:KEYS, 0:P])
                dve.tensor_copy(probsT[:, s, P:3 * P], p_bank[1][:, P:3 * P]).then_inc(odd_copied, 1)

            def invert_sums(b):
                wait(dve, mixed_ready, TPB * b)
                for u in range(TPB):
                    at = slice(u * L2_HEADS, (u + 1) * L2_HEADS)
                    dve.wait_ge(probs_ready, SH * b + (u + 1) * L2_HEADS)
                    dve.reciprocal(inverse[:, at], total[:, at]).then_inc(sums_inverted, 1)

            def normalise(b, u):
                t = TPB * b + u
                at = slice(u * L2_HEADS, (u + 1) * L2_HEADS)
                dve.wait_ge(sums_inverted, t + 1)
                dve.wait_ge(attended, t + 1)
                wait(dve, mixed_transposed, b)
                dve.tensor_tensor(mixed[:, u, :].rearrange("p (h d) -> p h d", h=L2_HEADS),
                                  o_bank[:, 0:DIM].rearrange("p (h d) -> p h d", h=L2_HEADS),
                                  inverse[:, at].unsqueeze(2).to_broadcast([P, L2_HEADS, L2_HEAD]),
                                  ALU.mult).then_inc(mixed_ready, 1)

            def update_x(t, u):
                dve.wait_ge(out_ready, t + 1)
                dve.wait_ge(x_biased, t + 1)
                dve.scalar_tensor_tensor(out=nth(chip.x, t), in0=y_bank[:, 0:DIM], scalar=chip.gate[:, gate:gate + 1],
                                         in1=nth(chip.x, t), op0=ALU.mult, op1=ALU.add).then_inc(norm.x_updated, 1)
                norm.vector_stats(dve, (t, u))

            norm_context()
            constants()
            norm_context_keys()
            for u in range(TPB):
                rms_sums(0, u)
                rms_norm(0, u)
            for s in range(SH):
                maximum(0, s)
                if s in (4, 6):
                    rms_norm(1, s // 2 - 2)
                if s in (2, 4):
                    rms_sums(1, s // 2 - 1)

            def batch(b, ahead):
                invert_sums(b)
                for s in range(SH):
                    if ahead >= 1:
                        maximum(b + 1, s)
                    if s % 2 == 1:
                        copy_probsT(b, s)
                    if s == L2_HEADS:
                        normalise(b, 0)
                    if ahead >= 2 and s in (4, 6):
                        rms_norm(b + 2, s // 2 - 2)
                    if not is_step(b, 0):
                        if s in (3, 4):
                            update_x(TPB * b - TPB + s - 3, s - 3)
                        if s in (5, 6):
                            norm.vector_apply(dve, TPB * b - TPB + s - 5, s - 5)
                    if ahead >= 2 and s in (2, 4):
                        rms_sums(b + 2, s // 2 - 1)
                normalise(b, 1)

            batches(dve, batch)
            for u in range(TPB):
                update_x(TILES - TPB + u, u)
            for u in range(TPB):
                norm.vector_apply(dve, TILES - TPB + u, u)

        @block.gpsimd
        def _(pool):
            def root(sums, ready, count, done):
                pool.wait_ge(ready, count)
                pool.tensor_tensor(sums[:, 2, :], sums[:, 1, :],
                                   chip.powers[0:sums.shape[0], 0:1].to_broadcast([sums.shape[0], sums.shape[2]]),
                                   ALU.pow).then_inc(done, 1)

            def scale_context():
                pool.wait_ge(c_moments_ready, BATCH)
                pool.tensor_tensor(c_rstd[:, :], c_mv[:, :, 1:2].rearrange("p b n -> p (b n)"),
                                   chip.powers[0:KEYS, 1:2].to_broadcast([KEYS, BATCH]), ALU.add).then_inc(c_var_eps_done, 1)
                pool.wait_ge(c_var_eps_done, 1)
                pool.tensor_tensor(c_rstd[:, :], c_rstd[:, :], chip.powers[0:KEYS, 0:1].to_broadcast([KEYS, BATCH]),
                                   ALU.pow).then_inc(c_rstd_ready, 1)
                for b in range(BATCH):
                    root(c_rms[:, :, b * L2_HEADS:(b + 1) * L2_HEADS], c_clamped, b + 1, c_rooted)

            def place_context(b):
                wait(pool, scores_ready, SH * b)
                for k in range(KD):
                    pool.tensor_copy(kT[:, k, 0:KEYS], c_kT[:, k, span(b, KEYS)]).then_inc(c_kT_placed, 1)
                pool.tensor_copy(mask_now[:, :], mask_row[:, span(b, KEYS)]).then_inc(c_kT_placed, 1)

            scale_context()
            pool.wait_ge(loaded, 16 * loads)
            pool.wait_ge(consts_ready, consts)
            for b in range(2):
                for u in range(TPB):
                    root(rms, clamped, TPB * b + u + 1, rooted)
                if b == 0:
                    pool.wait_ge(c_kT_ready, BATCH)
                place_context(b)

            def batch(b, ahead):
                for u in range(TPB):
                    t = TPB * b + u
                    pool.tensor_tensor(nth(chip.x, t), nth(chip.x, t), b_out[:, :],
                                       ALU.add).then_inc(x_biased, 1)
                if ahead >= 2:
                    root(rms, clamped, TPB * b + 2 * TPB + 1, rooted)
                if not is_step(b, 0):
                    for u in range(TPB):
                        norm.gpsimd(pool, TPB * b - TPB + u, u)
                if ahead >= 2:
                    root(rms, clamped, TPB * b + 2 * TPB + 2, rooted)
                    place_context(b + 2)

            batches(pool, batch)
            for u in range(TPB):
                norm.gpsimd(pool, TILES - TPB + u, u)


class Chain:

    def __init__(self, eng, sem):
        self.eng, self.sem, self.count = eng, sem, 0

    def __call__(self, instruction):
        self.count += 1
        instruction.then_inc(self.sem, 1)
        self.eng.wait_ge(self.sem, self.count)


class Feed:

    def __init__(self, st, dram, high, low, chunk, name=""):
        self.dram, self.high_part, self.low_part, self.chunk = dram, high, low, chunk
        self.chunks = dram.shape[1] // chunk
        self.staging = st.sb(f"{name}staging", [P, 2, chunk])
        self.loaded = [st.sem(f"{name}weights_loaded{u}") for u in range(2)]
        self.high_ready = st.sem(f"{name}high_ready")
        self.low_ready = st.sem(f"{name}low_ready")

    def sync(self, sp, i, u):
        c = 2 * i + u
        wait(sp, self.low_ready, c - 1)
        sp.dma_start(self.staging[:, u, :], self.dram[:, span(c, self.chunk)]).then_inc(self.loaded[u], 16)

    def sync_all(self, sp):
        pairs(sp, self.chunks, lambda i, u: self.sync(sp, i, u))

    def high(self, act, i, u):
        c = 2 * i + u
        act.wait_ge(self.loaded[u], 16 * i + 16)
        act.activation(self.high_part[:, span(c, self.chunk)], self.staging[:, u, :],
                       ACT.Copy).then_inc(self.high_ready, 1)

    def low(self, eng, i, u):
        c = 2 * i + u
        eng.wait_ge(self.high_ready, c + 1)
        eng.tensor_tensor(self.low_part[:, span(c, self.chunk)], self.staging[:, u, :],
                          self.high_part[:, span(c, self.chunk)], ALU.subtract).then_inc(self.low_ready, 1)


def pairs(eng, n, body):
    def pair(i):
        for u in range(2):
            body(i, u)
    steps(eng, n // 2, pair)


def wide(column):
    return column[:, :].unsqueeze(2).to_broadcast([P, TILES, EXPERTS])


def tall(row):
    return row[:, :].unsqueeze(1).to_broadcast([P, TILES, EXPERTS])


def pick_largest(dve, chain, values, order, picked, work, column):
    chain(dve.tensor_reduce(column[:, :], values[:, :, :], AX_X, ALU.max))
    chain(dve.tensor_tensor(work[:, :, :], values[:, :, :], wide(column), ALU.is_equal))
    chain(dve.tensor_tensor(work[:, :, :], work[:, :, :], tall(order), ALU.mult))
    chain(dve.tensor_reduce(column[:, :], work[:, :, :], AX_X, ALU.min))
    chain(dve.tensor_tensor(picked[:, :, :], tall(order), wide(column), ALU.is_equal))


HIDE = 1e30


def relu_square_experts(chip, a, ahead):
    nc = chip.nc
    gate = 4 + 2
    with ExitStack() as ctx:
        st = Stage(chip, "l2f", ctx)
        bank = chip.bank
        norm = NextNorm(st, [bank[:, n, :] for n in (6, 7)], depth=8)
        sb, sem = st.sb, st.sem
        ws1, ws2 = sb("Ws1", [P, KD, P]), sb("Ws2", [P, DIM])
        order, ones = sb("order", [P, EXPERTS]), sb("ones", [P, P])
        logits, rest, work = (sb(n, [P, TILES, EXPERTS]) for n in ("logits", "rest", "work"))
        first, prob = sb("first", [P, TILES, EXPERTS]), sb("prob", [P, TILES, EXPERTS])
        top, second, column = (sb(n, [P, TILES]) for n in ("top", "second", "column"))
        used, count = sb("used", [P, 1]), sb("count", [1, 1], I32)
        blocks, width = 4, 512
        per = width // P
        r, h = sb("r", [P, width]), sb("h", [P, width])
        s_r, s_h = sb("shared_r", [P, blocks, width]), sb("shared_h", [P, blocks, width])
        w1, w2 = sb("W1", [P, KD, P]), sb("W2", [P, DIM])
        loaded, logits_ready, routed, chained = sem("loaded"), sem("logits_ready"), sem("routed"), sem("chained")
        exp_ready, exp_wanted, counted, count_ready = sem("exp_ready"), sem("exp_wanted"), sem("counted"), sem("count_ready")
        hidden_ready, relu_ready, squared, out_ready = (sem(n) for n in (
            "hidden_ready", "relu_ready", "squared", "out_ready"))

        with nc.Block() as block:
            @block.sync
            def _(sp):
                sp.dma_start(order[:, :], a["order"].partition_broadcast(P)).then_inc(loaded, 16)
                sp.dma_start(ws1[:, :, :], load_rows(a["L2_ffn_Ws1"])).then_inc(loaded, 16)
                sp.dma_start(ws2[:, :], a["L2_ffn_Ws2"]).then_inc(loaded, 16)

            @block.tensor
            def _(pe):
                chip.logits.rest(pe, logits_ready)
                pe.wait_ge(loaded, 48)
                for n in range(blocks):
                    for k in range(KD):
                        last = pe.matmul(bank[:, 4 + n, :], ws1[:, k, :], chip.xnT[:, k, span(n, width)],
                                         start=(k == 0), stop=(k == KD - 1))
                    last.then_inc(hidden_ready, 1)
                pe.wait_ge(routed, 1)
                pe.matmul(bank[:, 1, 0:1], ones[:, :], used[:, :], start=True, stop=True).then_inc(counted, 1)
                pe.wait_ge(relu_ready, blocks)

                def results(n):
                    pe.wait_ge(squared, n + 1)
                    for j in range(per):
                        wait(pe, norm.x_updated, per * (n - 1) + j + 1)
                        hidden = s_h[:, n, j * P:(j + 1) * P]
                        pe.matmul(bank[:, 4 + j, 0:DIM], hidden, ws2[:, :], start=True, stop=True).then_inc(out_ready, 1)
                for n in range(blocks):
                    results(n)

            @block.scalar
            def _(act):
                act.wait_ge(exp_wanted, 1)
                act.activation(second[:, :], second[:, :], ACT.Exp).then_inc(exp_ready, 1)
                for n in range(blocks):
                    act.wait_ge(hidden_ready, n + 1)
                    act.activation(s_r[:, n, :], bank[:, 4 + n, :], ACT.Relu).then_inc(relu_ready, 1)

            @block.gpsimd
            def _(pool):
                for n in range(blocks):
                    pool.wait_ge(relu_ready, n + 1)
                    pool.tensor_tensor(s_h[:, n, :], s_r[:, n, :], s_r[:, n, :], ALU.mult).then_inc(squared, 1)

            @block.vector
            def _(dve):
                chain = Chain(dve, chained)
                chain(dve.memset(ones[:, :], 1.0))
                dve.wait_ge(loaded, 48)
                dve.wait_ge(logits_ready, 1)
                chain(dve.tensor_copy(logits[:, :, :], bank[:, 0, 0:TILES * EXPERTS].rearrange(
                    "p (t e) -> p t e", t=TILES)))
                pick_largest(dve, chain, logits, order, first, work, column)
                chain(dve.tensor_reduce(top[:, :], logits[:, :, :], AX_X, ALU.max))
                chain(dve.scalar_tensor_tensor(out=rest[:, :, :], in0=first[:, :, :], scalar=-HIDE, in1=logits[:, :, :],
                                               op0=ALU.mult, op1=ALU.add))
                chain(dve.tensor_reduce(second[:, :], rest[:, :, :], AX_X, ALU.max))
                chain(dve.tensor_tensor(second[:, :], second[:, :], top[:, :], ALU.subtract))
                dve.sem_inc(exp_wanted, 1)
                dve.wait_ge(exp_ready, 1)
                chain(dve.tensor_scalar(second[:, :], second[:, :], 1.0, None, ALU.add))
                chain(dve.reciprocal(second[:, :], second[:, :]))
                chain(dve.tensor_scalar(second[:, :], second[:, :], 1.0, None, ALU.is_ge))
                chain(dve.tensor_tensor(prob[:, :, :], first[:, :, :], wide(second), ALU.mult))
                dve.tensor_reduce(used[:, :], second[:, :], AX_X, ALU.add).then_inc(routed, 1)
                chain(dve.tensor_scalar(prob[:, :, :], prob[:, :, :], chip.gate[:, gate:gate + 1], None, ALU.mult))
                dve.wait_ge(counted, 1)
                dve.tensor_copy(count[:, :], bank[0:1, 1, 0:1]).then_inc(count_ready, 1)

                def add(n):
                    for j in range(per):
                        t = per * n + j
                        dve.wait_ge(out_ready, t + 1)
                        dve.scalar_tensor_tensor(out=nth(chip.x, t), in0=bank[:, 4 + j, 0:DIM],
                                                 scalar=chip.gate[:, gate:gate + 1], in1=nth(chip.x, t), op0=ALU.mult,
                                                 op1=ALU.add).then_inc(norm.x_updated, 1)
                steps(dve, blocks, add)

        w_loaded, w_used, h_ready, r_ready, h2_ready = (sem(n) for n in (
            "w_loaded", "w_used", "h_ready", "r_ready", "h2_ready"))
        y_ready, added = sem("y_ready"), sem("added")

        def if_routed(eng, body):
            n = eng.value_load(count[0:1, 0:1])
            with eng.If(n != 0):
                body()

        with nc.Block() as block:
            @block.sync
            def _(sp):
                def body():
                    def expert(e):
                        wait(sp, added, TILES * e)
                        sp.dma_start(w1[:, :, :].rearrange("p k n -> p (k n)"),
                                     nth_row(a["L2_ffn_W1"], e)).then_inc(w_loaded, 16)
                        sp.dma_start(w2[:, :], nth_row(a["L2_ffn_W2"], e)).then_inc(w_loaded, 16)
                    steps(sp, EXPERTS, expert)
                if_routed(sp, body)

            @block.tensor
            def _(pe):
                def body():
                    def expert(e):
                        pe.wait_ge(w_loaded, 32 * e + 32)
                        for n in range(blocks):
                            wait(pe, h2_ready, blocks * e + n)
                            for k in range(KD):
                                last = pe.matmul(bank[:, 0, :], w1[:, k, :], chip.xnT[:, k, n * width:(n + 1) * width],
                                                 start=(k == 0), stop=(k == KD - 1))
                            last.then_inc(h_ready, 1)
                            pe.wait_ge(h2_ready, blocks * e + n + 1)
                            for j in range(per):
                                wait(pe, added, TILES * e + n * per + j)
                                pe.matmul(bank[:, 1, 0:DIM], h[:, j * P:(j + 1) * P], w2[:, :], start=True,
                                          stop=True).then_inc(y_ready, 1)
                    steps(pe, EXPERTS, expert)
                if_routed(pe, body)

            @block.scalar
            def _(act):
                def body():
                    def expert(e):
                        for n in range(blocks):
                            act.wait_ge(h_ready, blocks * e + n + 1)
                            wait(act, h2_ready, blocks * e + n)
                            act.activation(r[:, :], bank[:, 0, :], ACT.Relu).then_inc(r_ready, 1)
                    steps(act, EXPERTS, expert)
                if_routed(act, body)

            @block.vector
            def _(dve):
                def body():
                    def expert(e):
                        for n in range(blocks):
                            dve.wait_ge(r_ready, blocks * e + n + 1)
                            wait(dve, y_ready, TILES * e + n * per)
                            dve.tensor_tensor(h[:, :], r[:, :], r[:, :], ALU.mult).then_inc(h2_ready, 1)
                            for j in range(per):
                                t = n * per + j
                                dve.wait_ge(y_ready, TILES * e + t + 1)
                                share = prob[:, t, e:e + 1] if isinstance(e, int) else prob[:, t, bass.ds(e, 1)]
                                dve.scalar_tensor_tensor(out=chip.x[:, t, :], in0=bank[:, 1, 0:DIM], scalar=share,
                                                         in1=chip.x[:, t, :], op0=ALU.mult,
                                                         op1=ALU.add).then_inc(added, 1)
                    steps(dve, EXPERTS, expert)
                if_routed(dve, body)

        with nc.Block() as block:
            tiles = AllTiles(norm)

            @block.sync
            def _(sp):
                ahead.sync(sp)

            @block.tensor
            def _(pe):
                tiles.tensor(pe)

            @block.scalar
            def _(act):
                tiles.scalar(act)

            @block.gpsimd
            def _(pool):
                tiles.gpsimd(pool)

            @block.vector
            def _(dve):
                tiles.vector(dve)


def nth_row(dram, i):
    if isinstance(i, int):
        return dram[i]
    return dram[bass.ds(i, 1), :, :].rearrange("a p m -> p (a m)")


def linear_experts(chip, a, high, low, out):
    nc = chip.nc
    gate = 4 + 3
    with ExitStack() as ctx:
        st = Stage(chip, "l3f", ctx)
        bank = chip.bank
        sb, sem = st.sb, st.sem
        x_high, x_low = (sb(n, [P, KD, TOKENS], BF16) for n in ("x_high", "x_low"))
        bg, be = sb("bg", [P, EXPERTS]), sb("be", [EXPERTS, DIM])
        order = sb("order", [P, EXPERTS])
        gates, rest, work = (sb(n, [P, TILES, EXPERTS]) for n in ("gates", "rest", "work"))
        first, second = (sb(n, [P, TILES, EXPERTS]) for n in ("first", "second"))
        column = sb("column", [P, TILES])
        share = sb("share", [P, 2, EXPERTS])
        shareT = sb("shareT", [EXPERTS, P])
        total = sb("total", [P, 2, DIM])
        loaded, logits_ready, chained = sem("loaded"), sem("logits_ready"), sem("chained")
        exp_wanted, exp_ready, gates_ready = sem("exp_wanted"), sem("exp_ready"), sem("gates_ready")
        x_high_ready, x_split = sem("x_high_ready"), sem("x_split")
        share_ready, share_transposed, shareT_ready = sem("share_ready"), sem("share_transposed"), sem("shareT_ready")
        bias_ready, experts_ready, added, x_done = sem("bias_ready"), sem("experts_ready"), sem("added"), sem("x_done")
        passed, stored = sem("passed"), sem("stored")
        halves = EXPERTS // 2
        block = ctx.enter_context(nc.Block())

        @block.sync
        def _(sp):
            sp.dma_start(bg[:, :], a["L3_ffn_bg"].partition_broadcast(P)).then_inc(loaded, 16)
            sp.dma_start(be[:, :], a["L3_ffn_be"]).then_inc(loaded, 16)
            sp.dma_start(order[:, :], a["order"].partition_broadcast(P)).then_inc(loaded, 16)
            rows = out.rearrange("(t p) d -> p t d", p=P)
            for t in range(0, TILES, 2):
                sp.wait_ge(x_done, t + 2)
                sp.dma_start(rows[:, t:t + 2, :], chip.x[:, t:t + 2, :]).then_inc(stored, 16)
            sp.wait_ge(stored, 16 * TILES // 2)

        @block.tensor
        def _(pe):
            chip.logits.rest(pe, logits_ready)
            pe.wait_ge(loaded, 48)
            pe.wait_ge(x_split, KD)
            pe.wait_ge(chained, 1)

            def step(i):
                for u in range(2):
                    t = 2 * i + u
                    for j in range(halves):
                        wait(pe, added, EXPERTS * t - EXPERTS + 2 * j + 2)
                        n = 0
                        for left, right in ((x_high, high), (x_low, high), (x_high, low)):
                            for k in range(KD):
                                n += 1
                                at = k * EXPERTS * DIM + 2 * j * DIM
                                last = pe.matmul(bank[:, j, :], left[:, k, span(t, P)], right[:, at:at + 2 * DIM],
                                                 start=(n == 1), stop=(n == 3 * KD))
                        last.then_inc(experts_ready, 1)
                        if j == 2:
                            pe.wait_ge(share_ready, t + 1)
                            wait(pe, shareT_ready, t)
                            pe.transpose(bank[0:EXPERTS, 4, 0:P], share[:, u, :], chip.ident[:, :]).then_inc(share_transposed, 1)
                    pe.wait_ge(shareT_ready, t + 1)
                    wait(pe, x_done, t)
                    pe.matmul(bank[:, 5, 0:DIM], shareT[:, :], be[:, :], start=True, stop=True).then_inc(bias_ready, 1)

            steps(pe, TILES // 2, step)

        @block.scalar
        def _(act):
            for k in range(KD):
                act.activation(x_high[:, k, :], chip.xnT[:, k, :], ACT.Copy).then_inc(x_high_ready, 1)
            act.wait_ge(exp_wanted, 1)
            act.activation(gates[:, :, :], gates[:, :, :], ACT.Exp).then_inc(exp_ready, 1)

            def copy_share(t, u):
                wait(act, added, EXPERTS * (t - 1))
                wait(act, share_transposed, t - 1)
                act.activation(share[:, u, :], nth(gates, t), ACT.Copy).then_inc(share_ready, 1)

            act.wait_ge(gates_ready, 1)
            copy_share(0, 0)

            def step(i):
                for u in range(2):
                    t = 2 * i + u
                    if not (u == 1 and is_step(i, TILES // 2 - 1)):
                        copy_share(t + 1, 1 - u)
                    act.wait_ge(share_transposed, t + 1)
                    wait(act, bias_ready, t)
                    act.activation(shareT[:, :], bank[0:EXPERTS, 4, 0:P], ACT.Copy).then_inc(shareT_ready, 1)
            steps(act, TILES // 2, step)

        @block.vector
        def _(dve):
            chain = Chain(dve, chained)
            dve.wait_ge(loaded, 48)
            dve.wait_ge(logits_ready, 1)
            chain(dve.tensor_tensor(gates[:, :, :], bank[:, 0, 0:TILES * EXPERTS].rearrange(
                "p (t e) -> p t e", t=TILES), tall(bg), ALU.add))
            chain(dve.tensor_reduce(column[:, :], gates[:, :, :], AX_X, ALU.max))
            chain(dve.tensor_tensor(gates[:, :, :], gates[:, :, :], wide(column), ALU.subtract))
            dve.sem_inc(exp_wanted, 1)
            for k in range(KD):
                dve.wait_ge(x_high_ready, k + 1)
                dve.tensor_tensor(x_low[:, k, :], chip.xnT[:, k, :], x_high[:, k, :], ALU.subtract).then_inc(x_split, 1)
            dve.wait_ge(exp_ready, 1)
            chain(dve.tensor_reduce(column[:, :], gates[:, :, :], AX_X, ALU.add))
            chain(dve.reciprocal(column[:, :], column[:, :]))
            chain(dve.tensor_tensor(gates[:, :, :], gates[:, :, :], wide(column), ALU.mult))
            pick_largest(dve, chain, gates, order, first, work, column)
            chain(dve.scalar_tensor_tensor(out=rest[:, :, :], in0=first[:, :, :], scalar=-HIDE, in1=gates[:, :, :],
                                           op0=ALU.mult, op1=ALU.add))
            pick_largest(dve, chain, rest, order, second, work, column)
            chain(dve.tensor_tensor(first[:, :, :], first[:, :, :], second[:, :, :], ALU.add))
            chain(dve.tensor_tensor(gates[:, :, :], gates[:, :, :], first[:, :, :], ALU.mult))
            chain(dve.tensor_reduce(column[:, :], gates[:, :, :], AX_X, ALU.add))
            chain(dve.reciprocal(column[:, :], column[:, :]))
            chain(dve.tensor_scalar(column[:, :], column[:, :], chip.gate[:, gate:gate + 1], None, ALU.mult))
            chain(dve.tensor_tensor(gates[:, :, :], gates[:, :, :], wide(column), ALU.mult))
            dve.sem_inc(gates_ready, 1)

            def step(i):
                for u in range(2):
                    t = 2 * i + u
                    dve.wait_ge(share_ready, t + 1)
                    for e in range(EXPERTS):
                        j = e // 2
                        if e % 2 == 0:
                            dve.wait_ge(experts_ready, halves * t + j + 1)
                        source = bank[:, j, (e % 2) * DIM:(e % 2 + 1) * DIM]
                        if e == 0:
                            wait(dve, x_done, t - 1)
                            dve.tensor_scalar(total[:, u, :], source, share[:, u, 0:1], None,
                                              ALU.mult).then_inc(added, 1)
                        else:
                            dve.wait_ge(added, EXPERTS * t + e)
                            dve.scalar_tensor_tensor(out=total[:, u, :], in0=source, scalar=share[:, u, e:e + 1],
                                                     in1=total[:, u, :], op0=ALU.mult, op1=ALU.add).then_inc(added, 1)
                    dve.wait_ge(added, EXPERTS * t + EXPERTS)
                    dve.tensor_tensor(nth(chip.x, t), nth(chip.x, t), total[:, u, :], ALU.add).then_inc(passed, 1)
                    dve.wait_ge(passed, t + 1)
                    dve.wait_ge(bias_ready, t + 1)
                    dve.tensor_tensor(nth(chip.x, t), bank[:, 5, 0:DIM], nth(chip.x, t), ALU.add).then_inc(x_done, 1)
            steps(dve, TILES // 2, step)


class Scratch:

    def __init__(self, nc, name, slots):
        self.tiles = slots // P
        self.rows = nc.dram_tensor(f"{name}_rows", [slots, DIM], F32, kind="Internal").ap()
        self.results = nc.dram_tensor(f"{name}_results", [slots, DIM], F32, kind="Internal").ap()


def slot_tiles(picks):
    return picks * TILES + EXPERTS


class Sorting:

    def __init__(self, st, picks):
        self.picks, self.tiles = picks, slot_tiles(picks)
        sb, sem = st.sb, st.sem
        self.chosen = sb("chosen", [P, TILES, EXPERTS], BF16)
        self.chosen_sum = sb("chosen_sum", [P, EXPERTS])
        self.sum_parts = sb("chosen_sum_bf16", [P, EXPERTS], BF16)
        self.tri = sb("tri", [P, P])
        self.earlier, self.ones = sb("earlier", [P, P], BF16), sb("ones", [P, P], BF16)
        self.starts = sb("starts", [P, TILES])
        self.before = sb("before", [P, EXPERTS, EXPERTS])
        self.numbers = sb("numbers", [P, self.tiles])
        self.counts = sb("counts", [P, EXPERTS])
        self.more = sb("more", [P, EXPERTS, TILES])
        self.tiles_of = sb("tiles_of", [P, EXPERTS])
        self.begin = sb("begin", [P, EXPERTS])
        self.place = sb("place", [P, TILES, EXPERTS])
        self.own = sb("own", [P, TILES, EXPERTS]) if picks > 1 else self.place
        self.position = sb("position", [P, TILES])
        self.slot = [sb(f"slot{k}", [P, TILES], I32) for k in range(picks)]
        self.ended = sb("ended", [P, self.tiles, EXPERTS])
        self.expert = sb("expert", [P, self.tiles])
        self.expert_of = sb("expert_of", [P, self.tiles], I32)
        self.loaded, self.chosen_ready, self.ranked = sem("sort_loaded"), sem("chosen_ready"), sem("ranked")
        self.slots_ready = sem("slots_ready")
        self.loads = 4

    def sync(self, sp, a):
        sp.dma_start(self.tri[:, :], a["tri"]).then_inc(self.loaded, 16)
        sp.dma_start(self.starts[:, :], a["starts"].partition_broadcast(P)).then_inc(self.loaded, 16)
        sp.dma_start(self.before[:, :, :].rearrange("p a b -> p (a b)"),
                     a["before"].partition_broadcast(P)).then_inc(self.loaded, 16)
        sp.dma_start(self.numbers[:, :], a["numbers"][0:self.tiles].partition_broadcast(P)).then_inc(self.loaded, 16)

    def tensor(self, pe, rank_bank, count_bank):
        pe.wait_ge(self.chosen_ready, 1)
        every = self.chosen[:, :, :].rearrange("p t e -> p (t e)")
        width = TILES * EXPERTS
        pe.matmul(rank_bank[:, 0:width], self.earlier[:, :], every, start=True, stop=False)
        for s in range(1, TILES):
            pe.matmul(rank_bank[:, s * EXPERTS:width], self.ones[:, :], every[:, 0:width - s * EXPERTS],
                      start=False, stop=(s == TILES - 1))
        pe.matmul(count_bank[:, 0:EXPERTS], self.ones[:, :], self.sum_parts[:, :], start=True,
                  stop=True).then_inc(self.ranked, 1)

    def vector(self, dve, chain, masks, rank_bank, count_bank):
        chain(dve.memset(self.ones[:, :], 1.0))
        dve.wait_ge(self.loaded, 16 * self.loads)
        chain(dve.tensor_copy(self.earlier[:, :], self.tri[:, :]))
        if self.picks == 1:
            chain(dve.tensor_copy(self.chosen[:, :, :], masks[0][:, :, :]))
        else:
            chain(dve.tensor_tensor(self.chosen[:, :, :], masks[0][:, :, :], masks[1][:, :, :], ALU.add))
        chain(dve.tensor_reduce(self.chosen_sum[:, :], self.chosen[:, :, :].rearrange("p t e -> p e t"),
                                AX_X, ALU.add))
        chain(dve.tensor_copy(self.sum_parts[:, :], self.chosen_sum[:, :]))
        dve.sem_inc(self.chosen_ready, 1)
        dve.wait_ge(self.ranked, 1)
        chain(dve.tensor_copy(self.counts[:, :], count_bank[:, 0:EXPERTS]))
        shape = [P, EXPERTS, TILES]
        chain(dve.tensor_tensor(self.more[:, :, :], self.counts[:, :].unsqueeze(2).to_broadcast(shape),
                                self.starts[:, :].unsqueeze(1).to_broadcast(shape), ALU.is_gt))
        chain(dve.tensor_reduce(self.tiles_of[:, :], self.more[:, :, :], AX_X, ALU.add))
        chain(dve.tensor_tensor(self.before[:, :, :], self.before[:, :, :],
                                self.tiles_of[:, :].unsqueeze(1).to_broadcast([P, EXPERTS, EXPERTS]), ALU.mult))
        chain(dve.tensor_reduce(self.begin[:, :], self.before[:, :, :], AX_X, ALU.add))
        chain(dve.tensor_scalar(self.counts[:, :], self.begin[:, :], float(P), None, ALU.mult))
        chain(dve.tensor_tensor(self.place[:, :, :], rank_bank[:, 0:TILES * EXPERTS].rearrange(
            "p (t e) -> p t e", t=TILES), tall(self.counts), ALU.add))
        for k in range(self.picks):
            chain(dve.tensor_tensor(self.own[:, :, :], self.place[:, :, :], masks[k][:, :, :], ALU.mult))
            chain(dve.tensor_reduce(self.position[:, :], self.own[:, :, :], AX_X, ALU.add))
            chain(dve.tensor_copy(self.slot[k][:, :], self.position[:, :]))
        dve.sem_inc(self.slots_ready, 1)
        chain(dve.tensor_tensor(self.begin[:, :], self.begin[:, :], self.tiles_of[:, :], ALU.add))
        shape = [P, self.tiles, EXPERTS]
        chain(dve.tensor_tensor(self.ended[:, :, :], self.begin[:, :].unsqueeze(1).to_broadcast(shape),
                                self.numbers[:, :].unsqueeze(2).to_broadcast(shape), ALU.is_le))
        chain(dve.tensor_reduce(self.expert[:, :], self.ended[:, :, :], AX_X, ALU.add))
        chain(dve.tensor_scalar(self.expert[:, :], self.expert[:, :], float(EXPERTS - 1), None, ALU.min))
        chain(dve.tensor_copy(self.expert_of[:, :], self.expert[:, :]))


def scatter_rows(pool, slot, t, source, scratch, scattered):
    pool.indirect_dma_start(out=scratch.rows, out_offset=bass.IndirectOffsetOnAxis(ap=slot[:, t:t + 1], axis=0),
                            in_=source[:, t, :], in_offset=None).then_inc(scattered, 16)


def gather_rows(pool, slot, t, target, scratch, gathered):
    pool.indirect_dma_start(out=target[:, t, :], out_offset=None, in_=scratch.results,
                            in_offset=bass.IndirectOffsetOnAxis(ap=slot[:, t:t + 1], axis=0)).then_inc(gathered, 16)


def expert_part(weights, e, at, width):
    return weights[:, bass.ds(e, 1), :].rearrange("p a n -> p (a n)")[:, at:at + width]


PARTS = 3


class SharedExperts:

    WIDTH, CHUNKS = 2 * P, 4
    TILES_EACH = WIDTH // P

    def __init__(self, st, weights, half_gate):
        self.chip, self.weights, self.half_gate = st.chip, weights, half_gate
        self.bank = st.chip.bank
        width, chunks = self.WIDTH, self.CHUNKS
        self.x_high, self.x_low = (st.sb(n, [P, 2, KD, width], BF16) for n in ("x_high", "x_low"))
        self.hidden_high, self.hidden_low = (st.sb(n, [P, 2, chunks, width], BF16) for n in ("s_high", "s_low"))
        self.squash, self.hidden = (st.sb(n, [P, 2, width]) for n in ("s_squash", "s_hidden"))
        self.x_high_ready, self.x_low_ready, self.h_ready, self.squashed = (st.sem(n) for n in (
            "x_high_ready", "x_low_ready", "s_h_ready", "s_squashed"))
        self.gated, self.hidden_ready, self.high_ready, self.low_ready = (st.sem(n) for n in (
            "s_gated", "s_hidden_ready", "s_high_ready", "s_low_ready"))
        self.out_ready, self.x_added = st.sem("s_out_ready"), st.sem("s_x_added")

    def up(self, pe, n):
        width = self.WIDTH
        pe.wait_ge(self.x_low_ready, n + 1)
        for c in range(self.CHUNKS):
            wait(pe, self.hidden_ready, self.CHUNKS * (n - 1) + c + 1)
            for branch in range(2):
                i = 0
                for x, w in ((self.x_high, 0), (self.x_low, 0), (self.x_high, 1)):
                    for k in range(KD):
                        i += 1
                        at = k * 4 * DIM + branch * 2 * DIM + c * P
                        last = pe.matmul(self.bank[:, c, branch * width:(branch + 1) * width],
                                         self.weights[w][:, at:at + P], x[:, n % 2, k, :],
                                         start=(i == 1), stop=(i == PARTS * KD))
            last.then_inc(self.h_ready, 1)

    def down(self, pe, n):
        pe.wait_ge(self.low_ready, self.CHUNKS * n + self.CHUNKS)
        for j in range(self.TILES_EACH):
            wait(pe, self.x_added, self.TILES_EACH * n + j - 1)
            i = 0
            for h, w in ((self.hidden_high, 0), (self.hidden_low, 0), (self.hidden_high, 1)):
                for c in range(self.CHUNKS):
                    i += 1
                    at = 8 * DIM + c * DIM
                    last = pe.matmul(self.bank[:, 4 + j, 0:DIM], h[:, n % 2, c, j * P:(j + 1) * P],
                                     self.weights[w][:, at:at + DIM], start=(i == 1), stop=(i == PARTS * self.CHUNKS))
            last.then_inc(self.out_ready, 1)

    def high_x(self, act, n):
        wait(act, self.h_ready, self.CHUNKS * (n - 1))
        act.activation(self.x_high[:, n % 2, :, :], self.chip.xnT[:, :, span(n, self.WIDTH)],
                       ACT.Copy).then_inc(self.x_high_ready, 1)

    def low_x(self, dve, n):
        dve.wait_ge(self.x_high_ready, n + 1)
        dve.tensor_tensor(self.x_low[:, n % 2, :, :], self.chip.xnT[:, :, span(n, self.WIDTH)],
                          self.x_high[:, n % 2, :, :], ALU.subtract).then_inc(self.x_low_ready, 1)

    def scalar(self, act, n):
        for c in range(self.CHUNKS):
            m = self.CHUNKS * n + c
            act.wait_ge(self.h_ready, m + 1)
            wait(act, self.gated, m - 1)
            act.activation(self.squash[:, c % 2, :], self.bank[:, c, 0:self.WIDTH], ACT.Tanh,
                           scale=0.5).then_inc(self.squashed, 1)
            act.wait_ge(self.hidden_ready, m + 1)
            if c == 0:
                wait(act, self.out_ready, self.TILES_EACH * (n - 1))
            act.activation(self.hidden_high[:, n % 2, c, :], self.hidden[:, c % 2, :], ACT.Copy).then_inc(self.high_ready, 1)

    def vector(self, dve, n):
        def low(c):
            dve.wait_ge(self.high_ready, self.CHUNKS * n + c + 1)
            dve.tensor_tensor(self.hidden_low[:, n % 2, c, :], self.hidden[:, c % 2, :], self.hidden_high[:, n % 2, c, :],
                              ALU.subtract).then_inc(self.low_ready, 1)

        for c in range(self.CHUNKS):
            m = self.CHUNKS * n + c
            dve.wait_ge(self.squashed, m + 1)
            wait(dve, self.low_ready, m - 1)
            dve.scalar_tensor_tensor(out=self.squash[:, c % 2, :], in0=self.squash[:, c % 2, :], scalar=1.0,
                                     in1=self.bank[:, c, 0:self.WIDTH], op0=ALU.add, op1=ALU.mult).then_inc(self.gated, 1)
            dve.wait_ge(self.gated, m + 1)
            dve.tensor_tensor(self.hidden[:, c % 2, :], self.squash[:, c % 2, :],
                              self.bank[:, c, self.WIDTH:2 * self.WIDTH], ALU.mult).then_inc(self.hidden_ready, 1)
            if c > 0:
                low(c - 1)
        low(self.CHUNKS - 1)

    def add(self, dve, n):
        for j in range(self.TILES_EACH):
            t = self.TILES_EACH * n + j
            dve.wait_ge(self.out_ready, t + 1)
            dve.scalar_tensor_tensor(out=nth(self.chip.x, t), in0=self.bank[:, 4 + j, 0:DIM], scalar=self.half_gate[:, 0:1],
                                     in1=nth(self.chip.x, t), op0=ALU.mult, op1=ALU.add).then_inc(self.x_added, 1)

    def tensor_part(self, pe, part, between=lambda n: None):
        self.up(pe, part[0])
        for n in part:
            if n + 1 in part:
                self.up(pe, n + 1)
            self.down(pe, n)
            between(n)

    def scalar_part(self, act, part, between=lambda n: None):
        self.high_x(act, part[0])
        for n in part:
            if n + 1 in part:
                self.high_x(act, n + 1)
            self.scalar(act, n)
            between(n)

    def vector_part(self, dve, part, between=lambda n: None):
        self.low_x(dve, part[0])
        for n in part:
            if n + 1 in part:
                self.low_x(dve, n + 1)
            self.vector(dve, n)
            if n > part[0]:
                self.add(dve, n - 1)
            between(n)
        self.add(dve, part[-1])


def silu_experts(chip, a, weights, ahead):
    nc = chip.nc
    gate = 4 + 0
    with ExitStack() as ctx:
        st = Stage(chip, "l0f", ctx)
        bank = chip.bank
        sb, sem = st.sb, st.sem
        scratch = chip.scratch[0]
        experts_width = EXPERTS * 6 * DIM
        split = weights[:, :, 0:experts_width].rearrange("p w (e n) -> p w e n", e=EXPERTS)
        width = split.shape[3]
        sort = Sorting(st, 2)
        clearing = Clearing(st, scratch, 4, 1, 2)
        bg, order = sb("gate_bias", [P, EXPERTS]), sb("order", [P, EXPERTS])
        scores, biased, work = (sb(n, [P, TILES, EXPERTS]) for n in ("scores", "biased", "work"))
        masks = [sb(f"mask{k}", [P, TILES, EXPERTS]) for k in range(2)]
        weight = [sb(f"weight{k}", [P, TILES]) for k in range(2)]
        column, half_gate = sb("column", [P, TILES]), sb("half_gate", [P, 1])
        loaded, logits_ready, chained = sem("loaded"), sem("logits_ready"), sem("chained")
        weighed = sem("weighed")
        shared = SharedExperts(st, [weights[:, n, experts_width:] for n in range(2)], half_gate)
        blocks = range(TOKENS // SharedExperts.WIDTH)
        parts = blocks[:len(blocks) // 2], blocks[len(blocks) // 2:]
        exp_wanted, exp_ready, scattered = sem("exp_wanted"), sem("exp_ready"), sem("scattered")

        with nc.Block() as block:
            @block.sync
            def _(sp):
                sp.dma_start(bg[:, :], a["L0_ffn_gate_bias"].partition_broadcast(P)).then_inc(loaded, 16)
                sp.dma_start(order[:, :], a["order"].partition_broadcast(P)).then_inc(loaded, 16)
                sort.sync(sp, a)
                for n in range(clearing.strips):
                    clearing.sync(sp, n)
                clearing.finish(sp)

            @block.tensor
            def _(pe):
                chip.logits.rest(pe, logits_ready)
                pe.wait_ge(loaded, 32)
                sort.tensor(pe, bank[:, 1, :], bank[:, 2, :])

            @block.scalar
            def _(act):
                act.wait_ge(exp_wanted, 1)
                act.activation(scores[:, :, :], scores[:, :, :], ACT.Exp).then_inc(exp_ready, 1)

            @block.vector
            def _(dve):
                clearing.vector(dve)
                chain = Chain(dve, chained)
                dve.wait_ge(loaded, 32)
                dve.wait_ge(logits_ready, 1)
                logits = bank[:, 0, 0:TILES * EXPERTS].rearrange("p (t e) -> p t e", t=TILES)
                chain(dve.tensor_reduce(column[:, :], logits, AX_X, ALU.max))
                chain(dve.tensor_tensor(scores[:, :, :], logits, wide(column), ALU.subtract))
                dve.sem_inc(exp_wanted, 1)
                dve.wait_ge(exp_ready, 1)
                chain(dve.tensor_reduce(column[:, :], scores[:, :, :], AX_X, ALU.add))
                chain(dve.reciprocal(column[:, :], column[:, :]))
                chain(dve.tensor_tensor(scores[:, :, :], scores[:, :, :], wide(column), ALU.mult))
                chain(dve.tensor_tensor(biased[:, :, :], scores[:, :, :], tall(bg), ALU.add))
                pick_largest(dve, chain, biased, order, masks[0], work, column)
                chain(dve.scalar_tensor_tensor(out=biased[:, :, :], in0=masks[0][:, :, :], scalar=-HIDE,
                                               in1=biased[:, :, :], op0=ALU.mult, op1=ALU.add))
                pick_largest(dve, chain, biased, order, masks[1], work, column)
                sort.vector(dve, chain, masks, bank[:, 1, :], bank[:, 2, :])
                chain(dve.tensor_scalar(half_gate[:, :], chip.gate[:, gate:gate + 1], 0.5, None, ALU.mult))

        with nc.Block() as block:
            @block.gpsimd
            def _(pool):
                for k in range(2):
                    for t in range(TILES):
                        scatter_rows(pool, sort.slot[k], t, chip.keep, scratch, scattered)
                pool.wait_ge(scattered, 16 * 2 * TILES)

            @block.tensor
            def _(pe):
                shared.tensor_part(pe, parts[0])

            @block.scalar
            def _(act):
                shared.scalar_part(act, parts[0])

            @block.vector
            def _(dve):
                chain = Chain(dve, weighed)
                for k in range(2):
                    chain(dve.tensor_tensor(work[:, :, :], scores[:, :, :], masks[k][:, :, :], ALU.mult))
                    chain(dve.tensor_reduce(weight[k][:, :], work[:, :, :], AX_X, ALU.add))
                    chain(dve.tensor_scalar(weight[k][:, :], weight[k][:, :], half_gate[:, 0:1], None, ALU.mult))
                shared.vector_part(dve, parts[0])

        with ExitStack() as inner:
            st3 = Stage(chip, "l0r", inner)
            n = sort.tiles
            lanes = SlotLanes(st3, scratch, bank[:, 7, :], n, sort.expert_of)
            placed = PlacedWeights(st3, split, 4 * DIM, lanes.AHEAD)
            hidden_high, hidden_low = (st3.sb(nm, [P, 2, DIM], BF16) for nm in ("hidden_high", "hidden_low"))
            squash, hidden = (st3.sb(nm, [P, 2, DIM]) for nm in ("squash", "hidden"))
            sem3 = st3.sem
            h_ready, squashed, gated, hidden_ready = (sem3(nm) for nm in (
                "h_ready", "squashed", "gated", "hidden_ready"))
            high_ready, low_ready = sem3("high_ready"), sem3("low_ready")
            block = inner.enter_context(nc.Block())

            @block.sync
            def _(sp):
                lanes.sync(sp, placed, h_ready)

            @block.tensor
            def _(pe):
                def up(i, q):
                    j, u = lanes.AHEAD * i + q, q % 2
                    placed.ready(pe, i, q)
                    pe.wait_ge(lanes.low_ready, j + 1)
                    wait(pe, hidden_ready, j - 1)
                    for m in range(4):
                        s = 0
                        for x, w in ((lanes.high, 0), (lanes.low, 0), (lanes.high, 1)):
                            for k in range(KD):
                                s += 1
                                at = k * 2 * DIM + m * P
                                last = pe.matmul(bank[:, u, m * P:(m + 1) * P], placed.parts[w][:, q, at:at + P],
                                                 x[:, u, k, :], start=(s == 1), stop=(s == PARTS * KD))
                    last.then_inc(h_ready, 1)

                def down(i, q):
                    j, u = lanes.AHEAD * i + q, q % 2
                    e = lanes.expert(pe, j)
                    pe.wait_ge(low_ready, j + 1)
                    wait(pe, lanes.y_copied, j - 1)
                    s = 0
                    for h, w in ((hidden_high, 0), (hidden_low, 0), (hidden_high, 1)):
                        for c in range(KD):
                            s += 1
                            last = pe.matmul(bank[:, 2 + u, 0:DIM], h[:, u, c * P:(c + 1) * P],
                                             expert_part(split[:, w, :, :], e, 4 * DIM + c * DIM, DIM), start=(s == 1), stop=(s == PARTS * KD))
                    last.then_inc(lanes.y_ready, 1)

                lanes.tensor_loop(pe, up, down)

            @block.scalar
            def _(act):
                def step(i, q):
                    j, u = lanes.AHEAD * i + q, q % 2
                    act.wait_ge(h_ready, j + 1)
                    wait(act, gated, j - 1)
                    act.activation(squash[:, u, :], bank[:, u, 0:DIM], ACT.Tanh, scale=0.5).then_inc(squashed, 1)
                    act.wait_ge(hidden_ready, j + 1)
                    wait(act, lanes.y_ready, j - 1)
                    act.activation(hidden_high[:, u, :], hidden[:, u, :], ACT.Copy).then_inc(high_ready, 1)
                lanes.scalar_loop(act, step, bank)

            @block.vector
            def _(dve):
                def step(i, q):
                    j, u = lanes.AHEAD * i + q, q % 2
                    dve.wait_ge(squashed, j + 1)
                    wait(dve, low_ready, j - 1)
                    dve.scalar_tensor_tensor(out=squash[:, u, :], in0=squash[:, u, :], scalar=1.0,
                                             in1=bank[:, u, 0:DIM], op0=ALU.add, op1=ALU.mult).then_inc(gated, 1)
                    dve.wait_ge(gated, j + 1)
                    dve.tensor_tensor(hidden[:, u, :], squash[:, u, :], bank[:, u, DIM:2 * DIM],
                                      ALU.mult).then_inc(hidden_ready, 1)
                lanes.vector_loop(dve, step, bank)

            @block.gpsimd
            def _(pool):
                def step(i, q):
                    j, u = lanes.AHEAD * i + q, q % 2
                    pool.wait_ge(high_ready, j + 1)
                    pool.tensor_tensor(hidden_low[:, u, :], hidden[:, u, :], hidden_high[:, u, :],
                                       ALU.subtract).then_inc(low_ready, 1)
                lanes.gpsimd_loop(pool, step)

        combine(chip, "l0c", ahead, sort, scratch, weight, {}, shared, parts[1])


class PlacedWeights:

    def __init__(self, st, split, width, slots, room=None):
        self.split, self.width, self.slots = split, width, slots
        self.room = room or st.sb("placed", [P, slots, 2, width], BF16)
        self.parts = [self.room[:, :, n, :] for n in range(2)]
        self.copied = [st.sem(f"placed{q}") for q in range(slots)]

    def copy(self, sp, lanes, i, q, e, released):
        slot = q % self.slots
        wait(sp, released, lanes.AHEAD * i + q - self.slots + 1)
        sp.dma_start(self.room[:, slot, :, :],
                     self.split[:, :, bass.ds(e, 1), 0:self.width].rearrange("p w a n -> p w (a n)")).then_inc(
            self.copied[slot], 16)

    def ready(self, pe, i, q):
        rounds = SlotLanes.AHEAD // self.slots
        pe.wait_ge(self.copied[q % self.slots], 16 * (rounds * i + q // self.slots) + 16)


class TileConstants:

    def __init__(self, st, columns, rows):
        self.columns, self.rows = columns, rows
        self.columns_now = st.sb("columns_now", [P, SlotLanes.AHEAD, columns.shape[2]])
        self.row_now = st.sb("row_now", [P, SlotLanes.AHEAD, DIM])
        self.loaded = [st.sem(f"constants_loaded{q}") for q in range(SlotLanes.AHEAD)]

    def load(self, sp, lanes, i, q, e):
        wait(sp, lanes.y_copied, lanes.AHEAD * i + q - lanes.AHEAD + 1)
        sp.dma_start(self.columns_now[:, q, :], self.columns[:, bass.ds(e, 1), :].rearrange("p a n -> p (a n)")).then_inc(
            self.loaded[q], 16)
        sp.dma_start(self.row_now[:, q, :],
                     self.rows[bass.ds(e, 1), :].rearrange("a n -> (a n)").partition_broadcast(P)).then_inc(
            self.loaded[q], 16)

    def ready(self, eng, i, q):
        eng.wait_ge(self.loaded[q], 32 * i + 32)


class SlotLanes:

    AHEAD = 4

    def __init__(self, st, scratch, turn_bank, n, expert_of, room=None, constants=None):
        self.chip, self.scratch, self.turn_bank, self.n = st.chip, scratch, turn_bank, n
        self.expert_of, self.constants = expert_of, constants
        sb, sem = st.sb, st.sem
        if room is None:
            room = sb("room", [P, self.AHEAD + 2, DIM])
        self.rows, self.y = room[:, 0:self.AHEAD, :], room[:, self.AHEAD:self.AHEAD + 2, :]
        self.high, self.low = (sb(nm, [P, 2, KD, P], BF16) for nm in ("xT_high", "xT_low"))
        self.rows_loaded = [sem(f"rows_loaded{u}") for u in range(self.AHEAD)]
        self.turned, self.high_ready, self.low_ready = sem("turned"), sem("xT_high_ready"), sem("xT_low_ready")
        if constants is not None:
            self.scaled = sb("xT_scaled", [P, 2, KD, P])
            self.scaled_ready = sem("xT_scaled_ready")
        self.y_ready, self.y_copied = sem("y_ready"), sem("y_copied")
        self.stored = [sem(f"stored{u}") for u in range(2)]

    def rows_of(self, dram, j):
        return dram[span(j, P), :]

    def expert(self, eng, j):
        at = self.expert_of[0:1, j:j + 1] if isinstance(j, int) else self.expert_of[0:1, bass.ds(j, 1)]
        return eng.value_load(at, min_val=0, max_val=EXPERTS - 1)

    def sync(self, sp, placed, released):
        def load(i, q):
            j = self.AHEAD * i + q
            wait(sp, self.turned, j - self.AHEAD + 1)
            sp.dma_start(self.rows[:, q, :], self.rows_of(self.scratch.rows, j)).then_inc(self.rows_loaded[q], 16)

        def bring(i, q):
            e = self.expert(sp, self.AHEAD * i + q)
            if self.constants is not None:
                self.constants.load(sp, self, i, q, e)
            placed.copy(sp, self, i, q, e, released)

        for q in range(self.AHEAD):
            load(0, q)
            if q < placed.slots:
                bring(0, q)

        def step(i):
            for q in range(self.AHEAD):
                last = is_step(i, self.n // self.AHEAD - 1)
                if not last:
                    load(i + 1, q)
                if not (last and q + placed.slots >= self.AHEAD):
                    bring(i + (q + placed.slots) // self.AHEAD, (q + placed.slots) % self.AHEAD)
        steps(sp, self.n // self.AHEAD, step)

    def gpsimd_loop(self, pool, body):
        def store(i, q):
            j = self.AHEAD * i + q
            pool.wait_ge(self.y_copied, j + 1)
            pool.dma_start(self.rows_of(self.scratch.results, j), self.y[:, q % 2, :]).then_inc(self.stored[q % 2], 16)

        self.quads(pool, lambda i, q: None, body, store)
        for u in range(2):
            pool.wait_ge(self.stored[u], 16 * (self.n // 2))

    def tensor_loop(self, pe, up, down):
        def turn(i, q):
            j = self.AHEAD * i + q
            pe.wait_ge(self.rows_loaded[q], 16 * i + 16)
            wait(pe, self.scaled_ready if self.constants else self.low_ready, j)
            for k in range(KD):
                last = pe.transpose(self.turn_bank[:, k * P:(k + 1) * P], self.rows[:, q, k * P:(k + 1) * P],
                                    self.chip.ident[:, :])
            last.then_inc(self.turned, 1)

        groups = self.n // self.AHEAD
        turn(0, 0)

        def step(i):
            for q in range(self.AHEAD):
                j = self.AHEAD * i + q
                if q + 1 < self.AHEAD:
                    turn(i, q + 1)
                elif not is_step(i, groups - 1):
                    turn(i + 1, 0)
                up(i, q)
                if q > 0:
                    down(i, q - 1)
                elif not is_step(i, 0):
                    down(i - 1, self.AHEAD - 1)
        steps(pe, groups, step)
        down(groups - 1, self.AHEAD - 1)

    def y_stored(self, eng, i, q):
        wait(eng, self.stored[q % 2], 16 * (self.AHEAD // 2 * i + q // 2))

    def quads(self, eng, split, body, finish):
        groups = self.n // self.AHEAD
        split(0, 0)

        def step(i):
            for q in range(self.AHEAD):
                if q + 1 < self.AHEAD:
                    split(i, q + 1)
                elif not is_step(i, groups - 1):
                    split(i + 1, 0)
                body(i, q)
                if q > 0:
                    finish(i, q - 1)
                elif not is_step(i, 0):
                    finish(i - 1, self.AHEAD - 1)
        steps(eng, groups, step)
        finish(groups - 1, self.AHEAD - 1)

    def turned_rows(self):
        return self.turn_bank[:, 0:DIM].rearrange("p (k n) -> p k n", k=KD)

    def scalar_loop(self, act, body, bank):
        def split(i, q):
            j, u = self.AHEAD * i + q, q % 2
            act.wait_ge(self.turned, j + 1)
            rows = self.turned_rows()
            if self.constants is not None:
                self.constants.ready(act, i, q)
                wait(act, self.low_ready, j - 1)
                columns = self.constants.columns_now
                for k in range(KD):
                    last = act.activation(self.scaled[:, u, k, :], self.turn_bank[:, k * P:(k + 1) * P], ACT.Identity,
                                          scale=columns[:, q, k:k + 1], bias=columns[:, q, KD + k:KD + k + 1])
                last.then_inc(self.scaled_ready, 1)
                act.wait_ge(self.scaled_ready, j + 1)
                rows = self.scaled[:, u, :, :]
            wait(act, self.y_ready, j - 2)
            act.activation(self.high[:, u, :, :], rows, ACT.Copy).then_inc(self.high_ready, 1)

        def copy_y(i, q):
            if self.constants is None:
                act.wait_ge(self.y_ready, self.AHEAD * i + q + 1)
                self.y_stored(act, i, q)
                act.activation(self.y[:, q % 2, :], bank[:, 2 + q % 2, 0:DIM], ACT.Copy).then_inc(self.y_copied, 1)

        self.quads(act, split, body, copy_y)

    def vector_loop(self, dve, body, bank):
        def split(i, q):
            dve.wait_ge(self.high_ready, self.AHEAD * i + q + 1)
            rows = self.turned_rows() if self.constants is None else self.scaled[:, q % 2, :, :]
            dve.tensor_tensor(self.low[:, q % 2, :, :], rows, self.high[:, q % 2, :, :],
                              ALU.subtract).then_inc(self.low_ready, 1)

        def add_bias(i, q):
            if self.constants is not None:
                dve.wait_ge(self.y_ready, self.AHEAD * i + q + 1)
                self.y_stored(dve, i, q)
                dve.tensor_tensor(self.y[:, q % 2, :], bank[:, 2 + q % 2, 0:DIM], self.constants.row_now[:, q, :],
                                  ALU.add).then_inc(self.y_copied, 1)

        self.quads(dve, split, body, add_bias)


def combine(chip, name, ahead, sort, scratch, weight, norm_args, shared=None, part=(), areas=()):
    with ExitStack() as inner:
        st = LentStage(chip, name, inner, areas)
        groups = 4
        per = TILES // groups
        norm = NextNorm(st, [chip.bank[:, n, :] for n in (6, 7)], depth=2 * per, **norm_args)
        targets = [chip.keep] + [st.sb(f"gathered{k}", [P, TILES, DIM]) for k in range(1, sort.picks)]
        gathered = [st.sem(f"gathered{g}") for g in range(groups)]
        part_added = st.sem("part_added")
        early = 2

        def buffers(g):
            return [(per * g + u, g % 2 * per + u) for u in range(per)]

        def in_turn(shared_part, eng, group, after):
            beside = groups // 2 if shared_part else 0
            if shared_part:
                shared_part(eng, part, lambda n: group(n - part[after]) if n in part[after:after + beside] else None)
            for g in range(beside, groups + 1):
                group(g)

        block = inner.enter_context(chip.nc.Block())

        @block.sync
        def _(sp):
            sp.wait_ge(gathered[groups - 1], 16 * per * sort.picks)
            ahead.sync(sp)

        @block.gpsimd
        def _(pool):
            for g in range(groups + early):
                for t in range(per * g, min(per * g + per, TILES)):
                    for k in range(sort.picks):
                        gather_rows(pool, sort.slot[k], t, targets[k], scratch, gathered[g])
                if g >= early:
                    norm.gpsimd(pool, *buffers(g - early)[0], per)

        @block.vector
        def _(dve):
            def add_up(g):
                dve.wait_ge(gathered[g], 16 * per * sort.picks)
                for k in range(sort.picks):
                    for t, u in buffers(g):
                        if k > 0:
                            dve.wait_ge(part_added, (sort.picks - 1) * t + k)
                        dve.scalar_tensor_tensor(out=chip.x[:, t, :], in0=targets[k][:, t, :], scalar=weight[k][:, t:t + 1],
                                                 in1=chip.x[:, t, :], op0=ALU.mult, op1=ALU.add).then_inc(
                            norm.x_updated if k == sort.picks - 1 else part_added, 1)
                norm.vector_stats(dve, *buffers(g))

            def group(g):
                if g < groups:
                    add_up(g)
                if g > 0:
                    for t, u in buffers(g - 1):
                        norm.vector_apply(dve, t, u)

            in_turn(shared and shared.vector_part, dve, group, 0)

        @block.tensor
        def _(pe):
            def group(g):
                if g > 0:
                    for t, u in buffers(g - 1):
                        norm.tensor(pe, t, u)
            in_turn(shared and shared.tensor_part, pe, group, 2)

        @block.scalar
        def _(act):
            def group(g):
                if g > 0:
                    for t, u in buffers(g - 1):
                        norm.scalar(act, t, u)
            in_turn(shared and shared.scalar_part, act, group, 2)


def relu_experts(chip, a, weights, split_before, ahead):
    nc = chip.nc
    gate = 4 + 1
    with ExitStack() as ctx:
        st = Stage(chip, "l1f", ctx)
        bank = chip.bank
        sb, sem = st.sb, st.sem
        scratch = chip.scratch[1]
        hidden_width = (a["L1_ffn_columns"].shape[2] - 2 * KD) * P
        chunks = hidden_width // P
        per_expert = KD * hidden_width + chunks * DIM
        sort = Sorting(st, 1)
        order = sb("order", [P, EXPERTS])
        columns = sb("columns", [P, EXPERTS, 2 * KD + chunks])
        latent_g, latent_b = sb("ln_l_g", [P, KD]), sb("ln_l_b", [P, KD])
        nearness, work, mask = (sb(n, [P, TILES, EXPERTS]) for n in ("nearness", "work", "mask"))
        weight, column = sb("weight", [P, TILES]), sb("column", [P, TILES])
        high, low = (weights[:, n, :] for n in range(2))
        split = weights[:, :, :].rearrange("p w (e n) -> p w e n", e=EXPERTS)
        loaded, logits_ready, chained = sem("loaded"), sem("logits_ready"), sem("chained")
        scattered = sem("scattered")
        tanh_wanted, tanh_ready = sem("tanh_wanted"), sem("tanh_ready")
        columns_loaded = sem("columns_loaded")

        chunk, slots = 1024, 4
        group = slots
        first = split_before // chunk
        groups = (EXPERTS * per_expert // chunk - first) // group
        by_gpsimd = groups // 2
        staging = chip.room[:, 0:slots * chunk].rearrange("p (s n) -> p s n", s=slots)
        w_loaded, w_split = [sem(f"w_loaded{q}") for q in range(slots)], [sem(f"w_split{q}") for q in range(slots)]
        high_ready = sem("w_high_ready")

        def load_weights(sp, g):
            for n in range(group):
                c, turn = group * g + n, g
                wait(sp, w_split[n % slots], turn)
                sp.dma_start(staging[:, n % slots, :], a["L1_ffn_weights"][:, span(first + c, chunk)]).then_inc(
                    w_loaded[n % slots], 16)

        def high_parts(act, g):
            for n in range(group):
                c, turn = group * g + n, g
                act.wait_ge(w_loaded[n % slots], 16 * turn + 16)
                act.activation(high[:, span(first + c, chunk)], staging[:, n % slots, :], ACT.Copy).then_inc(high_ready, 1)

        def low_parts(eng, g):
            for n in range(group):
                c = group * g + n
                eng.wait_ge(high_ready, c + 1)
                eng.tensor_tensor(low[:, span(first + c, chunk)], staging[:, n % slots, :], high[:, span(first + c, chunk)],
                                  ALU.subtract).then_inc(w_split[n % slots], 1)

        with nc.Block() as block:
            @block.sync
            def _(sp):
                sp.dma_start(order[:, :], a["order"].partition_broadcast(P)).then_inc(loaded, 16)
                sort.sync(sp, a)
                load_weights(sp, 0)
                sp.dma_start(columns[:, :, :], a["L1_ffn_columns"]).then_inc(columns_loaded, 16)
                for rows, w in ((latent_g, "ln_l_g"), (latent_b, "ln_l_b")):
                    sp.dma_start(rows[:, :], a[f"L2_xattn_{w}"]).then_inc(columns_loaded, 16)
                for g in range(1, groups):
                    load_weights(sp, g)
                sp.wait_ge(columns_loaded, 16 * 3)

            @block.tensor
            def _(pe):
                chip.logits.rest(pe, logits_ready)
                pe.wait_ge(loaded, 16)
                sort.tensor(pe, bank[:, 1, :], bank[:, 2, :])

            @block.scalar
            def _(act):
                act.wait_ge(tanh_wanted, 1)
                act.activation(weight[:, :], weight[:, :], ACT.Tanh, scale=0.5).then_inc(tanh_ready, 1)
                for g in range(groups):
                    high_parts(act, g)

            @block.vector
            def _(dve):
                chain = Chain(dve, chained)
                dve.wait_ge(loaded, 16)
                dve.wait_ge(logits_ready, 1)
                chain(dve.tensor_copy(nearness[:, :, :], bank[:, 0, 0:TILES * EXPERTS].rearrange(
                    "p (t e) -> p t e", t=TILES)))
                chain(dve.tensor_reduce(weight[:, :], nearness[:, :, :], AX_X, ALU.max))
                dve.sem_inc(tanh_wanted, 1)
                pick_largest(dve, chain, nearness, order, mask, work, column)
                dve.wait_ge(tanh_ready, 1)
                chain(dve.tensor_scalar(weight[:, :], weight[:, :], 0.5, 0.5, ALU.mult, ALU.add))
                chain(dve.tensor_scalar(weight[:, :], weight[:, :], chip.gate[:, gate:gate + 1], None, ALU.mult))
                sort.vector(dve, chain, [mask], bank[:, 1, :], bank[:, 2, :])
                for g in range(by_gpsimd, groups):
                    low_parts(dve, g)

            @block.gpsimd
            def _(pool):
                for g in range(by_gpsimd):
                    low_parts(pool, g)
                pool.wait_ge(sort.slots_ready, 1)
                for t in range(TILES):
                    scatter_rows(pool, sort.slot[0], t, chip.keep, scratch, scattered)
                pool.wait_ge(scattered, 16 * TILES)


        with ExitStack() as inner:
            st2 = LentStage(chip, "l1r", inner, [chip.room])
            n = sort.tiles
            hidden_high, hidden_low = (st2.sb(nm, [P, 2, hidden_width], BF16) for nm in ("hidden_high", "hidden_low"))
            lane_tiles = hidden_width // DIM
            lanes = SlotLanes(st2, scratch, bank[:, 7, :], n, sort.expert_of, chip.keep[:, 2 * lane_tiles:, :],
                              TileConstants(st2, columns, a["L1_ffn_b2"]))
            hidden = [chip.keep[:, u * lane_tiles:(u + 1) * lane_tiles, :].rearrange("p a n -> p (a n)") for u in range(2)]
            places = chip.xnT[:, :, :].rearrange("p k n -> p (k n)").bitcast(BF16).rearrange(
                "p (s w n) -> p s w n", w=2, s=2)
            placed = PlacedWeights(st2, split, KD * hidden_width, 2, places)
            h_banks = hidden_width // 512
            h_bank = [bank[:, 4 * u:4 * u + h_banks, :].rearrange("p a n -> p (a n)") for u in range(2)]
            h_ready, biased, high_ready, low_ready = (st2.sem(nm) for nm in (
                "h_ready", "biased", "high_ready", "low_ready"))
            block = inner.enter_context(nc.Block())

            @block.sync
            def _(sp):
                lanes.sync(sp, placed, h_ready)

            @block.gpsimd
            def _(pool):
                lanes.gpsimd_loop(pool, lambda i, q: None)

            @block.tensor
            def _(pe):
                def up(i, q):
                    j, u = lanes.AHEAD * i + q, q % 2
                    placed.ready(pe, i, q)
                    pe.wait_ge(lanes.low_ready, j + 1)
                    wait(pe, biased, j - 1)
                    for m in range(chunks):
                        s = 0
                        for x, w in ((lanes.high, 0), (lanes.low, 0), (lanes.high, 1)):
                            for k in range(KD):
                                s += 1
                                at = k * hidden_width + m * P
                                last = pe.matmul(h_bank[u][:, m * P:(m + 1) * P], placed.parts[w][:, u, at:at + P],
                                                 x[:, u, k, :], start=(s == 1), stop=(s == PARTS * KD))
                    last.then_inc(h_ready, 1)

                def down(i, q):
                    j, u = lanes.AHEAD * i + q, q % 2
                    e = lanes.expert(pe, j)
                    pe.wait_ge(low_ready, j + 1)
                    wait(pe, lanes.y_copied, j - 1)
                    s = 0
                    for h, w in ((hidden_high, 0), (hidden_low, 0), (hidden_high, 1)):
                        for c in range(chunks):
                            s += 1
                            last = pe.matmul(bank[:, 2 + u, 0:DIM], h[:, u, c * P:(c + 1) * P],
                                             expert_part(split[:, w, :, :], e, KD * hidden_width + c * DIM, DIM),
                                             start=(s == 1), stop=(s == PARTS * chunks))
                    last.then_inc(lanes.y_ready, 1)

                lanes.tensor_loop(pe, up, down)

            @block.scalar
            def _(act):
                def step(i, q):
                    j, u = lanes.AHEAD * i + q, q % 2
                    act.wait_ge(biased, j + 1)
                    wait(act, lanes.y_ready, j - 1)
                    act.activation(hidden_high[:, u, :], hidden[u], ACT.Relu).then_inc(high_ready, 1)
                lanes.scalar_loop(act, step, bank)

            @block.vector
            def _(dve):
                def step(i, q):
                    j, u = lanes.AHEAD * i + q, q % 2
                    lanes.constants.ready(dve, i, q)
                    dve.wait_ge(h_ready, j + 1)
                    wait(dve, low_ready, j - 1)
                    dve.tensor_tensor(hidden[u].rearrange("p (c n) -> p c n", c=chunks),
                                      h_bank[u].rearrange("p (c n) -> p c n", c=chunks),
                                      lanes.constants.columns_now[:, q, 2 * KD:].unsqueeze(2).to_broadcast([P, chunks, P]),
                                      ALU.add).then_inc(biased, 1)
                    dve.wait_ge(high_ready, j + 1)
                    dve.scalar_tensor_tensor(out=hidden_low[:, u, :], in0=hidden[u], scalar=0.0, in1=hidden_high[:, u, :],
                                             op0=ALU.max, op1=ALU.subtract).then_inc(low_ready, 1)
                lanes.vector_loop(dve, step, bank)

        combine(chip, "l1c", ahead, sort, scratch, [weight], {"affine": (latent_g, latent_b)},
                areas=[weights[:, 0, :].bitcast(F32)])

def layer0(chip, a, given, ahead):
    with ExitStack() as ctx:
        st = Stage(chip, "l0", ctx)
        width = a["L0_ffn_weights"].shape[1]
        weights = st.sb("weights", [P, 2, width], BF16)
        with ExitStack() as inner:
            feed = Feed(Stage(chip, "l0w", inner), a["L0_ffn_weights"], weights[:, 0, :], weights[:, 1, :],
                        width // TILES)
            single_head_attention(chip, given, feed)
        silu_experts(chip, a, weights, ahead)


def layer1(chip, a, given, ahead):
    with ExitStack() as ctx:
        st = Stage(chip, "l1", ctx)
        width = a["L1_ffn_weights"].shape[1]
        weights = st.sb("weights", [P, 2, width], BF16)
        part = 3 * width // EXPERTS
        with ExitStack() as inner:
            lent = [weights[:, n, part:].bitcast(F32) for n in range(2)]
            staging = 2 * part // TILES
            feed = Feed(LentStage(chip, "l1w", inner, [lent[0][:, 0:staging]]), a["L1_ffn_weights"][:, 0:part], weights[:, 0, 0:part],
                        weights[:, 1, 0:part], part // TILES)
            multi_head_attention(chip, given, 1, 1, lambda st: {"keep_again": chip.keep, "share": chip.gate[:, 5:6]},
                                 feed, chip.scratch[1], [lent[0][:, staging:], lent[1]])
        chip.release()
        relu_experts(chip, a, weights, part, ahead)


def layer2(chip, a, given, ahead):
    latent_attention(chip, given)
    chip.release()
    relu_square_experts(chip, a, ahead)


def layer3(chip, a, given, ahead):
    with ExitStack() as ctx:
        st = Stage(chip, "l3", ctx)
        width = a["L3_ffn_We"].shape[1]
        high, low = (st.sb(n, [P, width], BF16) for n in ("We_high", "We_low"))
        with ExitStack() as inner:
            feed = Feed(Stage(chip, "l3w", inner), a["L3_ffn_We"], high, low, width // TILES)
            multi_head_attention(chip, given, 3, 3, lambda st: {}, feed)
        linear_experts(chip, a, high, low, chip.out)


LAYERS = [layer0, layer1, layer2, layer3]




def attention_loads(chip, a, layer, ctx):
    if layer == 0:
        return ContextOfOneHead(chip, a, ctx)
    if layer == 2:
        return latent_loads(chip, a)
    if layer < len(LAYERS):
        return multi_head_loads(chip, a, layer)
    return Loads(chip, "none")


def program(nc, a, out):
    with ExitStack() as ctx:
        chip = Chip(nc, ctx)
        chip.out = out
        chip.scratch = [Scratch(nc, "l0", slot_tiles(2) * P), Scratch(nc, "l1", slot_tiles(1) * P)]
        first = ctx.enter_context(ExitStack())
        given = attention_loads(chip, a, 0, first)
        begin(chip, a, given)
        for n in range(len(LAYERS)):
            ahead = attention_loads(chip, a, n + 1, first)
            LAYERS[n](chip, a, given, ahead)
            chip.release()
            first.close()
            given = ahead


def lay_out(inputs):
    import numpy as np

    a = {}
    a["x"] = inputs["x"].reshape(TOKENS, DIM)
    a["ctxT"] = inputs["ctx_1024"].reshape(CTX, DIM).T
    a["g_xattn"], a["g_ffn"] = inputs["g_xattn"], inputs["g_ffn"]
    a["ident"] = np.eye(P, dtype=np.float32)
    for n in ("Wq", "Wk", "Wv"):
        a[f"L0_xattn_{n}"] = inputs[f"L0_xattn_{n}"].T
    for n in ("bq", "bk"):
        a[f"L0_xattn_{n}"] = inputs[f"L0_xattn_{n}"].reshape(KD, P).T
    a["L0_xattn_bv"] = inputs["L0_xattn_bv"]
    for n in ("Wq", "Wk", "Wv", "Wo"):
        a[f"L1_xattn_{n}"] = inputs[f"L1_xattn_{n}"].T
    a["key_bias"] = inputs["fside_BxS2_0"].reshape(CTX)
    a["head_of"] = np.kron(np.eye(CHUNK_HEADS, dtype=np.float32), np.ones((HEAD, 1), np.float32))
    a["L3_xattn_Wq"], a["L3_xattn_Wo"] = inputs["L3_xattn_Wq"], inputs["L3_xattn_Wp"]
    kv = inputs["L3_xattn_Wkv"].reshape(DIM, HEADS, 2, HEAD)
    a["L3_xattn_Wk"], a["L3_xattn_Wv"] = (kv[:, :, n, :].reshape(DIM, DIM) for n in range(2))
    kv = inputs["L3_xattn_bkv"].reshape(HEADS, 2, HEAD)
    a["L3_xattn_bk"], a["L3_xattn_bv"] = kv[:, 0, :].reshape(KD, P).T, kv[:, 1, :].reshape(DIM)
    a["L3_xattn_bq"] = inputs["L3_xattn_bq"].reshape(KD, P).T
    a["L3_xattn_bp"] = inputs["L3_xattn_bp"]
    for n in ("W_q", "W_kv", "W_out", "b_out", "q_gamma", "k_gamma"):
        a[f"L2_xattn_{n}"] = inputs[f"L2_xattn_{n}"]
    for n in ("ln_x_g", "ln_x_b", "ln_l_g", "ln_l_b"):
        a[f"L2_xattn_{n}"] = inputs[f"L2_xattn_{n}"].reshape(KD, P).T
    a["context"] = inputs["ctx_1024"].reshape(CTX, DIM)
    a["mask"] = inputs["mask_BxS2_bk0"].reshape(CTX)
    a["order"] = np.arange(EXPERTS, dtype=np.float32) - EXPERTS
    for n in ("Ws1", "Ws2", "Wr"):
        a[f"L2_ffn_{n}"] = inputs[f"L2_ffn_{n}"]
    a["L2_ffn_W1"] = inputs["L2_ffn_W1"].reshape(EXPERTS, KD, P, P).transpose(0, 2, 1, 3).reshape(EXPERTS, P, DIM)
    a["L2_ffn_W2"] = inputs["L2_ffn_W2"]
    for n in ("Wg", "bg", "be"):
        a[f"L3_ffn_{n}"] = inputs[f"L3_ffn_{n}"]
    a["L3_ffn_We"] = inputs["L3_ffn_We"].reshape(EXPERTS, DIM, KD, P).transpose(3, 2, 0, 1).reshape(P, -1)
    a["tri"] = np.triu(np.ones((P, P), np.float32), 1)
    a["starts"] = np.arange(TILES, dtype=np.float32) * P
    a["before"] = np.tril(np.ones((EXPERTS, EXPERTS), np.float32), -1).reshape(-1)
    a["numbers"] = np.arange(slot_tiles(2), dtype=np.float32)
    a["L0_ffn_gate_w"], a["L0_ffn_gate_bias"] = inputs["L0_ffn_gate_w"].T, inputs["L0_ffn_gate_bias"]

    def by_rows(w, chunks):
        w = w.reshape(-1, w.shape[-2], chunks, P)
        return w.transpose(3, 0, 2, 1)

    up = np.concatenate([inputs["L0_ffn_w1"], inputs["L0_ffn_w3"]], axis=1)
    experts = np.concatenate([by_rows(up, KD).reshape(P, EXPERTS, -1),
                              by_rows(inputs["L0_ffn_w2"], KD).reshape(P, EXPERTS, -1)], axis=2)
    up = np.concatenate([inputs["L0_ffn_sw1"], inputs["L0_ffn_sw3"]], axis=0)
    a["L0_ffn_weights"] = np.concatenate([experts.reshape(P, -1), by_rows(up, KD).reshape(P, -1),
                                          by_rows(inputs["L0_ffn_sw2"], 4).reshape(P, -1)], axis=1)
    a["L1_ffn_centroids"] = inputs["L1_ffn_centroids"].T
    a["L1_ffn_b2"] = inputs["L1_ffn_b2"]
    a["L1_ffn_columns"] = np.concatenate([inputs[f"L1_ffn_{n}"].reshape(EXPERTS, -1, P) for n in ("ln_g", "ln_b", "b1")],
                                         axis=1).transpose(2, 0, 1)
    a["L1_ffn_weights"] = np.concatenate(
        [inputs[f"L1_ffn_{n}"].reshape(EXPERTS, -1, P, inputs[f"L1_ffn_{n}"].shape[2]).transpose(2, 0, 1, 3)
         .reshape(P, EXPERTS, -1) for n in ("w1", "w2")], axis=2).reshape(P, -1)
    return {n: np.ascontiguousarray(v) for n, v in a.items()}


def kernel(**inputs):
    import numpy as np
    import concourse.bacc as bacc
    from concourse.bass_utils import run_bass_kernel_spmd

    nc = bacc.Bacc("TRN2", target_bir_lowering=False, num_devices=1)
    arrays = {f"in_{n}": v for n, v in lay_out({n: np.asarray(v) for n, v in inputs.items()}).items()}
    places = {n[len("in_"):]: nc.dram_tensor(n, v.shape, mybir.dt.from_np(v.dtype), kind="ExternalInput").ap()
              for n, v in arrays.items()}
    out = nc.dram_tensor("out_x", [TOKENS, DIM], F32, kind="ExternalOutput").ap()
    program(nc, places, out)
    result = run_bass_kernel_spmd(nc, [arrays], core_ids=[0])
    return result.results[0]["out_x"].reshape(BATCH, SEQ, DIM)
```
